# Optimizing a Trainium2 kernel written in Bass

```python
import numpy as np
import jax
import jax.numpy as jnp

def _softmax(x, axis=-1):
    return jax.nn.softmax(x, axis=axis)

def _gelu(x):
    return jax.nn.gelu(x, approximate=True)

def _silu(x):
    return jax.nn.silu(x)

def _sigmoid(x):
    return jax.nn.sigmoid(x)

def _layernorm(x, axis=-1, eps=1e-05):
    m = jnp.mean(x, axis=axis, keepdims=True)
    v = jnp.var(x, axis=axis, keepdims=True)
    return (x - m) / jnp.sqrt(v + eps)

def _scatter_add(tgt, idx, src, axis=0):
    return tgt.at[idx].add(src)

def _segment_sum(src, seg, n):
    return jax.ops.segment_sum(src, seg, n)
kernel_name = 'mk_gnn_resnorm_d4_gnn_r64_dad18a'

def setup_inputs(seed: int=0):
    np.random.seed(seed)
    _w = jnp.asarray

    def _rec_inputs():
        import jax
        import jax.numpy as jnp
        _gk = jax.random.key(seed)
        x = -0.000202 + 1 * jax.random.normal(jax.random.fold_in(_gk, 1), (50000, 160), jnp.float32)
        src = jax.random.randint(jax.random.fold_in(_gk, 2), (25000,), 0, 50000, jnp.int32)
        dst = jax.random.randint(jax.random.fold_in(_gk, 3), (25000,), 0, 50000, jnp.int32)
        _o = jnp.argsort(dst, stable=True)
        src = src[_o]
        dst = dst[_o]
        edge_attr_3 = 0.00262751 + 0.999568 * jax.random.normal(jax.random.fold_in(_gk, 12), (25000, 3), jnp.float32)
        edge_attr_4 = -0.000414295 + 0.999828 * jax.random.normal(jax.random.fold_in(_gk, 13), (25000, 4), jnp.float32)
        edge_attr_64 = jax.random.uniform(jax.random.fold_in(_gk, 14), (25000, 64), jnp.float32, 0.0, 1)
        edge_attr_8 = jax.random.uniform(jax.random.fold_in(_gk, 15), (25000, 8), jnp.float32, 0.0, 1)
        node_vec1 = jax.random.uniform(jax.random.fold_in(_gk, 17), (50000, 1), jnp.float32, 0.0, 1)
        return (x, src, dst, edge_attr_3, edge_attr_4, edge_attr_64, edge_attr_8, node_vec1)
    x, src, dst, edge_attr_3, edge_attr_4, edge_attr_64, edge_attr_8, node_vec1 = _rec_inputs()

    def _L0_gnn_setup():
        import jax, jax.numpy as jnp
        import numpy as np
        N = 625
        E = 6250
        MUL0, MUL1 = (64, 32)
        RAD, HID = (8, 64)
        WNUM = 192
        NUM_NEIGHBORS = 10.0
        INV3 = 1.0 / np.sqrt(3.0)

        def _lin(s, v, Ws, Wv, attr):
            out_s = s @ Ws * attr * (1.0 / np.sqrt(Ws.shape[0]))
            out_v = jnp.einsum('nud,uv->nvd', v, Wv) * attr[..., None] * (1.0 / np.sqrt(Wv.shape[0]))
            return (out_s, out_v)
        key = jax.random.key(seed)
        ks = jax.random.split(key, 16)
        return {'node_input': jax.random.normal(ks[0], (N, MUL0 + 3 * MUL1), jnp.float32), 'node_attr': jnp.ones((N, 1), jnp.float32), 'edge_attr': jax.random.normal(ks[1], (E, 4), jnp.float32), 'edge_scalars': jax.random.uniform(ks[2], (E, RAD), jnp.float32), 'W_sc_s': jax.random.normal(ks[3], (MUL0, MUL0), jnp.float32), 'W_sc_v': jax.random.normal(ks[4], (MUL1, MUL1), jnp.float32), 'W1_s': jax.random.normal(ks[5], (MUL0, MUL0), jnp.float32), 'W1_v': jax.random.normal(ks[6], (MUL1, MUL1), jnp.float32), 'W2_s': jax.random.normal(ks[7], (MUL0 + MUL1, MUL0), jnp.float32), 'W2_v': jax.random.normal(ks[8], (MUL0 + MUL1, MUL1), jnp.float32), 'W3': jax.random.normal(ks[9], (MUL0 + MUL1, 1), jnp.float32), 'fcW1': jax.random.normal(ks[10], (RAD, HID), jnp.float32), 'fcW2': jax.random.normal(ks[11], (HID, WNUM), jnp.float32), 'edge_src': jax.random.randint(ks[12], (E,), 0, N, jnp.int32), 'edge_dst': jax.random.randint(ks[13], (E,), 0, N, jnp.int32)}
    _L0_gnn_all = _L0_gnn_setup()
    _L0_gnn_in = {k: v for k, v in _L0_gnn_all.items() if k in ('W_sc_s', 'W_sc_v', 'W1_s', 'W1_v', 'W2_s', 'W2_v', 'W3', 'fcW1', 'fcW2')}
    del _L0_gnn_all

    def _L1_gnn_setup():
        import jax, jax.numpy as jnp
        import numpy as np
        N_NODES = 10000
        N_EDGES = 5000
        NUM_NEIGHBORS = 32.0
        INV_SQRT3 = 1.0 / np.sqrt(3.0)

        def _fctp_scalar_attr(xs, xv, Ws, Wv, a):
            out_s = xs @ Ws * (a / np.sqrt(xs.shape[1]))[:, None]
            out_v = jnp.einsum('nuc,uw->nwc', xv, Wv) * (a / np.sqrt(xv.shape[1]))[:, None, None]
            return (out_s, out_v)
        key = jax.random.key(seed)
        ks = jax.random.split(key, 16)
        f32 = jnp.float32
        return {'node_input': jax.random.normal(ks[0], (N_NODES, 160), f32), 'node_attr': jnp.ones((N_NODES, 1), f32), 'edge_attr': jax.random.normal(ks[1], (N_EDGES, 4), f32), 'edge_scalar_attr': jax.random.normal(ks[2], (N_EDGES, 8), f32), 'Wsc0': jax.random.normal(ks[3], (64, 64), f32), 'Wsc1': jax.random.normal(ks[4], (32, 32), f32), 'Wl1_0': jax.random.normal(ks[5], (64, 64), f32), 'Wl1_1': jax.random.normal(ks[6], (32, 32), f32), 'Wfc1': jax.random.normal(ks[7], (8, 64), f32), 'Wfc2': jax.random.normal(ks[8], (64, 64), f32), 'Wfc3': jax.random.normal(ks[9], (64, 192), f32), 'Wl2_s': jax.random.normal(ks[10], (96, 64), f32), 'Wl2_v': jax.random.normal(ks[11], (96, 32), f32), 'Wa': jax.random.normal(ks[12], (96, 1), f32), 'edge_src': jax.random.randint(ks[13], (N_EDGES,), 0, N_NODES), 'edge_dst': jax.random.randint(ks[14], (N_EDGES,), 0, N_NODES)}
    _L1_gnn_all = _L1_gnn_setup()
    _L1_gnn_in = {k: v for k, v in _L1_gnn_all.items() if k in ('Wsc0', 'Wsc1', 'Wl1_0', 'Wl1_1', 'Wfc1', 'Wfc2', 'Wfc3', 'Wl2_s', 'Wl2_v', 'Wa')}
    del _L1_gnn_all

    def _L2_gnn_setup():
        import jax, jax.numpy as jnp
        import numpy as np
        N, E = (10000, 2500)
        C0, C1 = (64, 32)
        H, A = (8, 8)
        H0, H1 = (8, 4)
        M0, M1 = (128, 64)
        NG, RH = (64, 64)
        WN = C0 + C0 + C1 + C1 + C1
        DS, DV = (C0 + C1, C0 + 2 * C1)
        EPS = 1e-05
        SQ3 = np.float32(np.sqrt(3.0))
        SQ2 = np.float32(np.sqrt(2.0))

        def _split(x):
            return (x[:, :C0], x[:, C0:].reshape(x.shape[0], C1, 3))

        def _merge(s, v):
            return jnp.concatenate([s, v.reshape(v.shape[0], -1)], axis=1)

        def _eq_ln(x, w0, b0, w1):
            s, v = _split(x)
            s = s - s.mean(axis=1, keepdims=True)
            s = s * jax.lax.rsqrt(jnp.square(s).mean(axis=1, keepdims=True) + EPS) * w0 + b0
            v = v * jax.lax.rsqrt(jnp.square(v).mean(axis=(1, 2), keepdims=True) + EPS) * w1[None, :, None]
            return (s, v)

        def _eq_lin(s, v, ws, bs, wv):
            return (s @ ws + bs, jnp.einsum('nud,uk->nkd', v, wv))

        def _ln(x, g, b):
            xc = x - x.mean(-1, keepdims=True)
            return xc * jax.lax.rsqrt(jnp.square(xc).mean(-1, keepdims=True) + EPS) * g + b

        def _smooth_leaky(x, alpha=0.2):
            return 0.5 * (1 + alpha) * x + 0.5 * (1 - alpha) * x * (2.0 * jax.nn.sigmoid(x) - 1.0)

        def _forward(node_input, node_attr, edge_vec, edge_scalars, edge_src, edge_dst, ln1_w0, ln1_b0, ln1_w1, ln2_w0, ln2_b0, ln2_w1, msrc_ws, msrc_wv, mdst_ws, mdst_bs, mdst_wv, rw1, rb1, rg1, rbe1, rw2, rb2, rg2, rbe2, rw3, roff, lin_ws, lin_bs, lin_wv, alpha_dot, proj_ws, proj_bs, proj_wv, f1_ws, f1_bs, f1_wv, f2_ws, f2_bs, f2_wv):
            n = node_input.shape[0]
            s, v = _eq_ln(node_input, ln1_w0, ln1_b0, ln1_w1)
            src_s = s @ msrc_ws
            src_v = jnp.einsum('nud,uk->nkd', v, msrc_wv)
            dst_s = s @ mdst_ws + mdst_bs
            dst_v = jnp.einsum('nud,uk->nkd', v, mdst_wv)
            ms = src_s[edge_src] + dst_s[edge_dst]
            mv = src_v[edge_src] + dst_v[edge_dst]
            h = jax.nn.silu(_ln(edge_scalars @ rw1 + rb1, rg1, rbe1))
            h = jax.nn.silu(_ln(h @ rw2 + rb2, rg2, rbe2))
            w = h @ rw3 + roff
            rhat = edge_vec * jax.lax.rsqrt(jnp.sum(jnp.square(edge_vec), -1, keepdims=True) + 1e-12)
            Y1 = SQ3 * rhat
            w1, w2, w3, w4, w5 = jnp.split(w, [C0, 2 * C0, 2 * C0 + C1, 2 * C0 + 2 * C1], axis=1)
            o0a = w1 * ms
            o0b = w4 * (jnp.einsum('eud,ed->eu', mv, Y1) / SQ3)
            o1a = (w2 * ms)[:, :, None] * Y1[:, None, :]
            o1b = w3[:, :, None] * mv
            o1c = w5[:, :, None] * (jnp.cross(mv, Y1[:, None, :]) / SQ2)
            ds = jnp.concatenate([o0a, o0b], axis=1)
            dv = jnp.concatenate([o1a, o1b, o1c], axis=1)
            ls, lv = _eq_lin(ds, dv, lin_ws, lin_bs, lin_wv)
            e = ls.shape[0]
            alpha = ls[:, :H * A].reshape(e, H, A)
            vs = ls[:, H * A:].reshape(e, H, H0)
            vv = lv.reshape(e, H, H1, 3)
            a = jnp.einsum('ehk,hk->eh', _smooth_leaky(alpha), alpha_dot)
            amax = jax.lax.stop_gradient(jax.ops.segment_max(a, edge_dst, num_segments=n))
            a = jnp.exp(a - amax[edge_dst])
            a = a / (jax.ops.segment_sum(a, edge_dst, num_segments=n)[edge_dst] + 1e-12)
            ns = jax.ops.segment_sum(vs * a[..., None], edge_dst, num_segments=n).reshape(n, H * H0)
            nv = jax.ops.segment_sum(vv * a[..., None, None], edge_dst, num_segments=n).reshape(n, H * H1, 3)
            ps, pv = _eq_lin(ns, nv, proj_ws, proj_bs, proj_wv)
            x = node_input + _merge(ps, pv)
            s2, v2 = _eq_ln(x, ln2_w0, ln2_b0, ln2_w1)
            a0 = node_attr[:, :1]
            fs, fv = _eq_lin(s2, v2, f1_ws, f1_bs, f1_wv)
            fs = fs * a0
            fv = fv * a0[:, :, None]
            sc = jax.nn.silu(fs[:, :M0])
            fv = fv * jax.nn.sigmoid(fs[:, M0:])[:, :, None]
            os_, ov = _eq_lin(sc, fv, f2_ws, f2_bs, f2_wv)
            os_ = os_ * a0
            ov = ov * a0[:, :, None]
            return x + _merge(os_, ov)
        key = jax.random.key(seed)
        ks = iter(jax.random.split(key, 24))

        def nrm(shape, fan):
            return jax.random.normal(next(ks), shape, jnp.float32) / np.float32(np.sqrt(fan))
        inp = {}
        inp['node_input'] = jax.random.normal(next(ks), (N, C0 + 3 * C1), jnp.float32)
        inp['node_attr'] = jnp.ones((N, 1), jnp.float32)
        inp['edge_vec'] = jax.random.normal(next(ks), (E, 3), jnp.float32)
        inp['edge_scalars'] = jax.random.uniform(next(ks), (E, NG), dtype=jnp.float32)
        inp['edge_src'] = jax.random.randint(next(ks), (E,), 0, N)
        inp['edge_dst'] = jax.random.randint(next(ks), (E,), 0, N)
        inp['ln1_w0'] = jnp.ones((C0,), jnp.float32)
        inp['ln1_b0'] = jnp.zeros((C0,), jnp.float32)
        inp['ln1_w1'] = jnp.ones((C1,), jnp.float32)
        inp['ln2_w0'] = jnp.ones((C0,), jnp.float32)
        inp['ln2_b0'] = jnp.zeros((C0,), jnp.float32)
        inp['ln2_w1'] = jnp.ones((C1,), jnp.float32)
        inp['msrc_ws'] = nrm((C0, C0), C0)
        inp['msrc_wv'] = nrm((C1, C1), C1)
        inp['mdst_ws'] = nrm((C0, C0), C0)
        inp['mdst_bs'] = jnp.zeros((C0,), jnp.float32)
        inp['mdst_wv'] = nrm((C1, C1), C1)
        inp['rw1'] = nrm((NG, RH), NG)
        inp['rb1'] = jnp.zeros((RH,), jnp.float32)
        inp['rg1'] = jnp.ones((RH,), jnp.float32)
        inp['rbe1'] = jnp.zeros((RH,), jnp.float32)
        inp['rw2'] = nrm((RH, RH), RH)
        inp['rb2'] = jnp.zeros((RH,), jnp.float32)
        inp['rg2'] = jnp.ones((RH,), jnp.float32)
        inp['rbe2'] = jnp.zeros((RH,), jnp.float32)
        inp['rw3'] = nrm((RH, WN), RH)
        inp['roff'] = 0.1 * jax.random.normal(next(ks), (WN,), jnp.float32)
        inp['lin_ws'] = nrm((DS, H * A + H * H0), DS)
        inp['lin_bs'] = jnp.zeros((H * A + H * H0,), jnp.float32)
        inp['lin_wv'] = nrm((DV, H * H1), DV)
        inp['alpha_dot'] = nrm((H, A), A)
        inp['proj_ws'] = nrm((H * H0, C0), H * H0)
        inp['proj_bs'] = jnp.zeros((C0,), jnp.float32)
        inp['proj_wv'] = nrm((H * H1, C1), H * H1)
        inp['f1_ws'] = nrm((C0, M0 + M1), C0)
        inp['f1_bs'] = jnp.zeros((M0 + M1,), jnp.float32)
        inp['f1_wv'] = nrm((C1, M1), C1)
        inp['f2_ws'] = nrm((M0, C0), M0)
        inp['f2_bs'] = jnp.zeros((C0,), jnp.float32)
        inp['f2_wv'] = nrm((M1, C1), M1)
        return inp
    _L2_gnn_all = _L2_gnn_setup()
    _L2_gnn_in = {k: v for k, v in _L2_gnn_all.items() if k in ('ln1_w0', 'ln1_b0', 'ln1_w1', 'ln2_w0', 'ln2_b0', 'ln2_w1', 'msrc_ws', 'msrc_wv', 'mdst_ws', 'mdst_bs', 'mdst_wv', 'rw1', 'rb1', 'rg1', 'rbe1', 'rw2', 'rb2', 'rg2', 'rbe2', 'rw3', 'roff', 'lin_ws', 'lin_bs', 'lin_wv', 'alpha_dot', 'proj_ws', 'proj_bs', 'proj_wv', 'f1_ws', 'f1_bs', 'f1_wv', 'f2_ws', 'f2_bs', 'f2_wv')}
    del _L2_gnn_all

    def _L3_gnn_setup():
        import jax, jax.numpy as jnp
        import numpy as np
        N_NODES = 10000
        N_EDGES = 5000
        MUL0, MUL1 = (64, 32)
        EDGE_DIM = 64
        W_NUMEL = 224
        DENOM = 32.0
        SQRT3 = 3.0 ** 0.5
        INV_SQRT3 = 1.0 / SQRT3
        INV_SQRT2 = 2.0 ** (-0.5)

        def _forward(node_feature, edge_attr, edge_feature, W_skip0, W_skip1, W_nl0, W_nl1, W_fc1, W_fc2, W_out_s, W_out_v, edge_index):
            N = node_feature.shape[0]
            E = edge_attr.shape[0]
            s = node_feature[:, :MUL0]
            v = node_feature[:, MUL0:].reshape(N, MUL1, 3)
            skip_s = s @ W_skip0
            skip_v = jnp.einsum('nmi,mk->nki', v, W_skip1)
            s = s @ W_nl0
            v = jnp.einsum('nmi,mk->nki', v, W_nl1)
            rhat = edge_attr / jnp.linalg.norm(edge_attr, axis=-1, keepdims=True)
            sh1 = SQRT3 * rhat
            w = jax.nn.relu(edge_feature @ W_fc1) @ W_fc2
            w0, w1, w2, w3, w4 = jnp.split(w, [64, 128, 160, 192], axis=-1)
            src, dst = (edge_index[0], edge_index[1])
            xs = s[dst]
            xv = v[dst]
            out0a = w0 * xs
            out0b = w3 * (jnp.einsum('emi,ei->em', xv, sh1) * INV_SQRT3)
            out1a = (w1 * xs)[:, :, None] * sh1[:, None, :]
            out1b = w2[:, :, None] * xv
            out1c = w4[:, :, None] * (jnp.cross(xv, sh1[:, None, :]) * INV_SQRT2)
            tp = jnp.concatenate([out0a, out0b, out1a.reshape(E, -1), out1b.reshape(E, -1), out1c.reshape(E, -1)], axis=-1)
            agg = jax.ops.segment_sum(tp, src, num_segments=N) / DENOM
            agg_s = agg[:, :96]
            agg_v = agg[:, 96:].reshape(N, 128, 3)
            out_s = agg_s @ W_out_s + skip_s
            out_v = jnp.einsum('nmi,mk->nki', agg_v, W_out_v) + skip_v
            fs = jax.nn.silu(out_s[:, :MUL0])
            gate = jax.nn.sigmoid(out_s[:, MUL0:MUL0 + 32])
            gv = gate[:, :, None] * out_v
            return jnp.concatenate([fs, gv.reshape(N, -1)], axis=-1)
        key = jax.random.key(seed)
        ks = jax.random.split(key, 12)

        def lin(k, fi, fo):
            return jax.random.normal(k, (fi, fo), jnp.float32) / np.float32(np.sqrt(fi))
        return {'node_feature': jax.random.normal(ks[0], (N_NODES, MUL0 + 3 * MUL1), jnp.float32), 'edge_attr': jax.random.normal(ks[1], (N_EDGES, 3), jnp.float32), 'edge_feature': jax.random.normal(ks[2], (N_EDGES, EDGE_DIM), jnp.float32), 'W_skip0': lin(ks[3], MUL0, 96), 'W_skip1': lin(ks[4], MUL1, 32), 'W_nl0': lin(ks[5], MUL0, MUL0), 'W_nl1': lin(ks[6], MUL1, MUL1), 'W_fc1': lin(ks[7], EDGE_DIM, 64), 'W_fc2': lin(ks[8], 64, W_NUMEL), 'W_out_s': lin(ks[9], 96, 96), 'W_out_v': lin(ks[10], 128, 32), 'edge_index': jax.random.randint(ks[11], (2, N_EDGES), 0, N_NODES)}
    _L3_gnn_all = _L3_gnn_setup()
    _L3_gnn_in = {k: v for k, v in _L3_gnn_all.items() if k in ('W_skip0', 'W_skip1', 'W_nl0', 'W_nl1', 'W_fc1', 'W_fc2', 'W_out_s', 'W_out_v')}
    del _L3_gnn_all
    return {'x': x, 'src': src, 'dst': dst, 'edge_attr_3': edge_attr_3, 'edge_attr_4': edge_attr_4, 'edge_attr_64': edge_attr_64, 'edge_attr_8': edge_attr_8, 'node_vec1': node_vec1, 'L0_gnn_W_sc_s': _L0_gnn_in['W_sc_s'], 'L0_gnn_W_sc_v': _L0_gnn_in['W_sc_v'], 'L0_gnn_W1_s': _L0_gnn_in['W1_s'], 'L0_gnn_W1_v': _L0_gnn_in['W1_v'], 'L0_gnn_W2_s': _L0_gnn_in['W2_s'], 'L0_gnn_W2_v': _L0_gnn_in['W2_v'], 'L0_gnn_W3': _L0_gnn_in['W3'], 'L0_gnn_fcW1': _L0_gnn_in['fcW1'], 'L0_gnn_fcW2': _L0_gnn_in['fcW2'], 'L1_gnn_Wsc0': _L1_gnn_in['Wsc0'], 'L1_gnn_Wsc1': _L1_gnn_in['Wsc1'], 'L1_gnn_Wl1_0': _L1_gnn_in['Wl1_0'], 'L1_gnn_Wl1_1': _L1_gnn_in['Wl1_1'], 'L1_gnn_Wfc1': _L1_gnn_in['Wfc1'], 'L1_gnn_Wfc2': _L1_gnn_in['Wfc2'], 'L1_gnn_Wfc3': _L1_gnn_in['Wfc3'], 'L1_gnn_Wl2_s': _L1_gnn_in['Wl2_s'], 'L1_gnn_Wl2_v': _L1_gnn_in['Wl2_v'], 'L1_gnn_Wa': _L1_gnn_in['Wa'], 'L2_gnn_ln1_w0': _L2_gnn_in['ln1_w0'], 'L2_gnn_ln1_b0': _L2_gnn_in['ln1_b0'], 'L2_gnn_ln1_w1': _L2_gnn_in['ln1_w1'], 'L2_gnn_ln2_w0': _L2_gnn_in['ln2_w0'], 'L2_gnn_ln2_b0': _L2_gnn_in['ln2_b0'], 'L2_gnn_ln2_w1': _L2_gnn_in['ln2_w1'], 'L2_gnn_msrc_ws': _L2_gnn_in['msrc_ws'], 'L2_gnn_msrc_wv': _L2_gnn_in['msrc_wv'], 'L2_gnn_mdst_ws': _L2_gnn_in['mdst_ws'], 'L2_gnn_mdst_bs': _L2_gnn_in['mdst_bs'], 'L2_gnn_mdst_wv': _L2_gnn_in['mdst_wv'], 'L2_gnn_rw1': _L2_gnn_in['rw1'], 'L2_gnn_rb1': _L2_gnn_in['rb1'], 'L2_gnn_rg1': _L2_gnn_in['rg1'], 'L2_gnn_rbe1': _L2_gnn_in['rbe1'], 'L2_gnn_rw2': _L2_gnn_in['rw2'], 'L2_gnn_rb2': _L2_gnn_in['rb2'], 'L2_gnn_rg2': _L2_gnn_in['rg2'], 'L2_gnn_rbe2': _L2_gnn_in['rbe2'], 'L2_gnn_rw3': _L2_gnn_in['rw3'], 'L2_gnn_roff': _L2_gnn_in['roff'], 'L2_gnn_lin_ws': _L2_gnn_in['lin_ws'], 'L2_gnn_lin_bs': _L2_gnn_in['lin_bs'], 'L2_gnn_lin_wv': _L2_gnn_in['lin_wv'], 'L2_gnn_alpha_dot': _L2_gnn_in['alpha_dot'], 'L2_gnn_proj_ws': _L2_gnn_in['proj_ws'], 'L2_gnn_proj_bs': _L2_gnn_in['proj_bs'], 'L2_gnn_proj_wv': _L2_gnn_in['proj_wv'], 'L2_gnn_f1_ws': _L2_gnn_in['f1_ws'], 'L2_gnn_f1_bs': _L2_gnn_in['f1_bs'], 'L2_gnn_f1_wv': _L2_gnn_in['f1_wv'], 'L2_gnn_f2_ws': _L2_gnn_in['f2_ws'], 'L2_gnn_f2_bs': _L2_gnn_in['f2_bs'], 'L2_gnn_f2_wv': _L2_gnn_in['f2_wv'], 'L3_gnn_W_skip0': _L3_gnn_in['W_skip0'], 'L3_gnn_W_skip1': _L3_gnn_in['W_skip1'], 'L3_gnn_W_nl0': _L3_gnn_in['W_nl0'], 'L3_gnn_W_nl1': _L3_gnn_in['W_nl1'], 'L3_gnn_W_fc1': _L3_gnn_in['W_fc1'], 'L3_gnn_W_fc2': _L3_gnn_in['W_fc2'], 'L3_gnn_W_out_s': _L3_gnn_in['W_out_s'], 'L3_gnn_W_out_v': _L3_gnn_in['W_out_v']}

def reference(x, src, dst, edge_attr_3, edge_attr_4, edge_attr_64, edge_attr_8, node_vec1, L0_gnn_W_sc_s, L0_gnn_W_sc_v, L0_gnn_W1_s, L0_gnn_W1_v, L0_gnn_W2_s, L0_gnn_W2_v, L0_gnn_W3, L0_gnn_fcW1, L0_gnn_fcW2, L1_gnn_Wsc0, L1_gnn_Wsc1, L1_gnn_Wl1_0, L1_gnn_Wl1_1, L1_gnn_Wfc1, L1_gnn_Wfc2, L1_gnn_Wfc3, L1_gnn_Wl2_s, L1_gnn_Wl2_v, L1_gnn_Wa, L2_gnn_ln1_w0, L2_gnn_ln1_b0, L2_gnn_ln1_w1, L2_gnn_ln2_w0, L2_gnn_ln2_b0, L2_gnn_ln2_w1, L2_gnn_msrc_ws, L2_gnn_msrc_wv, L2_gnn_mdst_ws, L2_gnn_mdst_bs, L2_gnn_mdst_wv, L2_gnn_rw1, L2_gnn_rb1, L2_gnn_rg1, L2_gnn_rbe1, L2_gnn_rw2, L2_gnn_rb2, L2_gnn_rg2, L2_gnn_rbe2, L2_gnn_rw3, L2_gnn_roff, L2_gnn_lin_ws, L2_gnn_lin_bs, L2_gnn_lin_wv, L2_gnn_alpha_dot, L2_gnn_proj_ws, L2_gnn_proj_bs, L2_gnn_proj_wv, L2_gnn_f1_ws, L2_gnn_f1_bs, L2_gnn_f1_wv, L2_gnn_f2_ws, L2_gnn_f2_bs, L2_gnn_f2_wv, L3_gnn_W_skip0, L3_gnn_W_skip1, L3_gnn_W_nl0, L3_gnn_W_nl1, L3_gnn_W_fc1, L3_gnn_W_fc2, L3_gnn_W_out_s, L3_gnn_W_out_v):
    import jax
    import jax.numpy as jnp

    def _L0_gnn_ref(node_input, node_attr, edge_attr, edge_scalars, W_sc_s, W_sc_v, W1_s, W1_v, W2_s, W2_v, W3, fcW1, fcW2, edge_src, edge_dst):
        import jax, jax.numpy as jnp
        import numpy as np
        N = 625
        E = 6250
        MUL0, MUL1 = (64, 32)
        RAD, HID = (8, 64)
        WNUM = 192
        NUM_NEIGHBORS = 10.0
        INV3 = 1.0 / np.sqrt(3.0)

        def _lin(s, v, Ws, Wv, attr):
            out_s = s @ Ws * attr * (1.0 / np.sqrt(Ws.shape[0]))
            out_v = jnp.einsum('nud,uv->nvd', v, Wv) * attr[..., None] * (1.0 / np.sqrt(Wv.shape[0]))
            return (out_s, out_v)
        n = node_input.shape[0]
        s_in = node_input[:, :MUL0]
        v_in = node_input[:, MUL0:].reshape(n, MUL1, 3)
        sc_s, sc_v = _lin(s_in, v_in, W_sc_s, W_sc_v, node_attr)
        f_s, f_v = _lin(s_in, v_in, W1_s, W1_v, node_attr)
        h = jax.nn.silu(edge_scalars @ fcW1 * (1.0 / np.sqrt(RAD)))
        w = h @ fcW2 * (1.0 / np.sqrt(HID))
        wA, wB, wC, wD = (w[:, :64], w[:, 64:128], w[:, 128:160], w[:, 160:192])
        xs = f_s[edge_src]
        xv = f_v[edge_src]
        y0 = edge_attr[:, :1]
        y1 = edge_attr[:, 1:4]
        outA = wA * xs * y0
        outD = wD * jnp.einsum('eud,ed->eu', xv, y1) * INV3
        outB = wB[:, :, None] * xs[:, :, None] * y1[:, None, :]
        outC = wC[:, :, None] * xv * y0[:, :, None]
        edge_feat = jnp.concatenate([outA, outD, outB.reshape(-1, MUL0 * 3), outC.reshape(-1, MUL1 * 3)], axis=1)
        agg = jax.ops.segment_sum(edge_feat, edge_dst, num_segments=n)
        agg = agg * (1.0 / np.sqrt(NUM_NEIGHBORS))
        ms = agg[:, :MUL0 + MUL1]
        mv = agg[:, MUL0 + MUL1:].reshape(n, MUL0 + MUL1, 3)
        c_s, c_v = _lin(ms, mv, W2_s, W2_v, node_attr)
        conv = jnp.concatenate([c_s, c_v.reshape(n, -1)], axis=1)
        sc = jnp.concatenate([sc_s, sc_v.reshape(n, -1)], axis=1)
        angle = 0.1 * (ms @ W3) * node_attr * (1.0 / np.sqrt(MUL0 + MUL1))
        cos, sin = (jnp.cos(angle), jnp.sin(angle))
        return cos * sc + sin * conv

    def _L1_gnn_ref(node_input, node_attr, edge_attr, edge_scalar_attr, Wsc0, Wsc1, Wl1_0, Wl1_1, Wfc1, Wfc2, Wfc3, Wl2_s, Wl2_v, Wa, edge_src, edge_dst):
        import jax, jax.numpy as jnp
        import numpy as np
        N_NODES = 10000
        N_EDGES = 5000
        NUM_NEIGHBORS = 32.0
        INV_SQRT3 = 1.0 / np.sqrt(3.0)

        def _fctp_scalar_attr(xs, xv, Ws, Wv, a):
            out_s = xs @ Ws * (a / np.sqrt(xs.shape[1]))[:, None]
            out_v = jnp.einsum('nuc,uw->nwc', xv, Wv) * (a / np.sqrt(xv.shape[1]))[:, None, None]
            return (out_s, out_v)
        N = node_input.shape[0]
        a = node_attr[:, 0]
        xs = node_input[:, :64]
        xv = node_input[:, 64:].reshape(N, 32, 3)
        sc_s, sc_v = _fctp_scalar_attr(xs, xv, Wsc0, Wsc1, a)
        f_s, f_v = _fctp_scalar_attr(xs, xv, Wl1_0, Wl1_1, a)
        h = jax.nn.gelu(edge_scalar_attr @ Wfc1 / np.sqrt(8.0))
        h = jax.nn.gelu(h @ Wfc2 / np.sqrt(64.0))
        w = h @ Wfc3 / np.sqrt(64.0)
        w0, w1, w2, w3 = (w[:, :64], w[:, 64:128], w[:, 128:160], w[:, 160:192])
        gs = f_s[edge_src]
        gv = f_v[edge_src]
        y0 = edge_attr[:, 0]
        y1 = edge_attr[:, 1:4]
        mid0 = w0 * gs * y0[:, None]
        mid1 = w3 * jnp.einsum('euc,ec->eu', gv, y1) * INV_SQRT3
        mid2 = (w1 * gs)[:, :, None] * y1[:, None, :]
        mid3 = w2[:, :, None] * gv * y0[:, None, None]
        inv = 1.0 / np.sqrt(NUM_NEIGHBORS)
        seg = lambda x: jax.ops.segment_sum(x, edge_dst, num_segments=N) * inv
        ns0, ns1, nv2, nv3 = (seg(mid0), seg(mid1), seg(mid2), seg(mid3))
        mid_s = jnp.concatenate([ns0, ns1], axis=1)
        mid_v = jnp.concatenate([nv2, nv3], axis=1)
        out_s = mid_s @ Wl2_s * (a / np.sqrt(96.0))[:, None]
        out_v = jnp.einsum('nuc,uw->nwc', mid_v, Wl2_v) * (a / np.sqrt(96.0))[:, None, None]
        alpha = mid_s @ Wa * (a / np.sqrt(96.0))[:, None]
        res_s = sc_s + alpha * out_s
        res_v = sc_v + alpha[:, :, None] * out_v
        return jnp.concatenate([res_s, res_v.reshape(N, 96)], axis=1)

    def _L2_gnn_ref(node_input, node_attr, edge_vec, edge_scalars, edge_src, edge_dst, ln1_w0, ln1_b0, ln1_w1, ln2_w0, ln2_b0, ln2_w1, msrc_ws, msrc_wv, mdst_ws, mdst_bs, mdst_wv, rw1, rb1, rg1, rbe1, rw2, rb2, rg2, rbe2, rw3, roff, lin_ws, lin_bs, lin_wv, alpha_dot, proj_ws, proj_bs, proj_wv, f1_ws, f1_bs, f1_wv, f2_ws, f2_bs, f2_wv):
        import jax, jax.numpy as jnp
        import numpy as np
        N, E = (10000, 2500)
        C0, C1 = (64, 32)
        H, A = (8, 8)
        H0, H1 = (8, 4)
        M0, M1 = (128, 64)
        NG, RH = (64, 64)
        WN = C0 + C0 + C1 + C1 + C1
        DS, DV = (C0 + C1, C0 + 2 * C1)
        EPS = 1e-05
        SQ3 = np.float32(np.sqrt(3.0))
        SQ2 = np.float32(np.sqrt(2.0))

        def _split(x):
            return (x[:, :C0], x[:, C0:].reshape(x.shape[0], C1, 3))

        def _merge(s, v):
            return jnp.concatenate([s, v.reshape(v.shape[0], -1)], axis=1)

        def _eq_ln(x, w0, b0, w1):
            s, v = _split(x)
            s = s - s.mean(axis=1, keepdims=True)
            s = s * jax.lax.rsqrt(jnp.square(s).mean(axis=1, keepdims=True) + EPS) * w0 + b0
            v = v * jax.lax.rsqrt(jnp.square(v).mean(axis=(1, 2), keepdims=True) + EPS) * w1[None, :, None]
            return (s, v)

        def _eq_lin(s, v, ws, bs, wv):
            return (s @ ws + bs, jnp.einsum('nud,uk->nkd', v, wv))

        def _ln(x, g, b):
            xc = x - x.mean(-1, keepdims=True)
            return xc * jax.lax.rsqrt(jnp.square(xc).mean(-1, keepdims=True) + EPS) * g + b

        def _smooth_leaky(x, alpha=0.2):
            return 0.5 * (1 + alpha) * x + 0.5 * (1 - alpha) * x * (2.0 * jax.nn.sigmoid(x) - 1.0)

        def _forward(node_input, node_attr, edge_vec, edge_scalars, edge_src, edge_dst, ln1_w0, ln1_b0, ln1_w1, ln2_w0, ln2_b0, ln2_w1, msrc_ws, msrc_wv, mdst_ws, mdst_bs, mdst_wv, rw1, rb1, rg1, rbe1, rw2, rb2, rg2, rbe2, rw3, roff, lin_ws, lin_bs, lin_wv, alpha_dot, proj_ws, proj_bs, proj_wv, f1_ws, f1_bs, f1_wv, f2_ws, f2_bs, f2_wv):
            n = node_input.shape[0]
            s, v = _eq_ln(node_input, ln1_w0, ln1_b0, ln1_w1)
            src_s = s @ msrc_ws
            src_v = jnp.einsum('nud,uk->nkd', v, msrc_wv)
            dst_s = s @ mdst_ws + mdst_bs
            dst_v = jnp.einsum('nud,uk->nkd', v, mdst_wv)
            ms = src_s[edge_src] + dst_s[edge_dst]
            mv = src_v[edge_src] + dst_v[edge_dst]
            h = jax.nn.silu(_ln(edge_scalars @ rw1 + rb1, rg1, rbe1))
            h = jax.nn.silu(_ln(h @ rw2 + rb2, rg2, rbe2))
            w = h @ rw3 + roff
            rhat = edge_vec * jax.lax.rsqrt(jnp.sum(jnp.square(edge_vec), -1, keepdims=True) + 1e-12)
            Y1 = SQ3 * rhat
            w1, w2, w3, w4, w5 = jnp.split(w, [C0, 2 * C0, 2 * C0 + C1, 2 * C0 + 2 * C1], axis=1)
            o0a = w1 * ms
            o0b = w4 * (jnp.einsum('eud,ed->eu', mv, Y1) / SQ3)
            o1a = (w2 * ms)[:, :, None] * Y1[:, None, :]
            o1b = w3[:, :, None] * mv
            o1c = w5[:, :, None] * (jnp.cross(mv, Y1[:, None, :]) / SQ2)
            ds = jnp.concatenate([o0a, o0b], axis=1)
            dv = jnp.concatenate([o1a, o1b, o1c], axis=1)
            ls, lv = _eq_lin(ds, dv, lin_ws, lin_bs, lin_wv)
            e = ls.shape[0]
            alpha = ls[:, :H * A].reshape(e, H, A)
            vs = ls[:, H * A:].reshape(e, H, H0)
            vv = lv.reshape(e, H, H1, 3)
            a = jnp.einsum('ehk,hk->eh', _smooth_leaky(alpha), alpha_dot)
            amax = jax.lax.stop_gradient(jax.ops.segment_max(a, edge_dst, num_segments=n))
            a = jnp.exp(a - amax[edge_dst])
            a = a / (jax.ops.segment_sum(a, edge_dst, num_segments=n)[edge_dst] + 1e-12)
            ns = jax.ops.segment_sum(vs * a[..., None], edge_dst, num_segments=n).reshape(n, H * H0)
            nv = jax.ops.segment_sum(vv * a[..., None, None], edge_dst, num_segments=n).reshape(n, H * H1, 3)
            ps, pv = _eq_lin(ns, nv, proj_ws, proj_bs, proj_wv)
            x = node_input + _merge(ps, pv)
            s2, v2 = _eq_ln(x, ln2_w0, ln2_b0, ln2_w1)
            a0 = node_attr[:, :1]
            fs, fv = _eq_lin(s2, v2, f1_ws, f1_bs, f1_wv)
            fs = fs * a0
            fv = fv * a0[:, :, None]
            sc = jax.nn.silu(fs[:, :M0])
            fv = fv * jax.nn.sigmoid(fs[:, M0:])[:, :, None]
            os_, ov = _eq_lin(sc, fv, f2_ws, f2_bs, f2_wv)
            os_ = os_ * a0
            ov = ov * a0[:, :, None]
            return x + _merge(os_, ov)
        return _forward(node_input, node_attr, edge_vec, edge_scalars, edge_src, edge_dst, ln1_w0, ln1_b0, ln1_w1, ln2_w0, ln2_b0, ln2_w1, msrc_ws, msrc_wv, mdst_ws, mdst_bs, mdst_wv, rw1, rb1, rg1, rbe1, rw2, rb2, rg2, rbe2, rw3, roff, lin_ws, lin_bs, lin_wv, alpha_dot, proj_ws, proj_bs, proj_wv, f1_ws, f1_bs, f1_wv, f2_ws, f2_bs, f2_wv)

    def _L3_gnn_ref(node_feature, edge_attr, edge_feature, W_skip0, W_skip1, W_nl0, W_nl1, W_fc1, W_fc2, W_out_s, W_out_v, edge_index):
        import jax, jax.numpy as jnp
        import numpy as np
        N_NODES = 10000
        N_EDGES = 5000
        MUL0, MUL1 = (64, 32)
        EDGE_DIM = 64
        W_NUMEL = 224
        DENOM = 32.0
        SQRT3 = 3.0 ** 0.5
        INV_SQRT3 = 1.0 / SQRT3
        INV_SQRT2 = 2.0 ** (-0.5)

        def _forward(node_feature, edge_attr, edge_feature, W_skip0, W_skip1, W_nl0, W_nl1, W_fc1, W_fc2, W_out_s, W_out_v, edge_index):
            N = node_feature.shape[0]
            E = edge_attr.shape[0]
            s = node_feature[:, :MUL0]
            v = node_feature[:, MUL0:].reshape(N, MUL1, 3)
            skip_s = s @ W_skip0
            skip_v = jnp.einsum('nmi,mk->nki', v, W_skip1)
            s = s @ W_nl0
            v = jnp.einsum('nmi,mk->nki', v, W_nl1)
            rhat = edge_attr / jnp.linalg.norm(edge_attr, axis=-1, keepdims=True)
            sh1 = SQRT3 * rhat
            w = jax.nn.relu(edge_feature @ W_fc1) @ W_fc2
            w0, w1, w2, w3, w4 = jnp.split(w, [64, 128, 160, 192], axis=-1)
            src, dst = (edge_index[0], edge_index[1])
            xs = s[dst]
            xv = v[dst]
            out0a = w0 * xs
            out0b = w3 * (jnp.einsum('emi,ei->em', xv, sh1) * INV_SQRT3)
            out1a = (w1 * xs)[:, :, None] * sh1[:, None, :]
            out1b = w2[:, :, None] * xv
            out1c = w4[:, :, None] * (jnp.cross(xv, sh1[:, None, :]) * INV_SQRT2)
            tp = jnp.concatenate([out0a, out0b, out1a.reshape(E, -1), out1b.reshape(E, -1), out1c.reshape(E, -1)], axis=-1)
            agg = jax.ops.segment_sum(tp, src, num_segments=N) / DENOM
            agg_s = agg[:, :96]
            agg_v = agg[:, 96:].reshape(N, 128, 3)
            out_s = agg_s @ W_out_s + skip_s
            out_v = jnp.einsum('nmi,mk->nki', agg_v, W_out_v) + skip_v
            fs = jax.nn.silu(out_s[:, :MUL0])
            gate = jax.nn.sigmoid(out_s[:, MUL0:MUL0 + 32])
            gv = gate[:, :, None] * out_v
            return jnp.concatenate([fs, gv.reshape(N, -1)], axis=-1)
        return _forward(node_feature, edge_attr, edge_feature, W_skip0, W_skip1, W_nl0, W_nl1, W_fc1, W_fc2, W_out_s, W_out_v, edge_index)
    edge_index = jnp.stack([src, dst])
    x = _layernorm(x + _L0_gnn_ref(x, node_vec1, edge_attr_4, edge_attr_8, L0_gnn_W_sc_s, L0_gnn_W_sc_v, L0_gnn_W1_s, L0_gnn_W1_v, L0_gnn_W2_s, L0_gnn_W2_v, L0_gnn_W3, L0_gnn_fcW1, L0_gnn_fcW2, src, dst), axis=-1)
    x = _layernorm(x + _L1_gnn_ref(x, node_vec1, edge_attr_4, edge_attr_8, L1_gnn_Wsc0, L1_gnn_Wsc1, L1_gnn_Wl1_0, L1_gnn_Wl1_1, L1_gnn_Wfc1, L1_gnn_Wfc2, L1_gnn_Wfc3, L1_gnn_Wl2_s, L1_gnn_Wl2_v, L1_gnn_Wa, src, dst), axis=-1)
    x = _layernorm(x + _L2_gnn_ref(x, node_vec1, edge_attr_3, edge_attr_64, src, dst, L2_gnn_ln1_w0, L2_gnn_ln1_b0, L2_gnn_ln1_w1, L2_gnn_ln2_w0, L2_gnn_ln2_b0, L2_gnn_ln2_w1, L2_gnn_msrc_ws, L2_gnn_msrc_wv, L2_gnn_mdst_ws, L2_gnn_mdst_bs, L2_gnn_mdst_wv, L2_gnn_rw1, L2_gnn_rb1, L2_gnn_rg1, L2_gnn_rbe1, L2_gnn_rw2, L2_gnn_rb2, L2_gnn_rg2, L2_gnn_rbe2, L2_gnn_rw3, L2_gnn_roff, L2_gnn_lin_ws, L2_gnn_lin_bs, L2_gnn_lin_wv, L2_gnn_alpha_dot, L2_gnn_proj_ws, L2_gnn_proj_bs, L2_gnn_proj_wv, L2_gnn_f1_ws, L2_gnn_f1_bs, L2_gnn_f1_wv, L2_gnn_f2_ws, L2_gnn_f2_bs, L2_gnn_f2_wv), axis=-1)
    x = _layernorm(x + _L3_gnn_ref(x, edge_attr_3, edge_attr_64, L3_gnn_W_skip0, L3_gnn_W_skip1, L3_gnn_W_nl0, L3_gnn_W_nl1, L3_gnn_W_fc1, L3_gnn_W_fc2, L3_gnn_W_out_s, L3_gnn_W_out_v, edge_index), axis=-1)
    return x

_drawn_inputs = setup_inputs


def setup_inputs(seed=0):
    import zlib

    import numpy as np

    out = dict(_drawn_inputs(seed))
    spreads = {'L2_gnn_ln1_w0': (1.0, 0.2),
     'L2_gnn_ln1_b0': (0.0, 0.567),
     'L2_gnn_ln1_w1': (1.0, 0.6),
     'L2_gnn_ln2_w0': (1.0, 0.6),
     'L2_gnn_ln2_b0': (0.0, 0.8),
     'L2_gnn_ln2_w1': (1.0, 0.6),
     'L2_gnn_mdst_bs': (0.0, 0.8),
     'L2_gnn_rb1': (0.0, 0.1),
     'L2_gnn_rg1': (1.0, 0.2),
     'L2_gnn_rbe1': (0.0, 0.383),
     'L2_gnn_rb2': (0.0, 0.1),
     'L2_gnn_rg2': (1.0, 0.2),
     'L2_gnn_rbe2': (0.0, 0.376),
     'L2_gnn_lin_bs': (0.0, 0.416),
     'L2_gnn_proj_bs': (0.0, 0.1),
     'L2_gnn_f1_bs': (0.0, 0.8),
     'L2_gnn_f2_bs': (0.0, 0.458)}
    factors = {'edge_attr_4': 8.0,
     'edge_attr_8': 8.0,
     'L0_gnn_W1_s': 8.0,
     'L0_gnn_W1_v': 8.0,
     'L0_gnn_W2_s': 8.0,
     'L0_gnn_W2_v': 8.0,
     'L0_gnn_W3': 8.0,
     'L0_gnn_fcW1': 8.0,
     'L0_gnn_fcW2': 8.0,
     'L1_gnn_Wl1_0': 8.0,
     'L1_gnn_Wl1_1': 8.0,
     'L1_gnn_Wfc1': 8.0,
     'L1_gnn_Wfc2': 8.0,
     'L1_gnn_Wfc3': 8.0,
     'L1_gnn_Wl2_s': 8.0,
     'L1_gnn_Wl2_v': 8.0,
     'L1_gnn_Wa': 8.0,
     'L2_gnn_alpha_dot': 2.913,
     'L3_gnn_W_nl0': 8.0,
     'L3_gnn_W_nl1': 8.0,
     'L3_gnn_W_fc1': 8.0,
     'L3_gnn_W_fc2': 8.0,
     'L3_gnn_W_out_s': 8.0,
     'L3_gnn_W_out_v': 8.0}
    for name, (base, spread) in spreads.items():
        noise = np.random.default_rng([zlib.crc32(name.encode()), seed]).standard_normal(out[name].shape)
        drawn = base * np.exp(spread * noise) if base else spread * noise
        out[name] = jnp.asarray(drawn.astype(out[name].dtype))
    for name, factor in factors.items():
        out[name] = (out[name] * factor).astype(out[name].dtype)
    return out
```

```python
from contextlib import ExitStack

import numpy as np

import concourse.bass as bass
import concourse.mybir as mybir

F32 = mybir.dt.float32
I32 = mybir.dt.int32
U32 = mybir.dt.uint32
ALU = mybir.AluOpType
ACT = mybir.ActivationFunctionType
AX = mybir.AxisListType

P = 128
N, E = 50000, 25000
S0, V1 = 64, 32
V3 = 3 * V1
D = S0 + V3
XW = D + 1
T = 4
B = T * P
NB = 50
NBP = NB + 1
NC = N // B
LASTP = (N - NC * B) // T
NA = 396 * P
ZR = 12
AW = {0: 161, 1: 161, 2: 168, 3: 192}
EPS = 1e-5
MAGIC = 12582912.0

SLOTS = {}


def slot(name, rows, cols):
    at = sum(c for _, c, _ in SLOTS.values())
    SLOTS[name] = (rows, cols, at)


for _l in (0, 1):
    slot(f"h{_l}", 8, 64)
    slot(f"w1_{_l}", 64, 128)
    slot(f"w2_{_l}", 64, 128)
    slot(f"f1_{_l}", 128, 128)
    slot(f"f2_{_l}", 128, 128)
    slot(f"o1_{_l}", 128, 193)
    slot(f"o2_{_l}", 128, 161)
    slot(f"ns_{_l}", 64, 64)
    slot(f"nv_{_l}", 96, 96)
slot("hh1", 64, 64)
slot("ident", 128, 128)
slot("before", 128, T * B)
slot("spare", 128, T)
slot("mhalfn", 128, NBP * T)
slot("one", 1, 128)
slot("e64", 1, 65)
for _l in (2, 3):
    _so = 128 if _l == 2 else 96
    slot(f"w1_{_l}", 64, 128)
    slot(f"w2_{_l}", 64, 128)
    slot(f"w3_{_l}", 64, 96)
    for _s in range(2 if _l == 2 else 1):
        slot(f"f1_{_l}{_s}", 64, 128)
        slot(f"f2_{_l}{_s}", 128, 128)
    slot(f"o1_{_l}", 128, 32 + _so + 96)
    slot(f"o2_{_l}", 128, _so + 96)
    slot(f"o3_{_l}", 96, 96)
slot("h3", 64, 64)
slot("ns_3", 64, 96)
slot("nv_3", 96, 96)
slot("roff0", 128, 1)
slot("roff1", 128, 1)
slot("roff2", 96, 1)
slot("mb2", 128, 1)
slot("ln1w", 64, 1)
slot("ln1b", 64, 1)
slot("ln1v", 128, 1)
slot("adot", 128, 64)
slot("linb", 1, 224)
for _k in range(2):
    slot(f"rw{_k}", 64, 64)
    slot(f"rb{_k}", 1, 64)
    slot(f"rg{_k}", 64, 1)
    slot(f"rbe{_k}", 64, 1)
slot("pw", 64, 64)
slot("pb", 1, 64)
slot("pv", 96, 96)
slot("ln2w", 65, 1)
slot("ln2v", 96, 1)
slot("b0row", 64, 65)
slot("f1s", 65, 320)
slot("f1b", 1, 320)
slot("f1v", 96, 192)
slot("f2s", 128, 64)
slot("f2b", 1, 64)
slot("f2v0", 96, 96)
slot("f2v1", 96, 96)
WCOLS = sum(c for _, c, _ in SLOTS.values())


def due(count):
    return max(count, 0) if isinstance(count, int) else count


def semaphores(nc, ctx, named):
    made = []

    def over():
        nc.clear_and_free_semaphores(made)
        nc.all_engine_barrier()

    def sem(n):
        made.append(nc.alloc_semaphore(name=named(n)))
        return made[-1]

    ctx.callback(over)
    return sem


def by_twos(eng, n, step):
    for u in range(2):
        step(0, u)
    with eng.Fori(1, n // 2) as j:
        for u in range(2):
            step(j, u)


def edge_phase_01(nc, l, x, agg, dram, wt, later):
    W = AW[l]
    act_fn = ACT.Silu if l == 0 else ACT.Gelu_apprx_tanh
    NL = 5
    with ExitStack() as ctx:
        sb = lambda n, s, d=F32: ctx.enter_context(nc.sbuf_tensor(f"{n}_{l}", s, d))
        ps = lambda n, s: ctx.enter_context(nc.psum_tensor(f"{n}_{l}", s, F32))
        sem = semaphores(nc, ctx, lambda n: f"{n}_{l}")
        gidx = [sb(f"gidx{u}", [P, T], U32) for u in range(2)]
        tidx = [sb(f"tidx{u}", [P, T], I32) for u in range(2)]
        trow = [sb(f"trow{u}", [P, B], I32) for u in range(2)]
        esT = [sb(f"esT{u}", [8, B]) for u in range(2)]
        ea = [sb(f"ea{u}", [P, T, 4]) for u in range(2)]
        xg = [sb(f"xg{u}", [P, T, XW]) for u in range(2)]
        ya = [sb(f"ya{u}", [P, T, 4]) for u in range(2)]
        yb = [sb(f"yb{u}", [P, T, 8]) for u in range(2)]
        prod = sb("prod", [P, T, V3])
        rows = sb("rows", [P, T, 2 * P])
        ts = sb("ts", [P, 2, B])
        hs = sb("hs", [64, B])
        h2 = sb("h2", [64, B])
        ws = sb("ws", [P, 2, B])
        pr = sb("pr", [P, 2, B])
        tf = sb("tf", [P, T])
        same = sb("same", [P, T, B])
        junk = sb("junk", [P, T, B])
        cnt = sb("cnt", [P, T])
        away = sb("away", [P, T])
        cidx = [sb(f"cidx{u}", [P, T], U32) for u in range(2)]
        outer = sb("outer", [P, T, V3])
        ob = sb("ob", [P, T, 32 + W])
        summed = sb("summed", [P, T, W])
        zero = sb("zero", [P, ZR * 192]) if l == 0 else None

        pt = ps("pt", [P, 2, B])
        ph = ps("ph", [P, B])
        pf = ps("pf", [P, B])
        po = ps("po", [P, T, 256])
        pc = ps("pc", [P, T, 256])

        loaded = [sem("loaded0"), sem("loaded1")]
        freed = sem("freed")
        gathered = [sem("gathered0"), sem("gathered1")]
        y_ok = sem("y_ok")
        rows_v = sem("rows_v")
        rows_a = sem("rows_a")
        turned = sem("turned")
        ts_ok = sem("ts_ok")
        h_ps = sem("h_ps")
        h_ok = sem("h_ok")
        w_ps = sem("w_ps")
        w_ok = sem("w_ok")
        f_ps = sem("f_ps")
        prod_ok = sem("prod_ok")
        o_ps = sem("o_ps")
        msg_v = sem("msg_v")
        msg_a = sem("msg_a")
        same_ok = sem("same_ok")
        idx_step = sem("idx_step")
        idx_ok = sem("idx_ok")
        idx_out = sem("idx_out")
        c_ps = sem("c_ps")
        sum_ok = sem("sum_ok")
        added = sem("added")
        left = sem("left")
        cidx_in = [sem("cidx_in0"), sem("cidx_in1")]
        zset = sem("zset")
        zeroed = [sem(f"zeroed{k}") for k in range(4)] if l == 0 else None
        turn = sem("turn")

        def fence(eng):
            eng.sem_inc(turn, 1)

        block = ctx.enter_context(nc.Block())

        @block.sync
        def _(sp):
            def load(i, u):
                sp.wait_ge(freed, due(i - 1))
                sp.dma_start(gidx[u][:], dram["src_g"][bass.ds(i, 1)].rearrange("a p t -> (a p) t")).then_inc(loaded[u], 16)
                sp.dma_start(tidx[u][:], dram["dst_t"][bass.ds(i, 1)].rearrange("a p t -> (a p) t")).then_inc(loaded[u], 16)
                sp.dma_start(trow[u][:], dram["dst_r"][bass.ds(i, 1)].broadcast_to([P, B])).then_inc(loaded[u], 16)
                sp.dma_start(esT[u][:], dram["ea8T"][:, bass.ds(i * B, B)]).then_inc(loaded[u], 16)
                sp.dma_start(ea[u][:], dram["ea4"][bass.ds(i, 1)].rearrange("a p t c -> (a p) t c")).then_inc(loaded[u], 16)
                if l == 1:
                    sp.wait_ge(left, i)
                    sp.dma_start(cidx[u][:], dram["cidx"][bass.ds(i, 1)].rearrange("a p t -> (a p) t")).then_inc(cidx_in[u], 16)

            load(0, 0)
            if l == 0:
                sp.wait_ge(zset, 1)
                for k in range(4):
                    w = ZR * AW[k]
                    flat = later[k].rearrange("(p r) c -> p (r c)", p=P)
                    with sp.Fori(0, NA // P // ZR) as j:
                        sp.dma_start(flat[:, bass.ds(j * w, w)], zero[:, 0:w]).then_inc(zeroed[k], 16)
            def step(j, u):
                load(2 * j + u + 1, 1 - u)
                if l == 0:
                    sp.wait_ge(idx_ok, 2 * j + u + 1)
                    sp.dma_start(dram["cidx"][bass.ds(2 * j + u, 1)].rearrange("a p t -> (a p) t"), cidx[u][:]).then_inc(idx_out, 16)

            by_twos(sp, NB, step)
            if l == 0:
                sp.wait_ge(idx_out, 16 * NB)
                for k in range(1, 4):
                    sp.wait_ge(zeroed[k], 16 * (NA // P // ZR))

        @block.gpsimd
        def _(pool):
            def gather(u, k):
                pool.wait_ge(loaded[u], 16 * NL * (k + 1))
                fence(pool)
                for t in range(T):
                    pool.indirect_dma_start(xg[u][:, t, :], None, x, bass.IndirectOffsetOnAxis(ap=gidx[u][:, t:t + 1], axis=0)).then_inc(gathered[u], 16)

            if l == 0:
                pool.memset(zero[:], 0.0).then_inc(zset, 1)
            gather(0, 0)
            if l == 0:
                pool.wait_ge(zeroed[0], 16 * (NA // P // ZR))
            def step(j, u):
                i = 2 * j + u
                gather(1 - u, j + u)
                if l == 0:
                    pool.wait_ge(idx_ok, i + 1)
                    fence(pool)
                else:
                    pool.wait_ge(cidx_in[u], 16 * (j + 1))
                    fence(pool)
                pool.wait_ge(added, 16 * T * i)
                fence(pool)
                pool.sem_inc(left, 1)
                pool.wait_ge(sum_ok, i + 1)
                fence(pool)
                for t in range(T):
                    pool.indirect_dma_start(agg, bass.IndirectOffsetOnAxis(ap=cidx[u][:, t:t + 1], axis=0), summed[:, t, :], None, compute_op=ALU.add).then_inc(added, 16)

            by_twos(pool, NB, step)
            pool.wait_ge(added, 16 * T * NB)
            if l == 1:
                pool.wait_ge(cidx_in[0], 16 * (NB // 2 + 1))

        @block.vector
        def _(v):
            def front(n, u, k):
                v.wait_ge(gathered[u], 16 * T * (k + 1))
                v.tensor_tensor(ya[u][:], ea[u][:], xg[u][:, :, D:XW].to_broadcast([P, T, 4]), ALU.mult).then_inc(y_ok, 1)
                v.wait_ge(y_ok, 5 * n + 1)
                v.tensor_scalar(yb[u][:, :, 0:1], ya[u][:, :, 0:1], 1.0 / 8.0, None, ALU.mult).then_inc(y_ok, 1)
                v.tensor_scalar(yb[u][:, :, 1:2], ya[u][:, :, 0:1], 32.0 ** -0.5, None, ALU.mult).then_inc(y_ok, 1)
                v.tensor_scalar(yb[u][:, :, 2:5], ya[u][:, :, 1:4], 1.0 / 8.0, None, ALU.mult).then_inc(y_ok, 1)
                v.tensor_scalar(yb[u][:, :, 5:8], ya[u][:, :, 1:4], 96.0 ** -0.5, None, ALU.mult).then_inc(y_ok, 1)
                v.wait_ge(turned, 2 * n)
                v.wait_ge(y_ok, 5 * n + 5)
                v.tensor_tensor(prod[:].rearrange("p t (u c) -> p t u c", c=3), xg[u][:, :, S0:D].rearrange("p t (u c) -> p t u c", c=3),
                                yb[u][:, :, 5:8].unsqueeze(2).to_broadcast([P, T, V1, 3]), ALU.mult).then_inc(rows_v, 1)
                v.tensor_tensor(rows[:, :, 0:64], xg[u][:, :, 0:64], yb[u][:, :, 0:1].to_broadcast([P, T, 64]), ALU.mult).then_inc(rows_v, 1)
                v.tensor_tensor(rows[:, :, 160:256], xg[u][:, :, S0:D], yb[u][:, :, 1:2].to_broadcast([P, T, V3]), ALU.mult).then_inc(rows_v, 1)
                v.wait_ge(rows_v, 4 * n + 1)
                v.tensor_reduce(rows[:, :, 128:160], prod[:].rearrange("p t (u c) -> p t u c", c=3), AX.X, ALU.add).then_inc(rows_v, 1)

            def main(i, u):
                v.tensor_copy(tf[:], tidx[u][:]).then_inc(idx_step, 1)
                v.wait_ge(c_ps, i)
                v.wait_ge(idx_step, (i * 7 if l == 0 else i) + 1)
                for t in range(T):
                    v.tensor_scalar(same[:, t, :], trow[u][:], tf[:, t:t + 1], None, ALU.is_equal).then_inc(same_ok, 1)
                if l == 0:
                    for t in range(T):
                        m = (t + 1) * P
                        v.scalar_tensor_tensor(junk[:, t, 0:m], trow[u][:, 0:m], tf[:, t:t + 1], wt("before")[:, t * B:t * B + m],
                                               ALU.is_equal, ALU.mult, accum_out=cnt[:, t:t + 1]).then_inc(idx_step, 1)
                    v.tensor_tensor(away[:], wt("spare"), tf[:], ALU.subtract).then_inc(idx_step, 1)
                    v.wait_ge(idx_step, i * 7 + 6)
                    v.scalar_tensor_tensor(cnt[:], cnt[:], 1.0, away[:], ALU.min, ALU.mult).then_inc(idx_step, 1)
                    v.wait_ge(idx_step, i * 7 + 7)
                    v.wait_ge(idx_out, 16 * i)
                    v.wait_ge(left, i)
                    v.tensor_tensor(cidx[u][:], cnt[:], tf[:], ALU.add).then_inc(idx_ok, 1)
                v.wait_ge(o_ps, i)
                for g in range(2):
                    v.wait_ge(w_ok, 2 * i + g + 1)
                    v.wait_ge(f_ps, 2 * i + g + 1)
                    v.tensor_tensor(pr[:, g, :], pf[:], ws[:, g, :], ALU.mult).then_inc(prod_ok, 1)

            def messages(i, u):
                v.wait_ge(msg_a, i + 1)
                v.tensor_tensor(outer[:].rearrange("p t (u c) -> p t u c", c=3), ob[:, :, 0:32].unsqueeze(3).to_broadcast([P, T, V1, 3]),
                                yb[u][:, :, 2:5].unsqueeze(2).to_broadcast([P, T, V1, 3]), ALU.mult).then_inc(msg_v, 1)
                v.wait_ge(msg_v, 2 * i + 1)
                v.tensor_tensor(ob[:, :, 96:192], ob[:, :, 96:192], outer[:], ALU.add).then_inc(msg_v, 1)

            front(0, 0, 0)
            def step(j, u):
                i = 2 * j + u
                main(i, u)
                front(i + 1, 1 - u, j + u)
                messages(i, u)

            by_twos(v, NB, step)

        @block.scalar
        def _(a):
            def front(n, u, k):
                a.wait_ge(gathered[u], 16 * T * (k + 1))
                a.wait_ge(turned, 2 * n)
                a.activation(rows[:, :, 64:128], xg[u][:, :, 0:64], ACT.Copy).then_inc(rows_a, 1)
                for g in range(2):
                    a.wait_ge(f_ps, 2 * n)
                    a.wait_ge(turned, 2 * n + g + 1)
                    a.activation(ts[:, g, :], pt[:, g, :], ACT.Copy).then_inc(ts_ok, 1)

            def hidden(i):
                nh = 1 + l
                a.wait_ge(h_ps, nh * i + 1)
                a.activation(hs[:], ph[0:64, :], act_fn, scale=8.0 ** -0.5).then_inc(h_ok, 1)
                if l == 1:
                    a.wait_ge(h_ps, nh * i + 2)
                    a.activation(h2[:], ph[0:64, :], act_fn, scale=1.0 / 8.0).then_inc(h_ok, 1)
                for g in range(2):
                    a.wait_ge(w_ps, 2 * i + g + 1)
                    if g == 0:
                        a.wait_ge(prod_ok, 2 * i)
                    a.activation(ws[:, g, :], ph[:], ACT.Copy, scale=1.0 / 8.0).then_inc(w_ok, 1)

            def finish(i):
                a.wait_ge(o_ps, i + 1)
                a.wait_ge(c_ps, i)
                a.activation(ob[:], po[:, :, 0:32 + W], ACT.Copy).then_inc(msg_a, 1)
                a.wait_ge(added, 16 * T * i)
                a.wait_ge(c_ps, i + 1)
                a.activation(summed[:], pc[:, :, 0:W], ACT.Copy).then_inc(sum_ok, 1)

            front(0, 0, 0)
            def step(j, u):
                i = 2 * j + u
                hidden(i)
                front(i + 1, 1 - u, j + u)
                finish(i)

            by_twos(a, NB, step)

        @block.tensor
        def _(pe):
            def front(n, g):
                pe.wait_ge(rows_v, 4 * n + 4)
                pe.wait_ge(rows_a, n + 1)
                pe.wait_ge(ts_ok, 2 * n)
                for t in range(T):
                    last = pe.transpose(pt[:, g, t * P:(t + 1) * P], rows[:, t, g * P:(g + 1) * P], wt("ident"))
                last.then_inc(turned, 1)

            front(0, 0)
            front(0, 1)
            def step(j, u):
                i = 2 * j + u
                nh = 1 + l
                pe.wait_ge(loaded[u], 16 * NL * (j + 1))
                pe.wait_ge(w_ok, 2 * i)
                pe.matmul(ph[0:64, :], wt(f"h{l}"), esT[u][:], start=True, stop=True).then_inc(h_ps, 1)
                pe.wait_ge(ts_ok, 2 * i + 1)
                pe.wait_ge(prod_ok, 2 * i)
                pe.matmul(pf[:], wt(f"f1_{l}"), ts[:, 0, :], start=True, stop=True).then_inc(f_ps, 1)
                if l == 1:
                    pe.wait_ge(h_ok, nh * i + 1)
                    fence(pe)
                    pe.matmul(ph[0:64, :], wt("hh1"), hs[:], start=True, stop=True).then_inc(h_ps, 1)
                pe.wait_ge(h_ok, nh * (i + 1))
                hid = hs if l == 0 else h2
                pe.matmul(ph[:], wt(f"w1_{l}"), hid[:], start=True, stop=True).then_inc(w_ps, 1)
                pe.wait_ge(ts_ok, 2 * i + 2)
                pe.wait_ge(prod_ok, 2 * i + 1)
                pe.matmul(pf[:], wt(f"f2_{l}"), ts[:, 1, :], start=True, stop=True).then_inc(f_ps, 1)
                pe.wait_ge(w_ok, 2 * i + 1)
                pe.matmul(ph[:], wt(f"w2_{l}"), hid[:], start=True, stop=True).then_inc(w_ps, 1)
                front(i + 1, 0)
                front(i + 1, 1)
                pe.wait_ge(prod_ok, 2 * i + 2)
                pe.wait_ge(msg_a, i)
                for t in range(T):
                    pe.matmul(po[:, t, 0:193], pr[:, 0, t * P:(t + 1) * P], wt(f"o1_{l}"), start=True, stop=False)
                    last = pe.matmul(po[:, t, 32:193], pr[:, 1, t * P:(t + 1) * P], wt(f"o2_{l}"), start=False, stop=True)
                last.then_inc(o_ps, 1)
                pe.wait_ge(msg_v, 2 * i + 2)
                pe.wait_ge(same_ok, T * (i + 1))
                pe.wait_ge(sum_ok, i)
                for t in range(T):
                    for s in range(T):
                        last = pe.matmul(pc[:, t, 0:W], same[:, s, t * P:(t + 1) * P], ob[:, s, 32:32 + W], start=(s == 0), stop=(s == T - 1))
                last.then_inc(c_ps, 1)
                pe.wait_ge(c_ps, i + 1)
                pe.sem_inc(freed, 1)

            by_twos(pe, NB, step)


def node_phase_01(nc, l, x, agg, xo, wt, width):
    with ExitStack() as ctx:
        tag = f"n{l}"
        sb = lambda n, s, d=F32: ctx.enter_context(nc.sbuf_tensor(f"{n}_{tag}", s, d))
        ps = lambda n, s: ctx.enter_context(nc.psum_tensor(f"{n}_{tag}", s, F32))
        sem = semaphores(nc, ctx, lambda n: f"{n}_{tag}")
        xr = [sb(f"xr{u}", [P, T, XW]) for u in range(2)]
        ar = [sb(f"ar{u}", [P, T, 161]) for u in range(2)]
        tss = sb("tss", [64, B])
        tsv = sb("tsv", [96, B])
        th = sb("th", [P, 2, T])
        rn = sb("rn", [P, 2, T])
        sc = sb("sc", [P, 2, T])
        at = sb("at", [P, T])
        cf = sb("cf", [P, 3, T])
        ag = sb("ag", [P, T, D])
        sk = sb("sk", [P, T, D])
        y = [sb(f"y{u}", [P, T, D]) for u in range(2)]
        st = sb("st", [P, T, 6])
        mv = sb("mv", [P, T, 2])
        ve = sb("ve", [P, T])
        nm = [sb(f"nm{u}", [P, T]) for u in range(2)]
        rs = [sb(f"rs{u}", [P, T]) for u in range(2)]
        nr = [sb(f"nr{u}", [P, T]) for u in range(2)]
        xn = [sb(f"xn{u}", [P, T, XW]) for u in range(2)]
        pts = ps("pts", [64, B])
        ptv = ps("ptv", [96, B])
        pk = [ps(f"pk{u}", [P, T, 256]) for u in range(2)]
        loaded = [sem("loaded0"), sem("loaded1")]
        used = sem("used")
        turned = sem("turned")
        ts_ok = sem("ts_ok")
        k_ps = sem("k_ps")
        co = sem("co")
        th_ok = sem("th_ok")
        sc_ok = sem("sc_ok")
        ag_ok = sem("ag_ok")
        cf_ok = sem("cf_ok")
        y_ok = sem("y_ok")
        st_ok = sem("st_ok")
        ve_ok = sem("ve_ok")
        rs_ok = sem("rs_ok")
        xn_ok = sem("xn_ok")
        stored = [sem("stored0"), sem("stored1")]
        turn = sem("turn")
        C0 = 13 if l == 0 else 4

        def fence(eng):
            eng.sem_inc(turn, 1)

        def rows_of(t, c, parts, w):
            return t[bass.ds(c * B, parts * T), 0:w].rearrange("(p t) c -> p (t c)", t=T)

        block = ctx.enter_context(nc.Block())

        @block.sync
        def _(sp):
            def load(c, u, parts=P):
                sp.wait_ge(used, due(c - 1))
                sp.dma_start(xr[u][0:parts].rearrange("p t c -> p (t c)"), rows_of(x, c, parts, XW)).then_inc(loaded[u], 16)
                sp.dma_start(ar[u][0:parts].rearrange("p t c -> p (t c)"), rows_of(agg, c, parts, 161)).then_inc(loaded[u], 16)

            by_twos(sp, NC, lambda j, u: load(2 * j + u, u))
            load(NC - 1, (NC - 1) % 2)
            load(NC, NC % 2, LASTP)

        def blocks(eng, step):
            by_twos(eng, NC, lambda j, u: step(2 * j + u, u, j, P))
            step(NC - 1, (NC - 1) % 2, (NC - 1) // 2, P)
            step(NC, NC % 2, NC // 2, LASTP)

        @block.tensor
        def _(pe):
            def step(c, u, k, parts):
                pe.wait_ge(loaded[u], 32 * (k + 1))
                pe.wait_ge(ts_ok, 2 * c)
                for t in range(T):
                    last = pe.transpose(ptv[:, t * P:(t + 1) * P], xr[u][:, t, S0:D], wt("ident"))
                last.then_inc(turned, 1)
                for t in range(T):
                    last = pe.transpose(pts[:, t * P:(t + 1) * P], xr[u][:, t, 0:S0], wt("ident"))
                last.then_inc(turned, 1)
                pe.wait_ge(ts_ok, 2 * c + 2)
                pe.wait_ge(used, due(c - 1))
                for t in range(T):
                    pe.matmul(pk[u][:, t, S0:D], tsv[:, t * P:(t + 1) * P], wt(f"nv_{l}"), start=True, stop=True)
                    last = pe.matmul(pk[u][:, t, 0:S0], tss[:, t * P:(t + 1) * P], wt(f"ns_{l}"), start=True, stop=True)
                last.then_inc(k_ps, 1)

            blocks(pe, step)

        @block.scalar
        def _(a):
            def normalise(c, u):
                a.wait_ge(rs_ok, 2 * c + 2)
                for t in range(T):
                    a.activation(xn[u][:, t, 0:D], y[u][:, t, :], ACT.Identity, bias=nr[u][:, t:t + 1], scale=rs[u][:, t:t + 1]).then_inc(xn_ok, 1)

            def step(c, u, k, parts, first=False):
                a.wait_ge(k_ps, c)
                a.wait_ge(turned, 2 * c + 1)
                a.activation(tsv[:], ptv[:], ACT.Copy).then_inc(ts_ok, 1)
                a.wait_ge(turned, 2 * c + 2)
                a.activation(tss[:], pts[:], ACT.Copy).then_inc(ts_ok, 1)
                if l == 0:
                    a.wait_ge(th_ok, c + 1)
                    a.activation(sc[:], th[:], ACT.Sin, scale=6.2831845).then_inc(sc_ok, 1)
                a.wait_ge(stored[u], 16 * k)
                a.activation(xn[u][:, :, D:XW], xr[u][:, :, D:XW], ACT.Copy).then_inc(xn_ok, 1)
                normalise(c, u)

            blocks(a, step)

        @block.vector
        def _(v):
            def step(c, u, k, parts):
                v.wait_ge(loaded[u], 32 * (k + 1))
                if l == 0:
                    v.scalar_tensor_tensor(th[:, 0, :], ar[u][:, :, 160], 0.1 * 10.0 ** -0.5 * 96.0 ** -0.5 / (2 * np.pi), xr[u][:, :, D],
                                           ALU.mult, ALU.mult).then_inc(co, 1)
                    v.wait_ge(co, C0 * c + 1)
                    v.tensor_scalar(rn[:, 0, :], th[:, 0, :], MAGIC, None, ALU.add).then_inc(co, 1)
                    v.wait_ge(co, C0 * c + 2)
                    v.tensor_scalar(rn[:, 0, :], rn[:, 0, :], -MAGIC, None, ALU.add).then_inc(co, 1)
                    v.wait_ge(co, C0 * c + 3)
                    v.tensor_tensor(th[:, 0, :], th[:, 0, :], rn[:, 0, :], ALU.subtract).then_inc(co, 1)
                    v.wait_ge(co, C0 * c + 4)
                    v.tensor_scalar(th[:, 1, :], th[:, 0, :], 0.25, None, ALU.add).then_inc(co, 1)
                    v.wait_ge(co, C0 * c + 5)
                    v.tensor_scalar(rn[:, 1, :], th[:, 1, :], 0.5, None, ALU.is_gt).then_inc(co, 1)
                    v.wait_ge(co, C0 * c + 6)
                    v.tensor_tensor(th[:, 1, :], th[:, 1, :], rn[:, 1, :], ALU.subtract).then_inc(co, 1)
                    v.wait_ge(co, C0 * c + 7)
                    v.tensor_scalar(th[:], th[:], -0.4999999, 0.4999999, ALU.max, ALU.min).then_inc(th_ok, 1)
                    v.wait_ge(sc_ok, c + 1)
                    v.tensor_tensor(at[:], sc[:, 1, :], xr[u][:, :, D], ALU.mult).then_inc(co, 1)
                    v.wait_ge(co, C0 * c + 8)
                    v.tensor_scalar(cf[:, 0, :], at[:], 1.0 / 8.0, None, ALU.mult).then_inc(co, 1)
                    v.tensor_scalar(cf[:, 1, :], at[:], 32.0 ** -0.5, None, ALU.mult).then_inc(co, 1)
                    v.wait_ge(ag_ok, c)
                    v.scalar_tensor_tensor(cf[:, 2, :], sc[:, 0, :], 960.0 ** -0.5, xr[u][:, :, D], ALU.mult, ALU.mult).then_inc(co, 1)
                    v.sem_inc(turn, 1)
                    v.wait_ge(co, C0 * c + 11)
                    v.tensor_copy(rn[:, 0, :], cf[:, 2, :]).then_inc(co, 1)
                    v.tensor_copy(rn[:, 1, :], cf[:, 2, :]).then_inc(co, 1)
                    v.wait_ge(co, C0 * c + 13)
                else:
                    v.tensor_scalar(cf[:, 0, :], xr[u][:, :, D], 1.0 / 8.0, None, ALU.mult).then_inc(co, 1)
                    v.tensor_scalar(cf[:, 1, :], xr[u][:, :, D], 32.0 ** -0.5, None, ALU.mult).then_inc(co, 1)
                    v.scalar_tensor_tensor(at[:], ar[u][:, :, 160], 1.0 / 3072.0, xr[u][:, :, D], ALU.mult, ALU.mult).then_inc(co, 1)
                    v.wait_ge(co, C0 * c + 3)
                    v.wait_ge(ag_ok, c)
                    v.tensor_tensor(cf[:, 2, :], at[:], xr[u][:, :, D], ALU.mult).then_inc(co, 1)
                    v.wait_ge(co, C0 * c + 4)
                v.wait_ge(k_ps, c + 1)
                v.tensor_tensor(sk[:, :, 0:S0], pk[u][:, :, 0:S0], cf[:, 0, :].unsqueeze(2).to_broadcast([P, T, S0]), ALU.mult).then_inc(cf_ok, 1)
                v.tensor_tensor(sk[:, :, S0:D], pk[u][:, :, S0:D], cf[:, 1, :].unsqueeze(2).to_broadcast([P, T, V3]), ALU.mult).then_inc(cf_ok, 1)
                v.wait_ge(cf_ok, 4 * c + 2)
                v.wait_ge(ag_ok, c + 1)
                v.tensor_tensor(sk[:], sk[:], ag[:], ALU.add).then_inc(cf_ok, 1)
                v.wait_ge(cf_ok, 4 * c + 3)
                v.tensor_tensor(y[u][:], sk[:], xr[u][:, :, 0:D], ALU.add).then_inc(cf_ok, 1)
                v.wait_ge(cf_ok, 4 * c + 4)
                for t in range(T):
                    v.bn_stats(st[:, t, :], y[u][:, t, :]).then_inc(st_ok, 1)
                v.wait_ge(st_ok, 8 * c + 4)
                v.sem_inc(turn, 1)
                for t in range(T):
                    v.bn_aggr(mv[:, t, :], st[:, t, :]).then_inc(st_ok, 1)
                v.wait_ge(st_ok, 8 * c + 8)
                v.wait_ge(rs_ok, 2 * c)
                v.tensor_scalar(ve[:], mv[:, :, 1], EPS, None, ALU.add).then_inc(ve_ok, 1)
                v.tensor_scalar(nm[u][:], mv[:, :, 0], -1.0, None, ALU.mult).then_inc(ve_ok, 1)

            blocks(v, step)

        @block.gpsimd
        def _(pool):
            def step(c, u, k, parts):
                pool.wait_ge(co, C0 * (c + 1))
                fence(pool)
                pool.wait_ge(cf_ok, 4 * c)
                fence(pool)
                pool.tensor_tensor(ag[:], ar[u][:, :, 0:D], cf[:, 2, :].unsqueeze(2).to_broadcast([P, T, D]), ALU.mult).then_inc(ag_ok, 1)
                pool.wait_ge(xn_ok, 5 * c)
                fence(pool)
                pool.wait_ge(ve_ok, 2 * c + 2)
                fence(pool)
                pool.tensor_tensor(rs[u][:], ve[:], wt("mhalf"), ALU.pow).then_inc(rs_ok, 1)
                pool.wait_ge(rs_ok, 2 * c + 1)
                fence(pool)
                pool.tensor_tensor(nr[u][:], nm[u][:], rs[u][:], ALU.mult).then_inc(rs_ok, 1)
                pool.wait_ge(xn_ok, 5 * (c + 1))
                fence(pool)
                pool.sem_inc(used, 1)
                pool.dma_start(rows_of(xo, c, parts, width), xn[u][0:parts].rearrange("p t c -> p (t c)") if width == XW else xn[u][0:parts, :, 0:width]).then_inc(stored[u], 16)

            blocks(pool, step)
            pool.wait_ge(stored[0], 16 * (NC // 2 + 1))
            pool.wait_ge(stored[1], 16 * ((NC + 1) // 2))


def edge_phase_23(nc, l, x, agg, dram, wt):
    SO = 128 if l == 2 else 96
    OW = 32 + SO + V3
    W = AW[l]
    sides = ("src", "dst") if l == 2 else ("dst",)
    NS = len(sides)
    NL = 1 + NS + (2 if l == 3 else 0)
    NY = NBP * T
    with ExitStack() as ctx:
        sb = lambda n, s, d=F32: ctx.enter_context(nc.sbuf_tensor(f"{n}_{l}", s, d))
        ps = lambda n, s: ctx.enter_context(nc.psum_tensor(f"{n}_{l}", s, F32))
        sem = semaphores(nc, ctx, lambda n: f"{n}_{l}")
        gidx = [[sb(f"gidx{s}{u}", [P, T], U32) for u in range(2)] for s in range(NS)]
        esT = [sb(f"esT{u}", [64, B]) for u in range(2)]
        xg = [[sb(f"xg{s}{u}", [P, T, 192]) for u in range(2)] for s in range(NS)]
        y3 = sb("y3", [P, NY, 3])
        yq = sb("yq", [P, NY, 3])
        ye = sb("ye", [P, NY, 5])
        ysq = sb("ysq", [P, NY, 3])
        yn = sb("yn", [P, NY])
        yh = sb("yh", [P, NY])
        prod = sb("prod", [P, T, V3])
        ts = sb("ts", [P, 2 * NS, B])
        hs = sb("hs", [64, B])
        ws = sb("ws", [P, 3, B])
        pr = sb("pr", [P, 3, B])
        ob = sb("ob", [P, T, OW])
        e5 = sb("e5", [P, T, V1, 5])
        m1 = sb("m1", [P, T, V3])
        m2 = sb("m2", [P, T, V3])
        if l == 3:
            tidx = [sb(f"tidx{u}", [P, T], I32) for u in range(2)]
            trow = [sb(f"trow{u}", [P, B], I32) for u in range(2)]
            tf = sb("tf", [P, T])
            same = sb("same", [P, T, B])
            junk = sb("junk", [P, T, B])
            cnt = sb("cnt", [P, T])
            away = sb("away", [P, T])
            cidx = [sb(f"cidx{u}", [P, T], U32) for u in range(2)]
            summed = sb("summed", [P, T, W])
        else:
            sq = sb("sq", [P, T, V3])
            st = sb("st", [P, T, 6])
            mv = sb("mv", [P, T, 2])
            var = sb("var", [P, 2, T])
            rs = sb("rs", [P, 2, T])
            sl = sb("sl", [P, T, 64])
            sm = sb("sm", [P, T, 64])
            val = sb("val", [P, T, W])

        pt = ps("pt", [P, 2, B])
        ph = ps("ph", [P, B])
        pf = ps("pf", [P, B])
        po = ps("po", [P, 2, 512])
        pc = ps("pc", [P, T, 256]) if l == 3 else None

        y_in = sem("y_in")
        y_ok = sem("y_ok")
        n_ok = sem("n_ok")
        loaded = [sem("loaded0"), sem("loaded1")]
        freed = sem("freed")
        gathered = [sem("gathered0"), sem("gathered1")]
        sq_ok = sem("sq_ok")
        st_ok = sem("st_ok")
        rs_ok = sem("rs_ok")
        nrm = sem("nrm")
        rows_v = sem("rows_v")
        turned = sem("turned")
        ts_ok = sem("ts_ok")
        h_ps = sem("h_ps")
        h_ok = sem("h_ok")
        w_ps = sem("w_ps")
        w_ok = sem("w_ok")
        f_ps = sem("f_ps")
        prod_ok = sem("prod_ok")
        o_ps = sem("o_ps")
        ob_ok = sem("ob_ok")
        msg_v = sem("msg_v")
        same_ok = sem("same_ok")
        idx_step = sem("idx_step")
        idx_ok = sem("idx_ok")
        c_ps = sem("c_ps")
        sum_ok = sem("sum_ok")
        added = sem("added")
        left = sem("left")
        sl_ok = sem("sl_ok")
        sm_ok = sem("sm_ok")
        val_ok = sem("val_ok")
        kept = sem("kept")
        turn = sem("turn")
        MV = 6

        def fence(eng):
            eng.sem_inc(turn, 1)

        block = ctx.enter_context(nc.Block())

        @block.sync
        def _(sp):
            sp.dma_start(y3[:].rearrange("p n c -> p (n c)"), dram["ea3"]).then_inc(y_in, 16)

            def load(i, u):
                sp.wait_ge(freed, due(i - 1))
                for s, side in enumerate(sides):
                    sp.dma_start(gidx[s][u][:], dram[side + "_g"][bass.ds(i, 1)].rearrange("a p t -> (a p) t")).then_inc(loaded[u], 16)
                if l == 3:
                    sp.dma_start(esT[u][:], dram["ea64T"][:, bass.ds(i * B, B)]).then_inc(loaded[u], 16)
                    sp.dma_start(tidx[u][:], dram["src_t"][bass.ds(i, 1)].rearrange("a p t -> (a p) t")).then_inc(loaded[u], 16)
                    sp.dma_start(trow[u][:], dram["src_r"][bass.ds(i, 1)].broadcast_to([P, B])).then_inc(loaded[u], 16)
                else:
                    sp.dma_start(esT[u][:], dram["hid"][:, bass.ds(i * B, B)]).then_inc(loaded[u], 16)

            load(0, 0)

            def step(j, u):
                load(2 * j + u + 1, 1 - u)

            by_twos(sp, NB, step)

        @block.gpsimd
        def _(pool):
            def gather(u, k):
                pool.wait_ge(loaded[u], 16 * NL * (k + 1))
                fence(pool)
                for s in range(NS):
                    for t in range(T):
                        pool.indirect_dma_start(xg[s][u][:, t, 0:XW], None, x, bass.IndirectOffsetOnAxis(ap=gidx[s][u][:, t:t + 1], axis=0)).then_inc(gathered[u], 16)

            def powers(n):
                for s in range(NS):
                    pool.wait_ge(st_ok, 10 * NS * n + 10 * (s + 1))
                    fence(pool)
                    pool.wait_ge(nrm, 3 * (NS * n + s))
                    fence(pool)
                    pool.tensor_tensor(rs[:], var[:], wt("mhalf8").rearrange("p (a t) -> p a t", a=2), ALU.pow).then_inc(rs_ok, 1)

            pool.wait_ge(y_ok, 3)
            pool.tensor_tensor(yn[:], yh[:], wt("mhalfn"), ALU.pow).then_inc(n_ok, 1)
            gather(0, 0)
            if l == 2:
                powers(0)

            def step(j, u):
                i = 2 * j + u
                gather(1 - u, j + u)
                if l == 2:
                    powers(i + 1)
                    pool.wait_ge(val_ok, 4 * (i + 1))
                    fence(pool)
                    pool.dma_start(dram["val"][bass.ds(i, 1)].rearrange("a p t c -> (a p) t c"), val[:]).then_inc(kept, 16)
                    pool.dma_start(dram["att"][bass.ds(i * B, B)].rearrange("(t p) h -> p t h", p=P), val[:, :, 160:168]).then_inc(kept, 16)
                else:
                    pool.wait_ge(idx_ok, i + 1)
                    fence(pool)
                    pool.wait_ge(added, 16 * T * i)
                    fence(pool)
                    pool.sem_inc(left, 1)
                    pool.wait_ge(sum_ok, i + 1)
                    fence(pool)
                    for t in range(T):
                        pool.indirect_dma_start(agg, bass.IndirectOffsetOnAxis(ap=cidx[u][:, t:t + 1], axis=0), summed[:, t, :], None, compute_op=ALU.add).then_inc(added, 16)

            by_twos(pool, NB, step)
            if l == 3:
                pool.wait_ge(added, 16 * T * NB)
            else:
                pool.wait_ge(kept, 32 * NB)

        @block.vector
        def _(v):
            v.wait_ge(y_in, 16)
            v.tensor_tensor(ysq[:], y3[:], y3[:], ALU.mult).then_inc(y_ok, 1)
            v.wait_ge(y_ok, 1)
            v.tensor_reduce(yh[:], ysq[:], AX.X, ALU.add).then_inc(y_ok, 1)
            v.wait_ge(y_ok, 2)
            v.tensor_scalar(yh[:], yh[:], 1e-12 if l == 2 else 0.0, None, ALU.add).then_inc(y_ok, 1)
            v.wait_ge(n_ok, 1)
            v.tensor_tensor(y3[:], y3[:], yn[:].unsqueeze(2).to_broadcast([P, NY, 3]), ALU.mult).then_inc(y_ok, 1)
            v.wait_ge(y_ok, 4)
            v.tensor_scalar(yq[:], y3[:], 3.0 ** 0.5, None, ALU.mult).then_inc(y_ok, 1)
            v.tensor_scalar(ye[:, :, 0:3], y3[:], 1.5 ** 0.5, None, ALU.mult).then_inc(y_ok, 1)
            v.tensor_scalar(ye[:, :, 3:5], y3[:, :, 0:2], 1.5 ** 0.5, None, ALU.mult).then_inc(y_ok, 1)
            v.wait_ge(y_ok, 7)

            def at(y, n, lo, hi):
                return y[:, bass.ds(n * T, T), lo:hi].unsqueeze(2).to_broadcast([P, T, V1, hi - lo])

            def front(n, u, k):
                for s in range(NS):
                    if s == 0:
                        v.wait_ge(gathered[u], 16 * T * NS * (k + 1))
                    rows = xg[s][u]
                    if l == 2:
                        q = NS * n + s
                        v.wait_ge(rs_ok, q)
                        for t in range(T):
                            v.bn_stats(st[:, t, :], rows[:, t, 0:S0]).then_inc(st_ok, 1)
                        v.wait_ge(st_ok, 10 * q + 4)
                        fence(v)
                        for t in range(T):
                            v.bn_aggr(mv[:, t, :], st[:, t, :]).then_inc(st_ok, 1)
                        v.wait_ge(sq_ok, 2 * q + 1)
                        v.tensor_reduce(var[:, 1, :], sq[:], AX.X, ALU.add).then_inc(sq_ok, 1)
                        v.wait_ge(st_ok, 10 * q + 8)
                        v.tensor_scalar(var[:, 0, :], mv[:, :, 1], EPS, None, ALU.add).then_inc(st_ok, 1)
                        v.wait_ge(sq_ok, 2 * q + 2)
                        v.tensor_scalar(var[:, 1, :], var[:, 1, :], 1.0 / V3, EPS, ALU.mult, ALU.add).then_inc(st_ok, 1)
                        v.tensor_tensor(rows[:, :, 0:S0], rows[:, :, 0:S0], mv[:, :, 0:1].to_broadcast([P, T, S0]), ALU.subtract).then_inc(nrm, 1)
                        v.wait_ge(rs_ok, q + 1)
                        v.wait_ge(nrm, 3 * q + 1)
                        v.tensor_tensor(rows[:, :, 0:S0], rows[:, :, 0:S0], rs[:, 0, :].unsqueeze(2).to_broadcast([P, T, S0]), ALU.mult).then_inc(nrm, 1)
                        v.tensor_tensor(rows[:, :, S0:D], rows[:, :, S0:D], rs[:, 1, :].unsqueeze(2).to_broadcast([P, T, V3]), ALU.mult).then_inc(nrm, 1)
                        v.wait_ge(nrm, 3 * q + 3)
                    v.wait_ge(rows_v, 2 * (NS * n + s))
                    v.tensor_tensor(prod[:].rearrange("p t (u c) -> p t u c", c=3), rows[:, :, S0:D].rearrange("p t (u c) -> p t u c", c=3),
                                    at(y3, n, 0, 3), ALU.mult).then_inc(rows_v, 1)
                    v.wait_ge(rows_v, 2 * (NS * n + s) + 1)
                    v.tensor_reduce(rows[:, :, D:D + V1], prod[:].rearrange("p t (u c) -> p t u c", c=3), AX.X, ALU.add).then_inc(rows_v, 1)

            def main(i, u):
                if l == 3:
                    v.tensor_copy(tf[:], tidx[u][:]).then_inc(idx_step, 1)
                    v.wait_ge(c_ps, i)
                    v.wait_ge(idx_step, i * 7 + 1)
                    for t in range(T):
                        v.tensor_scalar(same[:, t, :], trow[u][:], tf[:, t:t + 1], None, ALU.is_equal).then_inc(same_ok, 1)
                    for t in range(T):
                        m = (t + 1) * P
                        v.scalar_tensor_tensor(junk[:, t, 0:m], trow[u][:, 0:m], tf[:, t:t + 1], wt("before")[:, t * B:t * B + m],
                                               ALU.is_equal, ALU.mult, accum_out=cnt[:, t:t + 1]).then_inc(idx_step, 1)
                    v.tensor_tensor(away[:], wt("spare"), tf[:], ALU.subtract).then_inc(idx_step, 1)
                    v.wait_ge(idx_step, i * 7 + 6)
                    v.scalar_tensor_tensor(cnt[:], cnt[:], 1.0, away[:], ALU.min, ALU.mult).then_inc(idx_step, 1)
                    v.wait_ge(idx_step, i * 7 + 7)
                    v.wait_ge(left, i)
                    v.tensor_tensor(cidx[u][:], cnt[:], tf[:], ALU.add).then_inc(idx_ok, 1)
                v.wait_ge(o_ps, T * i)
                for g in range(3):
                    v.wait_ge(w_ok, 3 * i + g + 1)
                    v.wait_ge(f_ps, 2 * i + min(g, 1) + 1)
                    r = (P, P, V3)[g]
                    if g == 0 and l == 2:
                        v.scalar_tensor_tensor(pr[0:r, g, :], pf[0:r], wt("mb2"), ws[0:r, g, :], ALU.add, ALU.mult).then_inc(prod_ok, 1)
                    else:
                        v.tensor_tensor(pr[0:r, g, :], pf[0:r], ws[0:r, g, :], ALU.mult).then_inc(prod_ok, 1)

            def messages(i, u):
                c3 = lambda a: a.rearrange("p t (u c) -> p t u c", c=3)
                vec = ob[:, :, 32 + SO:OW]
                v.wait_ge(ob_ok, 3 * T * (i + 1))
                v.tensor_tensor(c3(m1[:]), e5[:, :, :, 1:4], at(ye, i, 2, 5), ALU.mult).then_inc(msg_v, 1)
                v.tensor_tensor(c3(m2[:]), e5[:, :, :, 2:5], at(ye, i, 1, 4), ALU.mult).then_inc(msg_v, 1)
                v.wait_ge(msg_v, MV * i + 2)
                v.tensor_tensor(m1[:], m1[:], m2[:], ALU.subtract).then_inc(msg_v, 1)
                v.wait_ge(msg_v, MV * i + 3)
                v.tensor_tensor(c3(m2[:]), ob[:, :, 0:32].unsqueeze(3).to_broadcast([P, T, V1, 3]), at(yq, i, 0, 3), ALU.mult).then_inc(msg_v, 1)
                v.tensor_tensor(vec, vec, m1[:], ALU.add).then_inc(msg_v, 1)
                v.wait_ge(msg_v, MV * i + 5)
                if l == 2:
                    v.wait_ge(kept, 32 * i)
                    v.tensor_tensor(val[:, :, 64:160], vec, m2[:], ALU.add).then_inc(val_ok, 1)
                    v.tensor_copy(val[:, :, 0:64], ob[:, :, 96:160]).then_inc(val_ok, 1)
                    v.wait_ge(sl_ok, i + 1)
                    v.scalar_tensor_tensor(sm[:], ob[:, :, 32:96], 0.25, sl[:], ALU.mult, ALU.add).then_inc(msg_v, 1)
                    v.wait_ge(msg_v, MV * i + 6)
                    v.tensor_tensor(sm[:], sm[:], wt("adot").unsqueeze(1).to_broadcast([P, T, 64]), ALU.mult).then_inc(val_ok, 1)
                    v.wait_ge(val_ok, 4 * i + 3)
                    v.tensor_reduce(val[:, :, 160:168], sm[:].rearrange("p t (h k) -> p t h k", k=8), AX.X, ALU.add).then_inc(val_ok, 1)
                else:
                    v.tensor_tensor(vec, vec, m2[:], ALU.add).then_inc(msg_v, 1)

            front(0, 0, 0)

            def step(j, u):
                i = 2 * j + u
                main(i, u)
                front(i + 1, 1 - u, j + u)
                messages(i, u)

            by_twos(v, NB, step)

        @block.scalar
        def _(a):
            def front(n, u, k):
                if l == 2:
                    for s in range(NS):
                        q = NS * n + s
                        a.wait_ge(gathered[u], 16 * T * NS * (k + 1))
                        a.wait_ge(sq_ok, 2 * q)
                        a.activation(sq[:], xg[s][u][:, :, S0:D], ACT.Square).then_inc(sq_ok, 1)

            def copies(n):
                for s in range(NS):
                    for g in range(2):
                        q = 2 * (NS * n + s) + g
                        a.wait_ge(f_ps, 2 * n)
                        a.wait_ge(turned, q + 1)
                        r = (S0, P)[g]
                        if l == 3:
                            a.activation(ts[0:r, 2 * s + g, :], pt[0:r, g, :], ACT.Copy).then_inc(ts_ok, 1)
                        elif g == 0:
                            a.activation(ts[0:r, 2 * s + g, :], pt[0:r, g, :], ACT.Identity, scale=wt("ln1w"), bias=wt("ln1b")).then_inc(ts_ok, 1)
                        else:
                            a.activation(ts[0:r, 2 * s + g, :], pt[0:r, g, :], ACT.Copy, scale=wt("ln1v")).then_inc(ts_ok, 1)

            def hidden(i, u, j):
                if l == 3:
                    a.wait_ge(h_ps, i + 1)
                    a.activation(hs[:], ph[0:64, :], ACT.Relu).then_inc(h_ok, 1)
                for g in range(3):
                    r = (P, P, V3)[g]
                    a.wait_ge(w_ps, 3 * i + g + 1)
                    if g == 0:
                        a.wait_ge(prod_ok, 3 * i)
                    if l == 3:
                        a.activation(ws[0:r, g, :], ph[0:r], ACT.Copy).then_inc(w_ok, 1)
                    else:
                        a.activation(ws[0:r, g, :], ph[0:r], ACT.Identity, bias=wt(f"roff{g}")).then_inc(w_ok, 1)

            def finish(i):
                if l == 2:
                    a.wait_ge(val_ok, 4 * i)
                else:
                    a.wait_ge(c_ps, i)
                for t in range(T):
                    a.wait_ge(o_ps, T * i + t + 1)
                    a.activation(ob[:, t, :], po[:, t % 2, 0:OW], ACT.Copy).then_inc(ob_ok, 1)
                    e = po[:, t % 2, OW:OW + V3].rearrange("p (u c) -> p u c", c=3)
                    a.activation(e5[:, t, :, 0:3], e, ACT.Copy).then_inc(ob_ok, 1)
                    a.activation(e5[:, t, :, 3:5], e[:, :, 0:2], ACT.Copy).then_inc(ob_ok, 1)
                if l == 2:
                    a.wait_ge(ob_ok, 3 * T * (i + 1))
                    a.activation(sl[:], ob[:, :, 32:96], ACT.Silu).then_inc(sl_ok, 1)
                else:
                    a.wait_ge(added, 16 * T * i)
                    a.wait_ge(c_ps, i + 1)
                    a.activation(summed[:], pc[:, :, 0:W], ACT.Copy).then_inc(sum_ok, 1)

            front(0, 0, 0)
            copies(0)

            def step(j, u):
                i = 2 * j + u
                hidden(i, u, j)
                front(i + 1, 1 - u, j + u)
                copies(i + 1)
                finish(i)

            by_twos(a, NB, step)

        @block.tensor
        def _(pe):
            def front(n, u):
                for s in range(NS):
                    q = NS * n + s
                    pe.wait_ge(rows_v, 2 * (q + 1))
                    pe.wait_ge(ts_ok, 2 * q)
                    fence(pe)
                    for t in range(T):
                        last = pe.transpose(pt[0:S0, 0, t * P:(t + 1) * P], xg[s][u][:, t, 0:S0], wt("ident"))
                    last.then_inc(turned, 1)
                    for t in range(T):
                        last = pe.transpose(pt[:, 1, t * P:(t + 1) * P], xg[s][u][:, t, S0:192], wt("ident"))
                    last.then_inc(turned, 1)

            front(0, 0)

            def step(j, u):
                i = 2 * j + u
                hid = hs
                pe.wait_ge(loaded[u], 16 * NL * (j + 1))
                if l == 3:
                    pe.wait_ge(w_ok, 3 * i)
                    fence(pe)
                    pe.matmul(ph[0:64, :], wt("h3"), esT[u][:], start=True, stop=True).then_inc(h_ps, 1)
                else:
                    hid = esT[u]
                def transformed(g):
                    pe.wait_ge(ts_ok, 2 * NS * (i + 1))
                    pe.wait_ge(prod_ok, 3 * i + g)
                    r = (S0, P)[g]
                    for s in range(NS):
                        last = pe.matmul(pf[:], wt(f"f{g + 1}_{l}{s}"), ts[0:r, 2 * s + g, :], start=(s == 0), stop=(s == NS - 1))
                    last.then_inc(f_ps, 1)

                def weights(g):
                    pe.wait_ge(w_ok, 3 * i + g)
                    pe.matmul(ph[0:(P, P, V3)[g]], wt(f"w{g + 1}_{l}"), hid[:], start=True, stop=True).then_inc(w_ps, 1)

                transformed(0)
                if l == 3:
                    pe.wait_ge(h_ok, i + 1)
                weights(0)
                weights(1)
                transformed(1)
                weights(2)
                front(i + 1, 1 - u)
                pe.wait_ge(prod_ok, 3 * i + 3)
                for t in range(T):
                    pe.wait_ge(ob_ok, due(3 * (T * i + t - 1)))
                    cut = slice(t * P, (t + 1) * P)
                    pe.matmul(po[:, t % 2, 0:OW], pr[:, 0, cut], wt(f"o1_{l}"), start=True, stop=False)
                    if l == 2:
                        pe.matmul(po[:, t % 2, 32:OW], wt("one"), wt("linb"), start=False, stop=False)
                    pe.matmul(po[:, t % 2, 32:OW], pr[:, 1, cut], wt(f"o2_{l}"), start=False, stop=True)
                    pe.matmul(po[:, t % 2, OW:OW + V3], pr[0:V3, 2, cut], wt(f"o3_{l}"), start=True, stop=True).then_inc(o_ps, 1)
                if l == 3:
                    pe.wait_ge(msg_v, MV * (i + 1))
                    pe.wait_ge(same_ok, T * (i + 1))
                    pe.wait_ge(sum_ok, i)
                    for t in range(T):
                        for s in range(T):
                            last = pe.matmul(pc[:, t, 0:W], same[:, s, t * P:(t + 1) * P], ob[:, s, 32:OW], start=(s == 0), stop=(s == T - 1))
                    last.then_inc(c_ps, 1)
                    pe.wait_ge(c_ps, i + 1)
                else:
                    pe.wait_ge(o_ps, T * (i + 1))
                pe.sem_inc(freed, 1)

            by_twos(pe, NB, step)


def hidden_phase(nc, dram, wt):
    with ExitStack() as ctx:
        sb = lambda n, s, d=F32: ctx.enter_context(nc.sbuf_tensor(f"{n}_h", s, d))
        ps = lambda n, s: ctx.enter_context(nc.psum_tensor(f"{n}_h", s, F32))
        sem = semaphores(nc, ctx, lambda n: f"{n}_h")
        both = lambda f, n, *a: [f(f"{n}{k}", *a) for k in range(2)]
        esT = both(sb, "esT", [64, B])
        lin = both(sb, "lin", [P, T, 64])
        st = both(sb, "st", [P, T, 6])
        mv = both(sb, "mv", [P, T, 2])
        ve = both(sb, "ve", [P, T])
        rs = both(sb, "rs", [P, T])
        hid = both(sb, "hid", [64, B])
        pl = both(ps, "pl", [P, T, 64])
        pt = both(ps, "pt", [64, B])
        loaded = both(sem, "loaded")
        lin_ps = both(sem, "lin_ps")
        lin_ok = both(sem, "lin_ok")
        st_ok = both(sem, "st_ok")
        rs_ok = both(sem, "rs_ok")
        nrm = both(sem, "nrm")
        turned = both(sem, "turned")
        hid_ok = both(sem, "hid_ok")
        kept = sem("kept")
        turn = sem("turn")

        def fence(eng):
            eng.sem_inc(turn, 1)

        def staged(eng, stages):
            for f in stages:
                f(0, 0)

            def step(j, u):
                for f in stages:
                    f(0, 2 * j + u + 1)
                    f(1, 2 * j + u)
            by_twos(eng, NB, step)

        block = ctx.enter_context(nc.Block())

        @block.sync
        def _(sp):
            def load(n, u):
                sp.wait_ge(lin_ps[0], due(n - 1))
                sp.dma_start(esT[u][:], dram["ea64T"][:, bass.ds(n * B, B)]).then_inc(loaded[u], 16)

            load(0, 0)

            def step(j, u):
                load(2 * j + u + 1, 1 - u)
                sp.wait_ge(hid_ok[1], 2 * j + u + 1)
                sp.dma_start(dram["hid"][:, bass.ds((2 * j + u) * B, B)], hid[1][:]).then_inc(kept, 16)

            by_twos(sp, NB, step)
            sp.wait_ge(kept, 16 * NB)

        @block.tensor
        def _(pe):
            def linear(k, n, es, got):
                pe.wait_ge(lin_ok[k], n)
                if k == 0:
                    pe.wait_ge(loaded[es], got)
                else:
                    pe.wait_ge(hid_ok[0], n + 1)
                fence(pe)
                src = esT[es] if k == 0 else hid[0]
                for t in range(T):
                    pe.matmul(pl[k][:, t, :], wt("one"), wt(f"rb{k}"), start=True, stop=False)
                    last = pe.matmul(pl[k][:, t, :], src[:, t * P:(t + 1) * P], wt(f"rw{k}"), start=False, stop=True)
                last.then_inc(lin_ps[k], 1)

            def turn_rows(k, n):
                pe.wait_ge(nrm[k], 2 * (n + 1))
                pe.wait_ge(hid_ok[k], n)
                fence(pe)
                for t in range(T):
                    last = pe.transpose(pt[k][:, t * P:(t + 1) * P], lin[k][:, t, :], wt("ident"))
                last.then_inc(turned[k], 1)

            linear(0, 0, 0, 16)
            turn_rows(0, 0)

            def step(j, u):
                i = 2 * j + u
                linear(0, i + 1, 1 - u, 16 * (j + u + 1))
                linear(1, i, 0, 0)
                turn_rows(0, i + 1)
                turn_rows(1, i)
            by_twos(pe, NB, step)

        @block.scalar
        def _(a):
            def copied(k, n):
                a.wait_ge(lin_ps[k], n + 1)
                a.wait_ge(turned[k], n)
                a.activation(lin[k][:], pl[k][:], ACT.Copy).then_inc(lin_ok[k], 1)

            def silu(k, n):
                a.wait_ge(turned[k], n + 1)
                if k == 0:
                    a.wait_ge(lin_ps[1], n)
                else:
                    a.wait_ge(kept, 16 * n)
                a.activation(hid[k][:], pt[k][:], ACT.Silu, scale=wt(f"rg{k}"), bias=wt(f"rbe{k}")).then_inc(hid_ok[k], 1)

            staged(a, (copied, silu))

        @block.vector
        def _(v):
            def stats(k, n):
                v.wait_ge(lin_ok[k], n + 1)
                v.wait_ge(rs_ok[k], n)
                for t in range(T):
                    v.bn_stats(st[k][:, t, :], lin[k][:, t, :]).then_inc(st_ok[k], 1)
                v.wait_ge(st_ok[k], 9 * n + 4)
                fence(v)
                for t in range(T):
                    v.bn_aggr(mv[k][:, t, :], st[k][:, t, :]).then_inc(st_ok[k], 1)
                v.wait_ge(st_ok[k], 9 * n + 8)
                v.tensor_scalar(ve[k][:], mv[k][:, :, 1], EPS, None, ALU.add).then_inc(st_ok[k], 1)
                v.tensor_tensor(lin[k][:], lin[k][:], mv[k][:, :, 0:1].to_broadcast([P, T, 64]), ALU.subtract).then_inc(nrm[k], 1)

            def scaled(k, n):
                v.wait_ge(rs_ok[k], n + 1)
                v.wait_ge(nrm[k], 2 * n + 1)
                v.tensor_tensor(lin[k][:], lin[k][:], rs[k][:].unsqueeze(2).to_broadcast([P, T, 64]), ALU.mult).then_inc(nrm[k], 1)

            staged(v, (stats, scaled))

        @block.gpsimd
        def _(pool):
            def powers(k, n):
                pool.wait_ge(nrm[k], 2 * n)
                fence(pool)
                pool.wait_ge(st_ok[k], 9 * (n + 1))
                fence(pool)
                pool.tensor_tensor(rs[k][:], ve[k][:], wt("mhalf"), ALU.pow).then_inc(rs_ok[k], 1)

            staged(pool, (powers,))


def attention_max_phase(nc, dram, mx, wt):
    H = 8
    with ExitStack() as ctx:
        sb = lambda n, s, d=F32: ctx.enter_context(nc.sbuf_tensor(f"{n}_m", s, d))
        ps = lambda n, s: ctx.enter_context(nc.psum_tensor(f"{n}_m", s, F32))
        sem = semaphores(nc, ctx, lambda n: f"{n}_m")
        tidx = [sb(f"tidx{u}", [P, T], I32) for u in range(2)]
        cidx = [sb(f"cidx{u}", [P, T], U32) for u in range(2)]
        trow = [sb(f"trow{u}", [P, B], I32) for u in range(2)]
        arow = [sb(f"arow{u}", [P, B * H]) for u in range(2)]
        least = sb("least", [P, NA // P * H])
        tf = sb("tf", [P, T])
        same = sb("same", [P, T, B])
        apart = sb("apart", [P, T, P])
        masked = sb("masked", [P, 2, H, P])
        junk = sb("junk", [P, T, P])
        cnt = sb("cnt", [P, T])
        first = sb("first", [P, T])
        top = sb("top", [P, T, H])
        rep = sb("rep", [P, T, H + 1])
        bl = sb("bl", [P, T * T, H + 1])
        gone = sb("gone", [P, T * T])
        blk = sb("blk", [P, T, H])
        old = sb("old", [P, T, H])
        new = sb("new", [P, T, H])
        pm = ps("pm", [P, T * T, H + 1])
        l_set = sem("l_set")
        l_out = sem("l_out")
        loaded = [sem("loaded0"), sem("loaded1")]
        freed = sem("freed")
        tf_ok = sem("tf_ok")
        same_ok = sem("same_ok")
        ap_ok = sem("ap_ok")
        mk_ok = sem("mk_ok")
        top_ok = sem("top_ok")
        rep_ok = sem("rep_ok")
        m_ps = sem("m_ps")
        blk_ok = sem("blk_ok")
        old_in = sem("old_in")
        new_ok = sem("new_ok")
        sent = sem("sent")
        turn = sem("turn")

        def fence(eng):
            eng.sem_inc(turn, 1)

        block = ctx.enter_context(nc.Block())

        @block.sync
        def _(sp):
            sp.wait_ge(l_set, 1)
            sp.dma_start(mx.rearrange("(p r) c -> p (r c)", p=P), least[:]).then_inc(l_out, 16)

            def step(j, u):
                i = 2 * j + u
                sp.wait_ge(freed, due(i - 1))
                sp.dma_start(tidx[u][:], dram["dst_t"][bass.ds(i, 1)].rearrange("a p t -> (a p) t")).then_inc(loaded[u], 16)
                sp.dma_start(cidx[u][:], dram["cidx"][bass.ds(i, 1)].rearrange("a p t -> (a p) t")).then_inc(loaded[u], 16)
                sp.dma_start(trow[u][:], dram["dst_r"][bass.ds(i, 1)].broadcast_to([P, B])).then_inc(loaded[u], 16)
                sp.dma_start(arow[u][:], dram["att"][bass.ds(i * B, B)].rearrange("(a e) h -> a (e h)", a=1).broadcast_to([P, B * H])).then_inc(loaded[u], 16)

            by_twos(sp, NB, step)

        @block.gpsimd
        def _(pool):
            pool.memset(least[:], -1e30).then_inc(l_set, 1)
            pool.wait_ge(l_out, 16)

            def step(j, u):
                i = 2 * j + u
                pool.wait_ge(loaded[u], 64 * (j + 1))
                fence(pool)
                pool.wait_ge(sent, 16 * T * i)
                fence(pool)
                pool.wait_ge(new_ok, i)
                fence(pool)
                for t in range(T):
                    pool.indirect_dma_start(old[:, t, :], None, mx, bass.IndirectOffsetOnAxis(ap=tidx[u][:, t:t + 1].bitcast(U32), axis=0)).then_inc(old_in, 16)
                pool.wait_ge(new_ok, i + 1)
                fence(pool)
                for t in range(T):
                    pool.indirect_dma_start(mx, bass.IndirectOffsetOnAxis(ap=cidx[u][:, t:t + 1], axis=0), new[:, t, :], None).then_inc(sent, 16)
                pool.wait_ge(sent, 16 * T * (i + 1))
                fence(pool)
                pool.sem_inc(freed, 1)

            by_twos(pool, NB, step)

        @block.vector
        def _(v):
            def step(j, u):
                i = 2 * j + u
                v.wait_ge(loaded[u], 64 * (j + 1))
                v.tensor_copy(tf[:], tidx[u][:]).then_inc(tf_ok, 1)
                v.wait_ge(tf_ok, i + 1)
                v.wait_ge(m_ps, i)
                for t in range(T):
                    v.tensor_scalar(same[:, t, :], trow[u][:], tf[:, t:t + 1], None, ALU.is_equal).then_inc(same_ok, 1)
                for t in range(T):
                    v.tensor_scalar(apart[:, t, :], trow[u][:, t * P:(t + 1) * P], tf[:, t:t + 1], -1e30, ALU.not_equal, ALU.mult).then_inc(ap_ok, 1)
                    v.scalar_tensor_tensor(junk[:, t, :], trow[u][:, t * P:(t + 1) * P], tf[:, t:t + 1], wt("before")[:, 0:P],
                                           ALU.is_equal, ALU.mult, accum_out=cnt[:, t:t + 1]).then_inc(ap_ok, 1)
                v.wait_ge(ap_ok, 9 * i + 8)
                v.tensor_scalar(first[:], cnt[:], 0.0, None, ALU.is_equal).then_inc(ap_ok, 1)
                for t in range(T):
                    v.wait_ge(top_ok, due(T * i + t - 1))
                    v.tensor_tensor(masked[:, t % 2], arow[u][:, t * P * H:(t + 1) * P * H].rearrange("p (e h) -> p h e", h=H),
                                    apart[:, t, :].unsqueeze(1).to_broadcast([P, H, P]), ALU.add).then_inc(mk_ok, 1)
                    v.wait_ge(mk_ok, T * i + t + 1)
                    v.tensor_reduce(top[:, t, :], masked[:, t % 2], AX.X, ALU.max).then_inc(top_ok, 1)
                v.wait_ge(ap_ok, 9 * i + 9)
                v.wait_ge(top_ok, T * (i + 1))
                v.tensor_tensor(rep[:, :, 0:H], top[:], first[:].unsqueeze(2).to_broadcast([P, T, H]), ALU.mult).then_inc(rep_ok, 1)
                v.tensor_copy(rep[:, :, H], first[:]).then_inc(rep_ok, 1)
                v.wait_ge(m_ps, i + 1)
                v.tensor_copy(bl[:], pm[:]).then_inc(blk_ok, 1)
                v.wait_ge(blk_ok, 4 * i + 1)
                v.tensor_scalar(gone[:], bl[:, :, H], -1.0, 1e30, ALU.add, ALU.mult).then_inc(blk_ok, 1)
                v.wait_ge(blk_ok, 4 * i + 2)
                v.tensor_tensor(bl[:, :, 0:H], bl[:, :, 0:H], gone[:].unsqueeze(2).to_broadcast([P, T * T, H]), ALU.add).then_inc(blk_ok, 1)
                v.wait_ge(blk_ok, 4 * i + 3)
                v.tensor_reduce(blk[:], bl[:, :, 0:H].rearrange("p (t s) h -> p t h s", s=T), AX.X, ALU.max).then_inc(blk_ok, 1)
                v.wait_ge(blk_ok, 4 * i + 4)
                v.wait_ge(old_in, 16 * T * (i + 1))
                v.tensor_tensor(new[:], blk[:], old[:], ALU.max).then_inc(new_ok, 1)

            by_twos(v, NB, step)

        @block.tensor
        def _(pe):
            def step(j, u):
                i = 2 * j + u
                pe.wait_ge(rep_ok, 2 * (i + 1))
                pe.wait_ge(same_ok, T * (i + 1))
                pe.wait_ge(blk_ok, 4 * i)
                for t in range(T):
                    for s in range(T):
                        last = pe.matmul(pm[:, T * t + s, :], same[:, s, t * P:(t + 1) * P], rep[:, s, :], start=True, stop=True)
                last.then_inc(m_ps, 1)

            by_twos(pe, NB, step)


def attention_sum_phase(nc, dram, mx, agg, wt):
    H = 8
    W = AW[2]
    with ExitStack() as ctx:
        sb = lambda n, s, d=F32: ctx.enter_context(nc.sbuf_tensor(f"{n}_a", s, d))
        ps = lambda n, s: ctx.enter_context(nc.psum_tensor(f"{n}_a", s, F32))
        sem = semaphores(nc, ctx, lambda n: f"{n}_a")
        tidx = [sb(f"tidx{u}", [P, T], I32) for u in range(2)]
        cidx = [sb(f"cidx{u}", [P, T], U32) for u in range(2)]
        trow = [sb(f"trow{u}", [P, B], I32) for u in range(2)]
        val = [sb(f"val{u}", [P, T, W]) for u in range(2)]
        big = [sb(f"big{u}", [P, T, H]) for u in range(2)]
        tf = [sb(f"tf{u}", [P, T]) for u in range(2)]
        same = [sb(f"same{u}", [P, T, B]) for u in range(2)]
        dif = sb("dif", [P, T, H])
        msg = [sb(f"msg{u}", [P, T, W]) for u in range(2)]
        summed = sb("summed", [P, T, W])
        pc = ps("pc", [P, T, 256])
        loaded = [sem("loaded0"), sem("loaded1")]
        big_in = [sem("big_in0"), sem("big_in1")]
        tf_ok = sem("tf_ok")
        same_ok = sem("same_ok")
        dif_ok = sem("dif_ok")
        ex_ok = sem("ex_ok")
        msg_ok = sem("msg_ok")
        c_ps = sem("c_ps")
        sum_ok = sem("sum_ok")
        added = sem("added")
        turn = sem("turn")

        def fence(eng):
            eng.sem_inc(turn, 1)

        block = ctx.enter_context(nc.Block())

        @block.sync
        def _(sp):
            def step(j, u):
                i = 2 * j + u
                sp.wait_ge(added, due(16 * T * (i - 1)))
                sp.dma_start(tidx[u][:], dram["dst_t"][bass.ds(i, 1)].rearrange("a p t -> (a p) t")).then_inc(loaded[u], 16)
                sp.dma_start(cidx[u][:], dram["cidx"][bass.ds(i, 1)].rearrange("a p t -> (a p) t")).then_inc(loaded[u], 16)
                sp.dma_start(trow[u][:], dram["dst_r"][bass.ds(i, 1)].broadcast_to([P, B])).then_inc(loaded[u], 16)
                sp.dma_start(val[u][:], dram["val"][bass.ds(i, 1)].rearrange("a p t c -> (a p) t c")).then_inc(loaded[u], 16)

            by_twos(sp, NB, step)

        @block.gpsimd
        def _(pool):
            def gather(i, u, k):
                pool.wait_ge(loaded[u], 64 * (k + 1))
                fence(pool)
                for t in range(T):
                    pool.indirect_dma_start(big[u][:, t, :], None, mx, bass.IndirectOffsetOnAxis(ap=tidx[u][:, t:t + 1].bitcast(U32), axis=0)).then_inc(big_in[u], 16)

            def send(i, u):
                pool.wait_ge(added, 16 * T * i)
                fence(pool)
                pool.wait_ge(sum_ok, i + 1)
                fence(pool)
                for t in range(T):
                    pool.indirect_dma_start(agg, bass.IndirectOffsetOnAxis(ap=cidx[u][:, t:t + 1], axis=0), summed[:, t, :], None, compute_op=ALU.add).then_inc(added, 16)

            gather(0, 0, 0)
            gather(1, 1, 0)
            send(0, 0)
            with pool.Fori(1, NB // 2) as j:
                gather(2 * j, 0, j)
                send(2 * j - 1, 1)
                gather(2 * j + 1, 1, j)
                send(2 * j, 0)
            send(NB - 1, 1)
            pool.wait_ge(added, 16 * T * NB)

        @block.vector
        def _(v):
            def step(j, u):
                i = 2 * j + u
                v.wait_ge(loaded[u], 64 * (j + 1))
                v.tensor_copy(tf[u][:], tidx[u][:]).then_inc(tf_ok, 1)
                v.wait_ge(big_in[u], 16 * T * (j + 1))
                v.tensor_tensor(dif[:], val[u][:, :, 160:168], big[u][:], ALU.subtract).then_inc(dif_ok, 1)
                v.wait_ge(tf_ok, i + 1)
                v.wait_ge(c_ps, due(i - 1))
                for t in range(T):
                    v.tensor_scalar(same[u][:, t, :], trow[u][:], tf[u][:, t:t + 1], None, ALU.is_equal).then_inc(same_ok, 1)
                v.wait_ge(ex_ok, i + 1)
                v.tensor_tensor(msg[u][:, :, 0:64].rearrange("p t (h k) -> p t h k", h=H), val[u][:, :, 0:64].rearrange("p t (h k) -> p t h k", h=H),
                                msg[u][:, :, 160:168].unsqueeze(3).to_broadcast([P, T, H, 8]), ALU.mult).then_inc(msg_ok, 1)
                v.tensor_tensor(msg[u][:, :, 64:160].rearrange("p t (h k) -> p t h k", h=H), val[u][:, :, 64:160].rearrange("p t (h k) -> p t h k", h=H),
                                msg[u][:, :, 160:168].unsqueeze(3).to_broadcast([P, T, H, 12]), ALU.mult).then_inc(msg_ok, 1)

            by_twos(v, NB, step)

        @block.scalar
        def _(a):
            def step(j, u):
                i = 2 * j + u
                a.wait_ge(dif_ok, i + 1)
                a.wait_ge(c_ps, due(i - 1))
                a.activation(msg[u][:, :, 160:168], dif[:], ACT.Exp, scale=0.8).then_inc(ex_ok, 1)
                a.wait_ge(c_ps, i + 1)
                a.wait_ge(added, 16 * T * i)
                a.activation(summed[:], pc[:, :, 0:W], ACT.Copy).then_inc(sum_ok, 1)

            by_twos(a, NB, step)

        @block.tensor
        def _(pe):
            def step(j, u):
                i = 2 * j + u
                pe.wait_ge(msg_ok, 2 * (i + 1))
                pe.wait_ge(same_ok, T * (i + 1))
                pe.wait_ge(sum_ok, i)
                for t in range(T):
                    for s in range(T):
                        last = pe.matmul(pc[:, t, 0:W], same[u][:, s, t * P:(t + 1) * P], msg[u][:, s, :], start=(s == 0), stop=(s == T - 1))
                last.then_inc(c_ps, 1)

            by_twos(pe, NB, step)


def rows_of(t, c, parts, w):
    return t[bass.ds(c * B, parts * T), 0:w].rearrange("(p t) c -> p (t c)", t=T)


def node_blocks(eng, step):
    by_twos(eng, NC, lambda j, u: step(2 * j + u, u, j, P))
    step(NC - 1, (NC - 1) % 2, (NC - 1) // 2, P)
    step(NC, NC % 2, NC // 2, LASTP)


def node_phase_3(nc, x, agg, out, wt):
    with ExitStack() as ctx:
        sb = lambda n, s, d=F32: ctx.enter_context(nc.sbuf_tensor(f"{n}_n3", s, d))
        ps = lambda n, s: ctx.enter_context(nc.psum_tensor(f"{n}_n3", s, F32))
        sem = semaphores(nc, ctx, lambda n: f"{n}_n3")
        xr = [sb(f"xr{u}", [P, T, XW]) for u in range(2)]
        ar = [sb(f"ar{u}", [P, T, 192]) for u in range(2)]
        tss = sb("tss", [64, B])
        tsv = sb("tsv", [96, B])
        so = sb("so", [P, T, 192])
        gt = sb("gt", [P, T, V1])
        sg = sb("sg", [P, T, D])
        y = [sb(f"y{u}", [P, T, D]) for u in range(2)]
        st = sb("st", [P, T, 6])
        mv = sb("mv", [P, T, 2])
        ve = sb("ve", [P, T])
        nm = sb("nm", [P, T])
        rs = [sb(f"rs{u}", [P, T]) for u in range(2)]
        nr = [sb(f"nr{u}", [P, T]) for u in range(2)]
        xn = [sb(f"xn{u}", [P, T, D]) for u in range(2)]
        pts = ps("pts", [64, B])
        ptv = ps("ptv", [96, B])
        pk = [ps(f"pk{u}", [P, T, 256]) for u in range(2)]
        loaded = [sem("loaded0"), sem("loaded1")]
        used = sem("used")
        turned = sem("turned")
        ts_ok = sem("ts_ok")
        k_ps = sem("k_ps")
        so_ok = sem("so_ok")
        act_ok = sem("act_ok")
        sg_ok = sem("sg_ok")
        y_ok = sem("y_ok")
        st_ok = sem("st_ok")
        rs_ok = sem("rs_ok")
        xn_ok = sem("xn_ok")
        stored = [sem("stored0"), sem("stored1")]
        turn = sem("turn")

        def fence(eng):
            eng.sem_inc(turn, 1)

        block = ctx.enter_context(nc.Block())

        @block.sync
        def _(sp):
            def load(c, u, k, parts):
                sp.wait_ge(used, due(c - 1))
                sp.dma_start(xr[u][0:parts].rearrange("p t c -> p (t c)"), rows_of(x, c, parts, XW)).then_inc(loaded[u], 16)
                sp.dma_start(ar[u][0:parts].rearrange("p t c -> p (t c)"), rows_of(agg, c, parts, 192)).then_inc(loaded[u], 16)

            node_blocks(sp, load)

        @block.tensor
        def _(pe):
            def step(c, u, k, parts):
                pe.wait_ge(loaded[u], 32 * (k + 1))
                pe.wait_ge(ts_ok, 2 * c)
                for t in range(T):
                    last = pe.transpose(ptv[:, t * P:(t + 1) * P], xr[u][:, t, S0:D], wt("ident"))
                last.then_inc(turned, 1)
                for t in range(T):
                    last = pe.transpose(pts[:, t * P:(t + 1) * P], xr[u][:, t, 0:S0], wt("ident"))
                last.then_inc(turned, 1)
                pe.wait_ge(ts_ok, 2 * c + 2)
                pe.wait_ge(so_ok, due(c - 1))
                for t in range(T):
                    pe.matmul(pk[u][:, t, 96:192], tsv[:, t * P:(t + 1) * P], wt("nv_3"), start=True, stop=True)
                    last = pe.matmul(pk[u][:, t, 0:96], tss[:, t * P:(t + 1) * P], wt("ns_3"), start=True, stop=True)
                last.then_inc(k_ps, 1)

            node_blocks(pe, step)

        @block.scalar
        def _(a):
            def step(c, u, k, parts):
                a.wait_ge(k_ps, c)
                a.wait_ge(turned, 2 * c + 1)
                a.activation(tsv[:], ptv[:], ACT.Copy).then_inc(ts_ok, 1)
                a.wait_ge(turned, 2 * c + 2)
                a.activation(tss[:], pts[:], ACT.Copy).then_inc(ts_ok, 1)
                a.wait_ge(so_ok, c + 1)
                a.wait_ge(y_ok, c)
                a.activation(sg[:, :, 0:S0], so[:, :, 0:S0], ACT.Silu).then_inc(act_ok, 1)
                a.activation(gt[:], so[:, :, S0:96], ACT.Tanh, scale=0.5).then_inc(act_ok, 1)
                a.wait_ge(rs_ok, 2 * c + 2)
                a.wait_ge(stored[u], 16 * k)
                for t in range(T):
                    a.activation(xn[u][:, t, :], y[u][:, t, :], ACT.Identity, bias=nr[u][:, t:t + 1], scale=rs[u][:, t:t + 1]).then_inc(xn_ok, 1)

            node_blocks(a, step)

        @block.vector
        def _(v):
            def step(c, u, k, parts):
                v.wait_ge(loaded[u], 32 * (k + 1))
                v.wait_ge(k_ps, c + 1)
                v.wait_ge(act_ok, 2 * c)
                v.scalar_tensor_tensor(so[:], ar[u][:], 1.0 / 32.0, pk[u][:, :, 0:192], ALU.mult, ALU.add).then_inc(so_ok, 1)
                v.wait_ge(act_ok, 2 * c + 2)
                v.tensor_scalar(gt[:], gt[:], 0.5, 0.5, ALU.mult, ALU.add).then_inc(sg_ok, 1)
                v.wait_ge(sg_ok, 2 * c + 1)
                v.tensor_tensor(sg[:, :, S0:D].rearrange("p t (u c) -> p t u c", c=3), so[:, :, 96:192].rearrange("p t (u c) -> p t u c", c=3),
                                gt[:].unsqueeze(3).to_broadcast([P, T, V1, 3]), ALU.mult).then_inc(sg_ok, 1)
                v.wait_ge(sg_ok, 2 * c + 2)
                v.wait_ge(xn_ok, due(T * (c - 1)))
                v.tensor_tensor(y[u][:], sg[:], xr[u][:, :, 0:D], ALU.add).then_inc(y_ok, 1)
                v.wait_ge(y_ok, c + 1)
                for t in range(T):
                    v.bn_stats(st[:, t, :], y[u][:, t, :]).then_inc(st_ok, 1)
                v.wait_ge(st_ok, 10 * c + 4)
                fence(v)
                for t in range(T):
                    v.bn_aggr(mv[:, t, :], st[:, t, :]).then_inc(st_ok, 1)
                v.wait_ge(st_ok, 10 * c + 8)
                v.wait_ge(rs_ok, 2 * c)
                v.tensor_scalar(ve[:], mv[:, :, 1], EPS, None, ALU.add).then_inc(st_ok, 1)
                v.tensor_scalar(nm[:], mv[:, :, 0], -1.0, None, ALU.mult).then_inc(st_ok, 1)

            node_blocks(v, step)

        @block.gpsimd
        def _(pool):
            def step(c, u, k, parts):
                pool.wait_ge(xn_ok, due(T * (c - 1)))
                fence(pool)
                pool.wait_ge(st_ok, 10 * (c + 1))
                fence(pool)
                pool.sem_inc(used, 1)
                pool.tensor_tensor(rs[u][:], ve[:], wt("mhalf"), ALU.pow).then_inc(rs_ok, 1)
                pool.wait_ge(rs_ok, 2 * c + 1)
                fence(pool)
                pool.tensor_tensor(nr[u][:], nm[:], rs[u][:], ALU.mult).then_inc(rs_ok, 1)
                pool.wait_ge(xn_ok, T * (c + 1))
                fence(pool)
                pool.dma_start(rows_of(out, c, parts, D), xn[u][0:parts].rearrange("p t c -> p (t c)")).then_inc(stored[u], 16)

            node_blocks(pool, step)
            pool.wait_ge(stored[0], 16 * (NC // 2 + 1))
            pool.wait_ge(stored[1], 16 * ((NC + 1) // 2))


def node_phase_2(nc, x, agg, xo, wt):
    H = 8
    with ExitStack() as ctx:
        sb = lambda n, s, d=F32: ctx.enter_context(nc.sbuf_tensor(f"{n}_n2", s, d))
        ps = lambda n, s: ctx.enter_context(nc.psum_tensor(f"{n}_n2", s, F32))
        sem = semaphores(nc, ctx, lambda n: f"{n}_n2")
        xr = [sb(f"xr{u}", [P, T, XW]) for u in range(2)]
        ar = [sb(f"ar{u}", [P, T, AW[2]]) for u in range(2)]
        den = sb("den", [P, T, H])
        an = sb("an", [P, T, D])
        tss = sb("tss", [64, B])
        tsv = sb("tsv", [96, B])
        x1 = sb("x1", [P, T, D])
        xx = [sb(f"xx{u}", [P, T, D]) for u in range(2)]
        st = sb("st", [P, T, 6])
        mv = sb("mv", [P, T, 2])
        sq = sb("sq", [P, T, V3])
        var = sb("var", [P, 2, T])
        rs1 = sb("rsa", [P, 2, T])
        hat = sb("hat", [P, T, XW])
        t2s = sb("t2s", [65, B])
        t2v = sb("t2v", [96, B])
        hc = sb("hc", [P, B])
        tg = sb("tg", [96, 2, B])
        gv = sb("gv", [96, 2, B])
        up = sb("up", [P, T, D])
        y = [sb(f"y{u}", [P, T, D]) for u in range(2)]
        st2 = sb("st2", [P, T, 6])
        mv2 = sb("mv2", [P, T, 2])
        ve = sb("ve", [P, T])
        nm = sb("nm", [P, T])
        rs = [sb(f"rs{u}", [P, T]) for u in range(2)]
        nr = [sb(f"nr{u}", [P, T]) for u in range(2)]
        xn = [sb(f"xn{u}", [P, T, XW]) for u in range(2)]
        pts = ps("pts", [65, B])
        ptv = ps("ptv", [96, B])
        pk = ps("pk", [P, T, 256])
        pf = [ps(f"pf{k}", [P, B]) for k in range(4)]
        b_ps = sem("b_ps")
        b_ok = sem("b_ok")
        loaded = [sem("loaded0"), sem("loaded1")]
        used = sem("used")
        den_ok = sem("den_ok")
        an_ok = sem("an_ok")
        turned = sem("turned")
        ts_ok = sem("ts_ok")
        k_ps = sem("k_ps")
        x1_ok = sem("x1_ok")
        xx_ok = sem("xx_ok")
        sq_ok = sem("sq_ok")
        st_ok = sem("st_ok")
        r1_ok = sem("r1_ok")
        hat_ok = sem("hat_ok")
        f_ps = sem("f_ps")
        act_ok = sem("act_ok")
        gv_ok = sem("gv_ok")
        up_ok = sem("up_ok")
        y_ok = sem("y_ok")
        s2_ok = sem("s2_ok")
        rs_ok = sem("rs_ok")
        at_ok = sem("at_ok")
        xn_ok = sem("xn_ok")
        stored = [sem("stored0"), sem("stored1")]
        turn = sem("turn")

        def fence(eng):
            eng.sem_inc(turn, 1)

        def staged(eng, order):
            for half, f in order:
                if half == "a":
                    f(0, 0, 0, P)

            def step(c, u, k, parts):
                for half, f in order:
                    if half == "b":
                        f(c, u, k, parts)
                    elif not (isinstance(c, int) and c == NC):
                        f(c + 1, 1 - u, k + u, P)
            node_blocks(eng, step)

        block = ctx.enter_context(nc.Block())

        @block.sync
        def _(sp):
            def load(c, u, k, parts):
                sp.wait_ge(used, due(c - 1))
                sp.dma_start(xr[u][0:parts].rearrange("p t c -> p (t c)"), rows_of(x, c, parts, XW)).then_inc(loaded[u], 16)
                sp.dma_start(ar[u][0:parts].rearrange("p t c -> p (t c)"), rows_of(agg, c, parts, AW[2])).then_inc(loaded[u], 16)

            node_blocks(sp, load)

        @block.tensor
        def _(pe):
            pe.matmul(pf[0][0:65, 0:320], wt("b0row"), wt("f1s")[0:64], start=True, stop=False)
            pe.matmul(pf[0][0:65, 0:320], wt("e64"), wt("f1b"), start=False, stop=True).then_inc(b_ps, 1)
            pe.wait_ge(b_ok, 1)

            def a_first(c, u, k, parts):
                pe.wait_ge(an_ok, 2 * (c + 1))
                pe.wait_ge(ts_ok, 4 * c)
                for t in range(T):
                    last = pe.transpose(ptv[:, t * P:(t + 1) * P], an[:, t, S0:D], wt("ident"))
                last.then_inc(turned, 1)
                for t in range(T):
                    last = pe.transpose(pts[0:64, t * P:(t + 1) * P], an[:, t, 0:S0], wt("ident"))
                last.then_inc(turned, 1)
                pe.wait_ge(ts_ok, 4 * c + 2)
                pe.wait_ge(up_ok, due(2 * (c - 1)))
                for t in range(T):
                    pe.matmul(pk[:, t, S0:D], tsv[:, t * P:(t + 1) * P], wt("pv"), start=True, stop=True)
                    pe.matmul(pk[:, t, 0:S0], wt("one"), wt("pb"), start=True, stop=False)
                    last = pe.matmul(pk[:, t, 0:S0], tss[:, t * P:(t + 1) * P], wt("pw"), start=False, stop=True)
                last.then_inc(k_ps, 1)

            def a_second(c, u, k, parts):
                pe.wait_ge(hat_ok, 4 * (c + 1))
                pe.wait_ge(ts_ok, 4 * c + 2)
                for t in range(T):
                    last = pe.transpose(ptv[:, t * P:(t + 1) * P], hat[:, t, 65:XW], wt("ident"))
                last.then_inc(turned, 1)
                for t in range(T):
                    last = pe.transpose(pts[:, t * P:(t + 1) * P], hat[:, t, 0:65], wt("ident"))
                last.then_inc(turned, 1)

            def b_first(c, u, k, parts):
                pe.wait_ge(ts_ok, 4 * c + 4)
                pe.wait_ge(act_ok, 3 * c)
                pe.wait_ge(gv_ok, 2 * c)
                pe.matmul(pf[0][:], wt("f1s")[:, 0:P], t2s[:], start=True, stop=True).then_inc(f_ps, 1)
                pe.matmul(pf[1][0:96], wt("f1s")[:, P:P + 96], t2s[:], start=True, stop=True).then_inc(f_ps, 1)
                pe.matmul(pf[2][0:96], wt("f1v")[:, 0:96], t2v[:], start=True, stop=True).then_inc(f_ps, 1)
                pe.matmul(pf[3][0:96], wt("f1v")[:, 96:192], t2v[:], start=True, stop=True).then_inc(f_ps, 1)
                pe.wait_ge(act_ok, 3 * c + 1)
                pe.matmul(pf[0][0:96], wt("f1s")[:, P + 96:P + 192], t2s[:], start=True, stop=True).then_inc(f_ps, 1)

            def b_second(c, u, k, parts):
                pe.wait_ge(act_ok, 3 * c + 3)
                pe.wait_ge(gv_ok, 2 * c + 2)
                pe.wait_ge(x1_ok, (c + 2) if not (isinstance(c, int) and c == NC) else c + 1)
                for t in range(T):
                    cut = slice(t * P, (t + 1) * P)
                    pe.matmul(pk[:, t, S0:D], gv[:, 0, cut], wt("f2v0"), start=True, stop=False)
                    pe.matmul(pk[:, t, S0:D], gv[:, 1, cut], wt("f2v1"), start=False, stop=True)
                    pe.matmul(pk[:, t, 0:S0], wt("one"), wt("f2b"), start=True, stop=False)
                    last = pe.matmul(pk[:, t, 0:S0], hc[:, cut], wt("f2s"), start=False, stop=True)
                last.then_inc(k_ps, 1)

            staged(pe, (("a", a_first), ("b", b_first), ("a", a_second), ("b", b_second)))

        def proj_at(c):
            return c + 1 if isinstance(c, int) and c == 0 else 2 * c

        def out_at(c):
            return 2 * c + 3 if not (isinstance(c, int) and c == NC) else 2 * c + 2

        @block.scalar
        def _(a):
            a.wait_ge(b_ps, 1)
            a.activation(wt("f1s")[64:65], pf[0][64:65, 0:320], ACT.Copy).then_inc(b_ok, 1)

            def a_first(c, u, k, parts):
                a.wait_ge(k_ps, due(2 * c - 1))
                a.wait_ge(turned, 4 * c + 1)
                a.activation(tsv[:], ptv[:], ACT.Copy).then_inc(ts_ok, 1)
                a.wait_ge(turned, 4 * c + 2)
                a.activation(tss[:], pts[0:64], ACT.Copy).then_inc(ts_ok, 1)
                a.wait_ge(x1_ok, c + 1)
                a.wait_ge(sq_ok, 2 * c)
                a.activation(sq[:], x1[:, :, S0:D], ACT.Square).then_inc(sq_ok, 1)

            def a_second(c, u, k, parts):
                a.wait_ge(f_ps, 5 * c)
                a.wait_ge(turned, 4 * c + 3)
                a.activation(t2v[:], ptv[:], ACT.Copy, scale=wt("ln2v")).then_inc(ts_ok, 1)
                a.wait_ge(turned, 4 * c + 4)
                a.activation(t2s[:], pts[:], ACT.Copy, scale=wt("ln2w")).then_inc(ts_ok, 1)

            def b_first(c, u, k, parts):
                a.wait_ge(f_ps, 5 * c + 1)
                a.wait_ge(k_ps, due(out_before(c)))
                a.activation(hc[:], pf[0][:], ACT.Silu).then_inc(act_ok, 1)
                a.wait_ge(f_ps, 5 * c + 2)
                a.wait_ge(gv_ok, 2 * c)
                a.activation(tg[:, 0, :], pf[1][0:96], ACT.Tanh, scale=0.5).then_inc(act_ok, 1)
                a.wait_ge(f_ps, 5 * c + 5)
                a.activation(tg[:, 1, :], pf[0][0:96], ACT.Tanh, scale=0.5).then_inc(act_ok, 1)

            def out_before(c):
                return 2 * c + 1 if not (isinstance(c, int) and c == 0) else 0

            def b_second(c, u, k, parts):
                a.wait_ge(rs_ok, 2 * c + 2)
                a.wait_ge(at_ok, c + 1)
                for t in range(T):
                    a.activation(xn[u][:, t, 0:D], y[u][:, t, :], ACT.Identity, bias=nr[u][:, t:t + 1], scale=rs[u][:, t:t + 1]).then_inc(xn_ok, 1)

            staged(a, (("a", a_first), ("b", b_first), ("a", a_second), ("b", b_second)))

        @block.vector
        def _(v):
            def a_den(c, u, k, parts):
                v.wait_ge(loaded[u], 32 * (k + 1))
                v.wait_ge(an_ok, 2 * c)
                v.tensor_scalar(den[:], ar[u][:, :, 160:168], 1e-12, None, ALU.add).then_inc(den_ok, 1)
                v.wait_ge(den_ok, 2 * c + 1)
                v.reciprocal(den[:], den[:]).then_inc(den_ok, 1)

            def a_first(c, u, k, parts):
                v.wait_ge(k_ps, proj_at(c))
                v.wait_ge(xx_ok, c)
                v.wait_ge(hat_ok, 4 * c)
                v.tensor_tensor(x1[:], pk[:, :, 0:D], xr[u][:, :, 0:D], ALU.add).then_inc(x1_ok, 1)
                v.wait_ge(x1_ok, c + 1)
                for t in range(T):
                    v.bn_stats(st[:, t, :], x1[:, t, 0:S0]).then_inc(st_ok, 1)
                v.wait_ge(st_ok, 10 * c + 4)
                fence(v)
                for t in range(T):
                    v.bn_aggr(mv[:, t, :], st[:, t, :]).then_inc(st_ok, 1)
                v.wait_ge(r1_ok, 2 * c)
                v.wait_ge(sq_ok, 2 * c + 1)
                v.tensor_reduce(var[:, 1, :], sq[:], AX.X, ALU.add).then_inc(sq_ok, 1)
                v.wait_ge(st_ok, 10 * c + 8)
                v.tensor_scalar(var[:, 0, :], mv[:, :, 1], EPS, None, ALU.add).then_inc(st_ok, 1)
                v.wait_ge(sq_ok, 2 * c + 2)
                v.tensor_scalar(var[:, 1, :], var[:, 1, :], 1.0 / V3, EPS, ALU.mult, ALU.add).then_inc(st_ok, 1)

            def b_first(c, u, k, parts):
                for g in range(2):
                    v.wait_ge(act_ok, 3 * c + 2 + g)
                    v.wait_ge(f_ps, 5 * c + 3 + g)
                    if g == 0:
                        v.wait_ge(k_ps, due(out_before(c)))
                    v.scalar_tensor_tensor(gv[:, g, :], tg[:, g, :], 1.0, pf[2 + g][0:96], ALU.add, ALU.mult).then_inc(gv_ok, 1)

            def out_before(c):
                return 2 * c + 1 if not (isinstance(c, int) and c == 0) else 0

            def a_second(c, u, k, parts):
                v.wait_ge(turned, 4 * c)
                v.wait_ge(r1_ok, 2 * c + 2)
                v.tensor_tensor(hat[:, :, 0:S0], x1[:, :, 0:S0], mv[:, :, 0:1].to_broadcast([P, T, S0]), ALU.subtract).then_inc(hat_ok, 1)
                v.tensor_tensor(hat[:, :, 65:XW], x1[:, :, S0:D], rs1[:, 1, :].unsqueeze(2).to_broadcast([P, T, V3]), ALU.mult).then_inc(hat_ok, 1)
                v.wait_ge(hat_ok, 4 * c + 1)
                v.tensor_tensor(hat[:, :, 0:S0], hat[:, :, 0:S0], rs1[:, 0, :].unsqueeze(2).to_broadcast([P, T, S0]), ALU.mult).then_inc(hat_ok, 1)
                v.tensor_copy(hat[:, :, S0], xr[u][:, :, D]).then_inc(hat_ok, 1)

            def b_second(c, u, k, parts):
                v.wait_ge(k_ps, out_at(c))
                v.wait_ge(y_ok, c)
                v.tensor_tensor(up[:, :, 0:S0], pk[:, :, 0:S0], xr[u][:, :, D:XW].to_broadcast([P, T, S0]), ALU.mult).then_inc(up_ok, 1)
                v.scalar_tensor_tensor(up[:, :, S0:D], pk[:, :, S0:D], 0.5, xr[u][:, :, D:XW].to_broadcast([P, T, V3]), ALU.mult, ALU.mult).then_inc(up_ok, 1)
                v.wait_ge(up_ok, 2 * c + 2)
                v.wait_ge(xx_ok, c + 1)
                v.wait_ge(xn_ok, due(T * (c - 1)))
                v.tensor_tensor(y[u][:], up[:], xx[u][:], ALU.add).then_inc(y_ok, 1)
                v.wait_ge(y_ok, c + 1)
                for t in range(T):
                    v.bn_stats(st2[:, t, :], y[u][:, t, :]).then_inc(s2_ok, 1)
                v.wait_ge(s2_ok, 10 * c + 4)
                fence(v)
                for t in range(T):
                    v.bn_aggr(mv2[:, t, :], st2[:, t, :]).then_inc(s2_ok, 1)
                v.wait_ge(s2_ok, 10 * c + 8)
                v.wait_ge(rs_ok, 2 * c)
                v.tensor_scalar(ve[:], mv2[:, :, 1], EPS, None, ALU.add).then_inc(s2_ok, 1)
                v.tensor_scalar(nm[:], mv2[:, :, 0], -1.0, None, ALU.mult).then_inc(s2_ok, 1)

            staged(v, (("a", a_den), ("a", a_first), ("b", b_first), ("a", a_second), ("b", b_second)))

        @block.gpsimd
        def _(pool):
            def a_sums(c, u, k, parts):
                pool.wait_ge(turned, due(4 * c - 2))
                fence(pool)
                pool.wait_ge(den_ok, 2 * c + 2)
                fence(pool)
                for lo, hi in ((0, 64), (64, 160)):
                    pool.tensor_tensor(an[:, :, lo:hi].rearrange("p t (h k) -> p t h k", h=H), ar[u][:, :, lo:hi].rearrange("p t (h k) -> p t h k", h=H),
                                       den[:].unsqueeze(3).to_broadcast([P, T, H, (hi - lo) // H]), ALU.mult).then_inc(an_ok, 1)

            def a_powers(c, u, k, parts):
                pool.wait_ge(st_ok, 10 * (c + 1))
                fence(pool)
                pool.wait_ge(hat_ok, 4 * c)
                fence(pool)
                pool.tensor_tensor(rs1[:], var[:], wt("mhalf8").rearrange("p (a t) -> p a t", a=2), ALU.pow).then_inc(r1_ok, 1)
                pool.wait_ge(r1_ok, 2 * c + 1)
                fence(pool)
                pool.tensor_tensor(rs1[:], rs1[:], xr[u][:, :, D].unsqueeze(1).to_broadcast([P, 2, T]), ALU.mult).then_inc(r1_ok, 1)
                pool.wait_ge(y_ok, due(c - 1))
                fence(pool)
                pool.tensor_tensor(xx[u][:], x1[:], xr[u][:, :, 0:D], ALU.add).then_inc(xx_ok, 1)

            def b_last(c, u, k, parts):
                pool.wait_ge(stored[u], 16 * k)
                fence(pool)
                pool.tensor_copy(xn[u][:, :, D:XW], xr[u][:, :, D:XW]).then_inc(at_ok, 1)
                pool.wait_ge(xn_ok, due(T * (c - 1)))
                fence(pool)
                pool.wait_ge(s2_ok, 10 * (c + 1))
                fence(pool)
                pool.tensor_tensor(rs[u][:], ve[:], wt("mhalf"), ALU.pow).then_inc(rs_ok, 1)
                pool.wait_ge(rs_ok, 2 * c + 1)
                fence(pool)
                pool.tensor_tensor(nr[u][:], nm[:], rs[u][:], ALU.mult).then_inc(rs_ok, 1)
                pool.wait_ge(at_ok, c + 1)
                fence(pool)
                pool.sem_inc(used, 1)
                pool.wait_ge(xn_ok, T * (c + 1))
                fence(pool)
                pool.dma_start(rows_of(xo, c, parts, XW), xn[u][0:parts].rearrange("p t c -> p (t c)")).then_inc(stored[u], 16)

            staged(pool, (("a", a_sums), ("a", a_powers), ("b", b_last)))
            pool.wait_ge(stored[0], 16 * (NC // 2 + 1))
            pool.wait_ge(stored[1], 16 * ((NC + 1) // 2))


def build(nc, ins, out):
    with ExitStack() as ctx:
        wsb = ctx.enter_context(nc.sbuf_tensor("wsb", [P, WCOLS], F32))
        w_in = ctx.enter_context(nc.semaphore("w_in"))

        def wt(name):
            if name in ("mhalf", "mhalf8"):
                return wt("mhalfn")[:, 0:T if name == "mhalf" else 2 * T]
            r, c, at = SLOTS[name]
            return wsb[0:r, at:at + c]

        def table(name, rows, w, d=F32):
            return nc.dram_tensor(name, (rows, w), d, kind="Internal").ap()

        agg = [table(f"agg{k}", NA, AW[k]) for k in range(4)]
        xs = [ins["x"]] + [table(f"x{k}", N, XW) for k in (1, 2, 3)]
        dram = dict(ins)
        dram["cidx"] = nc.dram_tensor("cidx", (NBP, P, T), U32, kind="Internal").ap()
        dram["hid"] = table("hid", 64, NBP * B)
        dram["val"] = nc.dram_tensor("val", (NB, P, T, AW[2]), F32, kind="Internal").ap()
        dram["att"] = table("att", NB * B, 8)
        mx = table("mx", NA, 8)
        with nc.Block() as block:
            @block.sync
            def _(sp):
                sp.dma_start(wsb[:], ins["w"]).then_inc(w_in, 16)
                sp.dma_start(dram["cidx"][NB:NBP].rearrange("a p t -> (a p) t"), ins["dst_t"][NB:NBP].rearrange("a p t -> (a p) t").bitcast(U32)).then_inc(w_in, 16)
                sp.dma_start(dram["hid"][:, NB * B:NBP * B], ins["ea64T"][:, NB * B:NBP * B]).then_inc(w_in, 16)
                sp.wait_ge(w_in, 48)
        edge_phase_01(nc, 0, xs[0], agg[0], dram, wt, agg)
        node_phase_01(nc, 0, xs[0], agg[0], xs[1], wt, XW)
        edge_phase_01(nc, 1, xs[1], agg[1], dram, wt, agg)
        node_phase_01(nc, 1, xs[1], agg[1], xs[2], wt, XW)
        hidden_phase(nc, dram, wt)
        edge_phase_23(nc, 2, xs[2], None, dram, wt)
        attention_max_phase(nc, dram, mx, wt)
        attention_sum_phase(nc, dram, mx, agg[2], wt)
        node_phase_2(nc, xs[2], agg[2], xs[3], wt)
        edge_phase_23(nc, 3, xs[3], agg[3], dram, wt)
        node_phase_3(nc, xs[3], agg[3], out, wt)


def lay_out(inputs):
    g = {k: np.asarray(v) for k, v in inputs.items()}
    w = np.zeros((P, WCOLS), np.float32)

    def put(name, r, c, a, step=1):
        rows, cols, at = SLOTS[name]
        w[r:r + step * (a.shape[0] - 1) + 1:step, at + c:at + c + step * (a.shape[1] - 1) + 1:step] = a

    def put3(name, r, c, a):
        for k in range(3):
            put(name, r + k, c + k, a, 3)

    def rep3(name, c, a):
        rows, cols, at = SLOTS[name]
        for k in range(3):
            w[0:a.shape[0], at + c + k:at + c + 3 * a.shape[1]:3] = a

    names = [("fcW1", "fcW2", "W1_s", "W1_v", "W2_s", "W2_v", "W3", "W_sc_s", "W_sc_v"),
             ("Wfc1", "Wfc3", "Wl1_0", "Wl1_1", "Wl2_s", "Wl2_v", "Wa", "Wsc0", "Wsc1")]
    for l in (0, 1):
        h, w2, ws, wv, os_, ov, oa, ns, nv = (g[f"L{l}_gnn_{n}"] for n in names[l])
        put(f"h{l}", 0, 0, h)
        put(f"w1_{l}", 0, 0, w2[:, 0:128])
        put(f"w2_{l}", 0, 0, w2[:, 160:192])
        rep3(f"w2_{l}", 32, w2[:, 128:160])
        put(f"f1_{l}", 0, 0, ws)
        put(f"f1_{l}", 64, 64, ws)
        put(f"f2_{l}", 0, 0, wv)
        put3(f"f2_{l}", 32, 32, wv)
        put(f"o1_{l}", 64, 0, ov[0:64])
        put(f"o1_{l}", 0, 32, os_[0:64])
        put(f"o1_{l}", 0, 192, oa[0:64])
        put(f"o2_{l}", 0, 0, os_[64:96])
        put(f"o2_{l}", 0, 160, oa[64:96])
        put3(f"o2_{l}", 32, 64, ov[64:96])
        put(f"ns_{l}", 0, 0, ns)
        put3(f"nv_{l}", 0, 0, nv)
    put("hh1", 0, 0, g["L1_gnn_Wfc2"])
    put("ident", 0, 0, np.eye(P, dtype=np.float32))
    e = np.arange(B).reshape(T, P)
    before = (np.arange(B)[None, None, :] < e.T[:, :, None]).astype(np.float32)
    put("before", 0, 0, before.reshape(P, T * B))
    put("spare", 0, 0, (N + e.T).astype(np.float32))
    put("mhalfn", 0, 0, np.full((P, NBP * T), -0.5, np.float32))
    put("one", 0, 0, np.ones((1, 128), np.float32))
    put("e64", 0, 64, np.ones((1, 1), np.float32))
    for l in (2, 3):
        so = 128 if l == 2 else 96
        k = "L2_gnn_" if l == 2 else "L3_gnn_"
        w2 = g[k + ("rw3" if l == 2 else "W_fc2")]
        put(f"w1_{l}", 0, 0, w2[:, 0:128])
        rep3(f"w2_{l}", 0, w2[:, 128:160])
        put(f"w2_{l}", 0, 96, w2[:, 160:192])
        rep3(f"w3_{l}", 0, w2[:, 192:224])
        ends = ((g[k + "msrc_ws"], g[k + "msrc_wv"]), (g[k + "mdst_ws"], g[k + "mdst_wv"])) if l == 2 else ((g[k + "W_nl0"], g[k + "W_nl1"]),)
        for s, (ws, wv) in enumerate(ends):
            put(f"f1_{l}{s}", 0, 0, ws)
            put(f"f1_{l}{s}", 0, 64, ws)
            put3(f"f2_{l}{s}", 0, 0, wv)
            put(f"f2_{l}{s}", 96, 96, wv)
        os_, ov = (g[k + "lin_ws"], g[k + "lin_wv"]) if l == 2 else (g[k + "W_out_s"], g[k + "W_out_v"])
        put(f"o1_{l}", 0, 32, os_[0:64])
        put(f"o1_{l}", 64, 0, ov[0:64])
        put3(f"o2_{l}", 0, so, ov[64:96])
        put(f"o2_{l}", 96, 0, os_[64:96])
        put3(f"o3_{l}", 0, 0, ov[96:128])
    put("h3", 0, 0, g["L3_gnn_W_fc1"])
    put("ns_3", 0, 0, g["L3_gnn_W_skip0"])
    put3("nv_3", 0, 0, g["L3_gnn_W_skip1"])
    q = {n[7:]: a for n, a in g.items() if n.startswith("L2_gnn_")}
    col = lambda a: np.reshape(a, (-1, 1))
    row = lambda a: np.reshape(a, (1, -1))

    def col3(name, r, a):
        for k in range(3):
            put(name, r + k, 0, col(a), 3)

    put("roff0", 0, 0, col(q["roff"][0:128]))
    col3("roff1", 0, q["roff"][128:160])
    put("roff1", 96, 0, col(q["roff"][160:192]))
    col3("roff2", 0, q["roff"][192:224])
    put("mb2", 0, 0, col(q["mdst_bs"]))
    put("mb2", 64, 0, col(q["mdst_bs"]))
    put("ln1w", 0, 0, col(q["ln1_w0"]))
    put("ln1b", 0, 0, col(q["ln1_b0"]))
    col3("ln1v", 0, q["ln1_w1"])
    put("ln1v", 96, 0, col(q["ln1_w1"]))
    put("adot", 0, 0, np.broadcast_to(row(q["alpha_dot"]), (P, 64)))
    put("linb", 0, 0, row(q["lin_bs"]))
    for k in range(2):
        put(f"rw{k}", 0, 0, q[f"rw{k + 1}"])
        put(f"rb{k}", 0, 0, row(q[f"rb{k + 1}"]))
        put(f"rg{k}", 0, 0, col(q[f"rg{k + 1}"]))
        put(f"rbe{k}", 0, 0, col(q[f"rbe{k + 1}"]))
    put("pw", 0, 0, q["proj_ws"])
    put("pb", 0, 0, row(q["proj_bs"]))
    put3("pv", 0, 0, q["proj_wv"])
    put("ln2w", 0, 0, col(q["ln2_w0"]))
    put("ln2w", 64, 0, np.ones((1, 1), np.float32))
    col3("ln2v", 0, q["ln2_w1"])
    put("b0row", 0, 64, col(q["ln2_b0"]))
    put("f1s", 0, 0, q["f1_ws"][:, 0:128])
    rep3("f1s", 128, q["f1_ws"][:, 128:192])
    put("f1b", 0, 0, row(q["f1_bs"][0:128]))
    rep3("f1b", 128, row(q["f1_bs"][128:192]))
    put3("f1v", 0, 0, q["f1_wv"])
    put("f2s", 0, 0, q["f2_ws"])
    put("f2b", 0, 0, row(q["f2_bs"]))
    put3("f2v0", 0, 0, q["f2_wv"][0:32])
    put3("f2v1", 0, 0, q["f2_wv"][32:64])

    def edges(a, fill):
        p = np.full((NBP * B,) + a.shape[1:], fill, a.dtype)
        p[0:E] = a
        return p

    def tiles(a):
        return np.ascontiguousarray(a.reshape((NBP, T, P) + a.shape[1:]).swapaxes(1, 2))

    x = np.empty((N, XW), np.float32)
    x[:, 0:D] = g["x"]
    x[:, D:] = g["node_vec1"]
    o = {"w": w, "x": x}
    for side in ("src", "dst"):
        o[side + "_g"] = tiles(edges(g[side], 0)).view(np.uint32)
        o[side + "_t"] = tiles(edges(g[side], N))
        o[side + "_r"] = edges(g[side], N).reshape(NBP, B)
    o["ea8T"] = np.ascontiguousarray(edges(g["edge_attr_8"], 1.0).T)
    o["ea64T"] = np.ascontiguousarray(edges(g["edge_attr_64"], 1.0).T)
    e3 = edges(g["edge_attr_3"], 1.0).reshape(NBP * T, P, 3)
    o["ea3"] = np.ascontiguousarray(e3.swapaxes(0, 1)).reshape(P, NBP * T * 3)
    o["ea4"] = tiles(edges(g["edge_attr_4"], 1.0))
    return o


def kernel(**inputs):
    from concourse import bacc
    from concourse.bass_utils import run_bass_kernel_spmd as run

    nc = bacc.Bacc("TRN2", target_bir_lowering=False, num_devices=1)
    arrays = lay_out(inputs)
    ins = {k: nc.dram_tensor(f"in_{k}", a.shape, mybir.dt.from_np(a.dtype), kind="ExternalInput").ap() for k, a in arrays.items()}
    out = nc.dram_tensor("out", (N, D), F32, kind="ExternalOutput").ap()
    build(nc, ins, out)
    r = run(nc, [{f"in_{k}": a for k, a in arrays.items()}], core_ids=[0])
    return r.results[0]["out"]
```

```python
from contextlib import ExitStack

import numpy as np

import concourse.bass as bass
import concourse.mybir as mybir

F32 = mybir.dt.float32
I32 = mybir.dt.int32
U32 = mybir.dt.uint32
ALU = mybir.AluOpType
ACT = mybir.ActivationFunctionType
AX = mybir.AxisListType

P = 128
N, E = 50000, 25000
S0, V1 = 64, 32
V3 = 3 * V1
D = S0 + V3
XW = D + 1
T = 4
R = 4
B = T * P
NB = 50
NBP = NB + 1
NC = N // B
LASTP = (N - NC * B) // T
NA = 396 * P
ZR = 12
AW = {0: 161, 1: 161, 2: 168, 3: 192}
EPS = 1e-5
MAGIC = 12582912.0

SLOTS = {}


def slot(name, rows, cols):
    at = sum(c for _, c, _ in SLOTS.values())
    SLOTS[name] = (rows, cols, at)


for _l in (0, 1):
    slot(f"h{_l}", 8, 64)
    slot(f"w1_{_l}", 64, 128)
    slot(f"w2_{_l}", 64, 128)
    slot(f"f1_{_l}", 128, 128)
    slot(f"f2_{_l}", 128, 128)
    slot(f"o1_{_l}", 128, 193)
    slot(f"o2_{_l}", 128, 161)
    slot(f"ns_{_l}", 64, 64)
    slot(f"nv_{_l}", 96, 96)
slot("hh1", 64, 64)
slot("ident", 128, 128)
slot("before", 128, T * B)
slot("spare", 128, T)
slot("mhalfn", 128, NBP * T)
slot("one", 1, 128)
slot("e64", 1, 65)
for _l in (2, 3):
    _so = 128 if _l == 2 else 96
    slot(f"w1_{_l}", 64, 128)
    slot(f"w2_{_l}", 64, 128)
    slot(f"w3_{_l}", 64, 96)
    for _s in range(2 if _l == 2 else 1):
        slot(f"f1_{_l}{_s}", 64, 128)
        slot(f"f2_{_l}{_s}", 128, 128)
    slot(f"o1_{_l}", 128, 32 + _so + 96)
    slot(f"o2_{_l}", 128, _so + 96)
    slot(f"o3_{_l}", 96, 96)
slot("h3", 64, 64)
slot("ns_3", 64, 96)
slot("nv_3", 96, 96)
slot("roff0", 128, 1)
slot("roff1", 128, 1)
slot("roff2", 96, 1)
slot("mb2", 128, 1)
slot("ln1w", 64, 1)
slot("ln1b", 64, 1)
slot("ln1v", 128, 1)
slot("adot", 128, 64)
slot("linb", 1, 224)
for _k in range(2):
    slot(f"rw{_k}", 64, 64)
    slot(f"rb{_k}", 1, 64)
    slot(f"rg{_k}", 64, 1)
    slot(f"rbe{_k}", 64, 1)
slot("pw", 65, 64)
slot("pv", 96, 96)
slot("ln2w", 65, 1)
slot("ln2v", 96, 1)
slot("b0row", 64, 65)
slot("f1s", 65, 320)
slot("f1b", 1, 320)
slot("f1v", 96, 192)
slot("f2s", 128, 64)
slot("f2b", 1, 64)
slot("f2v0", 96, 96)
slot("f2v1", 96, 96)
WCOLS = sum(c for _, c, _ in SLOTS.values())


def due(count):
    return max(count, 0) if isinstance(count, int) else count


def semaphores(nc, ctx, named):
    made = []

    def over():
        nc.clear_and_free_semaphores(made)
        nc.all_engine_barrier()

    def sem(n):
        made.append(nc.alloc_semaphore(name=named(n)))
        return made[-1]

    ctx.callback(over)
    return sem


def by_twos(eng, n, step):
    for u in range(2):
        step(0, u)
    with eng.Fori(1, n // 2) as j:
        for u in range(2):
            step(j, u)


def edge_phase_01(nc, l, x, agg, dram, wt, later):
    W = AW[l]
    act_fn = ACT.Silu if l == 0 else ACT.Gelu_apprx_tanh
    NL = 5
    with ExitStack() as ctx:
        sb = lambda n, s, d=F32: ctx.enter_context(nc.sbuf_tensor(f"{n}_{l}", s, d))
        ps = lambda n, s: ctx.enter_context(nc.psum_tensor(f"{n}_{l}", s, F32))
        sem = semaphores(nc, ctx, lambda n: f"{n}_{l}")
        gidx = [sb(f"gidx{u}", [P, T], U32) for u in range(2)]
        tidx = [sb(f"tidx{u}", [P, T], I32) for u in range(2)]
        trow = [sb(f"trow{u}", [P, B], I32) for u in range(2)]
        esT = [sb(f"esT{u}", [8, B]) for u in range(2)]
        ea = [sb(f"ea{u}", [P, T, 4]) for u in range(2)]
        xg = [sb(f"xg{u}", [P, T, XW]) for u in range(2)]
        ya = [sb(f"ya{u}", [P, T, 4]) for u in range(2)]
        yb = [sb(f"yb{u}", [P, T, 8]) for u in range(2)]
        prod = sb("prod", [P, T, V3])
        rows = sb("rows", [P, T, 2 * P])
        ts = sb("ts", [P, 2, B])
        hs = sb("hs", [64, B])
        h2 = sb("h2", [64, B])
        ws = sb("ws", [P, 2, B])
        pr = sb("pr", [P, 2, B])
        tf = sb("tf", [P, T])
        same = sb("same", [P, T, B])
        junk = sb("junk", [P, T, B])
        cnt = sb("cnt", [P, T])
        away = sb("away", [P, T])
        cidx = [sb(f"cidx{u}", [P, T], U32) for u in range(2)]
        outer = sb("outer", [P, T, V3])
        ob = sb("ob", [P, T, 32 + W])
        summed = sb("summed", [P, T, W])
        zero = sb("zero", [P, ZR * 192]) if l == 0 else None

        pt = ps("pt", [P, 2, B])
        ph = ps("ph", [P, B])
        pf = ps("pf", [P, B])
        po = ps("po", [P, T, 256])
        pc = ps("pc", [P, T, 256])

        loaded = [sem("loaded0"), sem("loaded1")]
        freed = sem("freed")
        gathered = [sem("gathered0"), sem("gathered1")]
        y_ok = sem("y_ok")
        rows_v = sem("rows_v")
        rows_a = sem("rows_a")
        turned = sem("turned")
        ts_ok = sem("ts_ok")
        h_ps = sem("h_ps")
        h_ok = sem("h_ok")
        w_ps = sem("w_ps")
        w_ok = sem("w_ok")
        f_ps = sem("f_ps")
        prod_ok = sem("prod_ok")
        o_ps = sem("o_ps")
        msg_v = sem("msg_v")
        msg_a = sem("msg_a")
        same_ok = sem("same_ok")
        idx_step = sem("idx_step")
        idx_ok = sem("idx_ok")
        idx_out = sem("idx_out")
        c_ps = sem("c_ps")
        sum_ok = sem("sum_ok")
        added = sem("added")
        left = sem("left")
        cidx_in = [sem("cidx_in0"), sem("cidx_in1")]
        zset = sem("zset")
        zeroed = [sem(f"zeroed{k}") for k in range(4)] if l == 0 else None
        turn = sem("turn")

        def fence(eng):
            eng.sem_inc(turn, 1)

        block = ctx.enter_context(nc.Block())

        @block.sync
        def _(sp):
            def load(i, u):
                sp.wait_ge(freed, due(i - 1))
                sp.dma_start(gidx[u][:], dram["src_g"][bass.ds(i, 1)].rearrange("a p t -> (a p) t")).then_inc(loaded[u], 16)
                sp.dma_start(tidx[u][:], dram["dst_t"][bass.ds(i, 1)].rearrange("a p t -> (a p) t")).then_inc(loaded[u], 16)
                sp.dma_start(trow[u][:], dram["dst_r"][bass.ds(i, 1)].broadcast_to([P, B])).then_inc(loaded[u], 16)
                sp.dma_start(esT[u][:], dram["ea8T"][:, bass.ds(i * B, B)]).then_inc(loaded[u], 16)
                sp.dma_start(ea[u][:], dram["ea4"][bass.ds(i, 1)].rearrange("a p t c -> (a p) t c")).then_inc(loaded[u], 16)
                if l == 1:
                    sp.wait_ge(left, i)
                    sp.dma_start(cidx[u][:], dram["cidx"][bass.ds(i, 1)].rearrange("a p t -> (a p) t")).then_inc(cidx_in[u], 16)

            load(0, 0)
            if l == 0:
                sp.wait_ge(zset, 1)
                for k in range(4):
                    w = ZR * AW[k]
                    flat = later[k].rearrange("(p r) c -> p (r c)", p=P)
                    with sp.Fori(0, NA // P // ZR) as j:
                        sp.dma_start(flat[:, bass.ds(j * w, w)], zero[:, 0:w]).then_inc(zeroed[k], 16)
            def step(j, u):
                load(2 * j + u + 1, 1 - u)
                if l == 0:
                    sp.wait_ge(idx_ok, 2 * j + u + 1)
                    sp.dma_start(dram["cidx"][bass.ds(2 * j + u, 1)].rearrange("a p t -> (a p) t"), cidx[u][:]).then_inc(idx_out, 16)

            by_twos(sp, NB, step)
            if l == 0:
                sp.wait_ge(idx_out, 16 * NB)
                for k in range(1, 4):
                    sp.wait_ge(zeroed[k], 16 * (NA // P // ZR))

        @block.gpsimd
        def _(pool):
            def gather(u, k):
                pool.wait_ge(loaded[u], 16 * NL * (k + 1))
                fence(pool)
                for t in range(T):
                    pool.indirect_dma_start(xg[u][:, t, :], None, x, bass.IndirectOffsetOnAxis(ap=gidx[u][:, t:t + 1], axis=0)).then_inc(gathered[u], 16)

            if l == 0:
                pool.memset(zero[:], 0.0).then_inc(zset, 1)
            gather(0, 0)
            if l == 0:
                pool.wait_ge(zeroed[0], 16 * (NA // P // ZR))
            def step(j, u):
                i = 2 * j + u
                gather(1 - u, j + u)
                if l == 0:
                    pool.wait_ge(idx_ok, i + 1)
                    fence(pool)
                else:
                    pool.wait_ge(cidx_in[u], 16 * (j + 1))
                    fence(pool)
                pool.wait_ge(added, 16 * T * i)
                fence(pool)
                pool.sem_inc(left, 1)
                pool.wait_ge(sum_ok, i + 1)
                fence(pool)
                for t in range(T):
                    pool.indirect_dma_start(agg, bass.IndirectOffsetOnAxis(ap=cidx[u][:, t:t + 1], axis=0), summed[:, t, :], None, compute_op=ALU.add).then_inc(added, 16)

            by_twos(pool, NB, step)
            pool.wait_ge(added, 16 * T * NB)
            if l == 1:
                pool.wait_ge(cidx_in[0], 16 * (NB // 2 + 1))

        @block.vector
        def _(v):
            def front(n, u, k):
                v.wait_ge(gathered[u], 16 * T * (k + 1))
                v.tensor_tensor(ya[u][:], ea[u][:], xg[u][:, :, D:XW].to_broadcast([P, T, 4]), ALU.mult).then_inc(y_ok, 1)
                v.wait_ge(y_ok, 5 * n + 1)
                v.tensor_scalar(yb[u][:, :, 0:1], ya[u][:, :, 0:1], 1.0 / 8.0, None, ALU.mult).then_inc(y_ok, 1)
                v.tensor_scalar(yb[u][:, :, 1:2], ya[u][:, :, 0:1], 32.0 ** -0.5, None, ALU.mult).then_inc(y_ok, 1)
                v.tensor_scalar(yb[u][:, :, 2:5], ya[u][:, :, 1:4], 1.0 / 8.0, None, ALU.mult).then_inc(y_ok, 1)
                v.tensor_scalar(yb[u][:, :, 5:8], ya[u][:, :, 1:4], 96.0 ** -0.5, None, ALU.mult).then_inc(y_ok, 1)
                v.wait_ge(turned, 2 * n)
                v.wait_ge(y_ok, 5 * n + 5)
                v.tensor_tensor(prod[:].rearrange("p t (u c) -> p t u c", c=3), xg[u][:, :, S0:D].rearrange("p t (u c) -> p t u c", c=3),
                                yb[u][:, :, 5:8].unsqueeze(2).to_broadcast([P, T, V1, 3]), ALU.mult).then_inc(rows_v, 1)
                v.tensor_tensor(rows[:, :, 0:64], xg[u][:, :, 0:64], yb[u][:, :, 0:1].to_broadcast([P, T, 64]), ALU.mult).then_inc(rows_v, 1)
                v.tensor_tensor(rows[:, :, 160:256], xg[u][:, :, S0:D], yb[u][:, :, 1:2].to_broadcast([P, T, V3]), ALU.mult).then_inc(rows_v, 1)
                v.wait_ge(rows_v, 4 * n + 1)
                v.tensor_reduce(rows[:, :, 128:160], prod[:].rearrange("p t (u c) -> p t u c", c=3), AX.X, ALU.add).then_inc(rows_v, 1)

            def main(i, u):
                v.tensor_copy(tf[:], tidx[u][:]).then_inc(idx_step, 1)
                v.wait_ge(c_ps, i)
                v.wait_ge(idx_step, (i * 7 if l == 0 else i) + 1)
                for t in range(T):
                    v.tensor_scalar(same[:, t, :], trow[u][:], tf[:, t:t + 1], None, ALU.is_equal).then_inc(same_ok, 1)
                if l == 0:
                    for t in range(T):
                        m = (t + 1) * P
                        v.scalar_tensor_tensor(junk[:, t, 0:m], trow[u][:, 0:m], tf[:, t:t + 1], wt("before")[:, t * B:t * B + m],
                                               ALU.is_equal, ALU.mult, accum_out=cnt[:, t:t + 1]).then_inc(idx_step, 1)
                    v.tensor_tensor(away[:], wt("spare"), tf[:], ALU.subtract).then_inc(idx_step, 1)
                    v.wait_ge(idx_step, i * 7 + 6)
                    v.scalar_tensor_tensor(cnt[:], cnt[:], 1.0, away[:], ALU.min, ALU.mult).then_inc(idx_step, 1)
                    v.wait_ge(idx_step, i * 7 + 7)
                    v.wait_ge(idx_out, 16 * i)
                    v.wait_ge(left, i)
                    v.tensor_tensor(cidx[u][:], cnt[:], tf[:], ALU.add).then_inc(idx_ok, 1)
                v.wait_ge(o_ps, i)
                for g in range(2):
                    v.wait_ge(w_ok, 2 * i + g + 1)
                    v.wait_ge(f_ps, 2 * i + g + 1)
                    v.tensor_tensor(pr[:, g, :], pf[:], ws[:, g, :], ALU.mult).then_inc(prod_ok, 1)

            def messages(i, u):
                v.wait_ge(msg_a, i + 1)
                v.tensor_tensor(outer[:].rearrange("p t (u c) -> p t u c", c=3), ob[:, :, 0:32].unsqueeze(3).to_broadcast([P, T, V1, 3]),
                                yb[u][:, :, 2:5].unsqueeze(2).to_broadcast([P, T, V1, 3]), ALU.mult).then_inc(msg_v, 1)
                v.wait_ge(msg_v, 2 * i + 1)
                v.tensor_tensor(ob[:, :, 96:192], ob[:, :, 96:192], outer[:], ALU.add).then_inc(msg_v, 1)

            front(0, 0, 0)
            def step(j, u):
                i = 2 * j + u
                main(i, u)
                front(i + 1, 1 - u, j + u)
                messages(i, u)

            by_twos(v, NB, step)

        @block.scalar
        def _(a):
            def front(n, u, k):
                a.wait_ge(gathered[u], 16 * T * (k + 1))
                a.wait_ge(turned, 2 * n)
                a.activation(rows[:, :, 64:128], xg[u][:, :, 0:64], ACT.Copy).then_inc(rows_a, 1)
                for g in range(2):
                    a.wait_ge(f_ps, 2 * n)
                    a.wait_ge(turned, 2 * n + g + 1)
                    a.activation(ts[:, g, :], pt[:, g, :], ACT.Copy).then_inc(ts_ok, 1)

            def hidden(i):
                nh = 1 + l
                a.wait_ge(h_ps, nh * i + 1)
                a.activation(hs[:], ph[0:64, :], act_fn, scale=8.0 ** -0.5).then_inc(h_ok, 1)
                if l == 1:
                    a.wait_ge(h_ps, nh * i + 2)
                    a.activation(h2[:], ph[0:64, :], act_fn, scale=1.0 / 8.0).then_inc(h_ok, 1)
                for g in range(2):
                    a.wait_ge(w_ps, 2 * i + g + 1)
                    if g == 0:
                        a.wait_ge(prod_ok, 2 * i)
                    a.activation(ws[:, g, :], ph[:], ACT.Copy, scale=1.0 / 8.0).then_inc(w_ok, 1)

            def finish(i):
                a.wait_ge(o_ps, i + 1)
                a.wait_ge(c_ps, i)
                a.activation(ob[:], po[:, :, 0:32 + W], ACT.Copy).then_inc(msg_a, 1)
                a.wait_ge(added, 16 * T * i)
                a.wait_ge(c_ps, i + 1)
                a.activation(summed[:], pc[:, :, 0:W], ACT.Copy).then_inc(sum_ok, 1)

            front(0, 0, 0)
            def step(j, u):
                i = 2 * j + u
                hidden(i)
                front(i + 1, 1 - u, j + u)
                finish(i)

            by_twos(a, NB, step)

        @block.tensor
        def _(pe):
            def front(n, g):
                pe.wait_ge(rows_v, 4 * n + 4)
                pe.wait_ge(rows_a, n + 1)
                pe.wait_ge(ts_ok, 2 * n)
                for t in range(T):
                    last = pe.transpose(pt[:, g, t * P:(t + 1) * P], rows[:, t, g * P:(g + 1) * P], wt("ident"))
                last.then_inc(turned, 1)

            front(0, 0)
            front(0, 1)
            def step(j, u):
                i = 2 * j + u
                nh = 1 + l
                pe.wait_ge(loaded[u], 16 * NL * (j + 1))
                pe.wait_ge(w_ok, 2 * i)
                pe.matmul(ph[0:64, :], wt(f"h{l}"), esT[u][:], start=True, stop=True).then_inc(h_ps, 1)
                pe.wait_ge(ts_ok, 2 * i + 1)
                pe.wait_ge(prod_ok, 2 * i)
                pe.matmul(pf[:], wt(f"f1_{l}"), ts[:, 0, :], start=True, stop=True).then_inc(f_ps, 1)
                if l == 1:
                    pe.wait_ge(h_ok, nh * i + 1)
                    fence(pe)
                    pe.matmul(ph[0:64, :], wt("hh1"), hs[:], start=True, stop=True).then_inc(h_ps, 1)
                pe.wait_ge(h_ok, nh * (i + 1))
                hid = hs if l == 0 else h2
                pe.matmul(ph[:], wt(f"w1_{l}"), hid[:], start=True, stop=True).then_inc(w_ps, 1)
                pe.wait_ge(ts_ok, 2 * i + 2)
                pe.wait_ge(prod_ok, 2 * i + 1)
                pe.matmul(pf[:], wt(f"f2_{l}"), ts[:, 1, :], start=True, stop=True).then_inc(f_ps, 1)
                pe.wait_ge(w_ok, 2 * i + 1)
                pe.matmul(ph[:], wt(f"w2_{l}"), hid[:], start=True, stop=True).then_inc(w_ps, 1)
                front(i + 1, 0)
                front(i + 1, 1)
                pe.wait_ge(prod_ok, 2 * i + 2)
                pe.wait_ge(msg_a, i)
                for t in range(T):
                    pe.matmul(po[:, t, 0:193], pr[:, 0, t * P:(t + 1) * P], wt(f"o1_{l}"), start=True, stop=False)
                    last = pe.matmul(po[:, t, 32:193], pr[:, 1, t * P:(t + 1) * P], wt(f"o2_{l}"), start=False, stop=True)
                last.then_inc(o_ps, 1)
                pe.wait_ge(msg_v, 2 * i + 2)
                pe.wait_ge(same_ok, T * (i + 1))
                pe.wait_ge(sum_ok, i)
                for t in range(T):
                    for s in range(T):
                        last = pe.matmul(pc[:, t, 0:W], same[:, s, t * P:(t + 1) * P], ob[:, s, 32:32 + W], start=(s == 0), stop=(s == T - 1))
                last.then_inc(c_ps, 1)
                pe.wait_ge(c_ps, i + 1)
                pe.sem_inc(freed, 1)

            by_twos(pe, NB, step)


def rows_of(t, c, parts, w):
    return t[bass.ds(c * B, parts * T), 0:w].rearrange("(p t) c -> p (t c)", t=T)


def node_pipeline(eng, stages):
    head, tail = 2 * R, NC // R * R

    def at(m):
        for lag, f in stages:
            c = m - lag
            if 0 <= c <= NC:
                f(c, c % R, c // R, LASTP if c == NC else P)

    for m in range(head):
        at(m)
    with eng.Fori(head // R, tail // R) as j:
        for q in range(R):
            for lag, f in stages:
                f(R * j + (q - lag), (q - lag) % R, j + (q - lag) // R, P)
    for m in range(tail, NC + 1 + max(lag for lag, f in stages)):
        at(m)


def upto(count, most):
    return min(count, most) if isinstance(count, int) else count


def node_phase_01(nc, l, x, agg, xo, wt, width):
    with ExitStack() as ctx:
        tag = f"n{l}"
        sb = lambda n, s, d=F32: ctx.enter_context(nc.sbuf_tensor(f"{n}_{tag}", s, d))
        ps = lambda n, s: ctx.enter_context(nc.psum_tensor(f"{n}_{tag}", s, F32))
        sem = semaphores(nc, ctx, lambda n: f"{n}_{tag}")
        xr = [sb(f"xr{r}", [P, T, XW]) for r in range(R)]
        ar = [sb(f"ar{r}", [P, T, 161]) for r in range(R)]
        tss = [sb(f"tss{u}", [64, B]) for u in range(2)]
        tsv = [sb(f"tsv{u}", [96, B]) for u in range(2)]
        th = [sb(f"th{u}", [P, 2, T]) for u in range(2)]
        rn = sb("rn", [P, 2, T])
        sc = [sb(f"sc{u}", [P, 2, T]) for u in range(2)]
        at = sb("at", [P, T])
        cf = [sb(f"cf{u}", [P, 3, T]) for u in range(2)]
        ag = [sb(f"ag{u}", [P, T, D]) for u in range(2)]
        sk = sb("sk", [P, T, D])
        y = [sb(f"y{u}", [P, T, D]) for u in range(2)]
        st = sb("st", [P, T, 6])
        mv = sb("mv", [P, T, 2])
        ve = sb("ve", [P, T])
        nm = [sb(f"nm{u}", [P, T]) for u in range(2)]
        rs = [sb(f"rs{u}", [P, T]) for u in range(2)]
        nr = [sb(f"nr{u}", [P, T]) for u in range(2)]
        xn = [sb(f"xn{r}", [P, T, XW]) for r in range(R)]
        pts = [ps(f"pts{u}", [64, B]) for u in range(2)]
        ptv = [ps(f"ptv{u}", [96, B]) for u in range(2)]
        pk = [ps(f"pk{u}", [P, T, 256]) for u in range(2)]
        loaded = [sem(f"loaded{r}") for r in range(R)]
        turned = sem("turned")
        ts_ok = sem("ts_ok")
        k_ps = sem("k_ps")
        an_ok = sem("an_ok")
        th_ok = sem("th_ok")
        sc_ok = sem("sc_ok")
        co_ok = sem("co_ok")
        ag_ok = sem("ag_ok")
        sk_ok = sem("sk_ok")
        y_ok = sem("y_ok")
        st_ok = sem("st_ok")
        ve_ok = sem("ve_ok")
        at_ok = sem("at_ok")
        rs_ok = sem("rs_ok")
        xn_ok = sem("xn_ok")
        stored = [sem(f"stored{r}") for r in range(R)]
        turn = sem("turn")

        def fence(eng):
            eng.sem_inc(turn, 1)

        block = ctx.enter_context(nc.Block())

        @block.sync
        def _(sp):
            def load(c, r, k, parts):
                sp.wait_ge(y_ok, due(c - 3))
                fence(sp)
                sp.wait_ge(at_ok, due(c - 3))
                fence(sp)
                sp.wait_ge(ag_ok, due(2 * (c - 3)))
                fence(sp)
                sp.dma_start(xr[r][0:parts].rearrange("p t c -> p (t c)"), rows_of(x, c, parts, XW)).then_inc(loaded[r], 16)
                sp.dma_start(ar[r][0:parts].rearrange("p t c -> p (t c)"), rows_of(agg, c, parts, 161)).then_inc(loaded[r], 16)

            def store(c, r, k, parts):
                sp.wait_ge(xn_ok, T * (c + 1))
                fence(sp)
                sp.wait_ge(at_ok, c + 1)
                fence(sp)
                sp.dma_start(rows_of(xo, c, parts, width), xn[r][0:parts].rearrange("p t c -> p (t c)") if width == XW else xn[r][0:parts, :, 0:width]).then_inc(stored[r], 16)

            node_pipeline(sp, ((0, load), (5, store)))
            for r in range(R):
                sp.wait_ge(stored[r], 16 * ((NC - r) // R + 1))

        @block.tensor
        def _(pe):
            def turn_rows(c, r, k, parts):
                u = r % 2
                pe.wait_ge(loaded[r], 32 * (k + 1))
                pe.wait_ge(ts_ok, due(2 * (c - 1)))
                for t in range(T):
                    last = pe.transpose(ptv[u][:, t * P:(t + 1) * P], xr[r][:, t, S0:D], wt("ident"))
                last.then_inc(turned, 1)
                for t in range(T):
                    last = pe.transpose(pts[u][:, t * P:(t + 1) * P], xr[r][:, t, 0:S0], wt("ident"))
                last.then_inc(turned, 1)

            def skip(c, r, k, parts):
                u = r % 2
                pe.wait_ge(ts_ok, 2 * c + 2)
                pe.wait_ge(sk_ok, due(2 * (c - 1)))
                for t in range(T):
                    pe.matmul(pk[u][:, t, S0:D], tsv[u][:, t * P:(t + 1) * P], wt(f"nv_{l}"), start=True, stop=True)
                    last = pe.matmul(pk[u][:, t, 0:S0], tss[u][:, t * P:(t + 1) * P], wt(f"ns_{l}"), start=True, stop=True)
                last.then_inc(k_ps, 1)

            node_pipeline(pe, ((0, turn_rows), (1, skip)))

        @block.scalar
        def _(a):
            def copy_turned(c, r, k, parts):
                u = r % 2
                a.wait_ge(k_ps, due(c - 1))
                a.wait_ge(turned, 2 * c + 1)
                a.activation(tsv[u][:], ptv[u][:], ACT.Copy).then_inc(ts_ok, 1)
                a.wait_ge(turned, 2 * c + 2)
                a.activation(tss[u][:], pts[u][:], ACT.Copy).then_inc(ts_ok, 1)

            def sines(c, r, k, parts):
                u = r % 2
                a.wait_ge(th_ok, c + 1)
                a.wait_ge(co_ok, due(4 * (c - 1)))
                a.activation(sc[u][:], th[u][:], ACT.Sin, scale=6.2831845).then_inc(sc_ok, 1)

            def normalise(c, r, k, parts):
                u = r % 2
                a.wait_ge(rs_ok, 2 * c + 2)
                a.wait_ge(stored[r], 16 * k)
                for t in range(T):
                    a.activation(xn[r][:, t, 0:D], y[u][:, t, :], ACT.Identity, bias=nr[u][:, t:t + 1], scale=rs[u][:, t:t + 1]).then_inc(xn_ok, 1)

            node_pipeline(a, ((0, copy_turned), (3, normalise)) + (((0, sines),) if l == 0 else ()))

        @block.vector
        def _(v):
            def angle(n):
                def f(c, r, k, parts):
                    u = r % 2
                    if n == 0:
                        v.wait_ge(loaded[r], 32 * (k + 1))
                        v.wait_ge(sc_ok, due(c - 1))
                        v.scalar_tensor_tensor(th[u][:, 0, :], ar[r][:, :, 160], 0.1 * 10.0 ** -0.5 * 96.0 ** -0.5 / (2 * np.pi), xr[r][:, :, D],
                                               ALU.mult, ALU.mult).then_inc(an_ok, 1)
                        return
                    v.wait_ge(an_ok, 7 * c + n)
                    if n == 1:
                        v.tensor_scalar(rn[:, 0, :], th[u][:, 0, :], MAGIC, None, ALU.add).then_inc(an_ok, 1)
                    elif n == 2:
                        v.tensor_scalar(rn[:, 0, :], rn[:, 0, :], -MAGIC, None, ALU.add).then_inc(an_ok, 1)
                    elif n == 3:
                        v.tensor_tensor(th[u][:, 0, :], th[u][:, 0, :], rn[:, 0, :], ALU.subtract).then_inc(an_ok, 1)
                    elif n == 4:
                        v.tensor_scalar(th[u][:, 1, :], th[u][:, 0, :], 0.25, None, ALU.add).then_inc(an_ok, 1)
                    elif n == 5:
                        v.tensor_scalar(rn[:, 1, :], th[u][:, 1, :], 0.5, None, ALU.is_gt).then_inc(an_ok, 1)
                    elif n == 6:
                        v.tensor_tensor(th[u][:, 1, :], th[u][:, 1, :], rn[:, 1, :], ALU.subtract).then_inc(an_ok, 1)
                    else:
                        v.tensor_scalar(th[u][:], th[u][:], -0.4999999, 0.4999999, ALU.max, ALU.min).then_inc(th_ok, 1)
                return f

            def factor(n):
                def f(c, r, k, parts):
                    u = r % 2
                    if n == 0:
                        v.wait_ge(loaded[r], 32 * (k + 1))
                        v.wait_ge(ag_ok, due(2 * (c - 1)))
                        v.wait_ge(sk_ok, due(2 * (c - 1)))
                        v.wait_ge(co_ok, 4 * c)
                        if l == 0:
                            v.wait_ge(sc_ok, c + 1)
                            v.tensor_tensor(at[:], sc[u][:, 1, :], xr[r][:, :, D], ALU.mult).then_inc(co_ok, 1)
                            v.scalar_tensor_tensor(cf[u][:, 2, :], sc[u][:, 0, :], 960.0 ** -0.5, xr[r][:, :, D], ALU.mult, ALU.mult).then_inc(co_ok, 1)
                        else:
                            v.scalar_tensor_tensor(at[:], ar[r][:, :, 160], 1.0 / 3072.0, xr[r][:, :, D], ALU.mult, ALU.mult).then_inc(co_ok, 1)
                            v.tensor_scalar(cf[u][:, 0, :], xr[r][:, :, D], 1.0 / 8.0, None, ALU.mult).then_inc(co_ok, 1)
                    elif n == 1:
                        v.wait_ge(co_ok, 4 * c + 1)
                        if l == 0:
                            v.tensor_scalar(cf[u][:, 0, :], at[:], 1.0 / 8.0, None, ALU.mult).then_inc(co_ok, 1)
                            v.tensor_scalar(cf[u][:, 1, :], at[:], 32.0 ** -0.5, None, ALU.mult).then_inc(co_ok, 1)
                        else:
                            v.tensor_tensor(cf[u][:, 2, :], at[:], xr[r][:, :, D], ALU.mult).then_inc(co_ok, 1)
                            v.tensor_scalar(cf[u][:, 1, :], xr[r][:, :, D], 32.0 ** -0.5, None, ALU.mult).then_inc(co_ok, 1)
                return f

            def skip_scalars(c, r, k, parts):
                u = r % 2
                v.wait_ge(k_ps, c + 1)
                v.wait_ge(co_ok, 4 * c + 4)
                v.wait_ge(y_ok, c)
                v.tensor_tensor(sk[:, :, 0:S0], pk[u][:, :, 0:S0], cf[u][:, 0, :].unsqueeze(2).to_broadcast([P, T, S0]), ALU.mult).then_inc(sk_ok, 1)

            def skip_vectors(c, r, k, parts):
                u = r % 2
                v.tensor_tensor(sk[:, :, S0:D], pk[u][:, :, S0:D], cf[u][:, 1, :].unsqueeze(2).to_broadcast([P, T, V3]), ALU.mult).then_inc(sk_ok, 1)

            def total(c, r, k, parts):
                u = r % 2
                v.wait_ge(sk_ok, 2 * c + 2)
                v.wait_ge(ag_ok, 2 * c + 2)
                v.wait_ge(xn_ok, due(T * (c - 1)))
                v.tensor_tensor(y[u][:], sk[:], ag[u][:], ALU.add).then_inc(y_ok, 1)

            def moments(c, r, k, parts):
                u = r % 2
                v.wait_ge(y_ok, c + 1)
                v.wait_ge(st_ok, 8 * c)
                for t in range(T):
                    v.bn_stats(st[:, t, :], y[u][:, t, :]).then_inc(st_ok, 1)

            def join(c, r, k, parts):
                v.wait_ge(st_ok, 8 * c + 4)
                v.wait_ge(ve_ok, 2 * c)
                fence(v)
                for t in range(T):
                    v.bn_aggr(mv[:, t, :], st[:, t, :]).then_inc(st_ok, 1)

            def variance(c, r, k, parts):
                u = r % 2
                v.wait_ge(st_ok, 8 * c + 8)
                v.wait_ge(rs_ok, 2 * c)
                v.tensor_scalar(ve[:], mv[:, :, 1], EPS, None, ALU.add).then_inc(ve_ok, 1)
                v.tensor_scalar(nm[u][:], mv[:, :, 0], -1.0, None, ALU.mult).then_inc(ve_ok, 1)

            if l == 0:
                node_pipeline(v, ((0, angle(0)), (2, skip_scalars), (0, angle(1)), (2, skip_vectors), (0, angle(2)), (1, factor(0)),
                                  (0, angle(3)), (2, total), (0, angle(4)), (1, factor(1)), (2, moments), (0, angle(5)), (0, angle(6)),
                                  (2, join), (0, angle(7)), (2, variance)))
            else:
                node_pipeline(v, ((1, factor(0)), (2, skip_scalars), (2, skip_vectors), (1, factor(1)), (2, total), (2, moments),
                                  (2, join), (2, variance)))

        @block.gpsimd
        def _(pool):
            def sums(c, r, k, parts):
                u = r % 2
                pool.wait_ge(co_ok, 4 * (c + 1))
                fence(pool)
                pool.wait_ge(y_ok, due(c - 1))
                fence(pool)
                pool.tensor_tensor(ag[u][:], ar[r][:, :, 0:D], cf[u][:, 2, :].unsqueeze(2).to_broadcast([P, T, D]), ALU.mult).then_inc(ag_ok, 1)
                pool.wait_ge(ag_ok, 2 * c + 1)
                fence(pool)
                pool.tensor_tensor(ag[u][:], ag[u][:], xr[r][:, :, 0:D], ALU.add).then_inc(ag_ok, 1)

            def attribute(c, r, k, parts):
                pool.wait_ge(stored[r], 16 * k)
                fence(pool)
                pool.tensor_copy(xn[r][:, :, D:XW], xr[r][:, :, D:XW]).then_inc(at_ok, 1)

            def deviation(c, r, k, parts):
                u = r % 2
                pool.wait_ge(xn_ok, due(T * (c - 1)))
                fence(pool)
                pool.wait_ge(ve_ok, 2 * c + 2)
                fence(pool)
                pool.tensor_tensor(rs[u][:], ve[:], wt("mhalf"), ALU.pow).then_inc(rs_ok, 1)
                pool.wait_ge(rs_ok, 2 * c + 1)
                fence(pool)
                pool.tensor_tensor(nr[u][:], nm[u][:], rs[u][:], ALU.mult).then_inc(rs_ok, 1)

            node_pipeline(pool, ((1, sums), (2, deviation), (1, attribute)))


def edge_phase_23(nc, l, x, agg, dram, wt):
    SO = 128 if l == 2 else 96
    OW = 32 + SO + V3
    W = AW[l]
    sides = ("src", "dst") if l == 2 else ("dst",)
    NS = len(sides)
    NL = 1 + NS + (2 if l == 3 else 0)
    NY = NBP * T
    with ExitStack() as ctx:
        sb = lambda n, s, d=F32: ctx.enter_context(nc.sbuf_tensor(f"{n}_{l}", s, d))
        ps = lambda n, s: ctx.enter_context(nc.psum_tensor(f"{n}_{l}", s, F32))
        sem = semaphores(nc, ctx, lambda n: f"{n}_{l}")
        gidx = [[sb(f"gidx{s}{u}", [P, T], U32) for u in range(2)] for s in range(NS)]
        esT = [sb(f"esT{u}", [64, B]) for u in range(2)]
        xg = [[sb(f"xg{s}{u}", [P, T, 192]) for u in range(2)] for s in range(NS)]
        y3 = sb("y3", [P, NY, 3])
        yq = sb("yq", [P, NY, 3])
        ye = sb("ye", [P, NY, 5])
        ysq = sb("ysq", [P, NY, 3])
        yn = sb("yn", [P, NY])
        yh = sb("yh", [P, NY])
        prod = sb("prod", [P, T, V3])
        ts = sb("ts", [P, 2 * NS, B])
        hs = sb("hs", [64, B])
        ws = sb("ws", [P, 3, B])
        pr = sb("pr", [P, 3, B])
        ob = sb("ob", [P, T, OW])
        e5 = sb("e5", [P, T, V1, 5])
        m1 = sb("m1", [P, T, V3])
        m2 = sb("m2", [P, T, V3])
        if l == 3:
            tidx = [sb(f"tidx{u}", [P, T], I32) for u in range(2)]
            trow = [sb(f"trow{u}", [P, B], I32) for u in range(2)]
            tf = sb("tf", [P, T])
            same = sb("same", [P, T, B])
            junk = sb("junk", [P, T, B])
            cnt = sb("cnt", [P, T])
            away = sb("away", [P, T])
            cidx = [sb(f"cidx{u}", [P, T], U32) for u in range(2)]
            summed = sb("summed", [P, T, W])
        else:
            sq = sb("sq", [P, T, V3])
            st = sb("st", [P, T, 6])
            mv = sb("mv", [P, T, 2])
            var = sb("var", [P, 2, T])
            rs = sb("rs", [P, 2, T])
            sl = sb("sl", [P, T, 64])
            sm = sb("sm", [P, T, 64])
            val = sb("val", [P, T, W])

        pt = ps("pt", [P, 2, B])
        ph = ps("ph", [P, B])
        pf = ps("pf", [P, B])
        po = ps("po", [P, 2, 512])
        pc = ps("pc", [P, T, 256]) if l == 3 else None

        y_in = sem("y_in")
        y_ok = sem("y_ok")
        n_ok = sem("n_ok")
        loaded = [sem("loaded0"), sem("loaded1")]
        freed = sem("freed")
        gathered = [sem("gathered0"), sem("gathered1")]
        sq_ok = sem("sq_ok")
        st_ok = sem("st_ok")
        rs_ok = sem("rs_ok")
        nrm = sem("nrm")
        rows_v = sem("rows_v")
        turned = sem("turned")
        ts_ok = sem("ts_ok")
        h_ps = sem("h_ps")
        h_ok = sem("h_ok")
        w_ps = sem("w_ps")
        w_ok = sem("w_ok")
        f_ps = sem("f_ps")
        prod_ok = sem("prod_ok")
        o_ps = sem("o_ps")
        ob_ok = sem("ob_ok")
        msg_v = sem("msg_v")
        same_ok = sem("same_ok")
        idx_step = sem("idx_step")
        idx_ok = sem("idx_ok")
        c_ps = sem("c_ps")
        sum_ok = sem("sum_ok")
        added = sem("added")
        left = sem("left")
        sl_ok = sem("sl_ok")
        sm_ok = sem("sm_ok")
        val_ok = sem("val_ok")
        kept = sem("kept")
        turn = sem("turn")
        MV = 6

        def fence(eng):
            eng.sem_inc(turn, 1)

        block = ctx.enter_context(nc.Block())

        @block.sync
        def _(sp):
            sp.dma_start(y3[:].rearrange("p n c -> p (n c)"), dram["ea3"]).then_inc(y_in, 16)

            def load(i, u):
                sp.wait_ge(freed, due(i - 1))
                for s, side in enumerate(sides):
                    sp.dma_start(gidx[s][u][:], dram[side + "_g"][bass.ds(i, 1)].rearrange("a p t -> (a p) t")).then_inc(loaded[u], 16)
                if l == 3:
                    sp.dma_start(esT[u][:], dram["ea64T"][:, bass.ds(i * B, B)]).then_inc(loaded[u], 16)
                    sp.dma_start(tidx[u][:], dram["src_t"][bass.ds(i, 1)].rearrange("a p t -> (a p) t")).then_inc(loaded[u], 16)
                    sp.dma_start(trow[u][:], dram["src_r"][bass.ds(i, 1)].broadcast_to([P, B])).then_inc(loaded[u], 16)
                else:
                    sp.dma_start(esT[u][:], dram["hid"][:, bass.ds(i * B, B)]).then_inc(loaded[u], 16)

            load(0, 0)

            def step(j, u):
                load(2 * j + u + 1, 1 - u)

            by_twos(sp, NB, step)

        @block.gpsimd
        def _(pool):
            def gather(u, k):
                pool.wait_ge(loaded[u], 16 * NL * (k + 1))
                fence(pool)
                for s in range(NS):
                    for t in range(T):
                        pool.indirect_dma_start(xg[s][u][:, t, 0:XW], None, x, bass.IndirectOffsetOnAxis(ap=gidx[s][u][:, t:t + 1], axis=0)).then_inc(gathered[u], 16)

            def powers(n):
                for s in range(NS):
                    pool.wait_ge(st_ok, 10 * NS * n + 10 * (s + 1))
                    fence(pool)
                    pool.wait_ge(nrm, 3 * (NS * n + s))
                    fence(pool)
                    pool.tensor_tensor(rs[:], var[:], wt("mhalf8").rearrange("p (a t) -> p a t", a=2), ALU.pow).then_inc(rs_ok, 1)

            pool.wait_ge(y_ok, 3)
            pool.tensor_tensor(yn[:], yh[:], wt("mhalfn"), ALU.pow).then_inc(n_ok, 1)
            gather(0, 0)
            if l == 2:
                powers(0)

            def step(j, u):
                i = 2 * j + u
                gather(1 - u, j + u)
                if l == 2:
                    powers(i + 1)
                    pool.wait_ge(val_ok, 4 * (i + 1))
                    fence(pool)
                    pool.dma_start(dram["val"][bass.ds(i, 1)].rearrange("a p t c -> (a p) t c"), val[:]).then_inc(kept, 16)
                    pool.dma_start(dram["att"][bass.ds(i * B, B)].rearrange("(t p) h -> p t h", p=P), val[:, :, 160:168]).then_inc(kept, 16)
                else:
                    pool.wait_ge(idx_ok, i + 1)
                    fence(pool)
                    pool.wait_ge(added, 16 * T * i)
                    fence(pool)
                    pool.sem_inc(left, 1)
                    pool.wait_ge(sum_ok, i + 1)
                    fence(pool)
                    for t in range(T):
                        pool.indirect_dma_start(agg, bass.IndirectOffsetOnAxis(ap=cidx[u][:, t:t + 1], axis=0), summed[:, t, :], None, compute_op=ALU.add).then_inc(added, 16)

            by_twos(pool, NB, step)
            if l == 3:
                pool.wait_ge(added, 16 * T * NB)
            else:
                pool.wait_ge(kept, 32 * NB)

        @block.vector
        def _(v):
            v.wait_ge(y_in, 16)
            v.tensor_tensor(ysq[:], y3[:], y3[:], ALU.mult).then_inc(y_ok, 1)
            v.wait_ge(y_ok, 1)
            v.tensor_reduce(yh[:], ysq[:], AX.X, ALU.add).then_inc(y_ok, 1)
            v.wait_ge(y_ok, 2)
            v.tensor_scalar(yh[:], yh[:], 1e-12 if l == 2 else 0.0, None, ALU.add).then_inc(y_ok, 1)
            v.wait_ge(n_ok, 1)
            v.tensor_tensor(y3[:], y3[:], yn[:].unsqueeze(2).to_broadcast([P, NY, 3]), ALU.mult).then_inc(y_ok, 1)
            v.wait_ge(y_ok, 4)
            v.tensor_scalar(yq[:], y3[:], 3.0 ** 0.5, None, ALU.mult).then_inc(y_ok, 1)
            v.tensor_scalar(ye[:, :, 0:3], y3[:], 1.5 ** 0.5, None, ALU.mult).then_inc(y_ok, 1)
            v.tensor_scalar(ye[:, :, 3:5], y3[:, :, 0:2], 1.5 ** 0.5, None, ALU.mult).then_inc(y_ok, 1)
            v.wait_ge(y_ok, 7)

            def at(y, n, lo, hi):
                return y[:, bass.ds(n * T, T), lo:hi].unsqueeze(2).to_broadcast([P, T, V1, hi - lo])

            def front(n, u, k):
                for s in range(NS):
                    if s == 0:
                        v.wait_ge(gathered[u], 16 * T * NS * (k + 1))
                    rows = xg[s][u]
                    if l == 2:
                        q = NS * n + s
                        v.wait_ge(rs_ok, q)
                        for t in range(T):
                            v.bn_stats(st[:, t, :], rows[:, t, 0:S0]).then_inc(st_ok, 1)
                        v.wait_ge(st_ok, 10 * q + 4)
                        fence(v)
                        for t in range(T):
                            v.bn_aggr(mv[:, t, :], st[:, t, :]).then_inc(st_ok, 1)
                        v.wait_ge(sq_ok, 2 * q + 1)
                        v.tensor_reduce(var[:, 1, :], sq[:], AX.X, ALU.add).then_inc(sq_ok, 1)
                        v.wait_ge(st_ok, 10 * q + 8)
                        v.tensor_scalar(var[:, 0, :], mv[:, :, 1], EPS, None, ALU.add).then_inc(st_ok, 1)
                        v.wait_ge(sq_ok, 2 * q + 2)
                        v.tensor_scalar(var[:, 1, :], var[:, 1, :], 1.0 / V3, EPS, ALU.mult, ALU.add).then_inc(st_ok, 1)
                        v.tensor_tensor(rows[:, :, 0:S0], rows[:, :, 0:S0], mv[:, :, 0:1].to_broadcast([P, T, S0]), ALU.subtract).then_inc(nrm, 1)
                        v.wait_ge(rs_ok, q + 1)
                        v.wait_ge(nrm, 3 * q + 1)
                        v.tensor_tensor(rows[:, :, 0:S0], rows[:, :, 0:S0], rs[:, 0, :].unsqueeze(2).to_broadcast([P, T, S0]), ALU.mult).then_inc(nrm, 1)
                        v.tensor_tensor(rows[:, :, S0:D], rows[:, :, S0:D], rs[:, 1, :].unsqueeze(2).to_broadcast([P, T, V3]), ALU.mult).then_inc(nrm, 1)
                        v.wait_ge(nrm, 3 * q + 3)
                    v.wait_ge(rows_v, 2 * (NS * n + s))
                    v.tensor_tensor(prod[:].rearrange("p t (u c) -> p t u c", c=3), rows[:, :, S0:D].rearrange("p t (u c) -> p t u c", c=3),
                                    at(y3, n, 0, 3), ALU.mult).then_inc(rows_v, 1)
                    v.wait_ge(rows_v, 2 * (NS * n + s) + 1)
                    v.tensor_reduce(rows[:, :, D:D + V1], prod[:].rearrange("p t (u c) -> p t u c", c=3), AX.X, ALU.add).then_inc(rows_v, 1)

            def main(i, u):
                if l == 3:
                    v.tensor_copy(tf[:], tidx[u][:]).then_inc(idx_step, 1)
                    v.wait_ge(c_ps, i)
                    v.wait_ge(idx_step, i * 7 + 1)
                    for t in range(T):
                        v.tensor_scalar(same[:, t, :], trow[u][:], tf[:, t:t + 1], None, ALU.is_equal).then_inc(same_ok, 1)
                    for t in range(T):
                        m = (t + 1) * P
                        v.scalar_tensor_tensor(junk[:, t, 0:m], trow[u][:, 0:m], tf[:, t:t + 1], wt("before")[:, t * B:t * B + m],
                                               ALU.is_equal, ALU.mult, accum_out=cnt[:, t:t + 1]).then_inc(idx_step, 1)
                    v.tensor_tensor(away[:], wt("spare"), tf[:], ALU.subtract).then_inc(idx_step, 1)
                    v.wait_ge(idx_step, i * 7 + 6)
                    v.scalar_tensor_tensor(cnt[:], cnt[:], 1.0, away[:], ALU.min, ALU.mult).then_inc(idx_step, 1)
                    v.wait_ge(idx_step, i * 7 + 7)
                    v.wait_ge(left, i)
                    v.tensor_tensor(cidx[u][:], cnt[:], tf[:], ALU.add).then_inc(idx_ok, 1)
                v.wait_ge(o_ps, T * i)
                for g in range(3):
                    v.wait_ge(w_ok, 3 * i + g + 1)
                    v.wait_ge(f_ps, 2 * i + min(g, 1) + 1)
                    r = (P, P, V3)[g]
                    if g == 0 and l == 2:
                        v.scalar_tensor_tensor(pr[0:r, g, :], pf[0:r], wt("mb2"), ws[0:r, g, :], ALU.add, ALU.mult).then_inc(prod_ok, 1)
                    else:
                        v.tensor_tensor(pr[0:r, g, :], pf[0:r], ws[0:r, g, :], ALU.mult).then_inc(prod_ok, 1)

            def messages(i, u):
                c3 = lambda a: a.rearrange("p t (u c) -> p t u c", c=3)
                vec = ob[:, :, 32 + SO:OW]
                v.wait_ge(ob_ok, 3 * T * (i + 1))
                v.tensor_tensor(c3(m1[:]), e5[:, :, :, 1:4], at(ye, i, 2, 5), ALU.mult).then_inc(msg_v, 1)
                v.tensor_tensor(c3(m2[:]), e5[:, :, :, 2:5], at(ye, i, 1, 4), ALU.mult).then_inc(msg_v, 1)
                v.wait_ge(msg_v, MV * i + 2)
                v.tensor_tensor(m1[:], m1[:], m2[:], ALU.subtract).then_inc(msg_v, 1)
                v.wait_ge(msg_v, MV * i + 3)
                v.tensor_tensor(c3(m2[:]), ob[:, :, 0:32].unsqueeze(3).to_broadcast([P, T, V1, 3]), at(yq, i, 0, 3), ALU.mult).then_inc(msg_v, 1)
                v.tensor_tensor(vec, vec, m1[:], ALU.add).then_inc(msg_v, 1)
                v.wait_ge(msg_v, MV * i + 5)
                if l == 2:
                    v.wait_ge(kept, 32 * i)
                    v.tensor_tensor(val[:, :, 64:160], vec, m2[:], ALU.add).then_inc(val_ok, 1)
                    v.tensor_copy(val[:, :, 0:64], ob[:, :, 96:160]).then_inc(val_ok, 1)
                    v.wait_ge(sl_ok, i + 1)
                    v.scalar_tensor_tensor(sm[:], ob[:, :, 32:96], 0.25, sl[:], ALU.mult, ALU.add).then_inc(msg_v, 1)
                    v.wait_ge(msg_v, MV * i + 6)
                    v.tensor_tensor(sm[:], sm[:], wt("adot").unsqueeze(1).to_broadcast([P, T, 64]), ALU.mult).then_inc(val_ok, 1)
                    v.wait_ge(val_ok, 4 * i + 3)
                    v.tensor_reduce(val[:, :, 160:168], sm[:].rearrange("p t (h k) -> p t h k", k=8), AX.X, ALU.add).then_inc(val_ok, 1)
                else:
                    v.tensor_tensor(vec, vec, m2[:], ALU.add).then_inc(msg_v, 1)

            front(0, 0, 0)

            def step(j, u):
                i = 2 * j + u
                main(i, u)
                front(i + 1, 1 - u, j + u)
                messages(i, u)

            by_twos(v, NB, step)

        @block.scalar
        def _(a):
            def front(n, u, k):
                if l == 2:
                    for s in range(NS):
                        q = NS * n + s
                        a.wait_ge(gathered[u], 16 * T * NS * (k + 1))
                        a.wait_ge(sq_ok, 2 * q)
                        a.activation(sq[:], xg[s][u][:, :, S0:D], ACT.Square).then_inc(sq_ok, 1)

            def copies(n):
                for s in range(NS):
                    for g in range(2):
                        q = 2 * (NS * n + s) + g
                        a.wait_ge(f_ps, 2 * n)
                        a.wait_ge(turned, q + 1)
                        r = (S0, P)[g]
                        if l == 3:
                            a.activation(ts[0:r, 2 * s + g, :], pt[0:r, g, :], ACT.Copy).then_inc(ts_ok, 1)
                        elif g == 0:
                            a.activation(ts[0:r, 2 * s + g, :], pt[0:r, g, :], ACT.Identity, scale=wt("ln1w"), bias=wt("ln1b")).then_inc(ts_ok, 1)
                        else:
                            a.activation(ts[0:r, 2 * s + g, :], pt[0:r, g, :], ACT.Copy, scale=wt("ln1v")).then_inc(ts_ok, 1)

            def hidden(i, u, j):
                if l == 3:
                    a.wait_ge(h_ps, i + 1)
                    a.activation(hs[:], ph[0:64, :], ACT.Relu).then_inc(h_ok, 1)
                for g in range(3):
                    r = (P, P, V3)[g]
                    a.wait_ge(w_ps, 3 * i + g + 1)
                    if g == 0:
                        a.wait_ge(prod_ok, 3 * i)
                    if l == 3:
                        a.activation(ws[0:r, g, :], ph[0:r], ACT.Copy).then_inc(w_ok, 1)
                    else:
                        a.activation(ws[0:r, g, :], ph[0:r], ACT.Identity, bias=wt(f"roff{g}")).then_inc(w_ok, 1)

            def finish(i):
                if l == 2:
                    a.wait_ge(val_ok, 4 * i)
                else:
                    a.wait_ge(c_ps, i)
                for t in range(T):
                    a.wait_ge(o_ps, T * i + t + 1)
                    a.activation(ob[:, t, :], po[:, t % 2, 0:OW], ACT.Copy).then_inc(ob_ok, 1)
                    e = po[:, t % 2, OW:OW + V3].rearrange("p (u c) -> p u c", c=3)
                    a.activation(e5[:, t, :, 0:3], e, ACT.Copy).then_inc(ob_ok, 1)
                    a.activation(e5[:, t, :, 3:5], e[:, :, 0:2], ACT.Copy).then_inc(ob_ok, 1)
                if l == 2:
                    a.wait_ge(ob_ok, 3 * T * (i + 1))
                    a.activation(sl[:], ob[:, :, 32:96], ACT.Silu).then_inc(sl_ok, 1)
                else:
                    a.wait_ge(added, 16 * T * i)
                    a.wait_ge(c_ps, i + 1)
                    a.activation(summed[:], pc[:, :, 0:W], ACT.Copy).then_inc(sum_ok, 1)

            front(0, 0, 0)
            copies(0)

            def step(j, u):
                i = 2 * j + u
                hidden(i, u, j)
                front(i + 1, 1 - u, j + u)
                copies(i + 1)
                finish(i)

            by_twos(a, NB, step)

        @block.tensor
        def _(pe):
            def front(n, u):
                for s in range(NS):
                    q = NS * n + s
                    pe.wait_ge(rows_v, 2 * (q + 1))
                    pe.wait_ge(ts_ok, 2 * q)
                    fence(pe)
                    for t in range(T):
                        last = pe.transpose(pt[0:S0, 0, t * P:(t + 1) * P], xg[s][u][:, t, 0:S0], wt("ident"))
                    last.then_inc(turned, 1)
                    for t in range(T):
                        last = pe.transpose(pt[:, 1, t * P:(t + 1) * P], xg[s][u][:, t, S0:192], wt("ident"))
                    last.then_inc(turned, 1)

            front(0, 0)

            def step(j, u):
                i = 2 * j + u
                hid = hs
                pe.wait_ge(loaded[u], 16 * NL * (j + 1))
                if l == 3:
                    pe.wait_ge(w_ok, 3 * i)
                    fence(pe)
                    pe.matmul(ph[0:64, :], wt("h3"), esT[u][:], start=True, stop=True).then_inc(h_ps, 1)
                else:
                    hid = esT[u]
                def transformed(g):
                    pe.wait_ge(ts_ok, 2 * NS * (i + 1))
                    pe.wait_ge(prod_ok, 3 * i + g)
                    r = (S0, P)[g]
                    for s in range(NS):
                        last = pe.matmul(pf[:], wt(f"f{g + 1}_{l}{s}"), ts[0:r, 2 * s + g, :], start=(s == 0), stop=(s == NS - 1))
                    last.then_inc(f_ps, 1)

                def weights(g):
                    pe.wait_ge(w_ok, 3 * i + g)
                    pe.matmul(ph[0:(P, P, V3)[g]], wt(f"w{g + 1}_{l}"), hid[:], start=True, stop=True).then_inc(w_ps, 1)

                transformed(0)
                if l == 3:
                    pe.wait_ge(h_ok, i + 1)
                weights(0)
                weights(1)
                transformed(1)
                weights(2)
                front(i + 1, 1 - u)
                pe.wait_ge(prod_ok, 3 * i + 3)
                for t in range(T):
                    pe.wait_ge(ob_ok, due(3 * (T * i + t - 1)))
                    cut = slice(t * P, (t + 1) * P)
                    pe.matmul(po[:, t % 2, 0:OW], pr[:, 0, cut], wt(f"o1_{l}"), start=True, stop=False)
                    if l == 2:
                        pe.matmul(po[:, t % 2, 32:OW], wt("one"), wt("linb"), start=False, stop=False)
                    pe.matmul(po[:, t % 2, 32:OW], pr[:, 1, cut], wt(f"o2_{l}"), start=False, stop=True)
                    pe.matmul(po[:, t % 2, OW:OW + V3], pr[0:V3, 2, cut], wt(f"o3_{l}"), start=True, stop=True).then_inc(o_ps, 1)
                if l == 3:
                    pe.wait_ge(msg_v, MV * (i + 1))
                    pe.wait_ge(same_ok, T * (i + 1))
                    pe.wait_ge(sum_ok, i)
                    for t in range(T):
                        for s in range(T):
                            last = pe.matmul(pc[:, t, 0:W], same[:, s, t * P:(t + 1) * P], ob[:, s, 32:OW], start=(s == 0), stop=(s == T - 1))
                    last.then_inc(c_ps, 1)
                    pe.wait_ge(c_ps, i + 1)
                else:
                    pe.wait_ge(o_ps, T * (i + 1))
                pe.sem_inc(freed, 1)

            by_twos(pe, NB, step)


def hidden_phase(nc, dram, wt):
    with ExitStack() as ctx:
        sb = lambda n, s, d=F32: ctx.enter_context(nc.sbuf_tensor(f"{n}_h", s, d))
        ps = lambda n, s: ctx.enter_context(nc.psum_tensor(f"{n}_h", s, F32))
        sem = semaphores(nc, ctx, lambda n: f"{n}_h")
        both = lambda f, n, *a: [f(f"{n}{k}", *a) for k in range(2)]
        esT = both(sb, "esT", [64, B])
        lin = both(sb, "lin", [P, T, 64])
        st = both(sb, "st", [P, T, 6])
        mv = both(sb, "mv", [P, T, 2])
        ve = both(sb, "ve", [P, T])
        rs = both(sb, "rs", [P, T])
        hid = both(sb, "hid", [64, B])
        pl = both(ps, "pl", [P, T, 64])
        pt = both(ps, "pt", [64, B])
        loaded = both(sem, "loaded")
        lin_ps = both(sem, "lin_ps")
        lin_ok = both(sem, "lin_ok")
        st_ok = both(sem, "st_ok")
        rs_ok = both(sem, "rs_ok")
        nrm = both(sem, "nrm")
        turned = both(sem, "turned")
        hid_ok = both(sem, "hid_ok")
        kept = sem("kept")
        turn = sem("turn")

        def fence(eng):
            eng.sem_inc(turn, 1)

        def staged(eng, stages):
            for f in stages:
                f(0, 0)

            def step(j, u):
                for f in stages:
                    f(0, 2 * j + u + 1)
                    f(1, 2 * j + u)
            by_twos(eng, NB, step)

        block = ctx.enter_context(nc.Block())

        @block.sync
        def _(sp):
            def load(n, u):
                sp.wait_ge(lin_ps[0], due(n - 1))
                sp.dma_start(esT[u][:], dram["ea64T"][:, bass.ds(n * B, B)]).then_inc(loaded[u], 16)

            load(0, 0)

            def step(j, u):
                load(2 * j + u + 1, 1 - u)
                sp.wait_ge(hid_ok[1], 2 * j + u + 1)
                sp.dma_start(dram["hid"][:, bass.ds((2 * j + u) * B, B)], hid[1][:]).then_inc(kept, 16)

            by_twos(sp, NB, step)
            sp.wait_ge(kept, 16 * NB)

        @block.tensor
        def _(pe):
            def linear(k, n, es, got):
                pe.wait_ge(lin_ok[k], n)
                if k == 0:
                    pe.wait_ge(loaded[es], got)
                else:
                    pe.wait_ge(hid_ok[0], n + 1)
                fence(pe)
                src = esT[es] if k == 0 else hid[0]
                for t in range(T):
                    pe.matmul(pl[k][:, t, :], wt("one"), wt(f"rb{k}"), start=True, stop=False)
                    last = pe.matmul(pl[k][:, t, :], src[:, t * P:(t + 1) * P], wt(f"rw{k}"), start=False, stop=True)
                last.then_inc(lin_ps[k], 1)

            def turn_rows(k, n):
                pe.wait_ge(nrm[k], 2 * (n + 1))
                pe.wait_ge(hid_ok[k], n)
                fence(pe)
                for t in range(T):
                    last = pe.transpose(pt[k][:, t * P:(t + 1) * P], lin[k][:, t, :], wt("ident"))
                last.then_inc(turned[k], 1)

            linear(0, 0, 0, 16)
            turn_rows(0, 0)

            def step(j, u):
                i = 2 * j + u
                linear(0, i + 1, 1 - u, 16 * (j + u + 1))
                linear(1, i, 0, 0)
                turn_rows(0, i + 1)
                turn_rows(1, i)
            by_twos(pe, NB, step)

        @block.scalar
        def _(a):
            def copied(k, n):
                a.wait_ge(lin_ps[k], n + 1)
                a.wait_ge(turned[k], n)
                a.activation(lin[k][:], pl[k][:], ACT.Copy).then_inc(lin_ok[k], 1)

            def silu(k, n):
                a.wait_ge(turned[k], n + 1)
                if k == 0:
                    a.wait_ge(lin_ps[1], n)
                else:
                    a.wait_ge(kept, 16 * n)
                a.activation(hid[k][:], pt[k][:], ACT.Silu, scale=wt(f"rg{k}"), bias=wt(f"rbe{k}")).then_inc(hid_ok[k], 1)

            staged(a, (copied, silu))

        @block.vector
        def _(v):
            def stats(k, n):
                v.wait_ge(lin_ok[k], n + 1)
                v.wait_ge(rs_ok[k], n)
                for t in range(T):
                    v.bn_stats(st[k][:, t, :], lin[k][:, t, :]).then_inc(st_ok[k], 1)
                v.wait_ge(st_ok[k], 9 * n + 4)
                fence(v)
                for t in range(T):
                    v.bn_aggr(mv[k][:, t, :], st[k][:, t, :]).then_inc(st_ok[k], 1)
                v.wait_ge(st_ok[k], 9 * n + 8)
                v.tensor_scalar(ve[k][:], mv[k][:, :, 1], EPS, None, ALU.add).then_inc(st_ok[k], 1)
                v.tensor_tensor(lin[k][:], lin[k][:], mv[k][:, :, 0:1].to_broadcast([P, T, 64]), ALU.subtract).then_inc(nrm[k], 1)

            def scaled(k, n):
                v.wait_ge(rs_ok[k], n + 1)
                v.wait_ge(nrm[k], 2 * n + 1)
                v.tensor_tensor(lin[k][:], lin[k][:], rs[k][:].unsqueeze(2).to_broadcast([P, T, 64]), ALU.mult).then_inc(nrm[k], 1)

            staged(v, (stats, scaled))

        @block.gpsimd
        def _(pool):
            def powers(k, n):
                pool.wait_ge(nrm[k], 2 * n)
                fence(pool)
                pool.wait_ge(st_ok[k], 9 * (n + 1))
                fence(pool)
                pool.tensor_tensor(rs[k][:], ve[k][:], wt("mhalf"), ALU.pow).then_inc(rs_ok[k], 1)

            staged(pool, (powers,))


def attention_max_phase(nc, dram, mx, wt):
    H = 8
    with ExitStack() as ctx:
        sb = lambda n, s, d=F32: ctx.enter_context(nc.sbuf_tensor(f"{n}_m", s, d))
        ps = lambda n, s: ctx.enter_context(nc.psum_tensor(f"{n}_m", s, F32))
        sem = semaphores(nc, ctx, lambda n: f"{n}_m")
        tidx = [sb(f"tidx{u}", [P, T], I32) for u in range(2)]
        cidx = [sb(f"cidx{u}", [P, T], U32) for u in range(2)]
        trow = [sb(f"trow{u}", [P, B], I32) for u in range(2)]
        arow = [sb(f"arow{u}", [P, B * H]) for u in range(2)]
        least = sb("least", [P, NA // P * H])
        tf = sb("tf", [P, T])
        same = sb("same", [P, T, B])
        apart = sb("apart", [P, T, P])
        masked = sb("masked", [P, 2, H, P])
        junk = sb("junk", [P, T, P])
        cnt = sb("cnt", [P, T])
        first = sb("first", [P, T])
        top = sb("top", [P, T, H])
        rep = sb("rep", [P, T, H + 1])
        bl = sb("bl", [P, T * T, H + 1])
        gone = sb("gone", [P, T * T])
        blk = sb("blk", [P, T, H])
        old = sb("old", [P, T, H])
        new = sb("new", [P, T, H])
        pm = ps("pm", [P, T * T, H + 1])
        l_set = sem("l_set")
        l_out = sem("l_out")
        loaded = [sem("loaded0"), sem("loaded1")]
        freed = sem("freed")
        tf_ok = sem("tf_ok")
        same_ok = sem("same_ok")
        ap_ok = sem("ap_ok")
        mk_ok = sem("mk_ok")
        top_ok = sem("top_ok")
        rep_ok = sem("rep_ok")
        m_ps = sem("m_ps")
        blk_ok = sem("blk_ok")
        old_in = sem("old_in")
        new_ok = sem("new_ok")
        sent = sem("sent")
        turn = sem("turn")

        def fence(eng):
            eng.sem_inc(turn, 1)

        block = ctx.enter_context(nc.Block())

        @block.sync
        def _(sp):
            sp.wait_ge(l_set, 1)
            sp.dma_start(mx.rearrange("(p r) c -> p (r c)", p=P), least[:]).then_inc(l_out, 16)

            def step(j, u):
                i = 2 * j + u
                sp.wait_ge(freed, due(i - 1))
                sp.dma_start(tidx[u][:], dram["dst_t"][bass.ds(i, 1)].rearrange("a p t -> (a p) t")).then_inc(loaded[u], 16)
                sp.dma_start(cidx[u][:], dram["cidx"][bass.ds(i, 1)].rearrange("a p t -> (a p) t")).then_inc(loaded[u], 16)
                sp.dma_start(trow[u][:], dram["dst_r"][bass.ds(i, 1)].broadcast_to([P, B])).then_inc(loaded[u], 16)
                sp.dma_start(arow[u][:], dram["att"][bass.ds(i * B, B)].rearrange("(a e) h -> a (e h)", a=1).broadcast_to([P, B * H])).then_inc(loaded[u], 16)

            by_twos(sp, NB, step)

        @block.gpsimd
        def _(pool):
            pool.memset(least[:], -1e30).then_inc(l_set, 1)
            pool.wait_ge(l_out, 16)

            def step(j, u):
                i = 2 * j + u
                pool.wait_ge(loaded[u], 64 * (j + 1))
                fence(pool)
                pool.wait_ge(sent, 16 * T * i)
                fence(pool)
                pool.wait_ge(new_ok, i)
                fence(pool)
                for t in range(T):
                    pool.indirect_dma_start(old[:, t, :], None, mx, bass.IndirectOffsetOnAxis(ap=tidx[u][:, t:t + 1].bitcast(U32), axis=0)).then_inc(old_in, 16)
                pool.wait_ge(new_ok, i + 1)
                fence(pool)
                for t in range(T):
                    pool.indirect_dma_start(mx, bass.IndirectOffsetOnAxis(ap=cidx[u][:, t:t + 1], axis=0), new[:, t, :], None).then_inc(sent, 16)
                pool.wait_ge(sent, 16 * T * (i + 1))
                fence(pool)
                pool.sem_inc(freed, 1)

            by_twos(pool, NB, step)

        @block.vector
        def _(v):
            def step(j, u):
                i = 2 * j + u
                v.wait_ge(loaded[u], 64 * (j + 1))
                v.tensor_copy(tf[:], tidx[u][:]).then_inc(tf_ok, 1)
                v.wait_ge(tf_ok, i + 1)
                v.wait_ge(m_ps, i)
                for t in range(T):
                    v.tensor_scalar(same[:, t, :], trow[u][:], tf[:, t:t + 1], None, ALU.is_equal).then_inc(same_ok, 1)
                for t in range(T):
                    v.tensor_scalar(apart[:, t, :], trow[u][:, t * P:(t + 1) * P], tf[:, t:t + 1], -1e30, ALU.not_equal, ALU.mult).then_inc(ap_ok, 1)
                    v.scalar_tensor_tensor(junk[:, t, :], trow[u][:, t * P:(t + 1) * P], tf[:, t:t + 1], wt("before")[:, 0:P],
                                           ALU.is_equal, ALU.mult, accum_out=cnt[:, t:t + 1]).then_inc(ap_ok, 1)
                v.wait_ge(ap_ok, 9 * i + 8)
                v.tensor_scalar(first[:], cnt[:], 0.0, None, ALU.is_equal).then_inc(ap_ok, 1)
                for t in range(T):
                    v.wait_ge(top_ok, due(T * i + t - 1))
                    v.tensor_tensor(masked[:, t % 2], arow[u][:, t * P * H:(t + 1) * P * H].rearrange("p (e h) -> p h e", h=H),
                                    apart[:, t, :].unsqueeze(1).to_broadcast([P, H, P]), ALU.add).then_inc(mk_ok, 1)
                    v.wait_ge(mk_ok, T * i + t + 1)
                    v.tensor_reduce(top[:, t, :], masked[:, t % 2], AX.X, ALU.max).then_inc(top_ok, 1)
                v.wait_ge(ap_ok, 9 * i + 9)
                v.wait_ge(top_ok, T * (i + 1))
                v.tensor_tensor(rep[:, :, 0:H], top[:], first[:].unsqueeze(2).to_broadcast([P, T, H]), ALU.mult).then_inc(rep_ok, 1)
                v.tensor_copy(rep[:, :, H], first[:]).then_inc(rep_ok, 1)
                v.wait_ge(m_ps, i + 1)
                v.tensor_copy(bl[:], pm[:]).then_inc(blk_ok, 1)
                v.wait_ge(blk_ok, 4 * i + 1)
                v.tensor_scalar(gone[:], bl[:, :, H], -1.0, 1e30, ALU.add, ALU.mult).then_inc(blk_ok, 1)
                v.wait_ge(blk_ok, 4 * i + 2)
                v.tensor_tensor(bl[:, :, 0:H], bl[:, :, 0:H], gone[:].unsqueeze(2).to_broadcast([P, T * T, H]), ALU.add).then_inc(blk_ok, 1)
                v.wait_ge(blk_ok, 4 * i + 3)
                v.tensor_reduce(blk[:], bl[:, :, 0:H].rearrange("p (t s) h -> p t h s", s=T), AX.X, ALU.max).then_inc(blk_ok, 1)
                v.wait_ge(blk_ok, 4 * i + 4)
                v.wait_ge(old_in, 16 * T * (i + 1))
                v.tensor_tensor(new[:], blk[:], old[:], ALU.max).then_inc(new_ok, 1)

            by_twos(v, NB, step)

        @block.tensor
        def _(pe):
            def step(j, u):
                i = 2 * j + u
                pe.wait_ge(rep_ok, 2 * (i + 1))
                pe.wait_ge(same_ok, T * (i + 1))
                pe.wait_ge(blk_ok, 4 * i)
                for t in range(T):
                    for s in range(T):
                        last = pe.matmul(pm[:, T * t + s, :], same[:, s, t * P:(t + 1) * P], rep[:, s, :], start=True, stop=True)
                last.then_inc(m_ps, 1)

            by_twos(pe, NB, step)


def attention_sum_phase(nc, dram, mx, agg, wt):
    H = 8
    W = AW[2]
    with ExitStack() as ctx:
        sb = lambda n, s, d=F32: ctx.enter_context(nc.sbuf_tensor(f"{n}_a", s, d))
        ps = lambda n, s: ctx.enter_context(nc.psum_tensor(f"{n}_a", s, F32))
        sem = semaphores(nc, ctx, lambda n: f"{n}_a")
        tidx = [sb(f"tidx{u}", [P, T], I32) for u in range(2)]
        cidx = [sb(f"cidx{u}", [P, T], U32) for u in range(2)]
        trow = [sb(f"trow{u}", [P, B], I32) for u in range(2)]
        val = [sb(f"val{u}", [P, T, W]) for u in range(2)]
        big = [sb(f"big{u}", [P, T, H]) for u in range(2)]
        tf = [sb(f"tf{u}", [P, T]) for u in range(2)]
        same = [sb(f"same{u}", [P, T, B]) for u in range(2)]
        dif = sb("dif", [P, T, H])
        msg = [sb(f"msg{u}", [P, T, W]) for u in range(2)]
        summed = sb("summed", [P, T, W])
        pc = ps("pc", [P, T, 256])
        loaded = [sem("loaded0"), sem("loaded1")]
        big_in = [sem("big_in0"), sem("big_in1")]
        tf_ok = sem("tf_ok")
        same_ok = sem("same_ok")
        dif_ok = sem("dif_ok")
        ex_ok = sem("ex_ok")
        msg_ok = sem("msg_ok")
        c_ps = sem("c_ps")
        sum_ok = sem("sum_ok")
        added = sem("added")
        turn = sem("turn")

        def fence(eng):
            eng.sem_inc(turn, 1)

        block = ctx.enter_context(nc.Block())

        @block.sync
        def _(sp):
            def step(j, u):
                i = 2 * j + u
                sp.wait_ge(added, due(16 * T * (i - 1)))
                sp.dma_start(tidx[u][:], dram["dst_t"][bass.ds(i, 1)].rearrange("a p t -> (a p) t")).then_inc(loaded[u], 16)
                sp.dma_start(cidx[u][:], dram["cidx"][bass.ds(i, 1)].rearrange("a p t -> (a p) t")).then_inc(loaded[u], 16)
                sp.dma_start(trow[u][:], dram["dst_r"][bass.ds(i, 1)].broadcast_to([P, B])).then_inc(loaded[u], 16)
                sp.dma_start(val[u][:], dram["val"][bass.ds(i, 1)].rearrange("a p t c -> (a p) t c")).then_inc(loaded[u], 16)

            by_twos(sp, NB, step)

        @block.gpsimd
        def _(pool):
            def gather(i, u, k):
                pool.wait_ge(loaded[u], 64 * (k + 1))
                fence(pool)
                for t in range(T):
                    pool.indirect_dma_start(big[u][:, t, :], None, mx, bass.IndirectOffsetOnAxis(ap=tidx[u][:, t:t + 1].bitcast(U32), axis=0)).then_inc(big_in[u], 16)

            def send(i, u):
                pool.wait_ge(added, 16 * T * i)
                fence(pool)
                pool.wait_ge(sum_ok, i + 1)
                fence(pool)
                for t in range(T):
                    pool.indirect_dma_start(agg, bass.IndirectOffsetOnAxis(ap=cidx[u][:, t:t + 1], axis=0), summed[:, t, :], None, compute_op=ALU.add).then_inc(added, 16)

            gather(0, 0, 0)
            gather(1, 1, 0)
            send(0, 0)
            with pool.Fori(1, NB // 2) as j:
                gather(2 * j, 0, j)
                send(2 * j - 1, 1)
                gather(2 * j + 1, 1, j)
                send(2 * j, 0)
            send(NB - 1, 1)
            pool.wait_ge(added, 16 * T * NB)

        @block.vector
        def _(v):
            def step(j, u):
                i = 2 * j + u
                v.wait_ge(loaded[u], 64 * (j + 1))
                v.tensor_copy(tf[u][:], tidx[u][:]).then_inc(tf_ok, 1)
                v.wait_ge(big_in[u], 16 * T * (j + 1))
                v.tensor_tensor(dif[:], val[u][:, :, 160:168], big[u][:], ALU.subtract).then_inc(dif_ok, 1)
                v.wait_ge(tf_ok, i + 1)
                v.wait_ge(c_ps, due(i - 1))
                for t in range(T):
                    v.tensor_scalar(same[u][:, t, :], trow[u][:], tf[u][:, t:t + 1], None, ALU.is_equal).then_inc(same_ok, 1)
                v.wait_ge(ex_ok, i + 1)
                v.tensor_tensor(msg[u][:, :, 0:64].rearrange("p t (h k) -> p t h k", h=H), val[u][:, :, 0:64].rearrange("p t (h k) -> p t h k", h=H),
                                msg[u][:, :, 160:168].unsqueeze(3).to_broadcast([P, T, H, 8]), ALU.mult).then_inc(msg_ok, 1)
                v.tensor_tensor(msg[u][:, :, 64:160].rearrange("p t (h k) -> p t h k", h=H), val[u][:, :, 64:160].rearrange("p t (h k) -> p t h k", h=H),
                                msg[u][:, :, 160:168].unsqueeze(3).to_broadcast([P, T, H, 12]), ALU.mult).then_inc(msg_ok, 1)

            by_twos(v, NB, step)

        @block.scalar
        def _(a):
            def step(j, u):
                i = 2 * j + u
                a.wait_ge(dif_ok, i + 1)
                a.wait_ge(c_ps, due(i - 1))
                a.activation(msg[u][:, :, 160:168], dif[:], ACT.Exp, scale=0.8).then_inc(ex_ok, 1)
                a.wait_ge(c_ps, i + 1)
                a.wait_ge(added, 16 * T * i)
                a.activation(summed[:], pc[:, :, 0:W], ACT.Copy).then_inc(sum_ok, 1)

            by_twos(a, NB, step)

        @block.tensor
        def _(pe):
            def step(j, u):
                i = 2 * j + u
                pe.wait_ge(msg_ok, 2 * (i + 1))
                pe.wait_ge(same_ok, T * (i + 1))
                pe.wait_ge(sum_ok, i)
                for t in range(T):
                    for s in range(T):
                        last = pe.matmul(pc[:, t, 0:W], same[u][:, s, t * P:(t + 1) * P], msg[u][:, s, :], start=(s == 0), stop=(s == T - 1))
                last.then_inc(c_ps, 1)

            by_twos(pe, NB, step)


def node_phase_3(nc, x, agg, out, wt):
    with ExitStack() as ctx:
        sb = lambda n, s, d=F32: ctx.enter_context(nc.sbuf_tensor(f"{n}_n3", s, d))
        ps = lambda n, s: ctx.enter_context(nc.psum_tensor(f"{n}_n3", s, F32))
        sem = semaphores(nc, ctx, lambda n: f"{n}_n3")
        xr = [sb(f"xr{r}", [P, T, XW]) for r in range(R)]
        ar = [sb(f"ar{r}", [P, T, 192]) for r in range(R)]
        tss = [sb(f"tss{u}", [64, B]) for u in range(2)]
        tsv = [sb(f"tsv{u}", [96, B]) for u in range(2)]
        so = [sb(f"so{u}", [P, T, 192]) for u in range(2)]
        gt = [sb(f"gt{u}", [P, T, V1]) for u in range(2)]
        sg = [sb(f"sg{u}", [P, T, D]) for u in range(2)]
        y = [sb(f"y{u}", [P, T, D]) for u in range(2)]
        st = sb("st", [P, T, 6])
        mv = sb("mv", [P, T, 2])
        ve = sb("ve", [P, T])
        nm = sb("nm", [P, T])
        rs = [sb(f"rs{u}", [P, T]) for u in range(2)]
        nr = [sb(f"nr{u}", [P, T]) for u in range(2)]
        xn = [sb(f"xn{r}", [P, T, D]) for r in range(R)]
        pts = [ps(f"pts{u}", [64, B]) for u in range(2)]
        ptv = [ps(f"ptv{u}", [96, B]) for u in range(2)]
        pk = [ps(f"pk{u}", [P, T, 256]) for u in range(2)]
        loaded = [sem(f"loaded{r}") for r in range(R)]
        turned = sem("turned")
        ts_ok = sem("ts_ok")
        k_ps = sem("k_ps")
        so_ok = sem("so_ok")
        act_ok = sem("act_ok")
        sg_ok = sem("sg_ok")
        y_ok = sem("y_ok")
        st_ok = sem("st_ok")
        rs_ok = sem("rs_ok")
        xn_ok = sem("xn_ok")
        stored = [sem(f"stored{r}") for r in range(R)]
        turn = sem("turn")

        def fence(eng):
            eng.sem_inc(turn, 1)

        block = ctx.enter_context(nc.Block())

        @block.sync
        def _(sp):
            def load(c, r, k, parts):
                sp.wait_ge(y_ok, due(c - 3))
                fence(sp)
                sp.dma_start(xr[r][0:parts].rearrange("p t c -> p (t c)"), rows_of(x, c, parts, XW)).then_inc(loaded[r], 16)
                sp.dma_start(ar[r][0:parts].rearrange("p t c -> p (t c)"), rows_of(agg, c, parts, 192)).then_inc(loaded[r], 16)

            def store(c, r, k, parts):
                sp.wait_ge(xn_ok, T * (c + 1))
                fence(sp)
                sp.dma_start(rows_of(out, c, parts, D), xn[r][0:parts].rearrange("p t c -> p (t c)")).then_inc(stored[r], 16)

            node_pipeline(sp, ((0, load), (5, store)))
            for r in range(R):
                sp.wait_ge(stored[r], 16 * ((NC - r) // R + 1))

        @block.tensor
        def _(pe):
            def turn_rows(c, r, k, parts):
                u = r % 2
                pe.wait_ge(loaded[r], 32 * (k + 1))
                pe.wait_ge(ts_ok, due(2 * (c - 1)))
                for t in range(T):
                    last = pe.transpose(ptv[u][:, t * P:(t + 1) * P], xr[r][:, t, S0:D], wt("ident"))
                last.then_inc(turned, 1)
                for t in range(T):
                    last = pe.transpose(pts[u][:, t * P:(t + 1) * P], xr[r][:, t, 0:S0], wt("ident"))
                last.then_inc(turned, 1)

            def skip(c, r, k, parts):
                u = r % 2
                pe.wait_ge(ts_ok, 2 * c + 2)
                pe.wait_ge(so_ok, due(c - 1))
                for t in range(T):
                    pe.matmul(pk[u][:, t, 96:192], tsv[u][:, t * P:(t + 1) * P], wt("nv_3"), start=True, stop=True)
                    last = pe.matmul(pk[u][:, t, 0:96], tss[u][:, t * P:(t + 1) * P], wt("ns_3"), start=True, stop=True)
                last.then_inc(k_ps, 1)

            node_pipeline(pe, ((0, turn_rows), (1, skip)))

        @block.scalar
        def _(a):
            def copy_turned(c, r, k, parts):
                u = r % 2
                a.wait_ge(k_ps, due(c - 1))
                a.wait_ge(turned, 2 * c + 1)
                a.activation(tsv[u][:], ptv[u][:], ACT.Copy).then_inc(ts_ok, 1)
                a.wait_ge(turned, 2 * c + 2)
                a.activation(tss[u][:], pts[u][:], ACT.Copy).then_inc(ts_ok, 1)

            def gates(c, r, k, parts):
                u = r % 2
                a.wait_ge(so_ok, c + 1)
                a.wait_ge(y_ok, due(c - 1))
                a.activation(sg[u][:, :, 0:S0], so[u][:, :, 0:S0], ACT.Silu).then_inc(act_ok, 1)
                a.activation(gt[u][:], so[u][:, :, S0:96], ACT.Tanh, scale=0.5).then_inc(act_ok, 1)

            def normalise(c, r, k, parts):
                u = r % 2
                a.wait_ge(rs_ok, 2 * c + 2)
                a.wait_ge(stored[r], 16 * k)
                for t in range(T):
                    a.activation(xn[r][:, t, :], y[u][:, t, :], ACT.Identity, bias=nr[u][:, t:t + 1], scale=rs[u][:, t:t + 1]).then_inc(xn_ok, 1)

            node_pipeline(a, ((0, copy_turned), (3, normalise), (1, gates)))

        @block.vector
        def _(v):
            def layer(c, r, k, parts):
                u = r % 2
                v.wait_ge(k_ps, c + 1)
                v.wait_ge(sg_ok, due(2 * (c - 1)))
                v.wait_ge(act_ok, due(2 * (c - 1)))
                v.scalar_tensor_tensor(so[u][:], ar[r][:], 1.0 / 32.0, pk[u][:, :, 0:192], ALU.mult, ALU.add).then_inc(so_ok, 1)

            def half_gates(c, r, k, parts):
                u = r % 2
                v.wait_ge(act_ok, 2 * c + 2)
                v.tensor_scalar(gt[u][:], gt[u][:], 0.5, 0.5, ALU.mult, ALU.add).then_inc(sg_ok, 1)

            def gate(c, r, k, parts):
                u = r % 2
                v.wait_ge(sg_ok, 2 * c + 1)
                v.tensor_tensor(sg[u][:, :, S0:D].rearrange("p t (u c) -> p t u c", c=3), so[u][:, :, 96:192].rearrange("p t (u c) -> p t u c", c=3),
                                gt[u][:].unsqueeze(3).to_broadcast([P, T, V1, 3]), ALU.mult).then_inc(sg_ok, 1)

            def total(c, r, k, parts):
                u = r % 2
                v.wait_ge(sg_ok, 2 * c + 2)
                v.wait_ge(xn_ok, due(T * (c - 1)))
                v.tensor_tensor(y[u][:], sg[u][:], xr[r][:, :, 0:D], ALU.add).then_inc(y_ok, 1)
                v.wait_ge(y_ok, c + 1)
                v.wait_ge(st_ok, 10 * c)
                for t in range(T):
                    v.bn_stats(st[:, t, :], y[u][:, t, :]).then_inc(st_ok, 1)

            def variance(c, r, k, parts):
                v.wait_ge(st_ok, 10 * c + 4)
                fence(v)
                for t in range(T):
                    v.bn_aggr(mv[:, t, :], st[:, t, :]).then_inc(st_ok, 1)
                v.wait_ge(st_ok, 10 * c + 8)
                v.wait_ge(rs_ok, 2 * c)
                v.tensor_scalar(ve[:], mv[:, :, 1], EPS, None, ALU.add).then_inc(st_ok, 1)
                v.tensor_scalar(nm[:], mv[:, :, 0], -1.0, None, ALU.mult).then_inc(st_ok, 1)

            node_pipeline(v, ((2, half_gates), (1, layer), (2, gate), (2, total), (2, variance)))

        @block.gpsimd
        def _(pool):
            def deviation(c, r, k, parts):
                u = r % 2
                pool.wait_ge(xn_ok, due(T * (c - 1)))
                fence(pool)
                pool.wait_ge(st_ok, 10 * (c + 1))
                fence(pool)
                pool.tensor_tensor(rs[u][:], ve[:], wt("mhalf"), ALU.pow).then_inc(rs_ok, 1)
                pool.wait_ge(rs_ok, 2 * c + 1)
                fence(pool)
                pool.tensor_tensor(nr[u][:], nm[:], rs[u][:], ALU.mult).then_inc(rs_ok, 1)

            node_pipeline(pool, ((2, deviation),))


def node_phase_2(nc, x, agg, xo, wt):
    H = 8
    with ExitStack() as ctx:
        sb = lambda n, s, d=F32: ctx.enter_context(nc.sbuf_tensor(f"{n}_n2", s, d))
        ps = lambda n, s: ctx.enter_context(nc.psum_tensor(f"{n}_n2", s, F32))
        sem = semaphores(nc, ctx, lambda n: f"{n}_n2")
        xr = [sb(f"xr{r}", [P, T, XW]) for r in range(R)]
        ar = [sb(f"ar{r}", [P, T, AW[2]]) for r in range(R)]
        den = [sb(f"den{u}", [P, T, H]) for u in range(2)]
        an = [sb(f"an{u}", [P, T, D]) for u in range(2)]
        tss = [sb(f"tss{u}", [65, B]) for u in range(2)]
        tsv = [sb(f"tsv{u}", [96, B]) for u in range(2)]
        x1 = [sb(f"x1{u}", [P, T, D]) for u in range(2)]
        xx = [sb(f"xx{r}", [P, T, D]) for r in range(R)]
        st = sb("st", [P, T, 6])
        mv = sb("mv", [P, T, 2])
        sq = sb("sq", [P, T, V3])
        var = sb("var", [P, 2, T])
        rs1 = sb("rsa", [P, 2, T])
        hat = sb("hat", [P, T, XW])
        t2s = sb("t2s", [65, B])
        t2v = sb("t2v", [96, B])
        hc = sb("hc", [P, B])
        tg = sb("tg", [96, 2, B])
        gv = sb("gv", [96, 2, B])
        up = sb("up", [P, T, D])
        y = [sb(f"y{u}", [P, T, D]) for u in range(2)]
        st2 = sb("st2", [P, T, 6])
        mv2 = sb("mv2", [P, T, 2])
        ve = sb("ve", [P, T])
        nm = sb("nm", [P, T])
        rs = [sb(f"rs{u}", [P, T]) for u in range(2)]
        nr = [sb(f"nr{u}", [P, T]) for u in range(2)]
        xn = [sb(f"xn{r}", [P, T, XW]) for r in range(R)]
        pts = ps("pts", [65, B])
        ptv = ps("ptv", [96, B])
        pk = ps("pk", [P, T, 256])
        pf = [ps(f"pf{k}", [P, B]) for k in range(4)]
        b_ps = sem("b_ps")
        b_ok = sem("b_ok")
        ones = sem("ones")
        loaded = [sem(f"loaded{r}") for r in range(R)]
        den_ok = sem("den_ok")
        an_ok = sem("an_ok")
        turned = sem("turned")
        ts_ok = sem("ts_ok")
        p_ps = sem("p_ps")
        x1_ok = sem("x1_ok")
        xx_ok = sem("xx_ok")
        sq_ok = sem("sq_ok")
        st_ok = sem("st_ok")
        r1_ok = sem("r1_ok")
        hat_ok = sem("hat_ok")
        turned2 = sem("turned2")
        t2_ok = sem("t2_ok")
        f_ps = sem("f_ps")
        act_ok = sem("act_ok")
        gv_ok = sem("gv_ok")
        o_ps = sem("o_ps")
        up_ok = sem("up_ok")
        y_ok = sem("y_ok")
        s2_ok = sem("s2_ok")
        rs_ok = sem("rs_ok")
        at_ok = sem("at_ok")
        xn_ok = sem("xn_ok")
        stored = [sem(f"stored{r}") for r in range(R)]
        turn = sem("turn")

        def fence(eng):
            eng.sem_inc(turn, 1)

        block = ctx.enter_context(nc.Block())

        @block.sync
        def _(sp):
            def load(c, r, k, parts):
                sp.wait_ge(hat_ok, due(4 * (c - 3)))
                fence(sp)
                sp.wait_ge(xx_ok, due(c - 3))
                fence(sp)
                sp.wait_ge(at_ok, due(c - 3))
                fence(sp)
                sp.dma_start(xr[r][0:parts].rearrange("p t c -> p (t c)"), rows_of(x, c, parts, XW)).then_inc(loaded[r], 16)
                sp.dma_start(ar[r][0:parts].rearrange("p t c -> p (t c)"), rows_of(agg, c, parts, AW[2])).then_inc(loaded[r], 16)

            def store(c, r, k, parts):
                sp.wait_ge(xn_ok, T * (c + 1))
                fence(sp)
                sp.dma_start(rows_of(xo, c, parts, XW), xn[r][0:parts].rearrange("p t c -> p (t c)")).then_inc(stored[r], 16)

            node_pipeline(sp, ((0, load), (6, store)))
            for r in range(R):
                sp.wait_ge(stored[r], 16 * ((NC - r) // R + 1))

        @block.tensor
        def _(pe):
            pe.matmul(pf[0][0:65, 0:320], wt("b0row"), wt("f1s")[0:64], start=True, stop=False)
            pe.matmul(pf[0][0:65, 0:320], wt("e64"), wt("f1b"), start=False, stop=True).then_inc(b_ps, 1)
            pe.wait_ge(b_ok, 1)
            pe.wait_ge(ones, 2)

            def turn_sums(c, r, k, parts):
                u = r % 2
                pe.wait_ge(an_ok, 2 * (c + 1))
                pe.wait_ge(ts_ok, 2 * c)
                pe.wait_ge(t2_ok, due(2 * (c - 1)))
                for t in range(T):
                    last = pe.transpose(ptv[:, t * P:(t + 1) * P], an[u][:, t, S0:D], wt("ident"))
                last.then_inc(turned, 1)
                for t in range(T):
                    last = pe.transpose(pts[0:64, t * P:(t + 1) * P], an[u][:, t, 0:S0], wt("ident"))
                last.then_inc(turned, 1)

            def project(c, r, k, parts):
                u = r % 2
                pe.wait_ge(ts_ok, 2 * c + 2)
                pe.wait_ge(x1_ok, c)
                pe.wait_ge(up_ok, due(2 * (c - 2)))
                for t in range(T):
                    pe.matmul(pk[:, t, S0:D], tsv[u][:, t * P:(t + 1) * P], wt("pv"), start=True, stop=True)
                    last = pe.matmul(pk[:, t, 0:S0], tss[u][:, t * P:(t + 1) * P], wt("pw"), start=True, stop=True)
                last.then_inc(p_ps, 1)

            def turn_rows(c, r, k, parts):
                pe.wait_ge(hat_ok, 4 * (c + 1))
                pe.wait_ge(t2_ok, 2 * c)
                pe.wait_ge(ts_ok, upto(2 * (c + 2), 2 * NC + 2))
                for t in range(T):
                    last = pe.transpose(ptv[:, t * P:(t + 1) * P], hat[:, t, 65:XW], wt("ident"))
                last.then_inc(turned2, 1)
                for t in range(T):
                    last = pe.transpose(pts[:, t * P:(t + 1) * P], hat[:, t, 0:65], wt("ident"))
                last.then_inc(turned2, 1)

            def first_product(c, r, k, parts):
                pe.wait_ge(t2_ok, 2 * c + 2)
                pe.wait_ge(act_ok, 3 * c)
                pe.wait_ge(gv_ok, 2 * c)
                pe.matmul(pf[0][:], wt("f1s")[:, 0:P], t2s[:], start=True, stop=True).then_inc(f_ps, 1)
                pe.matmul(pf[1][0:96], wt("f1s")[:, P:P + 96], t2s[:], start=True, stop=True).then_inc(f_ps, 1)
                pe.matmul(pf[2][0:96], wt("f1v")[:, 0:96], t2v[:], start=True, stop=True).then_inc(f_ps, 1)
                pe.matmul(pf[3][0:96], wt("f1v")[:, 96:192], t2v[:], start=True, stop=True).then_inc(f_ps, 1)

            def last_gates(c, r, k, parts):
                pe.wait_ge(act_ok, 3 * c + 1)
                pe.matmul(pf[0][0:96], wt("f1s")[:, P + 96:P + 192], t2s[:], start=True, stop=True).then_inc(f_ps, 1)

            def second_product(c, r, k, parts):
                pe.wait_ge(act_ok, 3 * c + 3)
                pe.wait_ge(gv_ok, 2 * c + 2)
                pe.wait_ge(up_ok, 2 * c)
                pe.wait_ge(x1_ok, upto(c + 3, NC + 1))
                for t in range(T):
                    cut = slice(t * P, (t + 1) * P)
                    pe.matmul(pk[:, t, S0:D], gv[:, 0, cut], wt("f2v0"), start=True, stop=False)
                    pe.matmul(pk[:, t, S0:D], gv[:, 1, cut], wt("f2v1"), start=False, stop=True)
                    pe.matmul(pk[:, t, 0:S0], wt("one"), wt("f2b"), start=True, stop=False)
                    last = pe.matmul(pk[:, t, 0:S0], hc[:, cut], wt("f2s"), start=False, stop=True)
                last.then_inc(o_ps, 1)

            node_pipeline(pe, ((1, project), (2, turn_rows), (3, second_product), (2, first_product), (0, turn_sums), (2, last_gates)))

        @block.scalar
        def _(a):
            a.wait_ge(b_ps, 1)
            a.activation(wt("f1s")[64:65], pf[0][64:65, 0:320], ACT.Copy).then_inc(b_ok, 1)

            def copy_sums(c, r, k, parts):
                u = r % 2
                a.wait_ge(p_ps, due(c - 1))
                a.wait_ge(turned, 2 * c + 1)
                a.activation(tsv[u][:], ptv[:], ACT.Copy).then_inc(ts_ok, 1)
                a.wait_ge(turned, 2 * c + 2)
                a.activation(tss[u][0:64], pts[0:64], ACT.Copy).then_inc(ts_ok, 1)

            def squares(c, r, k, parts):
                u = r % 2
                a.wait_ge(x1_ok, c + 1)
                a.wait_ge(sq_ok, 2 * c)
                a.activation(sq[:], x1[u][:, :, S0:D], ACT.Square).then_inc(sq_ok, 1)

            def copy_rows(c, r, k, parts):
                a.wait_ge(f_ps, 5 * c)
                a.wait_ge(turned2, 2 * c + 1)
                a.activation(t2v[:], ptv[:], ACT.Copy, scale=wt("ln2v")).then_inc(t2_ok, 1)
                a.wait_ge(turned2, 2 * c + 2)
                a.activation(t2s[:], pts[:], ACT.Copy, scale=wt("ln2w")).then_inc(t2_ok, 1)

            def activate(c, r, k, parts):
                a.wait_ge(f_ps, 5 * c + 1)
                a.wait_ge(o_ps, c)
                a.activation(hc[:], pf[0][:], ACT.Silu).then_inc(act_ok, 1)
                a.wait_ge(f_ps, 5 * c + 2)
                a.wait_ge(gv_ok, 2 * c)
                a.activation(tg[:, 0, :], pf[1][0:96], ACT.Tanh, scale=0.5).then_inc(act_ok, 1)

            def activate_last(c, r, k, parts):
                a.wait_ge(f_ps, 5 * c + 5)
                a.activation(tg[:, 1, :], pf[0][0:96], ACT.Tanh, scale=0.5).then_inc(act_ok, 1)

            def normalise(c, r, k, parts):
                u = r % 2
                a.wait_ge(rs_ok, 2 * c + 2)
                a.wait_ge(at_ok, c + 1)
                for t in range(T):
                    a.activation(xn[r][:, t, 0:D], y[u][:, t, :], ACT.Identity, bias=nr[u][:, t:t + 1], scale=rs[u][:, t:t + 1]).then_inc(xn_ok, 1)

            node_pipeline(a, ((4, normalise), (1, squares), (2, copy_rows), (2, activate), (0, copy_sums), (2, activate_last)))

        @block.vector
        def _(v):
            for u in range(2):
                v.memset(tss[u][64:65], 1.0).then_inc(ones, 1)

            def denominator(c, r, k, parts):
                u = r % 2
                v.wait_ge(loaded[r], 32 * (k + 1))
                v.wait_ge(an_ok, due(2 * (c - 1)))
                v.tensor_scalar(den[u][:], ar[r][:, :, 160:168], 1e-12, None, ALU.add).then_inc(den_ok, 1)
                v.wait_ge(den_ok, 2 * c + 1)
                v.reciprocal(den[u][:], den[u][:]).then_inc(den_ok, 1)

            def project(c, r, k, parts):
                u = r % 2
                v.wait_ge(p_ps, c + 1)
                v.wait_ge(xx_ok, due(c - 1))
                v.wait_ge(hat_ok, due(4 * (c - 1)))
                v.tensor_tensor(x1[u][:], pk[:, :, 0:D], xr[r][:, :, 0:D], ALU.add).then_inc(x1_ok, 1)
                v.wait_ge(x1_ok, c + 1)
                v.wait_ge(st_ok, 10 * c)
                for t in range(T):
                    v.bn_stats(st[:, t, :], x1[u][:, t, 0:S0]).then_inc(st_ok, 1)

            def moments(c, r, k, parts):
                v.wait_ge(st_ok, 10 * c + 4)
                v.wait_ge(hat_ok, 4 * c)
                fence(v)
                for t in range(T):
                    v.bn_aggr(mv[:, t, :], st[:, t, :]).then_inc(st_ok, 1)
                v.wait_ge(r1_ok, 2 * c)
                v.wait_ge(sq_ok, 2 * c + 1)
                v.tensor_reduce(var[:, 1, :], sq[:], AX.X, ALU.add).then_inc(sq_ok, 1)
                v.wait_ge(st_ok, 10 * c + 8)
                v.tensor_scalar(var[:, 0, :], mv[:, :, 1], EPS, None, ALU.add).then_inc(st_ok, 1)
                v.wait_ge(sq_ok, 2 * c + 2)
                v.tensor_scalar(var[:, 1, :], var[:, 1, :], 1.0 / V3, EPS, ALU.mult, ALU.add).then_inc(st_ok, 1)

            def gated(c, r, k, parts):
                for g in range(2):
                    v.wait_ge(act_ok, 3 * c + 2 + g)
                    v.wait_ge(f_ps, 5 * c + 3 + g)
                    if g == 0:
                        v.wait_ge(o_ps, c)
                    v.scalar_tensor_tensor(gv[:, g, :], tg[:, g, :], 1.0, pf[2 + g][0:96], ALU.add, ALU.mult).then_inc(gv_ok, 1)

            def hats(c, r, k, parts):
                u = r % 2
                v.wait_ge(turned2, 2 * c)
                v.tensor_tensor(hat[:, :, 0:S0], x1[u][:, :, 0:S0], mv[:, :, 0:1].to_broadcast([P, T, S0]), ALU.subtract).then_inc(hat_ok, 1)
                v.wait_ge(r1_ok, 2 * c + 2)
                v.tensor_tensor(hat[:, :, 65:XW], x1[u][:, :, S0:D], rs1[:, 1, :].unsqueeze(2).to_broadcast([P, T, V3]), ALU.mult).then_inc(hat_ok, 1)
                v.wait_ge(hat_ok, 4 * c + 1)
                v.tensor_tensor(hat[:, :, 0:S0], hat[:, :, 0:S0], rs1[:, 0, :].unsqueeze(2).to_broadcast([P, T, S0]), ALU.mult).then_inc(hat_ok, 1)
                v.tensor_copy(hat[:, :, S0], xr[r][:, :, D]).then_inc(hat_ok, 1)

            def output(c, r, k, parts):
                v.wait_ge(o_ps, c + 1)
                v.wait_ge(at_ok, c + 1)
                v.wait_ge(y_ok, c)
                v.tensor_tensor(up[:, :, 0:S0], pk[:, :, 0:S0], xn[r][:, :, D:XW].to_broadcast([P, T, S0]), ALU.mult).then_inc(up_ok, 1)
                v.scalar_tensor_tensor(up[:, :, S0:D], pk[:, :, S0:D], 0.5, xn[r][:, :, D:XW].to_broadcast([P, T, V3]), ALU.mult, ALU.mult).then_inc(up_ok, 1)

            def total(c, r, k, parts):
                u = r % 2
                v.wait_ge(up_ok, 2 * c + 2)
                v.wait_ge(xx_ok, c + 1)
                v.wait_ge(xn_ok, due(T * (c - 1)))
                v.tensor_tensor(y[u][:], up[:], xx[r][:], ALU.add).then_inc(y_ok, 1)
                v.wait_ge(y_ok, c + 1)
                v.wait_ge(s2_ok, 10 * c)
                for t in range(T):
                    v.bn_stats(st2[:, t, :], y[u][:, t, :]).then_inc(s2_ok, 1)

            def variance(c, r, k, parts):
                v.wait_ge(s2_ok, 10 * c + 4)
                fence(v)
                for t in range(T):
                    v.bn_aggr(mv2[:, t, :], st2[:, t, :]).then_inc(s2_ok, 1)
                v.wait_ge(s2_ok, 10 * c + 8)
                v.wait_ge(rs_ok, 2 * c)
                v.tensor_scalar(ve[:], mv2[:, :, 1], EPS, None, ALU.add).then_inc(s2_ok, 1)
                v.tensor_scalar(nm[:], mv2[:, :, 0], -1.0, None, ALU.mult).then_inc(s2_ok, 1)

            node_pipeline(v, ((0, denominator), (3, gated), (1, project), (1, moments), (3, output), (3, total), (1, hats), (3, variance)))

        @block.gpsimd
        def _(pool):
            def shares(c, r, k, parts):
                u = r % 2
                pool.wait_ge(turned, due(2 * (c - 1)))
                fence(pool)
                pool.wait_ge(den_ok, 2 * c + 2)
                fence(pool)
                for lo, hi in ((0, 64), (64, 160)):
                    pool.tensor_tensor(an[u][:, :, lo:hi].rearrange("p t (h k) -> p t h k", h=H), ar[r][:, :, lo:hi].rearrange("p t (h k) -> p t h k", h=H),
                                       den[u][:].unsqueeze(3).to_broadcast([P, T, H, (hi - lo) // H]), ALU.mult).then_inc(an_ok, 1)

            def powers(c, r, k, parts):
                pool.wait_ge(st_ok, 10 * (c + 1))
                fence(pool)
                pool.wait_ge(hat_ok, 4 * c)
                fence(pool)
                pool.tensor_tensor(rs1[:], var[:], wt("mhalf8").rearrange("p (a t) -> p a t", a=2), ALU.pow).then_inc(r1_ok, 1)
                pool.wait_ge(r1_ok, 2 * c + 1)
                fence(pool)
                pool.tensor_tensor(rs1[:], rs1[:], xr[r][:, :, D].unsqueeze(1).to_broadcast([P, 2, T]), ALU.mult).then_inc(r1_ok, 1)

            def attribute(c, r, k, parts):
                pool.wait_ge(stored[r], 16 * k)
                fence(pool)
                pool.tensor_copy(xn[r][:, :, D:XW], xr[r][:, :, D:XW]).then_inc(at_ok, 1)

            def twice(c, r, k, parts):
                u = r % 2
                pool.wait_ge(x1_ok, c + 1)
                fence(pool)
                pool.wait_ge(y_ok, due(c - 3))
                fence(pool)
                pool.tensor_tensor(xx[r][:], x1[u][:], xr[r][:, :, 0:D], ALU.add).then_inc(xx_ok, 1)

            def deviation(c, r, k, parts):
                u = r % 2
                pool.wait_ge(xn_ok, due(T * (c - 1)))
                fence(pool)
                pool.wait_ge(s2_ok, 10 * (c + 1))
                fence(pool)
                pool.tensor_tensor(rs[u][:], ve[:], wt("mhalf"), ALU.pow).then_inc(rs_ok, 1)
                pool.wait_ge(rs_ok, 2 * c + 1)
                fence(pool)
                pool.tensor_tensor(nr[u][:], nm[:], rs[u][:], ALU.mult).then_inc(rs_ok, 1)

            node_pipeline(pool, ((0, shares), (1, powers), (1, twice), (3, deviation), (1, attribute)))


def build(nc, ins, out):
    with ExitStack() as ctx:
        wsb = ctx.enter_context(nc.sbuf_tensor("wsb", [P, WCOLS], F32))
        w_in = ctx.enter_context(nc.semaphore("w_in"))

        def wt(name):
            if name in ("mhalf", "mhalf8"):
                return wt("mhalfn")[:, 0:T if name == "mhalf" else 2 * T]
            r, c, at = SLOTS[name]
            return wsb[0:r, at:at + c]

        def table(name, rows, w, d=F32):
            return nc.dram_tensor(name, (rows, w), d, kind="Internal").ap()

        agg = [table(f"agg{k}", NA, AW[k]) for k in range(4)]
        xs = [ins["x"]] + [table(f"x{k}", N, XW) for k in (1, 2, 3)]
        dram = dict(ins)
        dram["cidx"] = nc.dram_tensor("cidx", (NBP, P, T), U32, kind="Internal").ap()
        dram["hid"] = table("hid", 64, NBP * B)
        dram["val"] = nc.dram_tensor("val", (NB, P, T, AW[2]), F32, kind="Internal").ap()
        dram["att"] = table("att", NB * B, 8)
        mx = table("mx", NA, 8)
        with nc.Block() as block:
            @block.sync
            def _(sp):
                sp.dma_start(wsb[:], ins["w"]).then_inc(w_in, 16)
                sp.dma_start(dram["cidx"][NB:NBP].rearrange("a p t -> (a p) t"), ins["dst_t"][NB:NBP].rearrange("a p t -> (a p) t").bitcast(U32)).then_inc(w_in, 16)
                sp.dma_start(dram["hid"][:, NB * B:NBP * B], ins["ea64T"][:, NB * B:NBP * B]).then_inc(w_in, 16)
                sp.wait_ge(w_in, 48)
        edge_phase_01(nc, 0, xs[0], agg[0], dram, wt, agg)
        node_phase_01(nc, 0, xs[0], agg[0], xs[1], wt, XW)
        edge_phase_01(nc, 1, xs[1], agg[1], dram, wt, agg)
        node_phase_01(nc, 1, xs[1], agg[1], xs[2], wt, XW)
        hidden_phase(nc, dram, wt)
        edge_phase_23(nc, 2, xs[2], None, dram, wt)
        attention_max_phase(nc, dram, mx, wt)
        attention_sum_phase(nc, dram, mx, agg[2], wt)
        node_phase_2(nc, xs[2], agg[2], xs[3], wt)
        edge_phase_23(nc, 3, xs[3], agg[3], dram, wt)
        node_phase_3(nc, xs[3], agg[3], out, wt)


def lay_out(inputs):
    g = {k: np.asarray(v) for k, v in inputs.items()}
    w = np.zeros((P, WCOLS), np.float32)

    def put(name, r, c, a, step=1):
        rows, cols, at = SLOTS[name]
        w[r:r + step * (a.shape[0] - 1) + 1:step, at + c:at + c + step * (a.shape[1] - 1) + 1:step] = a

    def put3(name, r, c, a):
        for k in range(3):
            put(name, r + k, c + k, a, 3)

    def rep3(name, c, a):
        rows, cols, at = SLOTS[name]
        for k in range(3):
            w[0:a.shape[0], at + c + k:at + c + 3 * a.shape[1]:3] = a

    names = [("fcW1", "fcW2", "W1_s", "W1_v", "W2_s", "W2_v", "W3", "W_sc_s", "W_sc_v"),
             ("Wfc1", "Wfc3", "Wl1_0", "Wl1_1", "Wl2_s", "Wl2_v", "Wa", "Wsc0", "Wsc1")]
    for l in (0, 1):
        h, w2, ws, wv, os_, ov, oa, ns, nv = (g[f"L{l}_gnn_{n}"] for n in names[l])
        put(f"h{l}", 0, 0, h)
        put(f"w1_{l}", 0, 0, w2[:, 0:128])
        put(f"w2_{l}", 0, 0, w2[:, 160:192])
        rep3(f"w2_{l}", 32, w2[:, 128:160])
        put(f"f1_{l}", 0, 0, ws)
        put(f"f1_{l}", 64, 64, ws)
        put(f"f2_{l}", 0, 0, wv)
        put3(f"f2_{l}", 32, 32, wv)
        put(f"o1_{l}", 64, 0, ov[0:64])
        put(f"o1_{l}", 0, 32, os_[0:64])
        put(f"o1_{l}", 0, 192, oa[0:64])
        put(f"o2_{l}", 0, 0, os_[64:96])
        put(f"o2_{l}", 0, 160, oa[64:96])
        put3(f"o2_{l}", 32, 64, ov[64:96])
        put(f"ns_{l}", 0, 0, ns)
        put3(f"nv_{l}", 0, 0, nv)
    put("hh1", 0, 0, g["L1_gnn_Wfc2"])
    put("ident", 0, 0, np.eye(P, dtype=np.float32))
    e = np.arange(B).reshape(T, P)
    before = (np.arange(B)[None, None, :] < e.T[:, :, None]).astype(np.float32)
    put("before", 0, 0, before.reshape(P, T * B))
    put("spare", 0, 0, (N + e.T).astype(np.float32))
    put("mhalfn", 0, 0, np.full((P, NBP * T), -0.5, np.float32))
    put("one", 0, 0, np.ones((1, 128), np.float32))
    put("e64", 0, 64, np.ones((1, 1), np.float32))
    for l in (2, 3):
        so = 128 if l == 2 else 96
        k = "L2_gnn_" if l == 2 else "L3_gnn_"
        w2 = g[k + ("rw3" if l == 2 else "W_fc2")]
        put(f"w1_{l}", 0, 0, w2[:, 0:128])
        rep3(f"w2_{l}", 0, w2[:, 128:160])
        put(f"w2_{l}", 0, 96, w2[:, 160:192])
        rep3(f"w3_{l}", 0, w2[:, 192:224])
        ends = ((g[k + "msrc_ws"], g[k + "msrc_wv"]), (g[k + "mdst_ws"], g[k + "mdst_wv"])) if l == 2 else ((g[k + "W_nl0"], g[k + "W_nl1"]),)
        for s, (ws, wv) in enumerate(ends):
            put(f"f1_{l}{s}", 0, 0, ws)
            put(f"f1_{l}{s}", 0, 64, ws)
            put3(f"f2_{l}{s}", 0, 0, wv)
            put(f"f2_{l}{s}", 96, 96, wv)
        os_, ov = (g[k + "lin_ws"], g[k + "lin_wv"]) if l == 2 else (g[k + "W_out_s"], g[k + "W_out_v"])
        put(f"o1_{l}", 0, 32, os_[0:64])
        put(f"o1_{l}", 64, 0, ov[0:64])
        put3(f"o2_{l}", 0, so, ov[64:96])
        put(f"o2_{l}", 96, 0, os_[64:96])
        put3(f"o3_{l}", 0, 0, ov[96:128])
    put("h3", 0, 0, g["L3_gnn_W_fc1"])
    put("ns_3", 0, 0, g["L3_gnn_W_skip0"])
    put3("nv_3", 0, 0, g["L3_gnn_W_skip1"])
    q = {n[7:]: a for n, a in g.items() if n.startswith("L2_gnn_")}
    col = lambda a: np.reshape(a, (-1, 1))
    row = lambda a: np.reshape(a, (1, -1))

    def col3(name, r, a):
        for k in range(3):
            put(name, r + k, 0, col(a), 3)

    put("roff0", 0, 0, col(q["roff"][0:128]))
    col3("roff1", 0, q["roff"][128:160])
    put("roff1", 96, 0, col(q["roff"][160:192]))
    col3("roff2", 0, q["roff"][192:224])
    put("mb2", 0, 0, col(q["mdst_bs"]))
    put("mb2", 64, 0, col(q["mdst_bs"]))
    put("ln1w", 0, 0, col(q["ln1_w0"]))
    put("ln1b", 0, 0, col(q["ln1_b0"]))
    col3("ln1v", 0, q["ln1_w1"])
    put("ln1v", 96, 0, col(q["ln1_w1"]))
    put("adot", 0, 0, np.broadcast_to(row(q["alpha_dot"]), (P, 64)))
    put("linb", 0, 0, row(q["lin_bs"]))
    for k in range(2):
        put(f"rw{k}", 0, 0, q[f"rw{k + 1}"])
        put(f"rb{k}", 0, 0, row(q[f"rb{k + 1}"]))
        put(f"rg{k}", 0, 0, col(q[f"rg{k + 1}"]))
        put(f"rbe{k}", 0, 0, col(q[f"rbe{k + 1}"]))
    put("pw", 0, 0, q["proj_ws"])
    put("pw", 64, 0, row(q["proj_bs"]))
    put3("pv", 0, 0, q["proj_wv"])
    put("ln2w", 0, 0, col(q["ln2_w0"]))
    put("ln2w", 64, 0, np.ones((1, 1), np.float32))
    col3("ln2v", 0, q["ln2_w1"])
    put("b0row", 0, 64, col(q["ln2_b0"]))
    put("f1s", 0, 0, q["f1_ws"][:, 0:128])
    rep3("f1s", 128, q["f1_ws"][:, 128:192])
    put("f1b", 0, 0, row(q["f1_bs"][0:128]))
    rep3("f1b", 128, row(q["f1_bs"][128:192]))
    put3("f1v", 0, 0, q["f1_wv"])
    put("f2s", 0, 0, q["f2_ws"])
    put("f2b", 0, 0, row(q["f2_bs"]))
    put3("f2v0", 0, 0, q["f2_wv"][0:32])
    put3("f2v1", 0, 0, q["f2_wv"][32:64])

    def edges(a, fill):
        p = np.full((NBP * B,) + a.shape[1:], fill, a.dtype)
        p[0:E] = a
        return p

    def tiles(a):
        return np.ascontiguousarray(a.reshape((NBP, T, P) + a.shape[1:]).swapaxes(1, 2))

    x = np.empty((N, XW), np.float32)
    x[:, 0:D] = g["x"]
    x[:, D:] = g["node_vec1"]
    o = {"w": w, "x": x}
    for side in ("src", "dst"):
        o[side + "_g"] = tiles(edges(g[side], 0)).view(np.uint32)
        o[side + "_t"] = tiles(edges(g[side], N))
        o[side + "_r"] = edges(g[side], N).reshape(NBP, B)
    o["ea8T"] = np.ascontiguousarray(edges(g["edge_attr_8"], 1.0).T)
    o["ea64T"] = np.ascontiguousarray(edges(g["edge_attr_64"], 1.0).T)
    e3 = edges(g["edge_attr_3"], 1.0).reshape(NBP * T, P, 3)
    o["ea3"] = np.ascontiguousarray(e3.swapaxes(0, 1)).reshape(P, NBP * T * 3)
    o["ea4"] = tiles(edges(g["edge_attr_4"], 1.0))
    return o


def kernel(**inputs):
    from concourse import bacc
    from concourse.bass_utils import run_bass_kernel_spmd as run

    nc = bacc.Bacc("TRN2", target_bir_lowering=False, num_devices=1)
    arrays = lay_out(inputs)
    ins = {k: nc.dram_tensor(f"in_{k}", a.shape, mybir.dt.from_np(a.dtype), kind="ExternalInput").ap() for k, a in arrays.items()}
    out = nc.dram_tensor("out", (N, D), F32, kind="ExternalOutput").ap()
    build(nc, ins, out)
    r = run(nc, [{f"in_{k}": a for k, a in arrays.items()}], core_ids=[0])
    return r.results[0]["out"]
```

```python
from contextlib import ExitStack

import numpy as np

import concourse.bass as bass
import concourse.mybir as mybir

F32 = mybir.dt.float32
I32 = mybir.dt.int32
U32 = mybir.dt.uint32
ALU = mybir.AluOpType
ACT = mybir.ActivationFunctionType
AX = mybir.AxisListType

P = 128
N, E = 50000, 25000
S0, V1 = 64, 32
V3 = 3 * V1
D = S0 + V3
XW = D + 1
T = 4
R = 4
B = T * P
NB = 50
NBP = NB + 1
NC = N // B
LASTP = (N - NC * B) // T
NA = 400 * P
ZR = 20
ZS = NA // P // NB
AW = {0: 161, 1: 161, 2: 168, 3: 192}
EPS = 1e-5
MAGIC = 12582912.0

SLOTS = {}


def slot(name, rows, cols):
    at = sum(c for _, c, _ in SLOTS.values())
    SLOTS[name] = (rows, cols, at)


for _l in (0, 1):
    slot(f"h{_l}", 8, 64)
    slot(f"w1_{_l}", 64, 128)
    slot(f"w2_{_l}", 64, 128)
    slot(f"f1_{_l}", 128, 128)
    slot(f"f2_{_l}", 128, 128)
    slot(f"o1_{_l}", 128, 193)
    slot(f"o2_{_l}", 128, 161)
    slot(f"ns_{_l}", 64, 64)
    slot(f"nv_{_l}", 96, 96)
slot("hh1", 64, 64)
slot("ident", 128, 128)
slot("before", 128, T * B)
slot("spare", 128, T)
slot("mhalfn", 128, NBP * T)
slot("one", 1, 128)
slot("e64", 1, 65)
for _l in (2, 3):
    _so = 128 if _l == 2 else 96
    slot(f"w1_{_l}", 64, 128)
    slot(f"w2_{_l}", 64, 128)
    slot(f"w3_{_l}", 64, 96)
    for _s in range(2 if _l == 2 else 1):
        slot(f"f1_{_l}{_s}", 64, 128)
        slot(f"f2_{_l}{_s}", 128, 128)
    slot(f"o1_{_l}", 128, 32 + _so + 96)
    slot(f"o2_{_l}", 128, _so + 96)
    slot(f"o3_{_l}", 96, 96)
slot("h3", 64, 64)
slot("ns_3", 64, 96)
slot("nv_3", 96, 96)
slot("roff0", 128, 1)
slot("roff1", 128, 1)
slot("roff2", 96, 1)
slot("mb2", 128, 1)
slot("ln1w", 64, 1)
slot("ln1b", 64, 1)
slot("ln1v", 128, 1)
slot("adot", 128, 64)
slot("linb", 1, 224)
for _k in range(2):
    slot(f"rw{_k}", 64, 64)
    slot(f"rb{_k}", 1, 64)
    slot(f"rg{_k}", 64, 1)
    slot(f"rbe{_k}", 64, 1)
slot("pw", 65, 64)
slot("pv", 96, 96)
slot("ln2w", 65, 1)
slot("ln2v", 96, 1)
slot("b0row", 64, 65)
slot("f1s", 65, 320)
slot("f1b", 1, 320)
slot("f1v", 96, 192)
slot("f2s", 128, 64)
slot("f2b", 1, 64)
slot("f2v0", 96, 96)
slot("f2v1", 96, 96)
WCOLS = sum(c for _, c, _ in SLOTS.values())


def due(count):
    return max(count, 0) if isinstance(count, int) else count


def semaphores(nc, ctx, named):
    made = []

    def over():
        nc.clear_and_free_semaphores(made)
        nc.all_engine_barrier()

    def sem(n):
        made.append(nc.alloc_semaphore(name=named(n)))
        return made[-1]

    ctx.callback(over)
    return sem


def rows_of(t, c, parts, w):
    return t[bass.ds(c * B, parts * T), 0:w].rearrange("(p t) c -> p (t c)", t=T)


def pipeline(eng, n, head, stages):
    tail = (n - 1) // R * R

    def at(m):
        for lag, f in stages:
            c = m - lag
            if 0 <= c < n:
                f(c, c % R, c // R, LASTP if c == NC else P)

    for m in range(head):
        at(m)
    with eng.Fori(head // R, tail // R) as j:
        for q in range(R):
            for lag, f in stages:
                f(R * j + (q - lag), (q - lag) % R, j + (q - lag) // R, P)
    for m in range(tail, n + max(lag for lag, f in stages)):
        at(m)


def node_pipeline(eng, stages):
    pipeline(eng, NC + 1, 2 * R, stages)


def edge_pipeline(eng, stages):
    pipeline(eng, NB, 3 * R, stages)


def upto(count, most):
    return min(count, most) if isinstance(count, int) else count


def edge_phase_01(nc, l, x, agg, dram, wt, later):
    W = AW[l]
    act_fn = ACT.Silu if l == 0 else ACT.Gelu_apprx_tanh
    NH = 1 + l
    with ExitStack() as ctx:
        sb = lambda n, s, d=F32: ctx.enter_context(nc.sbuf_tensor(f"{n}_{l}", s, d))
        ps = lambda n, s: ctx.enter_context(nc.psum_tensor(f"{n}_{l}", s, F32))
        sem = semaphores(nc, ctx, lambda n: f"{n}_{l}")
        gidx = [sb(f"gidx{r}", [P, T], U32) for r in range(R)]
        tidx = [sb(f"tidx{r}", [P, T], I32) for r in range(R)]
        trow = [sb(f"trow{r}", [P, B], I32) for r in range(R)]
        esT = [sb(f"esT{r}", [8, B]) for r in range(R)]
        ea = [sb(f"ea{r}", [P, T, 4]) for r in range(R)]
        xg = [sb(f"xg{r}", [P, T, XW]) for r in range(R)]
        ya = sb("ya", [P, T, 4])
        yb = [sb(f"yb{r}", [P, T, 8]) for r in range(R)]
        prod = sb("prod", [P, T, V3])
        rows = [sb(f"rows{u}", [P, T, 2 * P]) for u in range(2)]
        ts = [sb(f"ts{u}", [P, 2, B]) for u in range(2)]
        hs = [sb(f"hs{n}", [64, B]) for n in range(NH)]
        ws = sb("ws", [P, 2, B])
        pr = [sb(f"pr{u}", [P, 2, B]) for u in range(2)]
        tf = sb("tf", [P, T])
        same = [sb(f"same{u}", [P, T, B]) for u in range(2)]
        cidx = [sb(f"cidx{r}", [P, T], U32) for r in range(R)]
        outer = sb("outer", [P, T, V3])
        ob = [sb(f"ob{u}", [P, T, 32 + W]) for u in range(2)]
        summed = [sb(f"summed{u}", [P, T, W]) for u in range(2)]
        if l == 0:
            product = sb("product", [P, T, B])
            cnt = sb("cnt", [P, T])
            away = sb("away", [P, T])
            zero = sb("zero", [P, ZR * 192])

        pt = ps("pt", [P, 2, B])
        ph = ps("ph", [P, B])
        pf = ps("pf", [P, B])
        po = ps("po", [P, T, 256])
        pc = ps("pc", [P, T, 256])

        loaded = [sem(f"loaded{r}") for r in range(R)]
        late = [sem(f"late{r}") for r in range(R)]
        gathered = [sem(f"gathered{r}") for r in range(R)]
        y_ok = sem("y_ok")
        rows_v = sem("rows_v")
        rows_a = sem("rows_a")
        turned = sem("turned")
        ts_ok = sem("ts_ok")
        h_ps = sem("h_ps")
        h_ok = sem("h_ok")
        w_ps = sem("w_ps")
        w_ok = sem("w_ok")
        f_ps = sem("f_ps")
        prod_ok = sem("prod_ok")
        o_ps = sem("o_ps")
        ob_ok = sem("ob_ok")
        msg_v = sem("msg_v")
        same_ok = sem("same_ok")
        idx_step = sem("idx_step")
        idx_ok = sem("idx_ok")
        idx_out = [sem(f"idx_out{r}") for r in range(R)]
        c_ps = sem("c_ps")
        sum_ok = sem("sum_ok")
        added = sem("added")
        cidx_in = [sem(f"cidx_in{r}") for r in range(R)]
        zset = sem("zset")
        zeroed = sem("zeroed")
        cleared = sem("cleared")
        turn = sem("turn")

        def fence(eng):
            eng.sem_inc(turn, 1)

        block = ctx.enter_context(nc.Block())

        @block.sync
        def _(sp):
            def load(i, r, k, parts):
                sp.wait_ge(gathered[r], 16 * T * k)
                fence(sp)
                sp.wait_ge(y_ok, due(5 * (i - 3)))
                fence(sp)
                sp.dma_start(gidx[r][:], dram["src_g"][bass.ds(i, 1)].rearrange("a p t -> (a p) t")).then_inc(loaded[r], 16)
                sp.dma_start(ea[r][:], dram["ea4"][bass.ds(i, 1)].rearrange("a p t c -> (a p) t c")).then_inc(loaded[r], 16)

            def load_late(i, r, k, parts):
                sp.wait_ge(h_ps, due(NH * (i - 3)))
                fence(sp)
                sp.wait_ge(idx_ok, due(i - 3))
                fence(sp)
                sp.dma_start(esT[r][:], dram["ea8T"][:, bass.ds(i * B, B)]).then_inc(late[r], 16)
                sp.dma_start(tidx[r][:], dram["dst_t"][bass.ds(i, 1)].rearrange("a p t -> (a p) t")).then_inc(late[r], 16)
                sp.dma_start(trow[r][:], dram["dst_r"][bass.ds(i, 1)].broadcast_to([P, B])).then_inc(late[r], 16)

            def load_cidx(i, r, k, parts):
                sp.wait_ge(added, due(16 * T * (i - 3)))
                fence(sp)
                sp.dma_start(cidx[r][:], dram["cidx"][bass.ds(i, 1)].rearrange("a p t -> (a p) t")).then_inc(cidx_in[r], 16)

            def keep_cidx(i, r, k, parts):
                sp.wait_ge(idx_ok, i + 1)
                fence(sp)
                sp.dma_start(dram["cidx"][bass.ds(i, 1)].rearrange("a p t -> (a p) t"), cidx[r][:]).then_inc(idx_out[r], 16)

            def clear_later(i, r, k, parts):
                for n in (1, 2, 3):
                    w = ZS * AW[n]
                    flat = later[n].rearrange("(p r) c -> p (r c)", p=P)
                    sp.dma_start(flat[:, bass.ds(i * w, w)], zero[:, 0:w]).then_inc(cleared, 16)

            if l == 0:
                sp.wait_ge(zset, 1)
                w = ZR * W
                flat = agg.rearrange("(p r) c -> p (r c)", p=P)
                with sp.Fori(0, NA // P // ZR) as j:
                    sp.dma_start(flat[:, bass.ds(j * w, w)], zero[:, 0:w]).then_inc(zeroed, 16)
                edge_pipeline(sp, ((0, load), (3, load_late), (7, keep_cidx), (7, clear_later)))
                for r in range(R):
                    sp.wait_ge(idx_out[r], 16 * ((NB - 1 - r) // R + 1))
                sp.wait_ge(cleared, 48 * NB)
            else:
                edge_pipeline(sp, ((0, load), (3, load_late), (5, load_cidx)))

        @block.gpsimd
        def _(pool):
            def gather(i, r, k, parts):
                pool.wait_ge(loaded[r], 32 * (k + 1))
                fence(pool)
                pool.wait_ge(rows_v, due(4 * (i - 3)))
                fence(pool)
                pool.wait_ge(rows_a, due(i - 3))
                fence(pool)
                for t in range(T):
                    pool.indirect_dma_start(xg[r][:, t, :], None, x, bass.IndirectOffsetOnAxis(ap=gidx[r][:, t:t + 1], axis=0)).then_inc(gathered[r], 16)

            def add(i, r, k, parts):
                u = r % 2
                if l == 0:
                    pool.wait_ge(idx_ok, i + 1)
                    fence(pool)
                else:
                    pool.wait_ge(cidx_in[r], 16 * (k + 1))
                    fence(pool)
                pool.wait_ge(added, 16 * T * i)
                fence(pool)
                pool.wait_ge(sum_ok, i + 1)
                fence(pool)
                if l == 0 and isinstance(i, int) and i == 0:
                    pool.wait_ge(zeroed, 16 * (NA // P // ZR))
                for t in range(T):
                    pool.indirect_dma_start(agg, bass.IndirectOffsetOnAxis(ap=cidx[r][:, t:t + 1], axis=0), summed[u][:, t, :], None, compute_op=ALU.add).then_inc(added, 16)

            if l == 0:
                pool.memset(zero[:], 0.0).then_inc(zset, 1)
            edge_pipeline(pool, ((0, gather), (6, add)))
            pool.wait_ge(added, 16 * T * NB)

        @block.vector
        def _(v):
            c3 = lambda a: a.rearrange("p t (u c) -> p t u c", c=3)

            def make_rows(i, r, k, parts):
                u = r % 2
                v.wait_ge(gathered[r], 16 * T * (k + 1))
                v.wait_ge(y_ok, 5 * i)
                v.wait_ge(msg_v, due(2 * (i - 3)))
                v.wait_ge(rows_v, 4 * i)
                v.tensor_tensor(ya[:], ea[r][:], xg[r][:, :, D:XW].to_broadcast([P, T, 4]), ALU.mult).then_inc(y_ok, 1)
                v.wait_ge(y_ok, 5 * i + 1)
                v.tensor_scalar(yb[r][:, :, 5:8], ya[:, :, 1:4], 96.0 ** -0.5, None, ALU.mult).then_inc(y_ok, 1)
                v.tensor_scalar(yb[r][:, :, 0:1], ya[:, :, 0:1], 1.0 / 8.0, None, ALU.mult).then_inc(y_ok, 1)
                v.tensor_scalar(yb[r][:, :, 1:2], ya[:, :, 0:1], 32.0 ** -0.5, None, ALU.mult).then_inc(y_ok, 1)
                v.tensor_scalar(yb[r][:, :, 2:5], ya[:, :, 1:4], 1.0 / 8.0, None, ALU.mult).then_inc(y_ok, 1)
                v.wait_ge(turned, due(2 * (i - 1)))
                v.wait_ge(y_ok, 5 * i + 5)
                v.tensor_tensor(c3(prod[:]), c3(xg[r][:, :, S0:D]), yb[r][:, :, 5:8].unsqueeze(2).to_broadcast([P, T, V1, 3]), ALU.mult).then_inc(rows_v, 1)
                v.tensor_tensor(rows[u][:, :, 0:64], xg[r][:, :, 0:64], yb[r][:, :, 0:1].to_broadcast([P, T, 64]), ALU.mult).then_inc(rows_v, 1)
                v.tensor_tensor(rows[u][:, :, 160:256], xg[r][:, :, S0:D], yb[r][:, :, 1:2].to_broadcast([P, T, V3]), ALU.mult).then_inc(rows_v, 1)
                v.wait_ge(rows_v, 4 * i + 1)
                v.tensor_reduce(rows[u][:, :, 128:160], c3(prod[:]), AX.X, ALU.add).then_inc(rows_v, 1)

            def targets(i, r, k, parts):
                u = r % 2
                v.wait_ge(late[r], 48 * (k + 1))
                v.wait_ge(idx_ok, i)
                v.wait_ge(c_ps, due(i - 1))
                if l == 1:
                    v.tensor_copy(tf[:], tidx[r][:]).then_inc(idx_step, 1)
                    v.wait_ge(idx_step, i + 1)
                    for t in range(T - 1):
                        v.tensor_scalar(same[u][:, t, :], trow[r][:], tf[:, t:t + 1], None, ALU.is_equal).then_inc(same_ok, 1)
                    v.tensor_scalar(same[u][:, T - 1, :], trow[r][:], tf[:, T - 1:T], None, ALU.is_equal).then_inc(same_ok, 1)
                    v.wait_ge(same_ok, T * (i + 1))
                    v.sem_inc(idx_ok, 1)
                    return
                v.tensor_copy(tf[:], tidx[r][:]).then_inc(idx_step, 1)
                v.wait_ge(idx_step, i * 7 + 1)
                for t in range(T):
                    v.tensor_scalar(same[u][:, t, :], trow[r][:], tf[:, t:t + 1], None, ALU.is_equal).then_inc(same_ok, 1)
                for t in range(T):
                    m = (t + 1) * P
                    v.scalar_tensor_tensor(product[:, t, 0:m], trow[r][:, 0:m], tf[:, t:t + 1], wt("before")[:, t * B:t * B + m],
                                           ALU.is_equal, ALU.mult, accum_out=cnt[:, t:t + 1]).then_inc(idx_step, 1)
                v.tensor_tensor(away[:], wt("spare"), tf[:], ALU.subtract).then_inc(idx_step, 1)
                v.wait_ge(idx_step, i * 7 + 6)
                v.scalar_tensor_tensor(cnt[:], cnt[:], 1.0, away[:], ALU.min, ALU.mult).then_inc(idx_step, 1)
                v.wait_ge(idx_step, i * 7 + 7)
                v.wait_ge(same_ok, T * (i + 1))
                v.wait_ge(idx_out[r], 16 * k)
                v.wait_ge(added, due(16 * T * (i - 3)))
                v.tensor_tensor(cidx[r][:], cnt[:], tf[:], ALU.add).then_inc(idx_ok, 1)

            def weigh(g):
                def f(i, r, k, parts):
                    u = r % 2
                    if g == 0:
                        v.wait_ge(o_ps, due(2 * (i - 1)))
                    v.wait_ge(w_ok, 2 * i + g + 1)
                    v.wait_ge(f_ps, 2 * i + g + 1)
                    v.tensor_tensor(pr[u][:, g, :], pf[:], ws[:, g, :], ALU.mult).then_inc(prod_ok, 1)
                return f

            def messages(i, r, k, parts):
                o = ob[r % 2]
                v.wait_ge(ob_ok, 2 * i + 2)
                v.wait_ge(msg_v, 2 * i)
                v.tensor_tensor(c3(outer[:]), o[:, :, 0:32].unsqueeze(3).to_broadcast([P, T, V1, 3]),
                                yb[r][:, :, 2:5].unsqueeze(2).to_broadcast([P, T, V1, 3]), ALU.mult).then_inc(msg_v, 1)
                v.wait_ge(msg_v, 2 * i + 1)
                v.tensor_tensor(o[:, :, 96:192], o[:, :, 96:192], outer[:], ALU.add).then_inc(msg_v, 1)

            edge_pipeline(v, ((5, messages), (3, weigh(0)), (4, targets), (3, weigh(1)), (1, make_rows)))

        @block.scalar
        def _(a):
            def copy_scalars(i, r, k, parts):
                a.wait_ge(gathered[r], 16 * T * (k + 1))
                a.wait_ge(turned, due(2 * (i - 1)))
                a.activation(rows[r % 2][:, :, 64:128], xg[r][:, :, 0:64], ACT.Copy).then_inc(rows_a, 1)

            def copies(i, r, k, parts):
                u = r % 2
                a.wait_ge(f_ps, due(2 * (i - 1)))
                for g in range(2):
                    a.wait_ge(turned, 2 * i + g + 1)
                    a.activation(ts[u][:, g, :], pt[:, g, :], ACT.Copy).then_inc(ts_ok, 1)

            def hidden(n):
                def f(i, r, k, parts):
                    a.wait_ge(h_ps, NH * i + n + 1)
                    if n == NH - 1:
                        a.wait_ge(w_ps, 2 * i)
                    a.activation(hs[n][:], ph[0:64, :], act_fn, scale=1.0 / 8.0 if n else 8.0 ** -0.5).then_inc(h_ok, 1)
                return f

            def weights(g):
                def f(i, r, k, parts):
                    a.wait_ge(w_ps, 2 * i + g + 1)
                    a.wait_ge(prod_ok, 2 * i)
                    a.activation(ws[:, g, :], ph[:], ACT.Copy, scale=1.0 / 8.0).then_inc(w_ok, 1)
                return f

            def outputs(g):
                def f(i, r, k, parts):
                    a.wait_ge(c_ps, due(i - 1))
                    a.wait_ge(o_ps, 2 * i + g + 1)
                    a.activation(ob[r % 2][:, 2 * g:2 * g + 2, :], po[:, 2 * g:2 * g + 2, 0:32 + W], ACT.Copy).then_inc(ob_ok, 1)
                return f

            def sums(i, r, k, parts):
                a.wait_ge(added, due(16 * T * (i - 1)))
                a.wait_ge(c_ps, i + 1)
                a.activation(summed[r % 2][:], pc[:, :, 0:W], ACT.Copy).then_inc(sum_ok, 1)

            edge_pipeline(a, ((1, copy_scalars), (3, weights(0)), (4, outputs(0)), (3, weights(1)), (4, outputs(1)), (2, hidden(0)), (5, sums))
                          + (((2, hidden(1)),) if l == 1 else ()) + ((2, copies),))

        @block.tensor
        def _(pe):
            def turn_rows(i, r, k, parts):
                u = r % 2
                pe.wait_ge(rows_v, 4 * i + 4)
                pe.wait_ge(rows_a, i + 1)
                pe.wait_ge(ts_ok, 2 * i)
                for g in range(2):
                    for t in range(T):
                        last = pe.transpose(pt[:, g, t * P:(t + 1) * P], rows[u][:, t, g * P:(g + 1) * P], wt("ident"))
                    last.then_inc(turned, 1)

            def hidden(n):
                def f(i, r, k, parts):
                    if n == 0:
                        pe.wait_ge(late[r], 48 * (k + 1))
                        pe.wait_ge(w_ok, 2 * i)
                        pe.matmul(ph[0:64, :], wt(f"h{l}"), esT[r][:], start=True, stop=True).then_inc(h_ps, 1)
                    else:
                        pe.wait_ge(h_ok, NH * i + 1)
                        fence(pe)
                        pe.matmul(ph[0:64, :], wt("hh1"), hs[0][:], start=True, stop=True).then_inc(h_ps, 1)
                return f

            def transformed(g):
                def f(i, r, k, parts):
                    pe.wait_ge(ts_ok, 2 * i + g + 1)
                    pe.wait_ge(prod_ok, 2 * i + g)
                    pe.matmul(pf[:], wt(f"f{g + 1}_{l}"), ts[r % 2][:, g, :], start=True, stop=True).then_inc(f_ps, 1)
                return f

            def weights(g):
                def f(i, r, k, parts):
                    pe.wait_ge(h_ok, NH * (i + 1))
                    pe.wait_ge(w_ok, 2 * i + g)
                    pe.matmul(ph[:], wt(f"w{g + 1}_{l}"), hs[NH - 1][:], start=True, stop=True).then_inc(w_ps, 1)
                return f

            def outputs(g):
                def f(i, r, k, parts):
                    u = r % 2
                    pe.wait_ge(prod_ok, 2 * i + 2)
                    pe.wait_ge(ob_ok, due(2 * i + g - 1))
                    for t in (2 * g, 2 * g + 1):
                        pe.matmul(po[:, t, 0:193], pr[u][:, 0, t * P:(t + 1) * P], wt(f"o1_{l}"), start=True, stop=False)
                        last = pe.matmul(po[:, t, 32:193], pr[u][:, 1, t * P:(t + 1) * P], wt(f"o2_{l}"), start=False, stop=True)
                    last.then_inc(o_ps, 1)
                return f

            def sums(i, r, k, parts):
                u = r % 2
                pe.wait_ge(msg_v, 2 * i + 2)
                pe.wait_ge(same_ok, T * (i + 1))
                pe.wait_ge(sum_ok, i)
                for t in range(T):
                    for s in range(T):
                        last = pe.matmul(pc[:, t, 0:W], same[u][:, s, t * P:(t + 1) * P], ob[u][:, s, 32:32 + W], start=(s == 0), stop=(s == T - 1))
                last.then_inc(c_ps, 1)

            edge_pipeline(pe, ((3, weights(0)), (3, transformed(0)), (4, outputs(0)), (3, weights(1)), (3, transformed(1)), (4, outputs(1)), (2, hidden(0)), (5, sums))
                          + (((2, hidden(1)),) if l == 1 else ()) + ((2, turn_rows),))


def node_phase_01(nc, l, x, agg, xo, wt, width):
    with ExitStack() as ctx:
        tag = f"n{l}"
        sb = lambda n, s, d=F32: ctx.enter_context(nc.sbuf_tensor(f"{n}_{tag}", s, d))
        ps = lambda n, s: ctx.enter_context(nc.psum_tensor(f"{n}_{tag}", s, F32))
        sem = semaphores(nc, ctx, lambda n: f"{n}_{tag}")
        xr = [sb(f"xr{r}", [P, T, XW]) for r in range(R)]
        ar = [sb(f"ar{r}", [P, T, 161]) for r in range(R)]
        tss = [sb(f"tss{u}", [64, B]) for u in range(2)]
        tsv = [sb(f"tsv{u}", [96, B]) for u in range(2)]
        th = [sb(f"th{u}", [P, 2, T]) for u in range(2)]
        rn = sb("rn", [P, 2, T])
        sc = [sb(f"sc{u}", [P, 2, T]) for u in range(2)]
        at = sb("at", [P, T])
        cf = [sb(f"cf{u}", [P, 3, T]) for u in range(2)]
        ag = [sb(f"ag{u}", [P, T, D]) for u in range(2)]
        sk = sb("sk", [P, T, D])
        y = [sb(f"y{u}", [P, T, D]) for u in range(2)]
        st = sb("st", [P, T, 6])
        mv = sb("mv", [P, T, 2])
        ve = sb("ve", [P, T])
        nm = [sb(f"nm{u}", [P, T]) for u in range(2)]
        rs = [sb(f"rs{u}", [P, T]) for u in range(2)]
        nr = [sb(f"nr{u}", [P, T]) for u in range(2)]
        xn = [sb(f"xn{r}", [P, T, XW]) for r in range(R)]
        pts = [ps(f"pts{u}", [64, B]) for u in range(2)]
        ptv = [ps(f"ptv{u}", [96, B]) for u in range(2)]
        pk = [ps(f"pk{u}", [P, T, 256]) for u in range(2)]
        loaded = [sem(f"loaded{r}") for r in range(R)]
        turned = sem("turned")
        ts_ok = sem("ts_ok")
        k_ps = sem("k_ps")
        an_ok = sem("an_ok")
        th_ok = sem("th_ok")
        sc_ok = sem("sc_ok")
        co_ok = sem("co_ok")
        ag_ok = sem("ag_ok")
        sk_ok = sem("sk_ok")
        y_ok = sem("y_ok")
        st_ok = sem("st_ok")
        ve_ok = sem("ve_ok")
        at_ok = sem("at_ok")
        rs_ok = sem("rs_ok")
        xn_ok = sem("xn_ok")
        stored = [sem(f"stored{r}") for r in range(R)]
        turn = sem("turn")

        def fence(eng):
            eng.sem_inc(turn, 1)

        block = ctx.enter_context(nc.Block())

        @block.sync
        def _(sp):
            def load(c, r, k, parts):
                sp.wait_ge(y_ok, due(c - 3))
                fence(sp)
                sp.wait_ge(at_ok, due(c - 3))
                fence(sp)
                sp.wait_ge(ag_ok, due(2 * (c - 3)))
                fence(sp)
                sp.dma_start(xr[r][0:parts].rearrange("p t c -> p (t c)"), rows_of(x, c, parts, XW)).then_inc(loaded[r], 16)
                sp.dma_start(ar[r][0:parts].rearrange("p t c -> p (t c)"), rows_of(agg, c, parts, 161)).then_inc(loaded[r], 16)

            def store(c, r, k, parts):
                sp.wait_ge(xn_ok, T * (c + 1))
                fence(sp)
                sp.wait_ge(at_ok, c + 1)
                fence(sp)
                sp.dma_start(rows_of(xo, c, parts, width), xn[r][0:parts].rearrange("p t c -> p (t c)") if width == XW else xn[r][0:parts, :, 0:width]).then_inc(stored[r], 16)

            node_pipeline(sp, ((0, load), (5, store)))
            for r in range(R):
                sp.wait_ge(stored[r], 16 * ((NC - r) // R + 1))

        @block.tensor
        def _(pe):
            def turn_rows(c, r, k, parts):
                u = r % 2
                pe.wait_ge(loaded[r], 32 * (k + 1))
                pe.wait_ge(ts_ok, due(2 * (c - 1)))
                for t in range(T):
                    last = pe.transpose(ptv[u][:, t * P:(t + 1) * P], xr[r][:, t, S0:D], wt("ident"))
                last.then_inc(turned, 1)
                for t in range(T):
                    last = pe.transpose(pts[u][:, t * P:(t + 1) * P], xr[r][:, t, 0:S0], wt("ident"))
                last.then_inc(turned, 1)

            def skip(c, r, k, parts):
                u = r % 2
                pe.wait_ge(ts_ok, 2 * c + 2)
                pe.wait_ge(sk_ok, due(2 * (c - 1)))
                for t in range(T):
                    pe.matmul(pk[u][:, t, S0:D], tsv[u][:, t * P:(t + 1) * P], wt(f"nv_{l}"), start=True, stop=True)
                    last = pe.matmul(pk[u][:, t, 0:S0], tss[u][:, t * P:(t + 1) * P], wt(f"ns_{l}"), start=True, stop=True)
                last.then_inc(k_ps, 1)

            node_pipeline(pe, ((0, turn_rows), (1, skip)))

        @block.scalar
        def _(a):
            def copy_turned(c, r, k, parts):
                u = r % 2
                a.wait_ge(k_ps, due(c - 1))
                a.wait_ge(turned, 2 * c + 1)
                a.activation(tsv[u][:], ptv[u][:], ACT.Copy).then_inc(ts_ok, 1)
                a.wait_ge(turned, 2 * c + 2)
                a.activation(tss[u][:], pts[u][:], ACT.Copy).then_inc(ts_ok, 1)

            def sines(c, r, k, parts):
                u = r % 2
                a.wait_ge(th_ok, c + 1)
                a.wait_ge(co_ok, due(4 * (c - 1)))
                a.activation(sc[u][:], th[u][:], ACT.Sin, scale=6.2831845).then_inc(sc_ok, 1)

            def normalise(c, r, k, parts):
                u = r % 2
                a.wait_ge(rs_ok, 2 * c + 2)
                a.wait_ge(stored[r], 16 * k)
                for t in range(T):
                    a.activation(xn[r][:, t, 0:D], y[u][:, t, :], ACT.Identity, bias=nr[u][:, t:t + 1], scale=rs[u][:, t:t + 1]).then_inc(xn_ok, 1)

            node_pipeline(a, ((0, copy_turned), (3, normalise)) + (((0, sines),) if l == 0 else ()))

        @block.vector
        def _(v):
            def angle(n):
                def f(c, r, k, parts):
                    u = r % 2
                    if n == 0:
                        v.wait_ge(loaded[r], 32 * (k + 1))
                        v.wait_ge(sc_ok, due(c - 1))
                        v.scalar_tensor_tensor(th[u][:, 0, :], ar[r][:, :, 160], 0.1 * 10.0 ** -0.5 * 96.0 ** -0.5 / (2 * np.pi), xr[r][:, :, D],
                                               ALU.mult, ALU.mult).then_inc(an_ok, 1)
                        return
                    v.wait_ge(an_ok, 7 * c + n)
                    if n == 1:
                        v.tensor_scalar(rn[:, 0, :], th[u][:, 0, :], MAGIC, None, ALU.add).then_inc(an_ok, 1)
                    elif n == 2:
                        v.tensor_scalar(rn[:, 0, :], rn[:, 0, :], -MAGIC, None, ALU.add).then_inc(an_ok, 1)
                    elif n == 3:
                        v.tensor_tensor(th[u][:, 0, :], th[u][:, 0, :], rn[:, 0, :], ALU.subtract).then_inc(an_ok, 1)
                    elif n == 4:
                        v.tensor_scalar(th[u][:, 1, :], th[u][:, 0, :], 0.25, None, ALU.add).then_inc(an_ok, 1)
                    elif n == 5:
                        v.tensor_scalar(rn[:, 1, :], th[u][:, 1, :], 0.5, None, ALU.is_gt).then_inc(an_ok, 1)
                    elif n == 6:
                        v.tensor_tensor(th[u][:, 1, :], th[u][:, 1, :], rn[:, 1, :], ALU.subtract).then_inc(an_ok, 1)
                    else:
                        v.tensor_scalar(th[u][:], th[u][:], -0.4999999, 0.4999999, ALU.max, ALU.min).then_inc(th_ok, 1)
                return f

            def factor(n):
                def f(c, r, k, parts):
                    u = r % 2
                    if n == 0:
                        v.wait_ge(loaded[r], 32 * (k + 1))
                        v.wait_ge(ag_ok, due(2 * (c - 1)))
                        v.wait_ge(sk_ok, due(2 * (c - 1)))
                        v.wait_ge(co_ok, 4 * c)
                        if l == 0:
                            v.wait_ge(sc_ok, c + 1)
                            v.tensor_tensor(at[:], sc[u][:, 1, :], xr[r][:, :, D], ALU.mult).then_inc(co_ok, 1)
                            v.scalar_tensor_tensor(cf[u][:, 2, :], sc[u][:, 0, :], 960.0 ** -0.5, xr[r][:, :, D], ALU.mult, ALU.mult).then_inc(co_ok, 1)
                        else:
                            v.scalar_tensor_tensor(at[:], ar[r][:, :, 160], 1.0 / 3072.0, xr[r][:, :, D], ALU.mult, ALU.mult).then_inc(co_ok, 1)
                            v.tensor_scalar(cf[u][:, 0, :], xr[r][:, :, D], 1.0 / 8.0, None, ALU.mult).then_inc(co_ok, 1)
                    elif n == 1:
                        v.wait_ge(co_ok, 4 * c + 1)
                        if l == 0:
                            v.tensor_scalar(cf[u][:, 0, :], at[:], 1.0 / 8.0, None, ALU.mult).then_inc(co_ok, 1)
                            v.tensor_scalar(cf[u][:, 1, :], at[:], 32.0 ** -0.5, None, ALU.mult).then_inc(co_ok, 1)
                        else:
                            v.tensor_tensor(cf[u][:, 2, :], at[:], xr[r][:, :, D], ALU.mult).then_inc(co_ok, 1)
                            v.tensor_scalar(cf[u][:, 1, :], xr[r][:, :, D], 32.0 ** -0.5, None, ALU.mult).then_inc(co_ok, 1)
                return f

            def skip_scalars(c, r, k, parts):
                u = r % 2
                v.wait_ge(k_ps, c + 1)
                v.wait_ge(co_ok, 4 * c + 4)
                v.wait_ge(y_ok, c)
                v.tensor_tensor(sk[:, :, 0:S0], pk[u][:, :, 0:S0], cf[u][:, 0, :].unsqueeze(2).to_broadcast([P, T, S0]), ALU.mult).then_inc(sk_ok, 1)

            def skip_vectors(c, r, k, parts):
                u = r % 2
                v.tensor_tensor(sk[:, :, S0:D], pk[u][:, :, S0:D], cf[u][:, 1, :].unsqueeze(2).to_broadcast([P, T, V3]), ALU.mult).then_inc(sk_ok, 1)

            def total(c, r, k, parts):
                u = r % 2
                v.wait_ge(sk_ok, 2 * c + 2)
                v.wait_ge(ag_ok, 2 * c + 2)
                v.wait_ge(xn_ok, due(T * (c - 1)))
                v.tensor_tensor(y[u][:], sk[:], ag[u][:], ALU.add).then_inc(y_ok, 1)

            def moments(c, r, k, parts):
                u = r % 2
                v.wait_ge(y_ok, c + 1)
                v.wait_ge(st_ok, 8 * c)
                for t in range(T):
                    v.bn_stats(st[:, t, :], y[u][:, t, :]).then_inc(st_ok, 1)

            def join(c, r, k, parts):
                v.wait_ge(st_ok, 8 * c + 4)
                v.wait_ge(ve_ok, 2 * c)
                fence(v)
                for t in range(T):
                    v.bn_aggr(mv[:, t, :], st[:, t, :]).then_inc(st_ok, 1)

            def variance(c, r, k, parts):
                u = r % 2
                v.wait_ge(st_ok, 8 * c + 8)
                v.wait_ge(rs_ok, 2 * c)
                v.tensor_scalar(ve[:], mv[:, :, 1], EPS, None, ALU.add).then_inc(ve_ok, 1)
                v.tensor_scalar(nm[u][:], mv[:, :, 0], -1.0, None, ALU.mult).then_inc(ve_ok, 1)

            if l == 0:
                node_pipeline(v, ((0, angle(0)), (2, skip_scalars), (0, angle(1)), (2, skip_vectors), (0, angle(2)), (1, factor(0)),
                                  (0, angle(3)), (2, total), (0, angle(4)), (1, factor(1)), (2, moments), (0, angle(5)), (0, angle(6)),
                                  (2, join), (0, angle(7)), (2, variance)))
            else:
                node_pipeline(v, ((1, factor(0)), (2, skip_scalars), (2, skip_vectors), (1, factor(1)), (2, total), (2, moments),
                                  (2, join), (2, variance)))

        @block.gpsimd
        def _(pool):
            def sums(c, r, k, parts):
                u = r % 2
                pool.wait_ge(co_ok, 4 * (c + 1))
                fence(pool)
                pool.wait_ge(y_ok, due(c - 1))
                fence(pool)
                pool.tensor_tensor(ag[u][:], ar[r][:, :, 0:D], cf[u][:, 2, :].unsqueeze(2).to_broadcast([P, T, D]), ALU.mult).then_inc(ag_ok, 1)
                pool.wait_ge(ag_ok, 2 * c + 1)
                fence(pool)
                pool.tensor_tensor(ag[u][:], ag[u][:], xr[r][:, :, 0:D], ALU.add).then_inc(ag_ok, 1)

            def attribute(c, r, k, parts):
                pool.wait_ge(stored[r], 16 * k)
                fence(pool)
                pool.tensor_copy(xn[r][:, :, D:XW], xr[r][:, :, D:XW]).then_inc(at_ok, 1)

            def deviation(c, r, k, parts):
                u = r % 2
                pool.wait_ge(xn_ok, due(T * (c - 1)))
                fence(pool)
                pool.wait_ge(ve_ok, 2 * c + 2)
                fence(pool)
                pool.tensor_tensor(rs[u][:], ve[:], wt("mhalf"), ALU.pow).then_inc(rs_ok, 1)
                pool.wait_ge(rs_ok, 2 * c + 1)
                fence(pool)
                pool.tensor_tensor(nr[u][:], nm[u][:], rs[u][:], ALU.mult).then_inc(rs_ok, 1)

            node_pipeline(pool, ((1, sums), (2, deviation), (1, attribute)))


def edge_phase_23(nc, l, x, agg, dram, wt):
    SO = 128 if l == 2 else 96
    OW = 32 + SO + V3
    W = AW[l]
    sides = ("src", "dst") if l == 2 else ("dst",)
    NS = len(sides)
    NY = NBP * T
    ROWS = (P, P, V3)
    with ExitStack() as ctx:
        sb = lambda n, s, d=F32: ctx.enter_context(nc.sbuf_tensor(f"{n}_{l}", s, d))
        ps = lambda n, s: ctx.enter_context(nc.psum_tensor(f"{n}_{l}", s, F32))
        sem = semaphores(nc, ctx, lambda n: f"{n}_{l}")
        gidx = [[sb(f"gidx{s}{r}", [P, T], U32) for r in range(R)] for s in range(NS)]
        esT = [sb(f"esT{r}", [64, B]) for r in range(R)]
        xg = [[sb(f"xg{s}{r}", [P, T, 192]) for r in range(R)] for s in range(NS)]
        y3 = sb("y3", [P, NY, 3])
        yq = sb("yq", [P, NY, 3])
        ye = sb("ye", [P, NY, 5])
        ysq = sb("ysq", [P, NY, 3])
        yn = sb("yn", [P, NY])
        yh = sb("yh", [P, NY])
        prod = sb("prod", [P, T, V3])
        ts = [sb(f"ts{u}", [P, 2 * NS, B]) for u in range(2)]
        hs = sb("hs", [64, B])
        ws = sb("ws", [P, 3, B])
        pr = [sb(f"pr{u}", [P, 3, B]) for u in range(2)]
        ob = [sb(f"ob{u}", [P, T, OW]) for u in range(2)]
        e5 = [sb(f"e5{u}", [P, T, V1, 5]) for u in range(2)]
        m1 = sb("m1", [P, T, V3])
        m2 = sb("m2", [P, T, V3])
        if l == 3:
            tidx = [sb(f"tidx{r}", [P, T], I32) for r in range(R)]
            trow = [sb(f"trow{r}", [P, B], I32) for r in range(R)]
            tf = sb("tf", [P, T])
            same = [sb(f"same{u}", [P, T, B]) for u in range(2)]
            product = sb("product", [P, T, B])
            cnt = sb("cnt", [P, T])
            away = sb("away", [P, T])
            cidx = [sb(f"cidx{r}", [P, T], U32) for r in range(R)]
            summed = [sb(f"summed{u}", [P, T, W]) for u in range(2)]
        else:
            sq = [sb(f"sq{s}", [P, T, V3]) for s in range(NS)]
            st = [sb(f"st{s}", [P, T, 6]) for s in range(NS)]
            mv = [[sb(f"mv{s}{u}", [P, T, 2]) for u in range(2)] for s in range(NS)]
            var = [[sb(f"var{s}{u}", [P, 2, T]) for u in range(2)] for s in range(NS)]
            rs = [[sb(f"rs{s}{u}", [P, 2, T]) for u in range(2)] for s in range(NS)]
            sl = sb("sl", [P, T, 64])
            sm = sb("sm", [P, T, 64])
            val = [sb(f"val{u}", [P, T, W]) for u in range(2)]

        pt = ps("pt", [P, 2, B])
        ph = ps("ph", [P, B])
        pf = ps("pf", [P, B])
        po = ps("po", [P, 2, 512])
        pc = ps("pc", [P, T, 256]) if l == 3 else None

        y_in = sem("y_in")
        y_ok = sem("y_ok")
        n_ok = sem("n_ok")
        loaded = [sem(f"loaded{r}") for r in range(R)]
        late = [sem(f"late{r}") for r in range(R)]
        gathered = [sem(f"gathered{r}") for r in range(R)]
        sq_ok = [sem(f"sq_ok{s}") for s in range(NS)]
        st_ok = [sem(f"st_ok{s}") for s in range(NS)]
        rs_ok = [sem(f"rs_ok{s}") for s in range(NS)]
        nrm = [sem(f"nrm{s}") for s in range(NS)]
        rows_v = sem("rows_v")
        turned = sem("turned")
        ts_ok = sem("ts_ok")
        h_ps = sem("h_ps")
        h_ok = sem("h_ok")
        w_ps = sem("w_ps")
        w_ok = sem("w_ok")
        f_ps = sem("f_ps")
        prod_ok = sem("prod_ok")
        o_ps = sem("o_ps")
        ob_ok = sem("ob_ok")
        msg_v = sem("msg_v")
        same_ok = sem("same_ok")
        idx_step = sem("idx_step")
        idx_ok = sem("idx_ok")
        c_ps = sem("c_ps")
        sum_ok = sem("sum_ok")
        added = sem("added")
        sl_ok = sem("sl_ok")
        val_ok = sem("val_ok")
        kept = [sem("kept0"), sem("kept1")]
        turn = sem("turn")
        MV = 6

        def fence(eng):
            eng.sem_inc(turn, 1)

        block = ctx.enter_context(nc.Block())

        @block.sync
        def _(sp):
            sp.dma_start(y3[:].rearrange("p n c -> p (n c)"), dram["ea3"]).then_inc(y_in, 16)

            def load(i, r, k, parts):
                sp.wait_ge(gathered[r], 16 * T * NS * k)
                fence(sp)
                for s, side in enumerate(sides):
                    sp.dma_start(gidx[s][r][:], dram[side + "_g"][bass.ds(i, 1)].rearrange("a p t -> (a p) t")).then_inc(loaded[r], 16)

            def load_late(i, r, k, parts):
                if l == 3:
                    sp.wait_ge(h_ps, due(i - 3))
                    fence(sp)
                    sp.wait_ge(idx_ok, due(i - 3))
                    fence(sp)
                    sp.dma_start(esT[r][:], dram["ea64T"][:, bass.ds(i * B, B)]).then_inc(late[r], 16)
                    sp.dma_start(tidx[r][:], dram["src_t"][bass.ds(i, 1)].rearrange("a p t -> (a p) t")).then_inc(late[r], 16)
                    sp.dma_start(trow[r][:], dram["src_r"][bass.ds(i, 1)].broadcast_to([P, B])).then_inc(late[r], 16)
                else:
                    sp.wait_ge(w_ps, due(3 * (i - 3)))
                    fence(sp)
                    sp.dma_start(esT[r][:], dram["hid"][:, bass.ds(i * B, B)]).then_inc(late[r], 16)

            def keep(i, r, k, parts):
                u = r % 2
                sp.wait_ge(val_ok, 4 * (i + 1))
                fence(sp)
                sp.dma_start(dram["val"][bass.ds(i, 1)].rearrange("a p t c -> (a p) t c"), val[u][:]).then_inc(kept[u], 16)
                sp.dma_start(dram["att"][bass.ds(i * B, B)].rearrange("(t p) h -> p t h", p=P), val[u][:, :, 160:168]).then_inc(kept[u], 16)

            if l == 3:
                edge_pipeline(sp, ((0, load), (4, load_late)))
            else:
                edge_pipeline(sp, ((0, load), (4, load_late), (8, keep)))
                for u in range(2):
                    sp.wait_ge(kept[u], 32 * (NB // 2))

        @block.gpsimd
        def _(pool):
            def gather(i, r, k, parts):
                pool.wait_ge(loaded[r], 16 * NS * (k + 1))
                fence(pool)
                pool.wait_ge(turned, due(2 * NS * (i - 3)))
                fence(pool)
                for s in range(NS):
                    for t in range(T):
                        pool.indirect_dma_start(xg[s][r][:, t, 0:XW], None, x, bass.IndirectOffsetOnAxis(ap=gidx[s][r][:, t:t + 1], axis=0)).then_inc(gathered[r], 16)

            def powers(s):
                def f(i, r, k, parts):
                    u = r % 2
                    pool.wait_ge(st_ok[s], 10 * (i + 1))
                    fence(pool)
                    pool.wait_ge(nrm[s], due(3 * (i - 1)))
                    fence(pool)
                    pool.tensor_tensor(rs[s][u][:], var[s][u][:], wt("mhalf8").rearrange("p (a t) -> p a t", a=2), ALU.pow).then_inc(rs_ok[s], 1)
                return f

            def add(i, r, k, parts):
                u = r % 2
                pool.wait_ge(idx_ok, i + 1)
                fence(pool)
                pool.wait_ge(added, 16 * T * i)
                fence(pool)
                pool.wait_ge(sum_ok, i + 1)
                fence(pool)
                for t in range(T):
                    pool.indirect_dma_start(agg, bass.IndirectOffsetOnAxis(ap=cidx[r][:, t:t + 1], axis=0), summed[u][:, t, :], None, compute_op=ALU.add).then_inc(added, 16)

            pool.wait_ge(y_ok, 3)
            pool.tensor_tensor(yn[:], yh[:], wt("mhalfn"), ALU.pow).then_inc(n_ok, 1)
            if l == 2:
                edge_pipeline(pool, ((0, gather), (1, powers(0)), (1, powers(1))))
            else:
                edge_pipeline(pool, ((0, gather), (7, add)))
                pool.wait_ge(added, 16 * T * NB)

        @block.vector
        def _(v):
            v.wait_ge(y_in, 16)
            v.tensor_tensor(ysq[:], y3[:], y3[:], ALU.mult).then_inc(y_ok, 1)
            v.wait_ge(y_ok, 1)
            v.tensor_reduce(yh[:], ysq[:], AX.X, ALU.add).then_inc(y_ok, 1)
            v.wait_ge(y_ok, 2)
            v.tensor_scalar(yh[:], yh[:], 1e-12 if l == 2 else 0.0, None, ALU.add).then_inc(y_ok, 1)
            v.wait_ge(n_ok, 1)
            v.tensor_tensor(y3[:], y3[:], yn[:].unsqueeze(2).to_broadcast([P, NY, 3]), ALU.mult).then_inc(y_ok, 1)
            v.wait_ge(y_ok, 4)
            v.tensor_scalar(yq[:], y3[:], 3.0 ** 0.5, None, ALU.mult).then_inc(y_ok, 1)
            v.tensor_scalar(ye[:, :, 0:3], y3[:], 1.5 ** 0.5, None, ALU.mult).then_inc(y_ok, 1)
            v.tensor_scalar(ye[:, :, 3:5], y3[:, :, 0:2], 1.5 ** 0.5, None, ALU.mult).then_inc(y_ok, 1)
            v.wait_ge(y_ok, 7)

            def at(y, n, lo, hi):
                return y[:, bass.ds(n * T, T), lo:hi].unsqueeze(2).to_broadcast([P, T, V1, hi - lo])

            def c3(a):
                return a.rearrange("p t (u c) -> p t u c", c=3)

            def moments(s):
                def f(i, r, k, parts):
                    u = r % 2
                    v.wait_ge(gathered[r], 16 * T * NS * (k + 1))
                    v.wait_ge(st_ok[s], 10 * i)
                    for t in range(T):
                        v.bn_stats(st[s][:, t, :], xg[s][r][:, t, 0:S0]).then_inc(st_ok[s], 1)
                    v.wait_ge(sq_ok[s], 2 * i + 1)
                    v.wait_ge(rs_ok[s], due(i - 1))
                    v.tensor_reduce(var[s][u][:, 1, :], sq[s][:], AX.X, ALU.add).then_inc(sq_ok[s], 1)
                    v.wait_ge(nrm[s], due(3 * (i - 1)))
                    v.wait_ge(st_ok[s], 10 * i + 4)
                    fence(v)
                    for t in range(T):
                        v.bn_aggr(mv[s][u][:, t, :], st[s][:, t, :]).then_inc(st_ok[s], 1)
                    v.wait_ge(sq_ok[s], 2 * i + 2)
                    v.tensor_scalar(var[s][u][:, 1, :], var[s][u][:, 1, :], 1.0 / V3, EPS, ALU.mult, ALU.add).then_inc(st_ok[s], 1)
                    v.wait_ge(st_ok[s], 10 * i + 9)
                    v.tensor_scalar(var[s][u][:, 0, :], mv[s][u][:, :, 1], EPS, None, ALU.add).then_inc(st_ok[s], 1)
                return f

            def normal(s):
                def f(i, r, k, parts):
                    u = r % 2
                    rows = xg[s][r]
                    v.tensor_tensor(rows[:, :, 0:S0], rows[:, :, 0:S0], mv[s][u][:, :, 0:1].to_broadcast([P, T, S0]), ALU.subtract).then_inc(nrm[s], 1)
                    v.wait_ge(rs_ok[s], i + 1)
                    v.tensor_tensor(rows[:, :, S0:D], rows[:, :, S0:D], rs[s][u][:, 1, :].unsqueeze(2).to_broadcast([P, T, V3]), ALU.mult).then_inc(nrm[s], 1)
                    v.wait_ge(nrm[s], 3 * i + 1)
                    v.tensor_tensor(rows[:, :, 0:S0], rows[:, :, 0:S0], rs[s][u][:, 0, :].unsqueeze(2).to_broadcast([P, T, S0]), ALU.mult).then_inc(nrm[s], 1)
                    v.wait_ge(nrm[s], 3 * i + 3)
                return f

            def dots(s):
                def f(i, r, k, parts):
                    rows = xg[s][r]
                    q = NS * i + s
                    if l == 3:
                        v.wait_ge(gathered[r], 16 * T * NS * (k + 1))
                    v.wait_ge(rows_v, 2 * q)
                    v.tensor_tensor(c3(prod[:]), c3(rows[:, :, S0:D]), at(y3, i, 0, 3), ALU.mult).then_inc(rows_v, 1)
                    v.wait_ge(rows_v, 2 * q + 1)
                    v.tensor_reduce(rows[:, :, D:D + V1], c3(prod[:]), AX.X, ALU.add).then_inc(rows_v, 1)
                return f

            def targets(i, r, k, parts):
                u = r % 2
                v.wait_ge(late[r], 48 * (k + 1))
                v.wait_ge(idx_ok, i)
                v.tensor_copy(tf[:], tidx[r][:]).then_inc(idx_step, 1)
                v.wait_ge(c_ps, due(i - 1))
                v.wait_ge(idx_step, i * 7 + 1)
                for t in range(T):
                    v.tensor_scalar(same[u][:, t, :], trow[r][:], tf[:, t:t + 1], None, ALU.is_equal).then_inc(same_ok, 1)
                for t in range(T):
                    m = (t + 1) * P
                    v.scalar_tensor_tensor(product[:, t, 0:m], trow[r][:, 0:m], tf[:, t:t + 1], wt("before")[:, t * B:t * B + m],
                                           ALU.is_equal, ALU.mult, accum_out=cnt[:, t:t + 1]).then_inc(idx_step, 1)
                v.tensor_tensor(away[:], wt("spare"), tf[:], ALU.subtract).then_inc(idx_step, 1)
                v.wait_ge(idx_step, i * 7 + 6)
                v.scalar_tensor_tensor(cnt[:], cnt[:], 1.0, away[:], ALU.min, ALU.mult).then_inc(idx_step, 1)
                v.wait_ge(idx_step, i * 7 + 7)
                v.wait_ge(same_ok, T * (i + 1))
                v.wait_ge(added, due(16 * T * (i - 3)))
                v.tensor_tensor(cidx[r][:], cnt[:], tf[:], ALU.add).then_inc(idx_ok, 1)

            def weigh(g):
                def f(i, r, k, parts):
                    u = r % 2
                    if g == 0:
                        v.wait_ge(o_ps, due(T * (i - 1)))
                    v.wait_ge(w_ok, 3 * i + g + 1)
                    v.wait_ge(f_ps, 2 * i + min(g, 1) + 1)
                    n = ROWS[g]
                    if g == 0 and l == 2:
                        v.scalar_tensor_tensor(pr[u][0:n, g, :], pf[0:n], wt("mb2"), ws[0:n, g, :], ALU.add, ALU.mult).then_inc(prod_ok, 1)
                    else:
                        v.tensor_tensor(pr[u][0:n, g, :], pf[0:n], ws[0:n, g, :], ALU.mult).then_inc(prod_ok, 1)
                return f

            def messages(i, r, k, parts):
                u = r % 2
                o, e = ob[u], e5[u]
                vec = o[:, :, 32 + SO:OW]
                v.wait_ge(ob_ok, 3 * T * (i + 1))
                v.wait_ge(msg_v, MV * i)
                if l == 2:
                    v.wait_ge(val_ok, 4 * i)
                v.tensor_tensor(c3(m1[:]), e[:, :, :, 1:4], at(ye, i, 2, 5), ALU.mult).then_inc(msg_v, 1)
                v.tensor_tensor(c3(m2[:]), e[:, :, :, 2:5], at(ye, i, 1, 4), ALU.mult).then_inc(msg_v, 1)
                v.wait_ge(msg_v, MV * i + 2)
                v.tensor_tensor(m1[:], m1[:], m2[:], ALU.subtract).then_inc(msg_v, 1)
                v.wait_ge(msg_v, MV * i + 3)
                v.tensor_tensor(c3(m2[:]), o[:, :, 0:32].unsqueeze(3).to_broadcast([P, T, V1, 3]), at(yq, i, 0, 3), ALU.mult).then_inc(msg_v, 1)
                v.tensor_tensor(vec, vec, m1[:], ALU.add).then_inc(msg_v, 1)
                if l == 2:
                    v.wait_ge(kept[u], 32 * (2 * k + r // 2))
                    v.tensor_copy(val[u][:, :, 0:64], o[:, :, 96:160]).then_inc(val_ok, 1)
                    v.wait_ge(sl_ok, i + 1)
                    v.scalar_tensor_tensor(sm[:], o[:, :, 32:96], 0.25, sl[:], ALU.mult, ALU.add).then_inc(msg_v, 1)
                    v.wait_ge(msg_v, MV * i + 6)
                    v.tensor_tensor(val[u][:, :, 64:160], vec, m2[:], ALU.add).then_inc(val_ok, 1)
                    v.tensor_tensor(sm[:], sm[:], wt("adot").unsqueeze(1).to_broadcast([P, T, 64]), ALU.mult).then_inc(val_ok, 1)
                    v.wait_ge(val_ok, 4 * i + 3)
                    v.tensor_reduce(val[u][:, :, 160:168], sm[:].rearrange("p t (h k) -> p t h k", k=8), AX.X, ALU.add).then_inc(val_ok, 1)
                else:
                    v.wait_ge(msg_v, MV * i + 5)
                    v.tensor_tensor(vec, vec, m2[:], ALU.add).then_inc(msg_v, 1)

            if l == 2:
                edge_pipeline(v, ((6, messages), (4, weigh(0)), (1, moments(0)), (4, weigh(1)), (2, normal(0)), (2, dots(0)),
                                  (4, weigh(2)), (1, moments(1)), (2, normal(1)), (2, dots(1))))
            else:
                edge_pipeline(v, ((6, messages), (4, weigh(0)), (5, targets), (4, weigh(1)), (2, dots(0)), (4, weigh(2))))

        @block.scalar
        def _(a):
            def squares(s):
                def f(i, r, k, parts):
                    a.wait_ge(gathered[r], 16 * T * NS * (k + 1))
                    a.wait_ge(sq_ok[s], 2 * i)
                    a.activation(sq[s][:], xg[s][r][:, :, S0:D], ACT.Square).then_inc(sq_ok[s], 1)
                return f

            def copies(i, r, k, parts):
                u = r % 2
                a.wait_ge(f_ps, due(2 * (i - 1)))
                for s in range(NS):
                    for g in range(2):
                        a.wait_ge(turned, 2 * (NS * i + s) + g + 1)
                        n = (S0, P)[g]
                        if l == 3:
                            a.activation(ts[u][0:n, 2 * s + g, :], pt[0:n, g, :], ACT.Copy).then_inc(ts_ok, 1)
                        elif g == 0:
                            a.activation(ts[u][0:n, 2 * s + g, :], pt[0:n, g, :], ACT.Identity, scale=wt("ln1w"), bias=wt("ln1b")).then_inc(ts_ok, 1)
                        else:
                            a.activation(ts[u][0:n, 2 * s + g, :], pt[0:n, g, :], ACT.Copy, scale=wt("ln1v")).then_inc(ts_ok, 1)

            def hidden(i, r, k, parts):
                a.wait_ge(h_ps, i + 1)
                a.wait_ge(w_ps, 3 * i)
                a.activation(hs[:], ph[0:64, :], ACT.Relu).then_inc(h_ok, 1)

            def weights(g):
                def f(i, r, k, parts):
                    n = ROWS[g]
                    a.wait_ge(w_ps, 3 * i + g + 1)
                    a.wait_ge(prod_ok, 3 * i)
                    if l == 3:
                        a.activation(ws[0:n, g, :], ph[0:n], ACT.Copy).then_inc(w_ok, 1)
                    else:
                        a.activation(ws[0:n, g, :], ph[0:n], ACT.Identity, bias=wt(f"roff{g}")).then_inc(w_ok, 1)
                return f

            def outputs(*tiles):
                def f(i, r, k, parts):
                    u = r % 2
                    if tiles[0] == 0:
                        if l == 2:
                            a.wait_ge(val_ok, due(4 * (i - 1)))
                        else:
                            a.wait_ge(c_ps, due(i - 1))
                    for t in tiles:
                        a.wait_ge(o_ps, T * i + t + 1)
                        a.activation(ob[u][:, t, :], po[:, t % 2, 0:OW], ACT.Copy).then_inc(ob_ok, 1)
                        e = po[:, t % 2, OW:OW + V3].rearrange("p (u c) -> p u c", c=3)
                        a.activation(e5[u][:, t, :, 0:3], e, ACT.Copy).then_inc(ob_ok, 1)
                        a.activation(e5[u][:, t, :, 3:5], e[:, :, 0:2], ACT.Copy).then_inc(ob_ok, 1)
                return f

            def silu(i, r, k, parts):
                a.wait_ge(ob_ok, 3 * T * (i + 1))
                a.wait_ge(val_ok, 4 * i)
                a.activation(sl[:], ob[r % 2][:, :, 32:96], ACT.Silu).then_inc(sl_ok, 1)

            def sums(i, r, k, parts):
                a.wait_ge(added, due(16 * T * (i - 1)))
                a.wait_ge(c_ps, i + 1)
                a.activation(summed[r % 2][:], pc[:, :, 0:W], ACT.Copy).then_inc(sum_ok, 1)

            if l == 2:
                edge_pipeline(a, ((1, squares(0)), (4, weights(0)), (5, outputs(0, 1)), (4, weights(1)), (1, squares(1)), (5, outputs(2, 3)),
                                  (4, weights(2)), (5, silu), (3, copies)))
            else:
                edge_pipeline(a, ((4, weights(0)), (5, outputs(0, 1)), (4, weights(1)), (5, outputs(2, 3)), (4, weights(2)), (3, hidden),
                                  (6, sums), (3, copies)))

        @block.tensor
        def _(pe):
            def turn_rows(i, r, k, parts):
                for s in range(NS):
                    q = NS * i + s
                    pe.wait_ge(rows_v, 2 * (q + 1))
                    pe.wait_ge(ts_ok, 2 * q)
                    fence(pe)
                    for t in range(T):
                        last = pe.transpose(pt[0:S0, 0, t * P:(t + 1) * P], xg[s][r][:, t, 0:S0], wt("ident"))
                    last.then_inc(turned, 1)
                    for t in range(T):
                        last = pe.transpose(pt[:, 1, t * P:(t + 1) * P], xg[s][r][:, t, S0:192], wt("ident"))
                    last.then_inc(turned, 1)

            def hidden(i, r, k, parts):
                pe.wait_ge(late[r], 48 * (k + 1))
                pe.wait_ge(w_ok, 3 * i)
                fence(pe)
                pe.matmul(ph[0:64, :], wt("h3"), esT[r][:], start=True, stop=True).then_inc(h_ps, 1)

            def transformed(g):
                def f(i, r, k, parts):
                    pe.wait_ge(ts_ok, 2 * NS * (i + 1))
                    pe.wait_ge(prod_ok, 3 * i + g)
                    n = (S0, P)[g]
                    for s in range(NS):
                        last = pe.matmul(pf[:], wt(f"f{g + 1}_{l}{s}"), ts[r % 2][0:n, 2 * s + g, :], start=(s == 0), stop=(s == NS - 1))
                    last.then_inc(f_ps, 1)
                return f

            def weights(g):
                def f(i, r, k, parts):
                    if l == 3:
                        pe.wait_ge(h_ok, i + 1)
                    else:
                        pe.wait_ge(late[r], 16 * (k + 1))
                    pe.wait_ge(w_ok, 3 * i + g)
                    pe.matmul(ph[0:ROWS[g]], wt(f"w{g + 1}_{l}"), (hs if l == 3 else esT[r])[:], start=True, stop=True).then_inc(w_ps, 1)
                return f

            def outputs(*tiles):
                def f(i, r, k, parts):
                    u = r % 2
                    pe.wait_ge(prod_ok, 3 * i + 3)
                    for t in tiles:
                        pe.wait_ge(ob_ok, due(3 * (T * i + t - 1)))
                        cut = slice(t * P, (t + 1) * P)
                        pe.matmul(po[:, t % 2, 0:OW], pr[u][:, 0, cut], wt(f"o1_{l}"), start=True, stop=False)
                        if l == 2:
                            pe.matmul(po[:, t % 2, 32:OW], wt("one"), wt("linb"), start=False, stop=False)
                        pe.matmul(po[:, t % 2, 32:OW], pr[u][:, 1, cut], wt(f"o2_{l}"), start=False, stop=True)
                        pe.matmul(po[:, t % 2, OW:OW + V3], pr[u][0:V3, 2, cut], wt(f"o3_{l}"), start=True, stop=True).then_inc(o_ps, 1)
                return f

            def sums(i, r, k, parts):
                u = r % 2
                pe.wait_ge(msg_v, MV * (i + 1))
                pe.wait_ge(same_ok, T * (i + 1))
                pe.wait_ge(sum_ok, i)
                for t in range(T):
                    for s in range(T):
                        last = pe.matmul(pc[:, t, 0:W], same[u][:, s, t * P:(t + 1) * P], ob[u][:, s, 32:OW], start=(s == 0), stop=(s == T - 1))
                last.then_inc(c_ps, 1)

            first = ((4, weights(0)), (4, transformed(0)), (5, outputs(0, 1)), (4, weights(1)), (4, transformed(1)), (5, outputs(2, 3)), (4, weights(2)))
            if l == 2:
                edge_pipeline(pe, first + ((3, turn_rows),))
            else:
                edge_pipeline(pe, first + ((3, hidden), (6, sums), (3, turn_rows)))


def hidden_phase(nc, dram, wt):
    with ExitStack() as ctx:
        sb = lambda n, s, d=F32: ctx.enter_context(nc.sbuf_tensor(f"{n}_h", s, d))
        ps = lambda n, s: ctx.enter_context(nc.psum_tensor(f"{n}_h", s, F32))
        sem = semaphores(nc, ctx, lambda n: f"{n}_h")
        each = lambda count, f, n, *a: [f(f"{n}{q}", *a) for q in range(count)]
        esT = each(R, sb, "esT", [64, B])
        lin = [each(R, sb, f"lin{y}", [P, T, 64]) for y in range(2)]
        st = [each(2, sb, f"st{y}", [P, T, 6]) for y in range(2)]
        mv = [each(2, sb, f"mv{y}", [P, T, 2]) for y in range(2)]
        ve = [each(2, sb, f"ve{y}", [P, T]) for y in range(2)]
        rs = [each(2, sb, f"rs{y}", [P, T]) for y in range(2)]
        hid = [each(2, sb, f"hid{y}", [64, B]) for y in range(2)]
        pl = each(2, ps, "pl", [P, T, 64])
        pt = each(2, ps, "pt", [64, B])
        loaded = each(R, sem, "loaded")
        lin_ps = each(2, sem, "lin_ps")
        lin_ok = each(2, sem, "lin_ok")
        st_ok = each(2, sem, "st_ok")
        rs_ok = each(2, sem, "rs_ok")
        centred = each(2, sem, "centred")
        nrm = each(2, sem, "nrm")
        turned = each(2, sem, "turned")
        hid_ok = each(2, sem, "hid_ok")
        kept = each(2, sem, "kept")
        turn = sem("turn")

        def fence(eng):
            eng.sem_inc(turn, 1)

        block = ctx.enter_context(nc.Block())

        @block.sync
        def _(sp):
            def load(i, r, k, parts):
                sp.wait_ge(lin_ps[0], due(i - 3))
                fence(sp)
                sp.dma_start(esT[r][:], dram["ea64T"][:, bass.ds(i * B, B)]).then_inc(loaded[r], 16)

            def keep(i, r, k, parts):
                u = r % 2
                sp.wait_ge(hid_ok[1], i + 1)
                fence(sp)
                sp.dma_start(dram["hid"][:, bass.ds(i * B, B)], hid[1][u][:]).then_inc(kept[u], 16)

            edge_pipeline(sp, ((0, load), (10, keep)))
            for u in range(2):
                sp.wait_ge(kept[u], 16 * (NB // 2))

        @block.tensor
        def _(pe):
            def linear(y):
                def f(i, r, k, parts):
                    pe.wait_ge(lin_ok[y], i)
                    if y == 0:
                        pe.wait_ge(loaded[r], 16 * (k + 1))
                    else:
                        pe.wait_ge(hid_ok[0], i + 1)
                    fence(pe)
                    src = hid[0][r % 2] if y else esT[r]
                    for t in range(T):
                        pe.matmul(pl[y][:, t, :], wt("one"), wt(f"rb{y}"), start=True, stop=False)
                        last = pe.matmul(pl[y][:, t, :], src[:, t * P:(t + 1) * P], wt(f"rw{y}"), start=False, stop=True)
                    last.then_inc(lin_ps[y], 1)
                return f

            def turn_rows(y):
                def f(i, r, k, parts):
                    pe.wait_ge(nrm[y], i + 1)
                    pe.wait_ge(hid_ok[y], i)
                    fence(pe)
                    for t in range(T):
                        last = pe.transpose(pt[y][:, t * P:(t + 1) * P], lin[y][r][:, t, :], wt("ident"))
                    last.then_inc(turned[y], 1)
                return f

            edge_pipeline(pe, ((4, linear(1)), (0, linear(0)), (3, turn_rows(0)), (7, turn_rows(1))))

        @block.scalar
        def _(a):
            def copied(y):
                def f(i, r, k, parts):
                    a.wait_ge(lin_ps[y], i + 1)
                    a.wait_ge(turned[y], due(i - 3))
                    a.activation(lin[y][r][:], pl[y][:], ACT.Copy).then_inc(lin_ok[y], 1)
                return f

            def silu(y):
                def f(i, r, k, parts):
                    u = r % 2
                    a.wait_ge(turned[y], i + 1)
                    if y == 0:
                        a.wait_ge(lin_ps[1], due(i - 1))
                    else:
                        a.wait_ge(kept[u], 16 * (2 * k + r // 2))
                    a.activation(hid[y][u][:], pt[y][:], ACT.Silu, scale=wt(f"rg{y}"), bias=wt(f"rbe{y}")).then_inc(hid_ok[y], 1)
                return f

            edge_pipeline(a, ((4, copied(1)), (0, copied(0)), (3, silu(0)), (7, silu(1))))

        @block.vector
        def _(v):
            def moments(y):
                def f(i, r, k, parts):
                    u = r % 2
                    v.wait_ge(lin_ok[y], i + 1)
                    v.wait_ge(st_ok[y], 9 * i)
                    for t in range(T):
                        v.bn_stats(st[y][u][:, t, :], lin[y][r][:, t, :]).then_inc(st_ok[y], 1)
                return f

            def centre(y):
                def f(i, r, k, parts):
                    u = r % 2
                    v.wait_ge(st_ok[y], 9 * i + 4)
                    fence(v)
                    for t in range(T):
                        v.bn_aggr(mv[y][u][:, t, :], st[y][u][:, t, :]).then_inc(st_ok[y], 1)
                    v.wait_ge(st_ok[y], 9 * i + 8)
                    v.wait_ge(rs_ok[y], due(i - 1))
                    v.tensor_scalar(ve[y][u][:], mv[y][u][:, :, 1], EPS, None, ALU.add).then_inc(st_ok[y], 1)
                    v.tensor_tensor(lin[y][r][:], lin[y][r][:], mv[y][u][:, :, 0:1].to_broadcast([P, T, 64]), ALU.subtract).then_inc(centred[y], 1)
                return f

            def scaled(y):
                def f(i, r, k, parts):
                    v.wait_ge(rs_ok[y], i + 1)
                    v.wait_ge(centred[y], i + 1)
                    v.tensor_tensor(lin[y][r][:], lin[y][r][:], rs[y][r % 2][:].unsqueeze(2).to_broadcast([P, T, 64]), ALU.mult).then_inc(nrm[y], 1)
                return f

            edge_pipeline(v, ((2, scaled(0)), (6, scaled(1)), (1, moments(0)), (5, moments(1)), (1, centre(0)), (5, centre(1))))

        @block.gpsimd
        def _(pool):
            def powers(y):
                def f(i, r, k, parts):
                    u = r % 2
                    pool.wait_ge(nrm[y], due(i - 1))
                    fence(pool)
                    pool.wait_ge(st_ok[y], 9 * (i + 1))
                    fence(pool)
                    pool.tensor_tensor(rs[y][u][:], ve[y][u][:], wt("mhalf"), ALU.pow).then_inc(rs_ok[y], 1)
                return f

            edge_pipeline(pool, ((1, powers(0)), (5, powers(1))))


def attention_max_phase(nc, dram, mx, wt):
    H = 8
    with ExitStack() as ctx:
        sb = lambda n, s, d=F32: ctx.enter_context(nc.sbuf_tensor(f"{n}_m", s, d))
        ps = lambda n, s: ctx.enter_context(nc.psum_tensor(f"{n}_m", s, F32))
        sem = semaphores(nc, ctx, lambda n: f"{n}_m")
        tidx = [sb(f"tidx{r}", [P, T], I32) for r in range(R)]
        gidx = [sb(f"gidx{r}", [P, T], I32) for r in range(R)]
        cidx = [sb(f"cidx{r}", [P, T], U32) for r in range(R)]
        trow = [sb(f"trow{r}", [P, B], I32) for r in range(R)]
        arow = [sb(f"arow{r}", [P, B * H]) for r in range(R)]
        least = sb("least", [P, NA // P * H])
        other = sb("other", [P, NA // P * H])
        tf = sb("tf", [P, T])
        same = [sb(f"same{u}", [P, T, B]) for u in range(2)]
        apart = sb("apart", [P, T, P])
        masked = sb("masked", [P, T, H, P])
        product = sb("product", [P, T, P])
        cnt = sb("cnt", [P, T])
        first = sb("first", [P, T])
        top = sb("top", [P, T, H])
        rep = [sb(f"rep{u}", [P, T, H + 1]) for u in range(2)]
        bl = sb("bl", [P, T * T, H + 1])
        gone = sb("gone", [P, T * T])
        blk = [sb(f"blk{r}", [P, T, H]) for r in range(R)]
        old = [sb(f"old{u}", [P, T, H]) for u in range(2)]
        new = [sb(f"new{u}", [P, T, H]) for u in range(2)]
        pm = ps("pm", [P, T * T, H + 1])
        l_set = sem("l_set")
        l_out = sem("l_out")
        loaded = [sem(f"loaded{r}") for r in range(R)]
        late = [sem(f"late{r}") for r in range(R)]
        tf_ok = sem("tf_ok")
        same_ok = sem("same_ok")
        ap_ok = sem("ap_ok")
        mk_v = sem("mk_v")
        mk_p = sem("mk_p")
        top_ok = sem("top_ok")
        rep_ok = sem("rep_ok")
        m_ps = sem("m_ps")
        blk_ok = sem("blk_ok")
        old_in = [sem(f"old_in{u}") for u in range(2)]
        new_ok = sem("new_ok")
        sent = [sem(f"sent{u}") for u in range(2)]
        both_in = sem("both_in")
        both_ok = sem("both_ok")
        both_out = sem("both_out")
        turn = sem("turn")

        def fence(eng):
            eng.sem_inc(turn, 1)

        block = ctx.enter_context(nc.Block())

        @block.sync
        def _(sp):
            sp.wait_ge(l_set, 1)
            flat = [mx[u].rearrange("(p r) c -> p (r c)", p=P) for u in range(2)]
            for u in range(2):
                sp.dma_start(flat[u], least[:]).then_inc(l_out, 16)

            def load(i, r, k, parts):
                sp.wait_ge(rep_ok, due(2 * (i - 3)))
                fence(sp)
                sp.dma_start(tidx[r][:], dram["dst_t"][bass.ds(i, 1)].rearrange("a p t -> (a p) t")).then_inc(loaded[r], 16)
                sp.dma_start(trow[r][:], dram["dst_r"][bass.ds(i, 1)].broadcast_to([P, B])).then_inc(loaded[r], 16)
                sp.dma_start(arow[r][:], dram["att"][bass.ds(i * B, B)].rearrange("(a e) h -> a (e h)", a=1).broadcast_to([P, B * H])).then_inc(loaded[r], 16)

            def load_late(i, r, k, parts):
                sp.wait_ge(sent[r % 2], due(16 * T * (2 * k + r // 2 - 1)))
                fence(sp)
                sp.dma_start(gidx[r][:], dram["dst_t"][bass.ds(i, 1)].rearrange("a p t -> (a p) t")).then_inc(late[r], 16)
                sp.dma_start(cidx[r][:], dram["cidx"][bass.ds(i, 1)].rearrange("a p t -> (a p) t")).then_inc(late[r], 16)

            edge_pipeline(sp, ((0, load), (3, load_late)))
            sp.wait_ge(l_out, 32)
            for u in range(2):
                sp.wait_ge(sent[u], 16 * T * (NB // 2))
                sp.dma_start((least, other)[u][:], flat[u]).then_inc(both_in, 16)
            sp.wait_ge(both_ok, 1)
            sp.dma_start(flat[0], least[:]).then_inc(both_out, 16)
            sp.wait_ge(both_out, 16)

        @block.gpsimd
        def _(pool):
            pool.memset(least[:], -1e30).then_inc(l_set, 1)
            pool.wait_ge(l_out, 32)

            def fetch(i, r, k, parts):
                u = r % 2
                pool.wait_ge(late[r], 32 * (k + 1))
                fence(pool)
                pool.wait_ge(sent[u], 16 * T * (2 * k + r // 2))
                fence(pool)
                pool.wait_ge(new_ok, due(i - 1))
                fence(pool)
                for t in range(T):
                    pool.indirect_dma_start(old[u][:, t, :], None, mx[u], bass.IndirectOffsetOnAxis(ap=gidx[r][:, t:t + 1].bitcast(U32), axis=0)).then_inc(old_in[u], 16)

            def send(i, r, k, parts):
                u = r % 2
                pool.wait_ge(new_ok, i + 1)
                fence(pool)
                for t in range(T):
                    pool.indirect_dma_start(mx[u], bass.IndirectOffsetOnAxis(ap=cidx[r][:, t:t + 1], axis=0), new[u][:, t, :], None).then_inc(sent[u], 16)

            def mask(t):
                def f(i, r, k, parts):
                    pool.wait_ge(ap_ok, 9 * i + T)
                    fence(pool)
                    pool.wait_ge(top_ok, T * i)
                    fence(pool)
                    pool.tensor_tensor(masked[:, t], arow[r][:, t * P * H:(t + 1) * P * H].rearrange("p (e h) -> p h e", h=H),
                                       apart[:, t, :].unsqueeze(1).to_broadcast([P, H, P]), ALU.add).then_inc(mk_p, 1)
                return f

            edge_pipeline(pool, ((0, mask(3)), (4, send), (3, fetch)))
            for u in range(2):
                pool.wait_ge(sent[u], 16 * T * (NB // 2))

        @block.vector
        def _(v):
            def targets(i, r, k, parts):
                u = r % 2
                v.wait_ge(loaded[r], 48 * (k + 1))
                v.wait_ge(ap_ok, 9 * i)
                v.wait_ge(same_ok, T * i)
                v.tensor_copy(tf[:], tidx[r][:]).then_inc(tf_ok, 1)
                v.wait_ge(tf_ok, i + 1)
                v.wait_ge(mk_p, i)
                v.wait_ge(mk_v, 3 * i)
                for t in range(T):
                    v.tensor_scalar(apart[:, t, :], trow[r][:, t * P:(t + 1) * P], tf[:, t:t + 1], -1e30, ALU.not_equal, ALU.mult).then_inc(ap_ok, 1)
                for t in range(T):
                    v.scalar_tensor_tensor(product[:, t, :], trow[r][:, t * P:(t + 1) * P], tf[:, t:t + 1], wt("before")[:, 0:P],
                                           ALU.is_equal, ALU.mult, accum_out=cnt[:, t:t + 1]).then_inc(ap_ok, 1)
                v.wait_ge(m_ps, due(i - 1))
                for t in range(T):
                    v.tensor_scalar(same[u][:, t, :], trow[r][:], tf[:, t:t + 1], None, ALU.is_equal).then_inc(same_ok, 1)
                v.wait_ge(ap_ok, 9 * i + 8)
                v.wait_ge(rep_ok, 2 * i)
                v.tensor_scalar(first[:], cnt[:], 0.0, None, ALU.is_equal).then_inc(ap_ok, 1)

            def mask(t):
                def f(i, r, k, parts):
                    v.wait_ge(top_ok, T * i)
                    v.tensor_tensor(masked[:, t], arow[r][:, t * P * H:(t + 1) * P * H].rearrange("p (e h) -> p h e", h=H),
                                    apart[:, t, :].unsqueeze(1).to_broadcast([P, H, P]), ALU.add).then_inc(mk_v, 1)
                return f

            def largest(t):
                def f(i, r, k, parts):
                    if t < 3:
                        v.wait_ge(mk_v, 3 * i + t + 1)
                    else:
                        v.wait_ge(mk_p, i + 1)
                    if t == 0:
                        v.wait_ge(rep_ok, 2 * i)
                    v.tensor_reduce(top[:, t, :], masked[:, t], AX.X, ALU.max).then_inc(top_ok, 1)
                return f

            def represent(i, r, k, parts):
                u = r % 2
                v.wait_ge(ap_ok, 9 * i + 9)
                v.wait_ge(top_ok, T * (i + 1))
                v.wait_ge(m_ps, due(i - 1))
                v.tensor_tensor(rep[u][:, :, 0:H], top[:], first[:].unsqueeze(2).to_broadcast([P, T, H]), ALU.mult).then_inc(rep_ok, 1)
                v.tensor_copy(rep[u][:, :, H], first[:]).then_inc(rep_ok, 1)

            def over_block(i, r, k, parts):
                v.wait_ge(m_ps, i + 1)
                v.wait_ge(blk_ok, 4 * i)
                v.tensor_copy(bl[:], pm[:]).then_inc(blk_ok, 1)
                v.wait_ge(blk_ok, 4 * i + 1)
                v.tensor_scalar(gone[:], bl[:, :, H], -1.0, 1e30, ALU.add, ALU.mult).then_inc(blk_ok, 1)
                v.wait_ge(blk_ok, 4 * i + 2)
                v.tensor_tensor(bl[:, :, 0:H], bl[:, :, 0:H], gone[:].unsqueeze(2).to_broadcast([P, T * T, H]), ALU.add).then_inc(blk_ok, 1)
                v.wait_ge(blk_ok, 4 * i + 3)
                v.wait_ge(new_ok, due(i - 3))
                v.tensor_reduce(blk[r][:], bl[:, :, 0:H].rearrange("p (t s) h -> p t h s", s=T), AX.X, ALU.max).then_inc(blk_ok, 1)

            def with_table(i, r, k, parts):
                u = r % 2
                v.wait_ge(old_in[u], 16 * T * (2 * k + r // 2 + 1))
                v.wait_ge(blk_ok, 4 * i + 4)
                v.wait_ge(sent[u], 16 * T * (2 * k + r // 2))
                v.tensor_tensor(new[u][:], blk[r][:], old[u][:], ALU.max).then_inc(new_ok, 1)

            edge_pipeline(v, ((2, over_block), (0, targets), (0, mask(0)), (0, mask(1)), (0, mask(2)), (4, with_table), (0, largest(0)), (0, largest(1)),
                              (0, largest(2)), (0, largest(3)), (0, represent)))
            v.wait_ge(both_in, 32)
            v.tensor_tensor(least[:], least[:], other[:], ALU.max).then_inc(both_ok, 1)

        @block.tensor
        def _(pe):
            def spread(i, r, k, parts):
                u = r % 2
                pe.wait_ge(rep_ok, 2 * (i + 1))
                pe.wait_ge(same_ok, T * (i + 1))
                pe.wait_ge(blk_ok, 4 * i)
                for t in range(T):
                    for s in range(T):
                        last = pe.matmul(pm[:, T * t + s, :], same[u][:, s, t * P:(t + 1) * P], rep[u][:, s, :], start=True, stop=True)
                last.then_inc(m_ps, 1)

            edge_pipeline(pe, ((1, spread),))


def attention_sum_phase(nc, dram, mx, agg, wt):
    H = 8
    W = AW[2]
    with ExitStack() as ctx:
        sb = lambda n, s, d=F32: ctx.enter_context(nc.sbuf_tensor(f"{n}_a", s, d))
        ps = lambda n, s: ctx.enter_context(nc.psum_tensor(f"{n}_a", s, F32))
        sem = semaphores(nc, ctx, lambda n: f"{n}_a")
        tidx = [sb(f"tidx{r}", [P, T], I32) for r in range(R)]
        cidx = [sb(f"cidx{r}", [P, T], U32) for r in range(R)]
        trow = [sb(f"trow{r}", [P, B], I32) for r in range(R)]
        val = [sb(f"val{r}", [P, T, W]) for r in range(R)]
        big = [sb(f"big{r}", [P, T, H]) for r in range(R)]
        tf = [sb(f"tf{u}", [P, T]) for u in range(2)]
        same = [sb(f"same{u}", [P, T, B]) for u in range(2)]
        dif = [sb(f"dif{u}", [P, T, H]) for u in range(2)]
        msg = [sb(f"msg{u}", [P, T, W]) for u in range(2)]
        summed = [sb(f"summed{u}", [P, T, W]) for u in range(2)]
        pc = ps("pc", [P, T, 256])
        loaded = [sem(f"loaded{r}") for r in range(R)]
        late = [sem(f"late{r}") for r in range(R)]
        big_in = [sem(f"big_in{r}") for r in range(R)]
        tf_ok = sem("tf_ok")
        same_ok = sem("same_ok")
        dif_ok = sem("dif_ok")
        ex_ok = sem("ex_ok")
        msg_ok = sem("msg_ok")
        c_ps = sem("c_ps")
        sum_ok = sem("sum_ok")
        added = sem("added")
        turn = sem("turn")

        def fence(eng):
            eng.sem_inc(turn, 1)

        block = ctx.enter_context(nc.Block())

        @block.sync
        def _(sp):
            def load(i, r, k, parts):
                sp.wait_ge(msg_ok, due(2 * (i - 3)))
                fence(sp)
                sp.dma_start(tidx[r][:], dram["dst_t"][bass.ds(i, 1)].rearrange("a p t -> (a p) t")).then_inc(loaded[r], 16)
                sp.dma_start(trow[r][:], dram["dst_r"][bass.ds(i, 1)].broadcast_to([P, B])).then_inc(loaded[r], 16)
                sp.dma_start(val[r][:], dram["val"][bass.ds(i, 1)].rearrange("a p t c -> (a p) t c")).then_inc(loaded[r], 16)

            def load_late(i, r, k, parts):
                sp.wait_ge(added, due(16 * T * (i - 3)))
                fence(sp)
                sp.dma_start(cidx[r][:], dram["cidx"][bass.ds(i, 1)].rearrange("a p t -> (a p) t")).then_inc(late[r], 16)

            edge_pipeline(sp, ((0, load), (3, load_late)))

        @block.gpsimd
        def _(pool):
            def gather(i, r, k, parts):
                pool.wait_ge(loaded[r], 48 * (k + 1))
                fence(pool)
                pool.wait_ge(dif_ok, due(i - 3))
                fence(pool)
                for t in range(T):
                    pool.indirect_dma_start(big[r][:, t, :], None, mx, bass.IndirectOffsetOnAxis(ap=tidx[r][:, t:t + 1].bitcast(U32), axis=0)).then_inc(big_in[r], 16)

            def add(i, r, k, parts):
                pool.wait_ge(late[r], 16 * (k + 1))
                fence(pool)
                pool.wait_ge(added, 16 * T * i)
                fence(pool)
                pool.wait_ge(sum_ok, i + 1)
                fence(pool)
                for t in range(T):
                    pool.indirect_dma_start(agg, bass.IndirectOffsetOnAxis(ap=cidx[r][:, t:t + 1], axis=0), summed[r % 2][:, t, :], None, compute_op=ALU.add).then_inc(added, 16)

            edge_pipeline(pool, ((0, gather), (4, add)))
            pool.wait_ge(added, 16 * T * NB)

        @block.vector
        def _(v):
            def targets(i, r, k, parts):
                u = r % 2
                v.wait_ge(big_in[r], 16 * T * (k + 1))
                v.wait_ge(loaded[r], 48 * (k + 1))
                v.wait_ge(ex_ok, due(i - 1))
                v.tensor_tensor(dif[u][:], val[r][:, :, 160:168], big[r][:], ALU.subtract).then_inc(dif_ok, 1)
                v.wait_ge(same_ok, due(T * (i - 1)))
                v.tensor_copy(tf[u][:], tidx[r][:]).then_inc(tf_ok, 1)
                v.wait_ge(tf_ok, i + 1)
                v.wait_ge(c_ps, due(i - 1))
                for t in range(T):
                    v.tensor_scalar(same[u][:, t, :], trow[r][:], tf[u][:, t:t + 1], None, ALU.is_equal).then_inc(same_ok, 1)

            def weighted(i, r, k, parts):
                u = r % 2
                v.wait_ge(ex_ok, i + 1)
                for lo, hi in ((0, 64), (64, 160)):
                    v.tensor_tensor(msg[u][:, :, lo:hi].rearrange("p t (h k) -> p t h k", h=H), val[r][:, :, lo:hi].rearrange("p t (h k) -> p t h k", h=H),
                                    msg[u][:, :, 160:168].unsqueeze(3).to_broadcast([P, T, H, (hi - lo) // H]), ALU.mult).then_inc(msg_ok, 1)

            edge_pipeline(v, ((2, weighted), (1, targets)))

        @block.scalar
        def _(a):
            def weights(i, r, k, parts):
                u = r % 2
                a.wait_ge(dif_ok, i + 1)
                a.wait_ge(c_ps, due(i - 1))
                a.activation(msg[u][:, :, 160:168], dif[u][:], ACT.Exp, scale=0.8).then_inc(ex_ok, 1)

            def sums(i, r, k, parts):
                a.wait_ge(c_ps, i + 1)
                a.wait_ge(added, due(16 * T * (i - 1)))
                a.activation(summed[r % 2][:], pc[:, :, 0:W], ACT.Copy).then_inc(sum_ok, 1)

            edge_pipeline(a, ((3, sums), (1, weights)))

        @block.tensor
        def _(pe):
            def sums(i, r, k, parts):
                u = r % 2
                pe.wait_ge(msg_ok, 2 * (i + 1))
                pe.wait_ge(same_ok, T * (i + 1))
                pe.wait_ge(sum_ok, i)
                for t in range(T):
                    for s in range(T):
                        last = pe.matmul(pc[:, t, 0:W], same[u][:, s, t * P:(t + 1) * P], msg[u][:, s, :], start=(s == 0), stop=(s == T - 1))
                last.then_inc(c_ps, 1)

            edge_pipeline(pe, ((3, sums),))


def node_phase_3(nc, x, agg, out, wt):
    with ExitStack() as ctx:
        sb = lambda n, s, d=F32: ctx.enter_context(nc.sbuf_tensor(f"{n}_n3", s, d))
        ps = lambda n, s: ctx.enter_context(nc.psum_tensor(f"{n}_n3", s, F32))
        sem = semaphores(nc, ctx, lambda n: f"{n}_n3")
        xr = [sb(f"xr{r}", [P, T, XW]) for r in range(R)]
        ar = [sb(f"ar{r}", [P, T, 192]) for r in range(R)]
        tss = [sb(f"tss{u}", [64, B]) for u in range(2)]
        tsv = [sb(f"tsv{u}", [96, B]) for u in range(2)]
        so = [sb(f"so{u}", [P, T, 192]) for u in range(2)]
        gt = [sb(f"gt{u}", [P, T, V1]) for u in range(2)]
        sg = [sb(f"sg{u}", [P, T, D]) for u in range(2)]
        y = [sb(f"y{u}", [P, T, D]) for u in range(2)]
        st = sb("st", [P, T, 6])
        mv = sb("mv", [P, T, 2])
        ve = sb("ve", [P, T])
        nm = sb("nm", [P, T])
        rs = [sb(f"rs{u}", [P, T]) for u in range(2)]
        nr = [sb(f"nr{u}", [P, T]) for u in range(2)]
        xn = [sb(f"xn{r}", [P, T, D]) for r in range(R)]
        pts = [ps(f"pts{u}", [64, B]) for u in range(2)]
        ptv = [ps(f"ptv{u}", [96, B]) for u in range(2)]
        pk = [ps(f"pk{u}", [P, T, 256]) for u in range(2)]
        loaded = [sem(f"loaded{r}") for r in range(R)]
        turned = sem("turned")
        ts_ok = sem("ts_ok")
        k_ps = sem("k_ps")
        so_ok = sem("so_ok")
        act_ok = sem("act_ok")
        sg_ok = sem("sg_ok")
        y_ok = sem("y_ok")
        st_ok = sem("st_ok")
        rs_ok = sem("rs_ok")
        xn_ok = sem("xn_ok")
        stored = [sem(f"stored{r}") for r in range(R)]
        turn = sem("turn")

        def fence(eng):
            eng.sem_inc(turn, 1)

        block = ctx.enter_context(nc.Block())

        @block.sync
        def _(sp):
            def load(c, r, k, parts):
                sp.wait_ge(y_ok, due(c - 3))
                fence(sp)
                sp.dma_start(xr[r][0:parts].rearrange("p t c -> p (t c)"), rows_of(x, c, parts, XW)).then_inc(loaded[r], 16)
                sp.dma_start(ar[r][0:parts].rearrange("p t c -> p (t c)"), rows_of(agg, c, parts, 192)).then_inc(loaded[r], 16)

            def store(c, r, k, parts):
                sp.wait_ge(xn_ok, T * (c + 1))
                fence(sp)
                sp.dma_start(rows_of(out, c, parts, D), xn[r][0:parts].rearrange("p t c -> p (t c)")).then_inc(stored[r], 16)

            node_pipeline(sp, ((0, load), (5, store)))
            for r in range(R):
                sp.wait_ge(stored[r], 16 * ((NC - r) // R + 1))

        @block.tensor
        def _(pe):
            def turn_rows(c, r, k, parts):
                u = r % 2
                pe.wait_ge(loaded[r], 32 * (k + 1))
                pe.wait_ge(ts_ok, due(2 * (c - 1)))
                for t in range(T):
                    last = pe.transpose(ptv[u][:, t * P:(t + 1) * P], xr[r][:, t, S0:D], wt("ident"))
                last.then_inc(turned, 1)
                for t in range(T):
                    last = pe.transpose(pts[u][:, t * P:(t + 1) * P], xr[r][:, t, 0:S0], wt("ident"))
                last.then_inc(turned, 1)

            def skip(c, r, k, parts):
                u = r % 2
                pe.wait_ge(ts_ok, 2 * c + 2)
                pe.wait_ge(so_ok, due(c - 1))
                for t in range(T):
                    pe.matmul(pk[u][:, t, 96:192], tsv[u][:, t * P:(t + 1) * P], wt("nv_3"), start=True, stop=True)
                    last = pe.matmul(pk[u][:, t, 0:96], tss[u][:, t * P:(t + 1) * P], wt("ns_3"), start=True, stop=True)
                last.then_inc(k_ps, 1)

            node_pipeline(pe, ((0, turn_rows), (1, skip)))

        @block.scalar
        def _(a):
            def copy_turned(c, r, k, parts):
                u = r % 2
                a.wait_ge(k_ps, due(c - 1))
                a.wait_ge(turned, 2 * c + 1)
                a.activation(tsv[u][:], ptv[u][:], ACT.Copy).then_inc(ts_ok, 1)
                a.wait_ge(turned, 2 * c + 2)
                a.activation(tss[u][:], pts[u][:], ACT.Copy).then_inc(ts_ok, 1)

            def gates(c, r, k, parts):
                u = r % 2
                a.wait_ge(so_ok, c + 1)
                a.wait_ge(y_ok, due(c - 1))
                a.activation(sg[u][:, :, 0:S0], so[u][:, :, 0:S0], ACT.Silu).then_inc(act_ok, 1)
                a.activation(gt[u][:], so[u][:, :, S0:96], ACT.Tanh, scale=0.5).then_inc(act_ok, 1)

            def normalise(c, r, k, parts):
                u = r % 2
                a.wait_ge(rs_ok, 2 * c + 2)
                a.wait_ge(stored[r], 16 * k)
                for t in range(T):
                    a.activation(xn[r][:, t, :], y[u][:, t, :], ACT.Identity, bias=nr[u][:, t:t + 1], scale=rs[u][:, t:t + 1]).then_inc(xn_ok, 1)

            node_pipeline(a, ((0, copy_turned), (3, normalise), (1, gates)))

        @block.vector
        def _(v):
            def layer(c, r, k, parts):
                u = r % 2
                v.wait_ge(k_ps, c + 1)
                v.wait_ge(sg_ok, due(2 * (c - 1)))
                v.wait_ge(act_ok, due(2 * (c - 1)))
                v.scalar_tensor_tensor(so[u][:], ar[r][:], 1.0 / 32.0, pk[u][:, :, 0:192], ALU.mult, ALU.add).then_inc(so_ok, 1)

            def half_gates(c, r, k, parts):
                u = r % 2
                v.wait_ge(act_ok, 2 * c + 2)
                v.tensor_scalar(gt[u][:], gt[u][:], 0.5, 0.5, ALU.mult, ALU.add).then_inc(sg_ok, 1)

            def gate(c, r, k, parts):
                u = r % 2
                v.wait_ge(sg_ok, 2 * c + 1)
                v.tensor_tensor(sg[u][:, :, S0:D].rearrange("p t (u c) -> p t u c", c=3), so[u][:, :, 96:192].rearrange("p t (u c) -> p t u c", c=3),
                                gt[u][:].unsqueeze(3).to_broadcast([P, T, V1, 3]), ALU.mult).then_inc(sg_ok, 1)

            def total(c, r, k, parts):
                u = r % 2
                v.wait_ge(sg_ok, 2 * c + 2)
                v.wait_ge(xn_ok, due(T * (c - 1)))
                v.tensor_tensor(y[u][:], sg[u][:], xr[r][:, :, 0:D], ALU.add).then_inc(y_ok, 1)
                v.wait_ge(y_ok, c + 1)
                v.wait_ge(st_ok, 10 * c)
                for t in range(T):
                    v.bn_stats(st[:, t, :], y[u][:, t, :]).then_inc(st_ok, 1)

            def variance(c, r, k, parts):
                v.wait_ge(st_ok, 10 * c + 4)
                fence(v)
                for t in range(T):
                    v.bn_aggr(mv[:, t, :], st[:, t, :]).then_inc(st_ok, 1)
                v.wait_ge(st_ok, 10 * c + 8)
                v.wait_ge(rs_ok, 2 * c)
                v.tensor_scalar(ve[:], mv[:, :, 1], EPS, None, ALU.add).then_inc(st_ok, 1)
                v.tensor_scalar(nm[:], mv[:, :, 0], -1.0, None, ALU.mult).then_inc(st_ok, 1)

            node_pipeline(v, ((2, half_gates), (1, layer), (2, gate), (2, total), (2, variance)))

        @block.gpsimd
        def _(pool):
            def deviation(c, r, k, parts):
                u = r % 2
                pool.wait_ge(xn_ok, due(T * (c - 1)))
                fence(pool)
                pool.wait_ge(st_ok, 10 * (c + 1))
                fence(pool)
                pool.tensor_tensor(rs[u][:], ve[:], wt("mhalf"), ALU.pow).then_inc(rs_ok, 1)
                pool.wait_ge(rs_ok, 2 * c + 1)
                fence(pool)
                pool.tensor_tensor(nr[u][:], nm[:], rs[u][:], ALU.mult).then_inc(rs_ok, 1)

            node_pipeline(pool, ((2, deviation),))


def node_phase_2(nc, x, agg, xo, wt):
    H = 8
    with ExitStack() as ctx:
        sb = lambda n, s, d=F32: ctx.enter_context(nc.sbuf_tensor(f"{n}_n2", s, d))
        ps = lambda n, s: ctx.enter_context(nc.psum_tensor(f"{n}_n2", s, F32))
        sem = semaphores(nc, ctx, lambda n: f"{n}_n2")
        xr = [sb(f"xr{r}", [P, T, XW]) for r in range(R)]
        ar = [sb(f"ar{r}", [P, T, AW[2]]) for r in range(R)]
        den = [sb(f"den{u}", [P, T, H]) for u in range(2)]
        an = [sb(f"an{u}", [P, T, D]) for u in range(2)]
        tss = [sb(f"tss{u}", [65, B]) for u in range(2)]
        tsv = [sb(f"tsv{u}", [96, B]) for u in range(2)]
        x1 = [sb(f"x1{u}", [P, T, D]) for u in range(2)]
        xx = [sb(f"xx{r}", [P, T, D]) for r in range(R)]
        st = sb("st", [P, T, 6])
        mv = sb("mv", [P, T, 2])
        sq = sb("sq", [P, T, V3])
        var = sb("var", [P, 2, T])
        rs1 = sb("rsa", [P, 2, T])
        hat = sb("hat", [P, T, XW])
        t2s = sb("t2s", [65, B])
        t2v = sb("t2v", [96, B])
        hc = sb("hc", [P, B])
        tg = sb("tg", [96, 2, B])
        gv = sb("gv", [96, 2, B])
        up = sb("up", [P, T, D])
        y = [sb(f"y{u}", [P, T, D]) for u in range(2)]
        st2 = sb("st2", [P, T, 6])
        mv2 = sb("mv2", [P, T, 2])
        ve = sb("ve", [P, T])
        nm = sb("nm", [P, T])
        rs = [sb(f"rs{u}", [P, T]) for u in range(2)]
        nr = [sb(f"nr{u}", [P, T]) for u in range(2)]
        xn = [sb(f"xn{r}", [P, T, XW]) for r in range(R)]
        pts = ps("pts", [65, B])
        ptv = ps("ptv", [96, B])
        pk = ps("pk", [P, T, 256])
        pf = [ps(f"pf{k}", [P, B]) for k in range(4)]
        b_ps = sem("b_ps")
        b_ok = sem("b_ok")
        ones = sem("ones")
        loaded = [sem(f"loaded{r}") for r in range(R)]
        den_ok = sem("den_ok")
        an_ok = sem("an_ok")
        turned = sem("turned")
        ts_ok = sem("ts_ok")
        p_ps = sem("p_ps")
        x1_ok = sem("x1_ok")
        xx_ok = sem("xx_ok")
        sq_ok = sem("sq_ok")
        st_ok = sem("st_ok")
        r1_ok = sem("r1_ok")
        hat_ok = sem("hat_ok")
        turned2 = sem("turned2")
        t2_ok = sem("t2_ok")
        f_ps = sem("f_ps")
        act_ok = sem("act_ok")
        gv_ok = sem("gv_ok")
        o_ps = sem("o_ps")
        up_ok = sem("up_ok")
        y_ok = sem("y_ok")
        s2_ok = sem("s2_ok")
        rs_ok = sem("rs_ok")
        at_ok = sem("at_ok")
        xn_ok = sem("xn_ok")
        stored = [sem(f"stored{r}") for r in range(R)]
        turn = sem("turn")

        def fence(eng):
            eng.sem_inc(turn, 1)

        block = ctx.enter_context(nc.Block())

        @block.sync
        def _(sp):
            def load(c, r, k, parts):
                sp.wait_ge(hat_ok, due(4 * (c - 3)))
                fence(sp)
                sp.wait_ge(xx_ok, due(c - 3))
                fence(sp)
                sp.wait_ge(at_ok, due(c - 3))
                fence(sp)
                sp.dma_start(xr[r][0:parts].rearrange("p t c -> p (t c)"), rows_of(x, c, parts, XW)).then_inc(loaded[r], 16)
                sp.dma_start(ar[r][0:parts].rearrange("p t c -> p (t c)"), rows_of(agg, c, parts, AW[2])).then_inc(loaded[r], 16)

            def store(c, r, k, parts):
                sp.wait_ge(xn_ok, T * (c + 1))
                fence(sp)
                sp.dma_start(rows_of(xo, c, parts, XW), xn[r][0:parts].rearrange("p t c -> p (t c)")).then_inc(stored[r], 16)

            node_pipeline(sp, ((0, load), (6, store)))
            for r in range(R):
                sp.wait_ge(stored[r], 16 * ((NC - r) // R + 1))

        @block.tensor
        def _(pe):
            pe.matmul(pf[0][0:65, 0:320], wt("b0row"), wt("f1s")[0:64], start=True, stop=False)
            pe.matmul(pf[0][0:65, 0:320], wt("e64"), wt("f1b"), start=False, stop=True).then_inc(b_ps, 1)
            pe.wait_ge(b_ok, 1)
            pe.wait_ge(ones, 2)

            def turn_sums(c, r, k, parts):
                u = r % 2
                pe.wait_ge(an_ok, 2 * (c + 1))
                pe.wait_ge(ts_ok, 2 * c)
                pe.wait_ge(t2_ok, due(2 * (c - 1)))
                for t in range(T):
                    last = pe.transpose(ptv[:, t * P:(t + 1) * P], an[u][:, t, S0:D], wt("ident"))
                last.then_inc(turned, 1)
                for t in range(T):
                    last = pe.transpose(pts[0:64, t * P:(t + 1) * P], an[u][:, t, 0:S0], wt("ident"))
                last.then_inc(turned, 1)

            def project(c, r, k, parts):
                u = r % 2
                pe.wait_ge(ts_ok, 2 * c + 2)
                pe.wait_ge(x1_ok, c)
                pe.wait_ge(up_ok, due(2 * (c - 2)))
                for t in range(T):
                    pe.matmul(pk[:, t, S0:D], tsv[u][:, t * P:(t + 1) * P], wt("pv"), start=True, stop=True)
                    last = pe.matmul(pk[:, t, 0:S0], tss[u][:, t * P:(t + 1) * P], wt("pw"), start=True, stop=True)
                last.then_inc(p_ps, 1)

            def turn_rows(c, r, k, parts):
                pe.wait_ge(hat_ok, 4 * (c + 1))
                pe.wait_ge(t2_ok, 2 * c)
                pe.wait_ge(ts_ok, upto(2 * (c + 2), 2 * NC + 2))
                for t in range(T):
                    last = pe.transpose(ptv[:, t * P:(t + 1) * P], hat[:, t, 65:XW], wt("ident"))
                last.then_inc(turned2, 1)
                for t in range(T):
                    last = pe.transpose(pts[:, t * P:(t + 1) * P], hat[:, t, 0:65], wt("ident"))
                last.then_inc(turned2, 1)

            def first_product(c, r, k, parts):
                pe.wait_ge(t2_ok, 2 * c + 2)
                pe.wait_ge(act_ok, 3 * c)
                pe.wait_ge(gv_ok, 2 * c)
                pe.matmul(pf[0][:], wt("f1s")[:, 0:P], t2s[:], start=True, stop=True).then_inc(f_ps, 1)
                pe.matmul(pf[1][0:96], wt("f1s")[:, P:P + 96], t2s[:], start=True, stop=True).then_inc(f_ps, 1)
                pe.matmul(pf[2][0:96], wt("f1v")[:, 0:96], t2v[:], start=True, stop=True).then_inc(f_ps, 1)
                pe.matmul(pf[3][0:96], wt("f1v")[:, 96:192], t2v[:], start=True, stop=True).then_inc(f_ps, 1)

            def last_gates(c, r, k, parts):
                pe.wait_ge(act_ok, 3 * c + 1)
                pe.matmul(pf[0][0:96], wt("f1s")[:, P + 96:P + 192], t2s[:], start=True, stop=True).then_inc(f_ps, 1)

            def second_product(c, r, k, parts):
                pe.wait_ge(act_ok, 3 * c + 3)
                pe.wait_ge(gv_ok, 2 * c + 2)
                pe.wait_ge(up_ok, 2 * c)
                pe.wait_ge(x1_ok, upto(c + 3, NC + 1))
                for t in range(T):
                    cut = slice(t * P, (t + 1) * P)
                    pe.matmul(pk[:, t, S0:D], gv[:, 0, cut], wt("f2v0"), start=True, stop=False)
                    pe.matmul(pk[:, t, S0:D], gv[:, 1, cut], wt("f2v1"), start=False, stop=True)
                    pe.matmul(pk[:, t, 0:S0], wt("one"), wt("f2b"), start=True, stop=False)
                    last = pe.matmul(pk[:, t, 0:S0], hc[:, cut], wt("f2s"), start=False, stop=True)
                last.then_inc(o_ps, 1)

            node_pipeline(pe, ((1, project), (2, turn_rows), (3, second_product), (2, first_product), (0, turn_sums), (2, last_gates)))

        @block.scalar
        def _(a):
            a.wait_ge(b_ps, 1)
            a.activation(wt("f1s")[64:65], pf[0][64:65, 0:320], ACT.Copy).then_inc(b_ok, 1)

            def copy_sums(c, r, k, parts):
                u = r % 2
                a.wait_ge(p_ps, due(c - 1))
                a.wait_ge(turned, 2 * c + 1)
                a.activation(tsv[u][:], ptv[:], ACT.Copy).then_inc(ts_ok, 1)
                a.wait_ge(turned, 2 * c + 2)
                a.activation(tss[u][0:64], pts[0:64], ACT.Copy).then_inc(ts_ok, 1)

            def squares(c, r, k, parts):
                u = r % 2
                a.wait_ge(x1_ok, c + 1)
                a.wait_ge(sq_ok, 2 * c)
                a.activation(sq[:], x1[u][:, :, S0:D], ACT.Square).then_inc(sq_ok, 1)

            def copy_rows(c, r, k, parts):
                a.wait_ge(f_ps, 5 * c)
                a.wait_ge(turned2, 2 * c + 1)
                a.activation(t2v[:], ptv[:], ACT.Copy, scale=wt("ln2v")).then_inc(t2_ok, 1)
                a.wait_ge(turned2, 2 * c + 2)
                a.activation(t2s[:], pts[:], ACT.Copy, scale=wt("ln2w")).then_inc(t2_ok, 1)

            def activate(c, r, k, parts):
                a.wait_ge(f_ps, 5 * c + 1)
                a.wait_ge(o_ps, c)
                a.activation(hc[:], pf[0][:], ACT.Silu).then_inc(act_ok, 1)
                a.wait_ge(f_ps, 5 * c + 2)
                a.wait_ge(gv_ok, 2 * c)
                a.activation(tg[:, 0, :], pf[1][0:96], ACT.Tanh, scale=0.5).then_inc(act_ok, 1)

            def activate_last(c, r, k, parts):
                a.wait_ge(f_ps, 5 * c + 5)
                a.activation(tg[:, 1, :], pf[0][0:96], ACT.Tanh, scale=0.5).then_inc(act_ok, 1)

            def normalise(c, r, k, parts):
                u = r % 2
                a.wait_ge(rs_ok, 2 * c + 2)
                a.wait_ge(at_ok, c + 1)
                for t in range(T):
                    a.activation(xn[r][:, t, 0:D], y[u][:, t, :], ACT.Identity, bias=nr[u][:, t:t + 1], scale=rs[u][:, t:t + 1]).then_inc(xn_ok, 1)

            node_pipeline(a, ((4, normalise), (1, squares), (2, copy_rows), (2, activate), (0, copy_sums), (2, activate_last)))

        @block.vector
        def _(v):
            for u in range(2):
                v.memset(tss[u][64:65], 1.0).then_inc(ones, 1)

            def denominator(c, r, k, parts):
                u = r % 2
                v.wait_ge(loaded[r], 32 * (k + 1))
                v.wait_ge(an_ok, due(2 * (c - 1)))
                v.tensor_scalar(den[u][:], ar[r][:, :, 160:168], 1e-12, None, ALU.add).then_inc(den_ok, 1)
                v.wait_ge(den_ok, 2 * c + 1)
                v.reciprocal(den[u][:], den[u][:]).then_inc(den_ok, 1)

            def project(c, r, k, parts):
                u = r % 2
                v.wait_ge(p_ps, c + 1)
                v.wait_ge(xx_ok, due(c - 1))
                v.wait_ge(hat_ok, due(4 * (c - 1)))
                v.tensor_tensor(x1[u][:], pk[:, :, 0:D], xr[r][:, :, 0:D], ALU.add).then_inc(x1_ok, 1)
                v.wait_ge(x1_ok, c + 1)
                v.wait_ge(st_ok, 10 * c)
                for t in range(T):
                    v.bn_stats(st[:, t, :], x1[u][:, t, 0:S0]).then_inc(st_ok, 1)

            def moments(c, r, k, parts):
                v.wait_ge(st_ok, 10 * c + 4)
                v.wait_ge(hat_ok, 4 * c)
                fence(v)
                for t in range(T):
                    v.bn_aggr(mv[:, t, :], st[:, t, :]).then_inc(st_ok, 1)
                v.wait_ge(r1_ok, 2 * c)
                v.wait_ge(sq_ok, 2 * c + 1)
                v.tensor_reduce(var[:, 1, :], sq[:], AX.X, ALU.add).then_inc(sq_ok, 1)
                v.wait_ge(st_ok, 10 * c + 8)
                v.tensor_scalar(var[:, 0, :], mv[:, :, 1], EPS, None, ALU.add).then_inc(st_ok, 1)
                v.wait_ge(sq_ok, 2 * c + 2)
                v.tensor_scalar(var[:, 1, :], var[:, 1, :], 1.0 / V3, EPS, ALU.mult, ALU.add).then_inc(st_ok, 1)

            def gated(c, r, k, parts):
                for g in range(2):
                    v.wait_ge(act_ok, 3 * c + 2 + g)
                    v.wait_ge(f_ps, 5 * c + 3 + g)
                    if g == 0:
                        v.wait_ge(o_ps, c)
                    v.scalar_tensor_tensor(gv[:, g, :], tg[:, g, :], 1.0, pf[2 + g][0:96], ALU.add, ALU.mult).then_inc(gv_ok, 1)

            def hats(c, r, k, parts):
                u = r % 2
                v.wait_ge(turned2, 2 * c)
                v.tensor_tensor(hat[:, :, 0:S0], x1[u][:, :, 0:S0], mv[:, :, 0:1].to_broadcast([P, T, S0]), ALU.subtract).then_inc(hat_ok, 1)
                v.wait_ge(r1_ok, 2 * c + 2)
                v.tensor_tensor(hat[:, :, 65:XW], x1[u][:, :, S0:D], rs1[:, 1, :].unsqueeze(2).to_broadcast([P, T, V3]), ALU.mult).then_inc(hat_ok, 1)
                v.wait_ge(hat_ok, 4 * c + 1)
                v.tensor_tensor(hat[:, :, 0:S0], hat[:, :, 0:S0], rs1[:, 0, :].unsqueeze(2).to_broadcast([P, T, S0]), ALU.mult).then_inc(hat_ok, 1)
                v.tensor_copy(hat[:, :, S0], xr[r][:, :, D]).then_inc(hat_ok, 1)

            def output(c, r, k, parts):
                v.wait_ge(o_ps, c + 1)
                v.wait_ge(at_ok, c + 1)
                v.wait_ge(y_ok, c)
                v.tensor_tensor(up[:, :, 0:S0], pk[:, :, 0:S0], xn[r][:, :, D:XW].to_broadcast([P, T, S0]), ALU.mult).then_inc(up_ok, 1)
                v.scalar_tensor_tensor(up[:, :, S0:D], pk[:, :, S0:D], 0.5, xn[r][:, :, D:XW].to_broadcast([P, T, V3]), ALU.mult, ALU.mult).then_inc(up_ok, 1)

            def total(c, r, k, parts):
                u = r % 2
                v.wait_ge(up_ok, 2 * c + 2)
                v.wait_ge(xx_ok, c + 1)
                v.wait_ge(xn_ok, due(T * (c - 1)))
                v.tensor_tensor(y[u][:], up[:], xx[r][:], ALU.add).then_inc(y_ok, 1)
                v.wait_ge(y_ok, c + 1)
                v.wait_ge(s2_ok, 10 * c)
                for t in range(T):
                    v.bn_stats(st2[:, t, :], y[u][:, t, :]).then_inc(s2_ok, 1)

            def variance(c, r, k, parts):
                v.wait_ge(s2_ok, 10 * c + 4)
                fence(v)
                for t in range(T):
                    v.bn_aggr(mv2[:, t, :], st2[:, t, :]).then_inc(s2_ok, 1)
                v.wait_ge(s2_ok, 10 * c + 8)
                v.wait_ge(rs_ok, 2 * c)
                v.tensor_scalar(ve[:], mv2[:, :, 1], EPS, None, ALU.add).then_inc(s2_ok, 1)
                v.tensor_scalar(nm[:], mv2[:, :, 0], -1.0, None, ALU.mult).then_inc(s2_ok, 1)

            node_pipeline(v, ((0, denominator), (3, gated), (1, project), (1, moments), (3, output), (3, total), (1, hats), (3, variance)))

        @block.gpsimd
        def _(pool):
            def shares(c, r, k, parts):
                u = r % 2
                pool.wait_ge(turned, due(2 * (c - 1)))
                fence(pool)
                pool.wait_ge(den_ok, 2 * c + 2)
                fence(pool)
                for lo, hi in ((0, 64), (64, 160)):
                    pool.tensor_tensor(an[u][:, :, lo:hi].rearrange("p t (h k) -> p t h k", h=H), ar[r][:, :, lo:hi].rearrange("p t (h k) -> p t h k", h=H),
                                       den[u][:].unsqueeze(3).to_broadcast([P, T, H, (hi - lo) // H]), ALU.mult).then_inc(an_ok, 1)

            def powers(c, r, k, parts):
                pool.wait_ge(st_ok, 10 * (c + 1))
                fence(pool)
                pool.wait_ge(hat_ok, 4 * c)
                fence(pool)
                pool.tensor_tensor(rs1[:], var[:], wt("mhalf8").rearrange("p (a t) -> p a t", a=2), ALU.pow).then_inc(r1_ok, 1)
                pool.wait_ge(r1_ok, 2 * c + 1)
                fence(pool)
                pool.tensor_tensor(rs1[:], rs1[:], xr[r][:, :, D].unsqueeze(1).to_broadcast([P, 2, T]), ALU.mult).then_inc(r1_ok, 1)

            def attribute(c, r, k, parts):
                pool.wait_ge(stored[r], 16 * k)
                fence(pool)
                pool.tensor_copy(xn[r][:, :, D:XW], xr[r][:, :, D:XW]).then_inc(at_ok, 1)

            def twice(c, r, k, parts):
                u = r % 2
                pool.wait_ge(x1_ok, c + 1)
                fence(pool)
                pool.wait_ge(y_ok, due(c - 3))
                fence(pool)
                pool.tensor_tensor(xx[r][:], x1[u][:], xr[r][:, :, 0:D], ALU.add).then_inc(xx_ok, 1)

            def deviation(c, r, k, parts):
                u = r % 2
                pool.wait_ge(xn_ok, due(T * (c - 1)))
                fence(pool)
                pool.wait_ge(s2_ok, 10 * (c + 1))
                fence(pool)
                pool.tensor_tensor(rs[u][:], ve[:], wt("mhalf"), ALU.pow).then_inc(rs_ok, 1)
                pool.wait_ge(rs_ok, 2 * c + 1)
                fence(pool)
                pool.tensor_tensor(nr[u][:], nm[:], rs[u][:], ALU.mult).then_inc(rs_ok, 1)

            node_pipeline(pool, ((0, shares), (1, powers), (1, twice), (3, deviation), (1, attribute)))


def build(nc, ins, out):
    with ExitStack() as ctx:
        wsb = ctx.enter_context(nc.sbuf_tensor("wsb", [P, WCOLS], F32))
        w_in = ctx.enter_context(nc.semaphore("w_in"))

        def wt(name):
            if name in ("mhalf", "mhalf8"):
                return wt("mhalfn")[:, 0:T if name == "mhalf" else 2 * T]
            r, c, at = SLOTS[name]
            return wsb[0:r, at:at + c]

        def table(name, rows, w, d=F32):
            return nc.dram_tensor(name, (rows, w), d, kind="Internal").ap()

        agg = [table(f"agg{k}", NA, AW[k]) for k in range(4)]
        xs = [ins["x"]] + [table(f"x{k}", N, XW) for k in (1, 2, 3)]
        dram = dict(ins)
        dram["cidx"] = nc.dram_tensor("cidx", (NBP, P, T), U32, kind="Internal").ap()
        dram["hid"] = table("hid", 64, NBP * B)
        dram["val"] = nc.dram_tensor("val", (NB, P, T, AW[2]), F32, kind="Internal").ap()
        dram["att"] = table("att", NB * B, 8)
        mx = [table(f"mx{u}", NA, 8) for u in range(2)]
        with nc.Block() as block:
            @block.sync
            def _(sp):
                sp.dma_start(wsb[:], ins["w"]).then_inc(w_in, 16)
                sp.dma_start(dram["cidx"][NB:NBP].rearrange("a p t -> (a p) t"), ins["dst_t"][NB:NBP].rearrange("a p t -> (a p) t").bitcast(U32)).then_inc(w_in, 16)
                sp.dma_start(dram["hid"][:, NB * B:NBP * B], ins["ea64T"][:, NB * B:NBP * B]).then_inc(w_in, 16)
                sp.wait_ge(w_in, 48)
        edge_phase_01(nc, 0, xs[0], agg[0], dram, wt, agg)
        node_phase_01(nc, 0, xs[0], agg[0], xs[1], wt, XW)
        edge_phase_01(nc, 1, xs[1], agg[1], dram, wt, agg)
        node_phase_01(nc, 1, xs[1], agg[1], xs[2], wt, XW)
        hidden_phase(nc, dram, wt)
        edge_phase_23(nc, 2, xs[2], None, dram, wt)
        attention_max_phase(nc, dram, mx, wt)
        attention_sum_phase(nc, dram, mx[0], agg[2], wt)
        node_phase_2(nc, xs[2], agg[2], xs[3], wt)
        edge_phase_23(nc, 3, xs[3], agg[3], dram, wt)
        node_phase_3(nc, xs[3], agg[3], out, wt)


def lay_out(inputs):
    g = {k: np.asarray(v) for k, v in inputs.items()}
    w = np.zeros((P, WCOLS), np.float32)

    def put(name, r, c, a, step=1):
        rows, cols, at = SLOTS[name]
        w[r:r + step * (a.shape[0] - 1) + 1:step, at + c:at + c + step * (a.shape[1] - 1) + 1:step] = a

    def put3(name, r, c, a):
        for k in range(3):
            put(name, r + k, c + k, a, 3)

    def rep3(name, c, a):
        rows, cols, at = SLOTS[name]
        for k in range(3):
            w[0:a.shape[0], at + c + k:at + c + 3 * a.shape[1]:3] = a

    names = [("fcW1", "fcW2", "W1_s", "W1_v", "W2_s", "W2_v", "W3", "W_sc_s", "W_sc_v"),
             ("Wfc1", "Wfc3", "Wl1_0", "Wl1_1", "Wl2_s", "Wl2_v", "Wa", "Wsc0", "Wsc1")]
    for l in (0, 1):
        h, w2, ws, wv, os_, ov, oa, ns, nv = (g[f"L{l}_gnn_{n}"] for n in names[l])
        put(f"h{l}", 0, 0, h)
        put(f"w1_{l}", 0, 0, w2[:, 0:128])
        put(f"w2_{l}", 0, 0, w2[:, 160:192])
        rep3(f"w2_{l}", 32, w2[:, 128:160])
        put(f"f1_{l}", 0, 0, ws)
        put(f"f1_{l}", 64, 64, ws)
        put(f"f2_{l}", 0, 0, wv)
        put3(f"f2_{l}", 32, 32, wv)
        put(f"o1_{l}", 64, 0, ov[0:64])
        put(f"o1_{l}", 0, 32, os_[0:64])
        put(f"o1_{l}", 0, 192, oa[0:64])
        put(f"o2_{l}", 0, 0, os_[64:96])
        put(f"o2_{l}", 0, 160, oa[64:96])
        put3(f"o2_{l}", 32, 64, ov[64:96])
        put(f"ns_{l}", 0, 0, ns)
        put3(f"nv_{l}", 0, 0, nv)
    put("hh1", 0, 0, g["L1_gnn_Wfc2"])
    put("ident", 0, 0, np.eye(P, dtype=np.float32))
    e = np.arange(B).reshape(T, P)
    before = (np.arange(B)[None, None, :] < e.T[:, :, None]).astype(np.float32)
    put("before", 0, 0, before.reshape(P, T * B))
    put("spare", 0, 0, (N + e.T).astype(np.float32))
    put("mhalfn", 0, 0, np.full((P, NBP * T), -0.5, np.float32))
    put("one", 0, 0, np.ones((1, 128), np.float32))
    put("e64", 0, 64, np.ones((1, 1), np.float32))
    for l in (2, 3):
        so = 128 if l == 2 else 96
        k = "L2_gnn_" if l == 2 else "L3_gnn_"
        w2 = g[k + ("rw3" if l == 2 else "W_fc2")]
        put(f"w1_{l}", 0, 0, w2[:, 0:128])
        rep3(f"w2_{l}", 0, w2[:, 128:160])
        put(f"w2_{l}", 0, 96, w2[:, 160:192])
        rep3(f"w3_{l}", 0, w2[:, 192:224])
        ends = ((g[k + "msrc_ws"], g[k + "msrc_wv"]), (g[k + "mdst_ws"], g[k + "mdst_wv"])) if l == 2 else ((g[k + "W_nl0"], g[k + "W_nl1"]),)
        for s, (ws, wv) in enumerate(ends):
            put(f"f1_{l}{s}", 0, 0, ws)
            put(f"f1_{l}{s}", 0, 64, ws)
            put3(f"f2_{l}{s}", 0, 0, wv)
            put(f"f2_{l}{s}", 96, 96, wv)
        os_, ov = (g[k + "lin_ws"], g[k + "lin_wv"]) if l == 2 else (g[k + "W_out_s"], g[k + "W_out_v"])
        put(f"o1_{l}", 0, 32, os_[0:64])
        put(f"o1_{l}", 64, 0, ov[0:64])
        put3(f"o2_{l}", 0, so, ov[64:96])
        put(f"o2_{l}", 96, 0, os_[64:96])
        put3(f"o3_{l}", 0, 0, ov[96:128])
    put("h3", 0, 0, g["L3_gnn_W_fc1"])
    put("ns_3", 0, 0, g["L3_gnn_W_skip0"])
    put3("nv_3", 0, 0, g["L3_gnn_W_skip1"])
    q = {n[7:]: a for n, a in g.items() if n.startswith("L2_gnn_")}
    col = lambda a: np.reshape(a, (-1, 1))
    row = lambda a: np.reshape(a, (1, -1))

    def col3(name, r, a):
        for k in range(3):
            put(name, r + k, 0, col(a), 3)

    put("roff0", 0, 0, col(q["roff"][0:128]))
    col3("roff1", 0, q["roff"][128:160])
    put("roff1", 96, 0, col(q["roff"][160:192]))
    col3("roff2", 0, q["roff"][192:224])
    put("mb2", 0, 0, col(q["mdst_bs"]))
    put("mb2", 64, 0, col(q["mdst_bs"]))
    put("ln1w", 0, 0, col(q["ln1_w0"]))
    put("ln1b", 0, 0, col(q["ln1_b0"]))
    col3("ln1v", 0, q["ln1_w1"])
    put("ln1v", 96, 0, col(q["ln1_w1"]))
    put("adot", 0, 0, np.broadcast_to(row(q["alpha_dot"]), (P, 64)))
    put("linb", 0, 0, row(q["lin_bs"]))
    for k in range(2):
        put(f"rw{k}", 0, 0, q[f"rw{k + 1}"])
        put(f"rb{k}", 0, 0, row(q[f"rb{k + 1}"]))
        put(f"rg{k}", 0, 0, col(q[f"rg{k + 1}"]))
        put(f"rbe{k}", 0, 0, col(q[f"rbe{k + 1}"]))
    put("pw", 0, 0, q["proj_ws"])
    put("pw", 64, 0, row(q["proj_bs"]))
    put3("pv", 0, 0, q["proj_wv"])
    put("ln2w", 0, 0, col(q["ln2_w0"]))
    put("ln2w", 64, 0, np.ones((1, 1), np.float32))
    col3("ln2v", 0, q["ln2_w1"])
    put("b0row", 0, 64, col(q["ln2_b0"]))
    put("f1s", 0, 0, q["f1_ws"][:, 0:128])
    rep3("f1s", 128, q["f1_ws"][:, 128:192])
    put("f1b", 0, 0, row(q["f1_bs"][0:128]))
    rep3("f1b", 128, row(q["f1_bs"][128:192]))
    put3("f1v", 0, 0, q["f1_wv"])
    put("f2s", 0, 0, q["f2_ws"])
    put("f2b", 0, 0, row(q["f2_bs"]))
    put3("f2v0", 0, 0, q["f2_wv"][0:32])
    put3("f2v1", 0, 0, q["f2_wv"][32:64])

    def edges(a, fill):
        p = np.full((NBP * B,) + a.shape[1:], fill, a.dtype)
        p[0:E] = a
        return p

    def tiles(a):
        return np.ascontiguousarray(a.reshape((NBP, T, P) + a.shape[1:]).swapaxes(1, 2))

    x = np.empty((N, XW), np.float32)
    x[:, 0:D] = g["x"]
    x[:, D:] = g["node_vec1"]
    o = {"w": w, "x": x}
    for side in ("src", "dst"):
        o[side + "_g"] = tiles(edges(g[side], 0)).view(np.uint32)
        o[side + "_t"] = tiles(edges(g[side], N))
        o[side + "_r"] = edges(g[side], N).reshape(NBP, B)
    o["ea8T"] = np.ascontiguousarray(edges(g["edge_attr_8"], 1.0).T)
    o["ea64T"] = np.ascontiguousarray(edges(g["edge_attr_64"], 1.0).T)
    e3 = edges(g["edge_attr_3"], 1.0).reshape(NBP * T, P, 3)
    o["ea3"] = np.ascontiguousarray(e3.swapaxes(0, 1)).reshape(P, NBP * T * 3)
    o["ea4"] = tiles(edges(g["edge_attr_4"], 1.0))
    return o


def kernel(**inputs):
    from concourse import bacc
    from concourse.bass_utils import run_bass_kernel_spmd as run

    nc = bacc.Bacc("TRN2", target_bir_lowering=False, num_devices=1)
    arrays = lay_out(inputs)
    ins = {k: nc.dram_tensor(f"in_{k}", a.shape, mybir.dt.from_np(a.dtype), kind="ExternalInput").ap() for k, a in arrays.items()}
    out = nc.dram_tensor("out", (N, D), F32, kind="ExternalOutput").ap()
    build(nc, ins, out)
    r = run(nc, [{f"in_{k}": a for k, a in arrays.items()}], core_ids=[0])
    return r.results[0]["out"]
```
